# Optimizing a Trainium2 kernel written in Bass

```python
import numpy as np
import jax
import jax.numpy as jnp

def _softmax(x, axis=-1):
    return jax.nn.softmax(x, axis=axis)

def _gelu(x):
    return jax.nn.gelu(x, approximate=True)

def _silu(x):
    return jax.nn.silu(x)

def _sigmoid(x):
    return jax.nn.sigmoid(x)

def _layernorm(x, axis=-1, eps=1e-05):
    m = jnp.mean(x, axis=axis, keepdims=True)
    v = jnp.var(x, axis=axis, keepdims=True)
    return (x - m) / jnp.sqrt(v + eps)

def _scatter_add(tgt, idx, src, axis=0):
    return tgt.at[idx].add(src)

def _segment_sum(src, seg, n):
    return jax.ops.segment_sum(src, seg, n)
kernel_name = 'mk_decoder_postln_d2_seqx_r8_d99d10'

def setup_inputs(seed: int=0):
    np.random.seed(seed)
    _w = jnp.asarray

    def _rec_inputs():
        import jax
        import jax.numpy as jnp
        _rk = jax.random.key(seed)
        x = -0.0002928 + 1 * jax.random.normal(jax.random.fold_in(_rk, 1), (64, 128, 128), jnp.float32)
        _lenS = 128 - jax.random.randint(jax.random.fold_in(_rk, 7), (64,), 0, max(1, 128 // 4) + 1, jnp.int32)
        _lenS2 = 77 - jax.random.randint(jax.random.fold_in(_rk, 8), (64,), 0, max(1, 77 // 4) + 1, jnp.int32)
        _ctx_1024P = jax.random.normal(jax.random.fold_in(_rk, 11), (64, 16, 128), jnp.float32)
        _ctx_1024c = jax.random.dirichlet(jax.random.fold_in(_rk, 511), 0.3 * jnp.ones((16,), jnp.float32), (64, 77))
        _ctx_1024t = jnp.einsum('bsk,bkd->bsd', _ctx_1024c, _ctx_1024P)
        _ctx_1024t = _ctx_1024t * jax.lax.rsqrt(jnp.mean(jnp.square(_ctx_1024t)) + 1e-12) * 0.953939
        ctx_1024 = -1.39393e-06 + 0.999914 * (_ctx_1024t + 0.3 * jax.random.normal(jax.random.fold_in(_rk, 611), (64, 77, 128), jnp.float32))
        fside_BxSxS2_0 = jax.random.uniform(jax.random.fold_in(_rk, 12), (64, 128, 77), jnp.float32, 0.0, 1)
        _validS = jnp.arange(128)[None, :] < _lenS[:, None]
        _validS2 = jnp.arange(77)[None, :] < _lenS2[:, None]
        _causal = jnp.tril(jnp.ones((128, 128), dtype=bool))
        mask_BxSxS2_ik1 = jnp.where(jnp.broadcast_to(_validS2[:, None, :], (64, 128, 77)), 1, 0).astype(jnp.int32)
        return (x, ctx_1024, fside_BxSxS2_0, mask_BxSxS2_ik1)
    x, ctx_1024, fside_BxSxS2_0, mask_BxSxS2_ik1 = _rec_inputs()

    def _L0_attn_setup():
        import jax, jax.numpy as jnp
        import numpy as np
        from jax import lax
        B, L, D_MODEL = (2, 256, 128)
        EXPAND = 2
        D_INNER = D_MODEL * EXPAND
        D_STATE = 16
        D_CONV = 4
        DT_RANK = (D_MODEL + 15) // 16
        EPS = 1e-05

        def _mamba_params(key, pfx, scale=0.02):
            ks = jax.random.split(key, 6)
            return {pfx + '_Win': jax.random.normal(ks[0], (D_MODEL, 2 * D_INNER), jnp.float32) * scale, pfx + '_convw': jax.random.normal(ks[1], (D_INNER, D_CONV), jnp.float32) * scale, pfx + '_convb': jnp.zeros((D_INNER,), jnp.float32), pfx + '_Wx': jax.random.normal(ks[2], (D_INNER, DT_RANK + 2 * D_STATE), jnp.float32) * scale, pfx + '_Wdt': jax.random.normal(ks[3], (DT_RANK, D_INNER), jnp.float32) * scale, pfx + '_bdt': jax.random.uniform(ks[4], (D_INNER,), jnp.float32, -4.0, -2.0), pfx + '_Alog': jnp.log(jnp.broadcast_to(jnp.arange(1, D_STATE + 1, dtype=jnp.float32), (D_INNER, D_STATE))).copy(), pfx + '_D': jnp.ones((D_INNER,), jnp.float32), pfx + '_Wout': jax.random.normal(ks[5], (D_INNER, D_MODEL), jnp.float32) * scale}

        def _layernorm(x, w, b):
            mu = x.mean(-1, keepdims=True)
            xc = x - mu
            v = (xc * xc).mean(-1, keepdims=True)
            return xc * lax.rsqrt(v + EPS) * w + b

        def _causal_dwconv(x, w, b):
            xc = x.transpose(0, 2, 1)
            out = lax.conv_general_dilated(xc, w[:, None, :], window_strides=(1,), padding=[(D_CONV - 1, 0)], feature_group_count=D_INNER, dimension_numbers=('NCH', 'OIH', 'NCH'))
            return (out + b[None, :, None]).transpose(0, 2, 1)

        def _selective_scan(u, dt, A, Bm, Cm, Dp):
            h0 = jnp.zeros((u.shape[0], D_INNER, D_STATE), u.dtype)

            def step(h, inp):
                u_t, dt_t, B_t, C_t = inp
                dA = jnp.exp(dt_t[:, :, None] * A)
                h = dA * h + (dt_t * u_t)[:, :, None] * B_t[:, None, :]
                y = jnp.einsum('bds,bs->bd', h, C_t)
                return (h, y)
            _, ys = lax.scan(step, h0, (u.transpose(1, 0, 2), dt.transpose(1, 0, 2), Bm.transpose(1, 0, 2), Cm.transpose(1, 0, 2)))
            return ys.transpose(1, 0, 2) + u * Dp

        def _mamba(x, Win, convw, convb, Wx, Wdt, bdt, Alog, Dp, Wout):
            xz = x @ Win
            xi, z = jnp.split(xz, 2, axis=-1)
            xi = jax.nn.silu(_causal_dwconv(xi, convw, convb))
            xdbc = xi @ Wx
            dt_in = xdbc[..., :DT_RANK]
            Bm = xdbc[..., DT_RANK:DT_RANK + D_STATE]
            Cm = xdbc[..., DT_RANK + D_STATE:]
            dt = jax.nn.softplus(dt_in @ Wdt + bdt)
            A = -jnp.exp(Alog)
            y = _selective_scan(xi, dt, A, Bm, Cm, Dp)
            return y * jax.nn.silu(z) @ Wout
        key = jax.random.key(seed)
        k = jax.random.split(key, 6)
        inp = {'x': jax.random.normal(k[0], (B, L, D_MODEL), jnp.float32)}
        inp.update(_mamba_params(k[1], 'fw'))
        inp.update(_mamba_params(k[2], 'bw'))
        inp.update({'fwn_w': jnp.ones((D_MODEL,), jnp.float32), 'fwn_b': jnp.zeros((D_MODEL,), jnp.float32), 'fin_w': jnp.ones((D_MODEL,), jnp.float32), 'fin_b': jnp.zeros((D_MODEL,), jnp.float32), 'ff_W1': jax.random.normal(k[3], (D_MODEL, D_MODEL * EXPAND), jnp.float32) * 0.02, 'ff_b1': jnp.zeros((D_MODEL * EXPAND,), jnp.float32), 'ff_W2': jax.random.normal(k[4], (D_MODEL * EXPAND, D_MODEL), jnp.float32) * 0.02, 'ff_b2': jnp.zeros((D_MODEL,), jnp.float32)})
        return inp
    _L0_attn_all = _L0_attn_setup()
    _L0_attn_in = {k: v for k, v in _L0_attn_all.items() if k in ('fw_Win', 'fw_convw', 'fw_convb', 'fw_Wx', 'fw_Wdt', 'fw_bdt', 'fw_Alog', 'fw_D', 'fw_Wout', 'bw_Win', 'bw_convw', 'bw_convb', 'bw_Wx', 'bw_Wdt', 'bw_bdt', 'bw_Alog', 'bw_D', 'bw_Wout', 'fwn_w', 'fwn_b', 'fin_w', 'fin_b', 'ff_W1', 'ff_b1', 'ff_W2', 'ff_b2')}
    del _L0_attn_all

    def _L0_xattn_setup():
        import jax, jax.numpy as jnp
        import numpy as np
        NUM_HEADS = 16
        HIDDEN = 128
        B, S = (2, 256)

        def _split_heads(x, H):
            b, s, d = x.shape
            return x.reshape(b, s, H, d // H).transpose(0, 2, 1, 3)
        key = jax.random.key(seed)
        ks = jax.random.split(key, 14)
        D = HIDDEN
        scale = 1.0 / np.sqrt(D)
        inp = {'query': jax.random.normal(ks[0], (B, S, D), jnp.float32), 'key_in': jax.random.normal(ks[1], (B, S, D), jnp.float32), 'value': jax.random.normal(ks[2], (B, S, D), jnp.float32), 'group_prob': jax.random.uniform(ks[3], (B, S, S), jnp.float32), 'mask': jax.random.randint(ks[4], (B, S, S), 0, 2, jnp.int32), 'wq_k': jax.random.normal(ks[5], (D, D), jnp.float32) * scale, 'wq_b': jnp.zeros((D,), jnp.float32), 'wk_k': jax.random.normal(ks[6], (D, D), jnp.float32) * scale, 'wk_b': jnp.zeros((D,), jnp.float32), 'wv_k': jax.random.normal(ks[7], (D, D), jnp.float32) * scale, 'wv_b': jnp.zeros((D,), jnp.float32), 'wo_k': jax.random.normal(ks[8], (D, D), jnp.float32) * scale, 'wo_b': jnp.zeros((D,), jnp.float32)}
        return inp
    _L0_xattn_all = _L0_xattn_setup()
    _L0_xattn_in = {k: v for k, v in _L0_xattn_all.items() if k in ('wq_k', 'wq_b', 'wk_k', 'wk_b', 'wv_k', 'wv_b', 'wo_k', 'wo_b')}
    del _L0_xattn_all

    def _L0_ffn_setup():
        import jax, jax.numpy as jnp
        import numpy as np
        B, S, H, NH, E, F = (4, 128, 128, 16, 8, 512)
        D = H // NH
        EPS = 1e-05

        def _layernorm(x, g, b):
            mu = jnp.mean(x, axis=-1, keepdims=True)
            var = jnp.var(x, axis=-1, keepdims=True)
            return (x - mu) * jax.lax.rsqrt(var + EPS) * g + b
        key = jax.random.key(seed)
        ks = jax.random.split(key, 16)
        s = 0.02
        return {'x': jax.random.normal(ks[0], (B, S, H), jnp.float32), 'ln1_g': jnp.ones((H,), jnp.float32), 'ln1_b': jnp.zeros((H,), jnp.float32), 'ln2_g': jnp.ones((H,), jnp.float32), 'ln2_b': jnp.zeros((H,), jnp.float32), 'wq': jax.random.normal(ks[1], (H, H), jnp.float32) * s, 'bq': jnp.zeros((H,), jnp.float32), 'wk': jax.random.normal(ks[2], (H, H), jnp.float32) * s, 'bk': jnp.zeros((H,), jnp.float32), 'wv': jax.random.normal(ks[3], (H, H), jnp.float32) * s, 'bv': jnp.zeros((H,), jnp.float32), 'wo': jax.random.normal(ks[4], (H, H), jnp.float32) * s, 'bo': jnp.zeros((H,), jnp.float32), 'gate_w': jax.random.normal(ks[5], (H, E), jnp.float32) * s, 'gate_b': jnp.zeros((E,), jnp.float32), 'w1': jax.random.normal(ks[6], (E, H, F), jnp.float32) * s, 'b1': jnp.zeros((E, F), jnp.float32), 'w2': jax.random.normal(ks[7], (E, F, H), jnp.float32) * s, 'b2': jnp.zeros((E, H), jnp.float32)}
    _L0_ffn_all = _L0_ffn_setup()
    _L0_ffn_in = {k: v for k, v in _L0_ffn_all.items() if k in ('ln1_g', 'ln1_b', 'ln2_g', 'ln2_b', 'wq', 'bq', 'wk', 'bk', 'wv', 'bv', 'wo', 'bo', 'gate_w', 'gate_b', 'w1', 'b1', 'w2', 'b2')}
    del _L0_ffn_all

    def _L1_attn_setup():
        import jax, jax.numpy as jnp
        import numpy as np
        NUM_HEADS = 16
        EPS = float(jnp.finfo(jnp.float32).eps)

        def rms_norm(x, w):
            ms = jnp.mean(x * x, axis=-1, keepdims=True)
            return x * jax.lax.rsqrt(ms + EPS) * w
        key = jax.random.key(seed)
        k = jax.random.split(key, 5)
        B, N, D = (4, 256, 128)
        Dh = D // NUM_HEADS
        return {'x': jax.random.normal(k[0], (B, N, D), dtype=jnp.float32), 'Wq': jax.random.normal(k[1], (D, D), dtype=jnp.float32) * 0.02, 'Wk': jax.random.normal(k[2], (D, D), dtype=jnp.float32) * 0.02, 'Wv': jax.random.normal(k[3], (D, D), dtype=jnp.float32) * 0.02, 'Wo': jax.random.normal(k[4], (D, D), dtype=jnp.float32) * 0.02, 'qn_w': jnp.ones((Dh,), dtype=jnp.float32), 'kn_w': jnp.ones((Dh,), dtype=jnp.float32)}
    _L1_attn_all = _L1_attn_setup()
    _L1_attn_in = {k: v for k, v in _L1_attn_all.items() if k in ('Wq', 'Wk', 'Wv', 'Wo', 'qn_w', 'kn_w')}
    del _L1_attn_all

    def _L1_xattn_setup():
        import jax, jax.numpy as jnp
        import numpy as np
        D_MODEL = 128
        NUM_HEADS = 16
        DEPTH = D_MODEL // NUM_HEADS

        def _split_heads(x):
            B, S, _ = x.shape
            return x.reshape(B, S, NUM_HEADS, DEPTH).transpose(0, 2, 1, 3)
        key = jax.random.key(seed)
        ks = jax.random.split(key, 12)
        B, S = (4, 256)
        scale = 1.0 / np.sqrt(D_MODEL)
        inp = {'v': jax.random.normal(ks[0], (B, S, D_MODEL), jnp.float32), 'k': jax.random.normal(ks[1], (B, S, D_MODEL), jnp.float32), 'q': jax.random.normal(ks[2], (B, S, D_MODEL), jnp.float32), 'wq_w': jax.random.normal(ks[3], (D_MODEL, D_MODEL), jnp.float32) * scale, 'wq_b': jnp.zeros((D_MODEL,), jnp.float32), 'wk_w': jax.random.normal(ks[4], (D_MODEL, D_MODEL), jnp.float32) * scale, 'wk_b': jnp.zeros((D_MODEL,), jnp.float32), 'wv_w': jax.random.normal(ks[5], (D_MODEL, D_MODEL), jnp.float32) * scale, 'wv_b': jnp.zeros((D_MODEL,), jnp.float32), 'wo_w': jax.random.normal(ks[6], (D_MODEL, D_MODEL), jnp.float32) * scale, 'wo_b': jnp.zeros((D_MODEL,), jnp.float32)}
        return inp
    _L1_xattn_all = _L1_xattn_setup()
    _L1_xattn_in = {k: v for k, v in _L1_xattn_all.items() if k in ('wq_w', 'wq_b', 'wk_w', 'wk_b', 'wv_w', 'wv_b', 'wo_w', 'wo_b')}
    del _L1_xattn_all

    def _L1_ffn_setup():
        import jax, jax.numpy as jnp
        import numpy as np
        QMAX = 127.0

        def _ste_round(v):
            return v + jax.lax.stop_gradient(jnp.round(v) - v)

        def _act_fake_quant(x, clip_factor):
            scale = jax.nn.sigmoid(clip_factor) * jnp.max(jnp.abs(x)) / QMAX
            return jnp.clip(_ste_round(x / scale), -QMAX - 1.0, QMAX) * scale

        def _weight_fake_quant(w):
            scale = jnp.max(jnp.abs(w), axis=1, keepdims=True) / QMAX
            return jnp.clip(_ste_round(w / scale), -QMAX - 1.0, QMAX) * scale
        key = jax.random.key(seed)
        k1, k2, k3, k4 = jax.random.split(key, 4)
        B, S, H, I = (8, 1024, 128, 352)
        return {'x': jax.random.normal(k1, (B, S, H), dtype=jnp.float32), 'clip_x': jnp.full((1,), 4.0, dtype=jnp.float32), 'clip_down': jnp.full((1,), 4.0, dtype=jnp.float32), 'w_gate': jax.random.normal(k2, (I, H), dtype=jnp.float32) * 0.02, 'w_up': jax.random.normal(k3, (I, H), dtype=jnp.float32) * 0.02, 'w_down': jax.random.normal(k4, (H, I), dtype=jnp.float32) * 0.02}
    _L1_ffn_all = _L1_ffn_setup()
    _L1_ffn_in = {k: v for k, v in _L1_ffn_all.items() if k in ('clip_x', 'clip_down', 'w_gate', 'w_up', 'w_down')}
    del _L1_ffn_all
    return {'x': x, 'ctx_1024': ctx_1024, 'fside_BxSxS2_0': fside_BxSxS2_0, 'mask_BxSxS2_ik1': mask_BxSxS2_ik1, 'L0_attn_fw_Win': _L0_attn_in['fw_Win'], 'L0_attn_fw_convw': _L0_attn_in['fw_convw'], 'L0_attn_fw_convb': _L0_attn_in['fw_convb'], 'L0_attn_fw_Wx': _L0_attn_in['fw_Wx'], 'L0_attn_fw_Wdt': _L0_attn_in['fw_Wdt'], 'L0_attn_fw_bdt': _L0_attn_in['fw_bdt'], 'L0_attn_fw_Alog': _L0_attn_in['fw_Alog'], 'L0_attn_fw_D': _L0_attn_in['fw_D'], 'L0_attn_fw_Wout': _L0_attn_in['fw_Wout'], 'L0_attn_bw_Win': _L0_attn_in['bw_Win'], 'L0_attn_bw_convw': _L0_attn_in['bw_convw'], 'L0_attn_bw_convb': _L0_attn_in['bw_convb'], 'L0_attn_bw_Wx': _L0_attn_in['bw_Wx'], 'L0_attn_bw_Wdt': _L0_attn_in['bw_Wdt'], 'L0_attn_bw_bdt': _L0_attn_in['bw_bdt'], 'L0_attn_bw_Alog': _L0_attn_in['bw_Alog'], 'L0_attn_bw_D': _L0_attn_in['bw_D'], 'L0_attn_bw_Wout': _L0_attn_in['bw_Wout'], 'L0_attn_fwn_w': _L0_attn_in['fwn_w'], 'L0_attn_fwn_b': _L0_attn_in['fwn_b'], 'L0_attn_fin_w': _L0_attn_in['fin_w'], 'L0_attn_fin_b': _L0_attn_in['fin_b'], 'L0_attn_ff_W1': _L0_attn_in['ff_W1'], 'L0_attn_ff_b1': _L0_attn_in['ff_b1'], 'L0_attn_ff_W2': _L0_attn_in['ff_W2'], 'L0_attn_ff_b2': _L0_attn_in['ff_b2'], 'L0_xattn_wq_k': _L0_xattn_in['wq_k'], 'L0_xattn_wq_b': _L0_xattn_in['wq_b'], 'L0_xattn_wk_k': _L0_xattn_in['wk_k'], 'L0_xattn_wk_b': _L0_xattn_in['wk_b'], 'L0_xattn_wv_k': _L0_xattn_in['wv_k'], 'L0_xattn_wv_b': _L0_xattn_in['wv_b'], 'L0_xattn_wo_k': _L0_xattn_in['wo_k'], 'L0_xattn_wo_b': _L0_xattn_in['wo_b'], 'L0_ffn_ln1_g': _L0_ffn_in['ln1_g'], 'L0_ffn_ln1_b': _L0_ffn_in['ln1_b'], 'L0_ffn_ln2_g': _L0_ffn_in['ln2_g'], 'L0_ffn_ln2_b': _L0_ffn_in['ln2_b'], 'L0_ffn_wq': _L0_ffn_in['wq'], 'L0_ffn_bq': _L0_ffn_in['bq'], 'L0_ffn_wk': _L0_ffn_in['wk'], 'L0_ffn_bk': _L0_ffn_in['bk'], 'L0_ffn_wv': _L0_ffn_in['wv'], 'L0_ffn_bv': _L0_ffn_in['bv'], 'L0_ffn_wo': _L0_ffn_in['wo'], 'L0_ffn_bo': _L0_ffn_in['bo'], 'L0_ffn_gate_w': _L0_ffn_in['gate_w'], 'L0_ffn_gate_b': _L0_ffn_in['gate_b'], 'L0_ffn_w1': _L0_ffn_in['w1'], 'L0_ffn_b1': _L0_ffn_in['b1'], 'L0_ffn_w2': _L0_ffn_in['w2'], 'L0_ffn_b2': _L0_ffn_in['b2'], 'L1_attn_Wq': _L1_attn_in['Wq'], 'L1_attn_Wk': _L1_attn_in['Wk'], 'L1_attn_Wv': _L1_attn_in['Wv'], 'L1_attn_Wo': _L1_attn_in['Wo'], 'L1_attn_qn_w': _L1_attn_in['qn_w'], 'L1_attn_kn_w': _L1_attn_in['kn_w'], 'L1_xattn_wq_w': _L1_xattn_in['wq_w'], 'L1_xattn_wq_b': _L1_xattn_in['wq_b'], 'L1_xattn_wk_w': _L1_xattn_in['wk_w'], 'L1_xattn_wk_b': _L1_xattn_in['wk_b'], 'L1_xattn_wv_w': _L1_xattn_in['wv_w'], 'L1_xattn_wv_b': _L1_xattn_in['wv_b'], 'L1_xattn_wo_w': _L1_xattn_in['wo_w'], 'L1_xattn_wo_b': _L1_xattn_in['wo_b'], 'L1_ffn_clip_x': _L1_ffn_in['clip_x'], 'L1_ffn_clip_down': _L1_ffn_in['clip_down'], 'L1_ffn_w_gate': _L1_ffn_in['w_gate'], 'L1_ffn_w_up': _L1_ffn_in['w_up'], 'L1_ffn_w_down': _L1_ffn_in['w_down']}

def reference(x, ctx_1024, fside_BxSxS2_0, mask_BxSxS2_ik1, L0_attn_fw_Win, L0_attn_fw_convw, L0_attn_fw_convb, L0_attn_fw_Wx, L0_attn_fw_Wdt, L0_attn_fw_bdt, L0_attn_fw_Alog, L0_attn_fw_D, L0_attn_fw_Wout, L0_attn_bw_Win, L0_attn_bw_convw, L0_attn_bw_convb, L0_attn_bw_Wx, L0_attn_bw_Wdt, L0_attn_bw_bdt, L0_attn_bw_Alog, L0_attn_bw_D, L0_attn_bw_Wout, L0_attn_fwn_w, L0_attn_fwn_b, L0_attn_fin_w, L0_attn_fin_b, L0_attn_ff_W1, L0_attn_ff_b1, L0_attn_ff_W2, L0_attn_ff_b2, L0_xattn_wq_k, L0_xattn_wq_b, L0_xattn_wk_k, L0_xattn_wk_b, L0_xattn_wv_k, L0_xattn_wv_b, L0_xattn_wo_k, L0_xattn_wo_b, L0_ffn_ln1_g, L0_ffn_ln1_b, L0_ffn_ln2_g, L0_ffn_ln2_b, L0_ffn_wq, L0_ffn_bq, L0_ffn_wk, L0_ffn_bk, L0_ffn_wv, L0_ffn_bv, L0_ffn_wo, L0_ffn_bo, L0_ffn_gate_w, L0_ffn_gate_b, L0_ffn_w1, L0_ffn_b1, L0_ffn_w2, L0_ffn_b2, L1_attn_Wq, L1_attn_Wk, L1_attn_Wv, L1_attn_Wo, L1_attn_qn_w, L1_attn_kn_w, L1_xattn_wq_w, L1_xattn_wq_b, L1_xattn_wk_w, L1_xattn_wk_b, L1_xattn_wv_w, L1_xattn_wv_b, L1_xattn_wo_w, L1_xattn_wo_b, L1_ffn_clip_x, L1_ffn_clip_down, L1_ffn_w_gate, L1_ffn_w_up, L1_ffn_w_down):
    import jax
    import jax.numpy as jnp

    def _L0_attn_ref(x, fw_Win, fw_convw, fw_convb, fw_Wx, fw_Wdt, fw_bdt, fw_Alog, fw_D, fw_Wout, bw_Win, bw_convw, bw_convb, bw_Wx, bw_Wdt, bw_bdt, bw_Alog, bw_D, bw_Wout, fwn_w, fwn_b, fin_w, fin_b, ff_W1, ff_b1, ff_W2, ff_b2):
        import jax, jax.numpy as jnp
        import numpy as np
        from jax import lax
        B, L, D_MODEL = (2, 256, 128)
        EXPAND = 2
        D_INNER = D_MODEL * EXPAND
        D_STATE = 16
        D_CONV = 4
        DT_RANK = (D_MODEL + 15) // 16
        EPS = 1e-05

        def _mamba_params(key, pfx, scale=0.02):
            ks = jax.random.split(key, 6)
            return {pfx + '_Win': jax.random.normal(ks[0], (D_MODEL, 2 * D_INNER), jnp.float32) * scale, pfx + '_convw': jax.random.normal(ks[1], (D_INNER, D_CONV), jnp.float32) * scale, pfx + '_convb': jnp.zeros((D_INNER,), jnp.float32), pfx + '_Wx': jax.random.normal(ks[2], (D_INNER, DT_RANK + 2 * D_STATE), jnp.float32) * scale, pfx + '_Wdt': jax.random.normal(ks[3], (DT_RANK, D_INNER), jnp.float32) * scale, pfx + '_bdt': jax.random.uniform(ks[4], (D_INNER,), jnp.float32, -4.0, -2.0), pfx + '_Alog': jnp.log(jnp.broadcast_to(jnp.arange(1, D_STATE + 1, dtype=jnp.float32), (D_INNER, D_STATE))).copy(), pfx + '_D': jnp.ones((D_INNER,), jnp.float32), pfx + '_Wout': jax.random.normal(ks[5], (D_INNER, D_MODEL), jnp.float32) * scale}

        def _layernorm(x, w, b):
            mu = x.mean(-1, keepdims=True)
            xc = x - mu
            v = (xc * xc).mean(-1, keepdims=True)
            return xc * lax.rsqrt(v + EPS) * w + b

        def _causal_dwconv(x, w, b):
            xc = x.transpose(0, 2, 1)
            out = lax.conv_general_dilated(xc, w[:, None, :], window_strides=(1,), padding=[(D_CONV - 1, 0)], feature_group_count=D_INNER, dimension_numbers=('NCH', 'OIH', 'NCH'))
            return (out + b[None, :, None]).transpose(0, 2, 1)

        def _selective_scan(u, dt, A, Bm, Cm, Dp):
            h0 = jnp.zeros((u.shape[0], D_INNER, D_STATE), u.dtype)

            def step(h, inp):
                u_t, dt_t, B_t, C_t = inp
                dA = jnp.exp(dt_t[:, :, None] * A)
                h = dA * h + (dt_t * u_t)[:, :, None] * B_t[:, None, :]
                y = jnp.einsum('bds,bs->bd', h, C_t)
                return (h, y)
            _, ys = lax.scan(step, h0, (u.transpose(1, 0, 2), dt.transpose(1, 0, 2), Bm.transpose(1, 0, 2), Cm.transpose(1, 0, 2)))
            return ys.transpose(1, 0, 2) + u * Dp

        def _mamba(x, Win, convw, convb, Wx, Wdt, bdt, Alog, Dp, Wout):
            xz = x @ Win
            xi, z = jnp.split(xz, 2, axis=-1)
            xi = jax.nn.silu(_causal_dwconv(xi, convw, convb))
            xdbc = xi @ Wx
            dt_in = xdbc[..., :DT_RANK]
            Bm = xdbc[..., DT_RANK:DT_RANK + D_STATE]
            Cm = xdbc[..., DT_RANK + D_STATE:]
            dt = jax.nn.softplus(dt_in @ Wdt + bdt)
            A = -jnp.exp(Alog)
            y = _selective_scan(xi, dt, A, Bm, Cm, Dp)
            return y * jax.nn.silu(z) @ Wout
        yf = _mamba(x, fw_Win, fw_convw, fw_convb, fw_Wx, fw_Wdt, fw_bdt, fw_Alog, fw_D, fw_Wout)
        yf = _layernorm(yf + x, fwn_w, fwn_b)
        yb = _mamba(jnp.flip(x, 1), bw_Win, bw_convw, bw_convb, bw_Wx, bw_Wdt, bw_bdt, bw_Alog, bw_D, bw_Wout)
        yb = _layernorm(jnp.flip(yb, 1) + x, fwn_w, fwn_b)
        y = yf + yb
        ff = jax.nn.relu(y @ ff_W1 + ff_b1) @ ff_W2 + ff_b2
        return _layernorm(ff + y, fin_w, fin_b)

    def _L0_xattn_ref(query, key_in, value, group_prob, mask, wq_k, wq_b, wk_k, wk_b, wv_k, wv_b, wo_k, wo_b):
        import jax, jax.numpy as jnp
        import numpy as np
        NUM_HEADS = 16
        HIDDEN = 128
        B, S = (2, 256)

        def _split_heads(x, H):
            b, s, d = x.shape
            return x.reshape(b, s, H, d // H).transpose(0, 2, 1, 3)
        H = NUM_HEADS
        dh = query.shape[-1] // H
        q = _split_heads(query @ wq_k + wq_b, H)
        k = _split_heads(key_in @ wk_k + wk_b, H)
        v = _split_heads(value @ wv_k + wv_b, H)
        logits = jnp.einsum('bhqd,bhkd->bhqk', q, k) / jnp.sqrt(jnp.asarray(dh, q.dtype))
        neg = (1.0 - mask.astype(q.dtype)) * -1000000000.0
        logits = logits + neg[:, None, :, :]
        attn = jax.nn.softmax(logits, axis=-1)
        attn = attn * group_prob[:, None, :, :]
        out = jnp.einsum('bhqk,bhkd->bhqd', attn, v)
        out = out.transpose(0, 2, 1, 3).reshape(query.shape[0], -1, H * dh)
        return out @ wo_k + wo_b

    def _L0_ffn_ref(x, ln1_g, ln1_b, ln2_g, ln2_b, wq, bq, wk, bk, wv, bv, wo, bo, gate_w, gate_b, w1, b1, w2, b2):
        import jax, jax.numpy as jnp
        import numpy as np
        B, S, H, NH, E, F = (4, 128, 128, 16, 8, 512)
        D = H // NH
        EPS = 1e-05

        def _layernorm(x, g, b):
            mu = jnp.mean(x, axis=-1, keepdims=True)
            var = jnp.var(x, axis=-1, keepdims=True)
            return (x - mu) * jax.lax.rsqrt(var + EPS) * g + b
        b, s, h = x.shape
        hn = _layernorm(x, ln1_g, ln1_b)
        q = (hn @ wq + bq).reshape(b, s, NH, D).transpose(0, 2, 1, 3)
        k = (hn @ wk + bk).reshape(b, s, NH, D).transpose(0, 2, 1, 3)
        v = (hn @ wv + bv).reshape(b, s, NH, D).transpose(0, 2, 1, 3)
        scores = jnp.einsum('bhqd,bhkd->bhqk', q, k) / jnp.sqrt(jnp.float32(D))
        attn = jax.nn.softmax(scores, axis=-1)
        o = jnp.einsum('bhqk,bhkd->bhqd', attn, v)
        o = o.transpose(0, 2, 1, 3).reshape(b, s, h)
        x = x + (o @ wo + bo)
        hn2 = _layernorm(x, ln2_g, ln2_b).reshape(-1, h)
        logits = hn2 @ gate_w + gate_b
        idx = jnp.argmax(logits, axis=-1)
        mid = jax.nn.relu(jnp.einsum('th,ehf->etf', hn2, w1) + b1[:, None, :])
        y = jnp.einsum('etf,efh->eth', mid, w2) + b2[:, None, :]
        moe = y[idx, jnp.arange(hn2.shape[0])]
        return x + moe.reshape(b, s, h)

    def _L1_attn_ref(x, Wq, Wk, Wv, Wo, qn_w, kn_w):
        import jax, jax.numpy as jnp
        import numpy as np
        NUM_HEADS = 16
        EPS = float(jnp.finfo(jnp.float32).eps)

        def rms_norm(x, w):
            ms = jnp.mean(x * x, axis=-1, keepdims=True)
            return x * jax.lax.rsqrt(ms + EPS) * w
        B, N, D = x.shape
        H = NUM_HEADS
        Dh = D // H
        scale = Dh ** (-0.5)

        def proj(W):
            return (x @ W.T).reshape(B, N, H, Dh).transpose(0, 2, 1, 3)
        q = rms_norm(proj(Wq), qn_w)
        k = rms_norm(proj(Wk), kn_w)
        v = proj(Wv)
        scores = jnp.einsum('bhnd,bhmd->bhnm', q, k) * scale
        attn = jax.nn.softmax(scores, axis=-1)
        out = jnp.einsum('bhnm,bhmd->bhnd', attn, v)
        out = out.transpose(0, 2, 1, 3).reshape(B, N, D)
        return out @ Wo.T

    def _L1_xattn_ref(v, k, q, wq_w, wq_b, wk_w, wk_b, wv_w, wv_b, wo_w, wo_b):
        import jax, jax.numpy as jnp
        import numpy as np
        D_MODEL = 128
        NUM_HEADS = 16
        DEPTH = D_MODEL // NUM_HEADS

        def _split_heads(x):
            B, S, _ = x.shape
            return x.reshape(B, S, NUM_HEADS, DEPTH).transpose(0, 2, 1, 3)
        B, S, _ = q.shape
        qh = _split_heads(q @ wq_w + wq_b)
        kh = _split_heads(k @ wk_w + wk_b)
        vh = _split_heads(v @ wv_w + wv_b)
        scale = 1.0 / jnp.sqrt(jnp.asarray(DEPTH, qh.dtype))
        logits = jnp.einsum('bhqd,bhkd->bhqk', qh, kh) * scale
        attn = jax.nn.softmax(logits, axis=-1)
        out = jnp.einsum('bhqk,bhkd->bhqd', attn, vh)
        out = out.transpose(0, 2, 1, 3).reshape(B, S, D_MODEL)
        return out @ wo_w + wo_b

    def _L1_ffn_ref(x, clip_x, clip_down, w_gate, w_up, w_down):
        import jax, jax.numpy as jnp
        import numpy as np
        QMAX = 127.0

        def _ste_round(v):
            return v + jax.lax.stop_gradient(jnp.round(v) - v)

        def _act_fake_quant(x, clip_factor):
            scale = jax.nn.sigmoid(clip_factor) * jnp.max(jnp.abs(x)) / QMAX
            return jnp.clip(_ste_round(x / scale), -QMAX - 1.0, QMAX) * scale

        def _weight_fake_quant(w):
            scale = jnp.max(jnp.abs(w), axis=1, keepdims=True) / QMAX
            return jnp.clip(_ste_round(w / scale), -QMAX - 1.0, QMAX) * scale
        xq = _act_fake_quant(x, clip_x[0])
        gate = jnp.einsum('bsh,ih->bsi', xq, _weight_fake_quant(w_gate))
        up = jnp.einsum('bsh,ih->bsi', xq, _weight_fake_quant(w_up))
        h = _act_fake_quant(jax.nn.silu(gate) * up, clip_down[0])
        return jnp.einsum('bsi,hi->bsh', h, _weight_fake_quant(w_down))
    x = _layernorm(x + _L0_attn_ref(x, L0_attn_fw_Win, L0_attn_fw_convw, L0_attn_fw_convb, L0_attn_fw_Wx, L0_attn_fw_Wdt, L0_attn_fw_bdt, L0_attn_fw_Alog, L0_attn_fw_D, L0_attn_fw_Wout, L0_attn_bw_Win, L0_attn_bw_convw, L0_attn_bw_convb, L0_attn_bw_Wx, L0_attn_bw_Wdt, L0_attn_bw_bdt, L0_attn_bw_Alog, L0_attn_bw_D, L0_attn_bw_Wout, L0_attn_fwn_w, L0_attn_fwn_b, L0_attn_fin_w, L0_attn_fin_b, L0_attn_ff_W1, L0_attn_ff_b1, L0_attn_ff_W2, L0_attn_ff_b2), axis=-1)
    x = _layernorm(x + _L0_xattn_ref(x, ctx_1024, ctx_1024, fside_BxSxS2_0, mask_BxSxS2_ik1, L0_xattn_wq_k, L0_xattn_wq_b, L0_xattn_wk_k, L0_xattn_wk_b, L0_xattn_wv_k, L0_xattn_wv_b, L0_xattn_wo_k, L0_xattn_wo_b), axis=-1)
    x = _layernorm(x + _L0_ffn_ref(x, L0_ffn_ln1_g, L0_ffn_ln1_b, L0_ffn_ln2_g, L0_ffn_ln2_b, L0_ffn_wq, L0_ffn_bq, L0_ffn_wk, L0_ffn_bk, L0_ffn_wv, L0_ffn_bv, L0_ffn_wo, L0_ffn_bo, L0_ffn_gate_w, L0_ffn_gate_b, L0_ffn_w1, L0_ffn_b1, L0_ffn_w2, L0_ffn_b2), axis=-1)
    x = _layernorm(x + _L1_attn_ref(x, L1_attn_Wq, L1_attn_Wk, L1_attn_Wv, L1_attn_Wo, L1_attn_qn_w, L1_attn_kn_w), axis=-1)
    x = _layernorm(x + _L1_xattn_ref(ctx_1024, ctx_1024, x, L1_xattn_wq_w, L1_xattn_wq_b, L1_xattn_wk_w, L1_xattn_wk_b, L1_xattn_wv_w, L1_xattn_wv_b, L1_xattn_wo_w, L1_xattn_wo_b), axis=-1)
    x = _layernorm(x + _L1_ffn_ref(x, L1_ffn_clip_x, L1_ffn_clip_down, L1_ffn_w_gate, L1_ffn_w_up, L1_ffn_w_down), axis=-1)
    return x

_drawn_inputs = setup_inputs


def setup_inputs(seed=0):
    import zlib

    import numpy as np

    out = dict(_drawn_inputs(seed))
    spreads = {'L0_attn_fw_convb': (0.0, 0.8),
     'L0_attn_fw_D': (1.0, 0.6),
     'L0_attn_bw_convb': (0.0, 0.8),
     'L0_attn_bw_D': (1.0, 0.6),
     'L0_attn_fwn_w': (1.0, 0.2),
     'L0_attn_fwn_b': (0.0, 0.1),
     'L0_attn_fin_w': (1.0, 0.2),
     'L0_attn_fin_b': (0.0, 0.1),
     'L0_attn_ff_b1': (0.0, 0.8),
     'L0_attn_ff_b2': (0.0, 0.409),
     'L0_xattn_wq_b': (0.0, 0.617),
     'L0_xattn_wk_b': (0.0, 0.8),
     'L0_xattn_wv_b': (0.0, 0.1),
     'L0_xattn_wo_b': (0.0, 0.1),
     'L0_ffn_ln1_g': (1.0, 0.6),
     'L0_ffn_ln1_b': (0.0, 0.8),
     'L0_ffn_ln2_g': (1.0, 0.534),
     'L0_ffn_ln2_b': (0.0, 0.464),
     'L0_ffn_bq': (0.0, 0.8),
     'L0_ffn_bk': (0.0, 0.8),
     'L0_ffn_bv': (0.0, 0.523),
     'L0_ffn_bo': (0.0, 0.1),
     'L0_ffn_gate_b': (0.0, 0.1),
     'L0_ffn_b1': (0.0, 0.594),
     'L0_ffn_b2': (0.0, 0.1),
     'L1_attn_qn_w': (1.0, 0.6),
     'L1_attn_kn_w': (1.0, 0.6),
     'L1_xattn_wq_b': (0.0, 0.318),
     'L1_xattn_wk_b': (0.0, 0.8),
     'L1_xattn_wv_b': (0.0, 0.1),
     'L1_xattn_wo_b': (0.0, 0.1)}
    factors = {'L0_attn_fw_Win': 8.0,
     'L0_attn_fw_convw': 8.0,
     'L0_attn_fw_Wx': 8.0,
     'L0_attn_fw_Wdt': 8.0,
     'L0_attn_fw_bdt': 8.0,
     'L0_attn_fw_Alog': 8.0,
     'L0_attn_fw_Wout': 8.0,
     'L0_attn_bw_Win': 8.0,
     'L0_attn_bw_convw': 8.0,
     'L0_attn_bw_Wx': 8.0,
     'L0_attn_bw_Wdt': 8.0,
     'L0_attn_bw_bdt': 8.0,
     'L0_attn_bw_Alog': 8.0,
     'L0_attn_bw_Wout': 8.0,
     'L0_attn_ff_W1': 2.762,
     'L0_ffn_wq': 8.0,
     'L0_ffn_wk': 8.0,
     'L0_ffn_wv': 5.78,
     'L0_ffn_wo': 3.44,
     'L1_attn_Wq': 8.0,
     'L1_attn_Wk': 8.0,
     'L1_attn_Wv': 3.945,
     'L1_attn_Wo': 4.039,
     'L1_ffn_w_gate': 5.82,
     'L1_ffn_w_up': 5.757,
     'L1_ffn_w_down': 5.775}
    for name, (base, spread) in spreads.items():
        noise = np.random.default_rng([zlib.crc32(name.encode()), seed]).standard_normal(out[name].shape)
        drawn = base * np.exp(spread * noise) if base else spread * noise
        out[name] = jnp.asarray(drawn.astype(out[name].dtype))
    for name, factor in factors.items():
        out[name] = (out[name] * factor).astype(out[name].dtype)
    return out
```

```python
from contextlib import ExitStack

import numpy as np
import concourse.bass as bass
from concourse import mybir

F32 = mybir.dt.float32
BF16 = mybir.dt.bfloat16
I32 = mybir.dt.int32
ALU = mybir.AluOpType
ACT = mybir.ActivationFunctionType
AX = mybir.AxisListType

P = 128
B, S, D = 64, 128, 128
S2 = 77
H, DH = 16, 8
GB = 4
NG = B // GB
GT = GB * S
EPS = 1e-5


class Count:

    def __init__(self, sem, per):
        self.sem, self.per = sem, per

    def at(self, t, j=0):
        v = t * self.per + j
        return max(v, 0) if isinstance(v, int) else v


class Chain:

    def __init__(self, sem):
        self.sem, self.base, self.n = sem, 0, 0

    def start(self, base):
        self.base, self.n = base, 0

    def next(self):
        self.n += 1
        return self.base + self.n


def looped(eng, sem, turns, per, prologue, body, tail):
    chain = Chain(sem)
    prologue(eng, chain)
    base = chain.n
    chain.start(base)
    body(eng, chain, 0)
    base += chain.n
    with eng.Fori(1, turns - 1) as i:
        chain.start((i - 1) * per + base)
        body(eng, chain, i)
    assert chain.n == per, chain.n
    base += (turns - 2) * per
    chain.start(base)
    body(eng, chain, turns - 1)
    chain.start(base + chain.n)
    tail(eng, chain)

def attention(nc, const, banks, tag, x_in, x_out, wq, wk, wv, wo, scale, bq=None, bk=None, bv=None, bo=None,
              ctx=None, mask=None, gate=None, ln=None, rms=None, normed=True):
    sk = S if ctx is None else S2
    kt = GB * sk
    PARTS, ROWS = 3, 6 * DH
    Q_ROWS, K_ROWS = (0, 0, 1, 1, 0, 2), (0, 1, 0, 1, 2, 0)
    VC = DH + 1
    VW = 8 * VC
    TURNS = NG // 2
    ident, identb, ones_row, sel = const["ident"], const["identb"], const["ones_row"], const["sel"]
    half_pow = const["half_pow"]
    uses = ["x"] + (["c"] if ctx is not None else []) + (["m", "g"] if mask is not None else [])
    uses += ["qt", "qn", "kt", "kn", "v"] if rms else ["q", "k", "v"]
    NU = len(uses)
    nu = {u: n for n, u in enumerate(uses)}
    LOADS = 1 + (ctx is not None) + (2 if mask is not None else 0)

    with ExitStack() as st:
        def sb(name, shape, dt=F32):
            return st.enter_context(nc.sbuf_tensor(f"{tag}_{name}", shape, dt))

        def sem(name, per=1):
            return Count(nc.alloc_semaphore(f"{tag}_{name}"), per)

        dram_q = nc.dram_tensor(f"{tag}_q_parts", (2, PARTS, P, GT), BF16, kind="Internal").ap()
        dram_k = nc.dram_tensor(f"{tag}_k_parts", (2, PARTS, P, kt), BF16, kind="Internal").ap()

        w = sb("w", [P, 4, D])
        bqk = sb("bqk", [P, 2])
        bvb = sb("bvb", [P, D])
        bor = sb("bor", [1, D])
        lnw = sb("lnw", [P, 2, D])
        xp = sb("xp", [P, 2, GB, D])
        xr = sb("xr", [P, 2, GB, D])
        cx = sb("cx", [P, GB, D]) if ctx is not None else None
        mi = sb("mi", [P, GB, S2], I32) if mask is not None else None
        neg = sb("neg", [P, 2, GB, S2]) if mask is not None else None
        gp = sb("gp", [P, GB, S2]) if mask is not None else None
        negT = sb("negT", [P, 2, GT]) if mask is not None else None
        gpT = sb("gpT", [P, 2, GT]) if mask is not None else None
        xn = sb("xn", [P, GB, D]) if ln is not None else None
        xT = sb("xT", [P, GT])
        cT = sb("cT", [P, kt]) if ctx is not None else xT
        qf = sb("qf", [P, 2, GT])
        qr = sb("qr", [P, 2, GT])
        qp = sb("qp", [P, 2, PARTS, GT], BF16)
        qtok = sb("qtok", [P, 2, GB, D]) if rms else None
        sq = sb("sq", [P, GB, D]) if rms else None
        ms = sb("ms", [P, 2, 3, GB * H]) if rms else None
        hpw = sb("hpw", [P, GB * H]) if rms else None
        Qs = sb("Qs", [ROWS, 2, H, GT], BF16)
        Ks = sb("Ks", [ROWS, 2, H, kt], BF16)
        vS = sb("vS", [P, 2, GB, D])
        vB = sb("vB", [P, 2, 2, 9 * VW])
        oB = sb("oB", [P, 2, 9 * VW]) if gate is not None else None
        sm = sb("sm", [P, 2, 4 * S2]) if mask is not None else None
        smT = sb("smT", [P, 2, 4 * S]) if mask is not None else None
        nm = sb("nm", [P, 2, 3, H])
        nmp = sb("nmp", [P, 2, PARTS, H], BF16)
        nmT = sb("nmT", [PARTS * H, 2, S], BF16)
        pT = sb("pT", [P, 2, H, S])
        pG = sb("pG", [P, 2, H, S]) if gate is not None else pT
        ou = sb("ou", [VW, 2, S])
        rden = sb("rden", [P, H])
        on = sb("on", [P, D])
        oT = sb("oT", [P, S])
        r = sb("r", [P, 2, D])
        stat = sb("stat", [P, 2, 8])
        var = sb("var", [P, 2, 2])
        lst = sb("lst", [P, GB, 8]) if ln is not None else None
        lvar = sb("lvar", [P, 2, GB]) if ln is not None else None

        s_w = sem("weights"); s_setup = sem("setup"); s_xp = sem("x_loaded"); s_xr = sem("residual_loaded")
        s_xpfree = sem("x_used"); s_pb = sem("proj_written", NU); s_pf = sem("proj_evacuated", NU)
        s_hi = sem("hi_ready", 2); s_r1 = sem("rest1_ready", 2)
        s_mid = sem("mid_ready", 2); s_lo = sem("lo_ready", 2)
        s_ps = sem("parts_stored", 1); s_stk = sem("stack_loaded", 1)
        s_ln = sem("front_var", 1); s_lp = sem("front_pow", 1); s_xn = sem("front_norm", 1)
        s_neg = sem("neg_ready"); s_sq = sem("squares", 2); s_ms = sem("mean_squares", 2); s_rp = sem("rms_pow", 2)
        s_S = sem("scores", 4); s_Sf = sem("scores_used", 4); s_nmp = sem("max_parts"); s_T = sem("max_transposed")
        s_nmT = sem("max_rows"); s_st = sem("shifted", 4); s_e = sem("exp", 4)
        s_sm = sem("masked", 4) if mask is not None else None
        s_stf = s_sm if mask is not None else s_e
        s_pg = sem("gated"); s_vb = sem("values_spread"); s_pv = sem("pv"); s_ou = sem("pv_evacuated")
        s_ot = sem("out_turned"); s_on = sem("out_normed"); s_o2 = sem("out_turned_back"); s_oT = sem("oT")
        s_y = sem("y"); s_r = sem("residual"); s_v = sem("var"); s_pw = sem("pow"); s_xo = sem("x_done") if normed else s_r
        s_store = sem("stored"); s_bq = sem("q_bias_scaled"); s_dve = nc.alloc_semaphore(f"{tag}_dve_done")
        s_pool = nc.alloc_semaphore(f"{tag}_pool_chain")
        s_step = nc.alloc_semaphore(f"{tag}_passed")
        bankS, bankT, bankO, bankP, bankM, bankY = banks[0:2], banks[2:4], banks[4], banks[5], banks[6], banks[7]
        bankMb = bankM.bitcast(BF16)
        NW = sum(1 for t in (bq, bk, bv, bo) if t is not None) + 4 + (2 if ln is not None else 0) + (2 if rms else 0)

        block = st.enter_context(nc.Block())
        x_g = x_in.rearrange("(g b) t d -> g t b d", b=GB)
        o_g = x_out.rearrange("(g b) t d -> g t b d", b=GB)

        def diagonal(t):
            return t.rearrange("p (h c) -> p h c", c=VW + VC)

        def heads(t):
            return t.rearrange("p (h d) -> p h d", h=H)

        @block.sync
        def _(sp):
            n = 0
            def load_w(dst, src):
                sp.dma_start(dst, src).then_inc(s_w.sem, 16)
            for j, t in enumerate((wq, wk, wv, wo)):
                load_w(w[:, j, :], t)
            for j, t in enumerate((bq, bk)):
                if t is not None:
                    load_w(bqk[:, j:j + 1], t.rearrange("(d a) -> d a", a=1))
            if rms:
                for j, t in enumerate(rms):
                    load_w(bqk[:, j:j + 1], t)
            if bv is not None:
                load_w(bvb[:], bv.rearrange("(a d) -> a d", a=1).to_broadcast([P, D]))
            if bo is not None:
                load_w(bor[:], bo.rearrange("(a d) -> a d", a=1))
            if ln is not None:
                for j, t in enumerate(ln):
                    load_w(lnw[:, j, :], t.rearrange("(a d) -> a d", a=1).to_broadcast([P, D]))

            def load_x(g, par):
                sp.wait_ge(s_xpfree.sem, s_xpfree.at(g - (2 if ctx is None else 1) + 1))
                sp.sem_inc(s_step, 1)
                sp.dma_start(xp[:, par], x_g[g]).then_inc(s_xp.sem, 16)
                if ctx is not None:
                    sp.dma_start(cx[0:S2], ctx.rearrange("(g b) t d -> g t b d", b=GB)[g]).then_inc(s_xp.sem, 16)
                if mask is not None:
                    sp.dma_start(mi[:], mask.rearrange("(g b) t d -> g t b d", b=GB)[g]).then_inc(s_xp.sem, 16)
                    sp.dma_start(gp[:], gate.rearrange("(g b) t d -> g t b d", b=GB)[g]).then_inc(s_xp.sem, 16)

            def stack(g, par):
                for t, (dram, n) in enumerate(((dram_q, GT), (dram_k, kt))):
                    sp.wait_ge(s_lo.sem, s_lo.at(g, t + 1))
                    sp.dma_start(dram[par].rearrange("a p t -> p a t"), qp[:, t, :, 0:n]).then_inc(s_ps.sem, 16)
                sp.wait_ge(s_ps.sem, s_ps.at((g + 1) * 32))
                sp.wait_ge(s_st.sem, s_st.at((g - 1) * GB))
                for t, (dram, n, rows) in enumerate(((dram_q, GT, Q_ROWS), (dram_k, kt, K_ROWS))):
                    dst = Qs if t == 0 else Ks
                    for k, a in enumerate(rows):
                        sp.dma_start(dst[k * DH:(k + 1) * DH, par],
                                     dram[par, a].rearrange("(h d) t -> d h t", d=DH)).then_inc(s_stk.sem, 16)

            def residual(g, par):
                sp.wait_ge(s_store.sem, s_store.at((g - 1) * 16))
                sp.sem_inc(s_step, 1)
                sp.dma_start(xr[:, par], x_g[g]).then_inc(s_xr.sem, 16)

            def store(g, par):
                sp.wait_ge(s_xo.sem, s_xo.at((g + 1) * GB))
                sp.sem_inc(s_step, 1)
                sp.dma_start(o_g[g], xr[:, par]).then_inc(s_store.sem, 16)

            def turn(i, last=False, first=False):
                for l in range(2):
                    g = 2 * i + l
                    residual(g, l)
                    if not (last and l):
                        load_x(g + 1, 1 - l)
                        stack(g + 1, 1 - l)
                    if not (first and not l):
                        store(g - 1, 1 - l)
            load_x(0, 0)
            stack(0, 0)
            turn(0, first=True)
            with sp.Fori(1, TURNS - 1) as i:
                turn(i)
            turn(TURNS - 1, last=True)
            store(NG - 1, 1)
            sp.wait_ge(s_store.sem, NG * 16)

        @block.tensor
        def _(pe):
            pe.wait_ge(s_w.sem, 16 * NW)

            def use(g, u):
                pe.wait_ge(s_pf.sem, s_pf.at(g, nu[u]))

            def done(ins):
                ins.then_inc(s_pb.sem, 1)

            def prep_a(g, par):
                use(g, "x")
                if ln is not None:
                    pe.wait_ge(s_xn.sem, s_xn.at(g + 1))
                else:
                    pe.wait_ge(s_xp.sem, (g + 1) * 16 * LOADS)
                for b in range(GB):
                    src = xn[:, b, :] if ln is not None else xp[:, par, b, :]
                    ins = pe.transpose(bankP[:, b * S:(b + 1) * S], src, ident[:])
                done(ins)
                if ctx is not None:
                    use(g, "c")
                    for b in range(GB):
                        ins = pe.transpose(bankP[:, b * S2:(b + 1) * S2], cx[0:S2, b, :], ident[0:S2, 0:S2])
                    done(ins)
                if mask is not None:
                    use(g, "m")
                    pe.wait_ge(s_neg.sem, s_neg.at(g + 1))
                    for b in range(GB):
                        ins = pe.transpose(bankP[0:S2, b * S:(b + 1) * S], neg[:, par, b, :], ident[:])
                    done(ins)
                    use(g, "g")
                    for b in range(GB):
                        ins = pe.transpose(bankP[0:S2, b * S:(b + 1) * S], gp[:, b, :], ident[:])
                    done(ins)

            def prep_b(g, par):
                if rms:
                    for t, (a, n) in enumerate((("qt", "qn"), ("kt", "kn"))):
                        use(g, a)
                        for b in range(GB):
                            ins = pe.matmul(bankP[:, b * S:(b + 1) * S], xT[:, b * S:(b + 1) * S], w[:, t, :],
                                            start=True, stop=True)
                        done(ins)
                        use(g, n)
                        for b in range(GB):
                            ins = pe.transpose(bankP[:, b * S:(b + 1) * S], qtok[:, t, b, :], ident[:])
                        done(ins)
                else:
                    use(g, "q")
                    done(pe.matmul(bankP[:], w[:, 0, :], xT[:], start=True, stop=True))
                    use(g, "k")
                    done(pe.matmul(bankP[:, 0:kt], w[:, 1, :], cT[:], start=True, stop=True))
                use(g, "v")
                for b in range(GB):
                    ins = pe.matmul(bankP[0:sk, b * D:(b + 1) * D], cT[:, b * sk:(b + 1) * sk], w[:, 2, :],
                                    start=True, stop=True)
                done(ins)

            def scores(i, lb, c):
                b, l, q = 8 * i + lb, lb // GB, lb % GB
                if c == 0 and q == 0:
                    pe.wait_ge(s_stk.sem, (2 * i + l + 1) * 16 * 2 * len(Q_ROWS))
                pe.wait_ge(s_Sf.sem, s_Sf.at(b, c + 1 - 2))
                for h in range(4):
                    hh = 4 * c + h
                    ins = pe.matmul(bankS[c % 2][:, h * sk:(h + 1) * sk], Qs[:, l, hh, q * S:(q + 1) * S],
                                    Ks[:, l, hh, q * sk:(q + 1) * sk], start=True, stop=True)
                ins.then_inc(s_S.sem, 1)

            def turn_max(b, lb):
                pe.wait_ge(s_nmp.sem, s_nmp.at(b + 1))
                pe.wait_ge(s_nmT.sem, s_nmT.at(b))
                pe.sem_inc(s_step, 1)
                pe.transpose(bankMb[0:PARTS * H, 0:S], nmp[:, lb % 2].rearrange("p a h -> p (a h)"),
                             identb[:]).then_inc(s_T.sem, 1)

            def shifted(b, lb):
                l, q = lb // GB, lb % GB
                pe.wait_ge(s_nmT.sem, s_nmT.at(b + 1))
                for c in range(4):
                    pe.wait_ge(s_stf.sem, s_stf.at(b, c + 1 - 2))
                    for h in range(4):
                        hh = 4 * c + h
                        o = bankT[c % 2][0:sk, h * S:(h + 1) * S]
                        pe.matmul(o, Ks[:, l, hh, q * sk:(q + 1) * sk], Qs[:, l, hh, q * S:(q + 1) * S],
                                  start=True, stop=False)
                        ins = pe.matmul(o, sel[:, hh, 0:sk], nmT[:, lb % 2, :], start=False, stop=True)
                    ins.then_inc(s_st.sem, 1)

            def values(b, lb, half):
                if half == 0:
                    pe.wait_ge(s_ou.sem, s_ou.at(b))
                    pe.wait_ge(s_vb.sem, s_vb.at(b + 1))
                    if gate is not None:
                        pe.wait_ge(s_pg.sem, s_pg.at(b + 1))
                    pe.wait_ge(s_e.sem, s_e.at(b, 4))
                for h in range(8):
                    hh = 8 * half + h
                    o = bankO[0:VW, half * S:(half + 1) * S]
                    ins = pe.matmul(o, vB[0:sk, lb % 2, half, h * VW:(h + 1) * VW], pG[0:sk, lb % 2, hh, :], start=(h == 0),
                                    stop=(h == 7 and gate is None))
                    if gate is not None:
                        ins = pe.matmul(o, oB[0:sk, half, h * VW:(h + 1) * VW], pT[0:sk, lb % 2, hh, :], start=False, stop=(h == 7))
                if half == 1:
                    ins.then_inc(s_pv.sem, 1)

            def turn_out(b):
                pe.wait_ge(s_ou.sem, s_ou.at(b + 1))
                pe.wait_ge(s_r.sem, s_r.at(b))
                pe.sem_inc(s_step, 1)
                for half in range(2):
                    ins = pe.transpose(bankY[:, half * VW:(half + 1) * VW], ou[:, half, :], ident[0:VW, 0:VW])
                ins.then_inc(s_ot.sem, 1)

            def turn_back(b):
                pe.wait_ge(s_on.sem, s_on.at(b + 1))
                pe.transpose(bankY[:, 0:S], on[:], ident[:]).then_inc(s_o2.sem, 1)

            def out(b):
                pe.wait_ge(s_oT.sem, s_oT.at(b + 1))
                ins = pe.matmul(bankY[:, 0:D], oT[:], w[:, 3, :], start=True, stop=(bo is None))
                if bo is not None:
                    ins = pe.matmul(bankY[:, 0:D], ones_row[:], bor[:], start=False, stop=True)
                ins.then_inc(s_y.sem, 1)

            def step(i, lb, live):
                b = 8 * i + lb
                if live(0):
                    scores(i, lb, 0)
                    scores(i, lb, 1)
                if live(3):
                    turn_out(b - 3)
                if live(2):
                    values(b - 2, (lb - 2) % 8, 0)
                if live(0):
                    scores(i, lb, 2)
                    scores(i, lb, 3)
                if live(1):
                    shifted(b - 1, (lb - 1) % 8)
                if live(3):
                    turn_back(b - 3)
                if live(2):
                    values(b - 2, (lb - 2) % 8, 1)
                if live(3):
                    out(b - 3)
                if live(0):
                    turn_max(b, lb)

            def turn(i, first=False, last=False):
                for lb in range(8):
                    step(i, lb, lambda k: not (first and lb < k))
                    l = lb // GB
                    if not (last and l):
                        if lb % GB == 0:
                            prep_a(2 * i + l + 1, 1 - l)
                        if lb % GB == 1:
                            prep_b(2 * i + l + 1, 1 - l)
            prep_a(0, 0)
            prep_b(0, 0)
            turn(0, first=True)
            with pe.Fori(1, TURNS - 1) as i:
                turn(i)
            turn(TURNS - 1, last=True)
            for k in range(4):
                step(TURNS, k, lambda n: k < n)

        @block.scalar
        def _(act):
            act.wait_ge(s_w.sem, 16 * NW)
            if rms or bq is not None:
                act.activation(bqk[:, 0:1], bqk[:, 0:1], ACT.Copy, scale=scale).then_inc(s_bq.sem, 1)
                act.wait_ge(s_bq.sem, 1)

            def evac(g, u, dst, src, **k):
                act.wait_ge(s_pb.sem, s_pb.at(g, nu[u] + 1))
                act.activation(dst, src, ACT.Identity, **k).then_inc(s_pf.sem, 1)

            def prep_a(g, par):
                evac(g, "x", xT[:], bankP[:])
                if ctx is not None:
                    evac(g, "c", cT[:], bankP[:, 0:kt])
                if mask is not None:
                    act.wait_ge(s_sm.sem, s_sm.at((g - 1) * GB))
                    act.wait_ge(s_pg.sem, s_pg.at((g - 1) * GB))
                    evac(g, "m", negT[0:S2, par, :], bankP[0:S2, :])
                    evac(g, "g", gpT[0:S2, par, :], bankP[0:S2, :])

            def prep_b(g, par):
                for t, (name, n, b) in enumerate((("q", GT, bq), ("k", kt, bk))):
                    if rms:
                        act.wait_ge(s_pb.sem, s_pb.at(g, nu[name + "t"] + 1))
                        act.wait_ge(s_ms.sem, s_ms.at(g, t))
                        act.activation(sq[:].rearrange("p b d -> p (b d)"), bankP[:], ACT.Square).then_inc(s_sq.sem, 1)
                    u = name + "n" if rms else name
                    act.wait_ge(s_pb.sem, s_pb.at(g, nu[u] + 1))
                    act.wait_ge(s_lo.sem, s_lo.at(g - 1, t + 1))
                    k = {"scale": scale} if t == 0 else {}
                    if rms:
                        k = {"scale": bqk[:, t:t + 1]}
                    elif b is not None:
                        k["bias"] = bqk[:, t:t + 1]
                    act.activation(qf[:, t, 0:n], bankP[:, 0:n], ACT.Identity, **k).then_inc(s_pf.sem, 1)

            def step(i, lb, live):
                b = 8 * i + lb
                if live(1):
                    p = (lb - 1) % 2
                    act.wait_ge(s_pv.sem, s_pv.at(b - 1 - 1))
                    if gate is not None:
                        act.wait_ge(s_pg.sem, s_pg.at(b - 1 - 1))
                    for c in range(4):
                        if mask is not None:
                            act.wait_ge(s_sm.sem, s_sm.at(b - 1, c + 1))
                            src = smT[0:sk, c % 2, :]
                        else:
                            act.wait_ge(s_st.sem, s_st.at(b - 1, c + 1))
                            src = bankT[c % 2][0:sk, :]
                        ins = act.activation(pT[0:sk, p, 4 * c:4 * c + 4, :].rearrange("p h t -> p (h t)"), src, ACT.Exp)
                        ins.then_inc(s_e.sem, 1)
                if live(3):
                    act.wait_ge(s_o2.sem, s_o2.at(b - 3 + 1))
                    act.wait_ge(s_y.sem, s_y.at(b - 3))
                    act.activation(oT[:], bankY[:, 0:S], ACT.Copy).then_inc(s_oT.sem, 1)
                if live(2):
                    act.wait_ge(s_pv.sem, s_pv.at(b - 2 + 1))
                    act.wait_ge(s_ot.sem, s_ot.at(b - 2))
                    act.activation(ou[:].rearrange("p a t -> p (a t)"), bankO[0:VW, 0:2 * S], ACT.Copy).then_inc(s_ou.sem, 1)

            def turn(i, first=False, last=False):
                for lb in range(8):
                    step(i, lb, lambda k: not (first and lb < k))
                    l = lb // GB
                    if not (last and l):
                        if lb % GB == 0:
                            prep_a(2 * i + l + 1, 1 - l)
                        if lb % GB == 1:
                            prep_b(2 * i + l + 1, 1 - l)
            prep_a(0, 0)
            prep_b(0, 0)
            turn(0, first=True)
            with act.Fori(1, TURNS - 1) as i:
                turn(i)
            turn(TURNS - 1, last=True)
            for k in range(4):
                step(TURNS, k, lambda n: k < n)

        @block.vector
        def _(dve):
            dve.wait_ge(s_w.sem, 16 * NW)
            dve.wait_ge(s_setup.sem, 1)

            def prep_0(v, ch, g, par):
                if ln is not None:
                    v.wait_ge(s_xp.sem, (g + 1) * 16 * LOADS)
                    for b in range(GB):
                        v.bn_stats(lst[:, b, 0:6], xp[:, par, b, :]).then_inc(ch.sem, 1)
                        v.wait_ge(ch.sem, ch.next())
                        v.sem_inc(s_step, 1)
                        v.bn_aggr(lst[:, b, 6:8], lst[:, b, 0:6]).then_inc(ch.sem, 1)
                        v.wait_ge(ch.sem, ch.next())
                    v.wait_ge(s_lp.sem, s_lp.at(g))
                    v.tensor_scalar(lvar[:, 0, :], lst[:, :, 7], EPS, None, ALU.add).then_inc(s_ln.sem, 1)
                    v.wait_ge(s_lp.sem, s_lp.at(g + 1))
                    v.wait_ge(s_pf.sem, s_pf.at(g - 1, nu["x"] + 1))
                    for b in range(GB):
                        v.tensor_scalar(xn[:, b, :], xp[:, par, b, :], lst[:, b, 6:7], lvar[:, 1, b:b + 1],
                                        ALU.subtract, ALU.mult).then_inc(ch.sem, 1)
                        v.wait_ge(ch.sem, ch.next())
                    v.tensor_tensor(xn[:], xn[:], lnw[:, 0, :].unsqueeze(1).to_broadcast([P, GB, D]), ALU.mult).then_inc(ch.sem, 1)
                    v.wait_ge(ch.sem, ch.next())
                    ins = v.tensor_tensor(xn[:], xn[:], lnw[:, 1, :].unsqueeze(1).to_broadcast([P, GB, D]), ALU.add)
                    ins.then_inc(s_xn.sem, 1)
                    ins2 = v.nop()
                    ins2.then_inc(s_xpfree.sem, 1)
                if mask is not None:
                    v.wait_ge(s_xp.sem, (g + 1) * 16 * LOADS)
                    v.wait_ge(s_Sf.sem, s_Sf.at((g - 1) * GB))
                    v.wait_ge(s_pf.sem, s_pf.at(g - 1))
                    v.tensor_scalar(neg[:, par], mi[:], 1.0, 1e9, ALU.subtract, ALU.mult).then_inc(s_neg.sem, 1)

            def prep_b(v, ch, g, par):
                for t, (name, n) in enumerate((("q", GT), ("k", kt))):
                    if rms:
                        v.wait_ge(s_sq.sem, s_sq.at(g, t + 1))
                        v.tensor_reduce(ms[:, t, 0, :], sq[:].rearrange("p b (h d) -> p (b h) d", d=DH), AX.X, ALU.add).then_inc(ch.sem, 1)
                        v.wait_ge(ch.sem, ch.next())
                        v.wait_ge(s_rp.sem, s_rp.at(g - 1, t + 1))
                        v.tensor_scalar(ms[:, t, 1, :], ms[:, t, 0, :], 1.0 / DH, float(np.finfo(np.float32).eps),
                                        ALU.mult, ALU.add).then_inc(s_ms.sem, 1)
                        v.wait_ge(s_rp.sem, s_rp.at(g, t + 1))
                        v.tensor_tensor(qtok[:, t].rearrange("p b (h d) -> p (b h) d", d=DH),
                                        bankP[:].rearrange("p (h d) -> p h d", d=DH),
                                        ms[:, t, 2, :].unsqueeze(2).to_broadcast([P, GB * H, DH]), ALU.mult).then_inc(s_pf.sem, 1)
                v.wait_ge(s_ps.sem, s_ps.at(g * 32))
                for t, (name, n) in enumerate((("q", GT), ("k", kt))):
                    v.wait_ge(s_pf.sem, s_pf.at(g, nu[name + "n" if rms else name] + 1))
                    v.tensor_copy(qp[:, t, 0, 0:n], qf[:, t, 0:n]).then_inc(s_hi.sem, 1)
                for t, n in enumerate((GT, kt)):
                    v.wait_ge(s_r1.sem, s_r1.at(g, t + 1))
                    v.tensor_copy(qp[:, t, 1, 0:n], qr[:, t, 0:n]).then_inc(s_mid.sem, 1)
                v.wait_ge(s_pb.sem, s_pb.at(g, nu["v"] + 1))
                v.wait_ge(s_vb.sem, s_vb.at((g - 1) * GB))
                src = bankP[0:sk, :].rearrange("p (b d) -> p b d", b=GB)
                if bv is not None:
                    ins = v.tensor_tensor(vS[0:sk, par], src, bvb[0:sk, :].unsqueeze(1).to_broadcast([sk, GB, D]), ALU.add)
                else:
                    ins = v.tensor_copy(vS[0:sk, par], src)
                ins.then_inc(s_pf.sem, 1)

            def step(v, ch, i, lb, live):
                b = 8 * i + lb
                l, q, p = lb // GB, lb % GB, lb % 2
                if live(0):
                    v.wait_ge(s_T.sem, s_T.at(b - 1))
                    for c in range(4):
                        v.wait_ge(s_S.sem, s_S.at(b, c + 1))
                        src = bankS[c % 2][:, 0:4 * sk].rearrange("p (h k) -> p h k", h=4)
                        if mask is not None:
                            v.tensor_tensor(sm[:, c % 2, :].rearrange("p (h k) -> p h k", h=4), src,
                                            neg[:, l, q, :].unsqueeze(1).to_broadcast([P, 4, S2]), ALU.add).then_inc(s_Sf.sem, 1)
                            v.wait_ge(s_Sf.sem, s_Sf.at(b, c + 1))
                            v.tensor_reduce(nm[:, p, 0, 4 * c:4 * c + 4],
                                            sm[:, c % 2, :].rearrange("p (h k) -> p h k", h=4), AX.X, ALU.max, negate=True).then_inc(ch.sem, 1)
                            v.wait_ge(ch.sem, ch.next())
                        else:
                            v.tensor_reduce(nm[:, p, 0, 4 * c:4 * c + 4], src, AX.X, ALU.max, negate=True).then_inc(s_Sf.sem, 1)
                    v.wait_ge(s_Sf.sem, s_Sf.at(b, 4))
                    v.tensor_copy(nmp[:, p, 0, :], nm[:, p, 0, :]).then_inc(ch.sem, 1)
                    v.wait_ge(ch.sem, ch.next())
                    v.tensor_tensor(nm[:, p, 1, :], nm[:, p, 0, :], nmp[:, p, 0, :], ALU.subtract).then_inc(ch.sem, 1)
                    v.wait_ge(ch.sem, ch.next())
                    v.tensor_copy(nmp[:, p, 1, :], nm[:, p, 1, :]).then_inc(ch.sem, 1)
                    v.wait_ge(ch.sem, ch.next())
                    v.tensor_tensor(nmp[:, p, 2, :], nm[:, p, 1, :], nmp[:, p, 1, :], ALU.subtract).then_inc(s_nmp.sem, 1)
                if live(3):
                    v.wait_ge(s_ot.sem, s_ot.at(b - 3 + 1))
                    v.wait_ge(s_o2.sem, s_o2.at(b - 3))
                    o = bankY[:, 0:2 * VW].rearrange("p (h c) -> p h c", c=VC)
                    v.reciprocal(rden[:], o[:, :, DH]).then_inc(ch.sem, 1)
                    v.wait_ge(ch.sem, ch.next())
                    v.tensor_tensor(heads(on[:]), o[:, :, 0:DH], rden[:].unsqueeze(2).to_broadcast([P, H, DH]),
                                    ALU.mult).then_inc(s_on.sem, 1)
                if mask is not None and live(1):
                    bb, lm = b - 1, (lb - 1) % 8
                    for c in range(4):
                        v.wait_ge(s_st.sem, s_st.at(bb, c + 1))
                        v.wait_ge(s_e.sem, s_e.at(bb, c + 1 - 2))
                        v.tensor_tensor(smT[0:sk, c % 2, :].rearrange("p (h t) -> p h t", h=4),
                                        bankT[c % 2][0:sk, :].rearrange("p (h t) -> p h t", h=4),
                                        negT[0:sk, lm // GB, (lm % GB) * S:(lm % GB + 1) * S].unsqueeze(1).to_broadcast([sk, 4, S]),
                                        ALU.add).then_inc(s_sm.sem, 1)
                if normed and live(4):
                    bb, lm = b - 4, (lb - 4) % 8
                    v.wait_ge(s_pw.sem, s_pw.at(bb + 1))
                    v.tensor_scalar(xr[:, lm // GB, lm % GB, :], r[:, lm % 2, :], stat[:, lm % 2, 6:7], var[:, lm % 2, 1:2],
                                    ALU.subtract, ALU.mult).then_inc(s_xo.sem, 1)
                if live(3):
                    bb, lm = b - 3, (lb - 3) % 8
                    v.wait_ge(s_y.sem, s_y.at(bb + 1))
                    if lm % GB == 0:
                        v.wait_ge(s_xr.sem, (2 * i + (lb - 3) // GB + 1) * 16)
                    xrow = xr[:, lm // GB, lm % GB, :]
                    if normed:
                        rr = r[:, lm % 2, :]
                        v.wait_ge(s_xo.sem, s_xo.at(bb - 1))
                        v.tensor_tensor(rr, bankY[:, 0:D], xrow, ALU.add).then_inc(s_r.sem, 1)
                        v.wait_ge(s_r.sem, s_r.at(bb + 1))
                        v.bn_stats(stat[:, lm % 2, 0:6], rr).then_inc(ch.sem, 1)
                        v.wait_ge(ch.sem, ch.next())
                        v.sem_inc(s_step, 1)
                        v.bn_aggr(stat[:, lm % 2, 6:8], stat[:, lm % 2, 0:6]).then_inc(ch.sem, 1)
                        v.wait_ge(ch.sem, ch.next())
                        v.tensor_scalar(var[:, lm % 2, 0:1], stat[:, lm % 2, 7:8], EPS, None, ALU.add).then_inc(s_v.sem, 1)
                    else:
                        v.tensor_tensor(xrow, bankY[:, 0:D], xrow, ALU.add).then_inc(s_r.sem, 1)
                if live(0):
                    v.wait_ge(s_T.sem, s_T.at(b + 1))
                    v.wait_ge(s_st.sem, s_st.at(b - 1))
                    v.tensor_copy(nmT[:, p, :], bankMb[0:PARTS * H, 0:S]).then_inc(s_nmT.sem, 1)

            def prologue(v, ch):
                prep_0(v, ch, 0, 0)
                prep_b(v, ch, 0, 0)

            def turn(v, ch, i):
                first, last = isinstance(i, int) and i == 0, isinstance(i, int) and i == TURNS - 1
                for lb in range(8):
                    step(v, ch, i, lb, lambda k: not (first and lb < k))
                    l = lb // GB
                    if not (last and l):
                        if lb % GB == 0:
                            prep_0(v, ch, 2 * i + l + 1, 1 - l)
                        if lb % GB == 1:
                            prep_b(v, ch, 2 * i + l + 1, 1 - l)

            def tail(v, ch):
                for k in range(4):
                    step(v, ch, TURNS, k, lambda n: k < n)
            of_seq = 4 + (4 if mask is not None else 0) + (2 if normed else 0)
            of_group = (3 * GB + 1 if ln is not None else 0) + (2 if rms else 0)
            looped(dve, s_dve, TURNS, 8 * of_seq + 2 * of_group, prologue, turn, tail)

        @block.gpsimd
        def _(pool):
            ins = pool.memset(vB[:], 0.0)
            ins.then_inc(s_pool, 1)
            pool.wait_ge(s_pool, 1)
            for p in range(2):
                for h2 in range(2):
                    pool.memset(diagonal(vB[:, p, h2, :])[:, :, DH:VC], 1.0 if gate is None else 0.0).then_inc(s_pool, 1)
            n = 5
            if gate is not None:
                pool.memset(oB[:], 0.0).then_inc(s_pool, 1)
                n += 1
                pool.wait_ge(s_pool, n)
                for h2 in range(2):
                    pool.memset(diagonal(oB[:, h2, :])[:, :, DH:VC], 1.0).then_inc(s_pool, 1)
                    n += 1
            if rms:
                pool.memset(hpw[:], -0.5).then_inc(s_pool, 1)
                n += 1
            pool.wait_ge(s_pool, n)
            pool.nop().then_inc(s_setup.sem, 1)

            def prep_0(g, par):
                if ln is not None:
                    pool.wait_ge(s_ln.sem, s_ln.at(g + 1))
                    pool.wait_ge(s_xn.sem, s_xn.at(g))
                    pool.tensor_tensor(lvar[:, 1, :], lvar[:, 0, :], half_pow[:, 0:GB], ALU.pow).then_inc(s_lp.sem, 1)
                else:
                    pool.wait_ge(s_pb.sem, s_pb.at(g, nu["g" if mask is not None else ("c" if ctx is not None else "x")] + 1))
                    pool.nop().then_inc(s_xpfree.sem, 1)

            def prep_b(g, par):
                if rms:
                    for t in range(2):
                        pool.wait_ge(s_ms.sem, s_ms.at(g, t + 1))
                        pool.wait_ge(s_pf.sem, s_pf.at(g - 1, nu["qt" if t == 0 else "kt"] + 1))
                        pool.tensor_tensor(ms[:, t, 2, :], ms[:, t, 1, :], hpw[:], ALU.pow).then_inc(s_rp.sem, 1)
                for t, n in enumerate((GT, kt)):
                    pool.wait_ge(s_hi.sem, s_hi.at(g, t + 1))
                    pool.wait_ge(s_lo.sem, s_lo.at(g - 1, t + 1))
                    pool.tensor_tensor(qr[:, t, 0:n], qf[:, t, 0:n], qp[:, t, 0, 0:n], ALU.subtract).then_inc(s_r1.sem, 1)
                    pool.wait_ge(s_mid.sem, s_mid.at(g, t + 1))
                    pool.wait_ge(s_ps.sem, s_ps.at(g * 32))
                    pool.wait_ge(s_r1.sem, s_r1.at(g, t + 1))
                    pool.tensor_tensor(qp[:, t, 2, 0:n], qr[:, t, 0:n], qp[:, t, 1, 0:n], ALU.subtract).then_inc(s_lo.sem, 1)

            def step(i, lb, live):
                b = 8 * i + lb
                l, q, p = lb // GB, lb % GB, lb % 2
                if live(0):
                    if q == 0:
                        pool.wait_ge(s_pf.sem, s_pf.at(2 * i + l, nu["v"] + 1))
                    pool.wait_ge(s_pv.sem, s_pv.at(b - 1))
                    pool.sem_inc(s_step, 1)
                    src = vS[0:sk, l, q, :].rearrange("p (a h d) -> p a h d", a=2, h=8)
                    for h2 in range(2):
                        ins = pool.tensor_copy(diagonal(vB[0:sk, p, h2, :])[:, :, 0:DH], src[:, h2])
                    ins.then_inc(s_vb.sem, 1)
                if gate is not None and live(1):
                    bb, lm = b - 1, (lb - 1) % 8
                    pool.wait_ge(s_e.sem, s_e.at(bb, 4))
                    pool.wait_ge(s_pv.sem, s_pv.at(bb - 1))
                    pool.tensor_tensor(pG[0:sk, lm % 2], pT[0:sk, lm % 2],
                                       gpT[0:sk, lm // GB, (lm % GB) * S:(lm % GB + 1) * S].unsqueeze(1).to_broadcast([sk, H, S]),
                                       ALU.mult).then_inc(s_pg.sem, 1)
                if normed and live(3):
                    lm = (lb - 3) % 8
                    pool.wait_ge(s_v.sem, s_v.at(b - 3 + 1))
                    pool.wait_ge(s_xo.sem, s_xo.at(b - 3 - 1))
                    pool.tensor_tensor(var[:, lm % 2, 1:2], var[:, lm % 2, 0:1], half_pow[:, 0:1], ALU.pow).then_inc(s_pw.sem, 1)

            def turn(i, first=False, last=False):
                for lb in range(8):
                    step(i, lb, lambda k: not (first and lb < k))
                    l = lb // GB
                    if not (last and l):
                        if lb % GB == 0:
                            prep_0(2 * i + l + 1, 1 - l)
                        if lb % GB == 1:
                            prep_b(2 * i + l + 1, 1 - l)
            prep_0(0, 0)
            prep_b(0, 0)
            turn(0, first=True)
            with pool.Fori(1, TURNS - 1) as i:
                turn(i)
            turn(TURNS - 1, last=True)
            for k in range(4):
                step(TURNS, k, lambda n: k < n)

def experts(nc, const, banks, x, x1, y, a):
    E, F = 8, 512
    FT = F // P
    TURNS = NG // 2
    ident, identb, half_pow = const["ident"], const["identb"], const["half_pow"]
    g_, b_, gw, gb, w1, b1, w2, b2 = [a["L0_ffn_" + n] for n in
                                      ("ln2_g", "ln2_b", "gate_w", "gate_b", "w1", "b1", "w2", "b2")]
    with ExitStack() as st:
        def sb(name, shape, dt=F32):
            return st.enter_context(nc.sbuf_tensor(f"moe_{name}", shape, dt))

        def sem(name, per=1):
            return Count(nc.alloc_semaphore(f"moe_{name}"), per)

        w1s = sb("w1", [P, E, F])
        w2s = sb("w2", [P, E, FT, D])
        b1s = sb("b1", [P, E, FT])
        b2s = sb("b2", [P, E])
        gws = sb("gw", [P, E])
        gbs = sb("gb", [P, E])
        lnw = sb("lnw", [P, 2, D])
        rank = sb("rank", [P, E])
        pick = sb("pick", [E, E, P], BF16)
        xa = sb("xa", [P, 2, GB, D])
        xb = sb("xb", [P, 2, GB, D])
        hn = sb("hn", [P, GB, D])
        hT = sb("hT", [P, 2, GT])
        lst = sb("lst", [P, GB, 8])
        lvar = sb("lvar", [P, 2, GB])
        ost = sb("ost", [P, GB, 8])
        ovar = sb("ovar", [P, 2, GB])
        lg = sb("lg", [P, GB, E])
        lmax = sb("lmax", [P, 2, GB])
        one = sb("one", [P, GB, E], BF16)
        oneT = sb("oneT", [E, 2, GT], BF16)
        mid = sb("mid", [P, 2, FT, GT])
        ye = sb("ye", [P, 2, GT])
        tm = sb("tm", [P, GT])
        acc = sb("acc", [P, 2, GT])

        s_w = sem("weights"); s_setup = sem("setup"); s_ld = sem("loaded", 32); s_store = sem("stored", 16)
        s_var = sem("front_var"); s_pw = sem("front_pow"); s_hn = sem("front_norm"); s_tp = sem("front_turned")
        s_hT = sem("front_copied"); s_lg = sem("logits"); s_one = sem("chosen"); s_ot = sem("choice_turned")
        s_oT = sem("choice_copied"); s_mid = sem("mid", FT); s_rl = sem("relu", FT); s_y = sem("expert_out")
        s_ye = sem("expert_biased"); s_mk = sem("mask"); s_tm = sem("masked"); s_acc = sem("accumulated")
        s_bk = sem("turned_back"); s_fin = sem("residual_added"); s_ov = sem("out_var"); s_op = sem("out_pow")
        s_o = sem("out_ready")
        s_dve = nc.alloc_semaphore("moe_dve_done")
        s_step = nc.alloc_semaphore("moe_passed")
        s_pool = nc.alloc_semaphore("moe_pool_setup")
        NW = 8 + E
        x_g, x1_g, o_g = [t.rearrange("(g b) t d -> g t b d", b=GB) for t in (x, x1, y)]
        bankA, bankL = banks[0], banks[1]
        bankLb = bankL.bitcast(BF16)
        block = st.enter_context(nc.Block())

        @block.sync
        def _(sp):
            def load_w(dst, src):
                sp.dma_start(dst, src).then_inc(s_w.sem, 16)

            def load(g, par):
                sp.wait_ge(s_hn.sem, s_hn.at(g))
                sp.sem_inc(s_step, 1)
                sp.wait_ge(s_store.sem, s_store.at(g - 1))
                sp.sem_inc(s_step, 1)
                sp.dma_start(xa[:, par], x_g[g]).then_inc(s_ld.sem, 16)
                sp.dma_start(xb[:, par], x1_g[g]).then_inc(s_ld.sem, 16)

            def store(g, par):
                sp.wait_ge(s_o.sem, s_o.at(g + 1))
                sp.sem_inc(s_step, 1)
                sp.dma_start(o_g[g], xb[:, par]).then_inc(s_store.sem, 16)

            load(0, 0)
            load_w(gws[:], gw)
            load_w(gbs[:], gb.rearrange("(a e) -> a e", a=1).to_broadcast([P, E]))
            load_w(lnw[:, 0, :], g_.rearrange("(a d) -> a d", a=1).to_broadcast([P, D]))
            load_w(lnw[:, 1, :], b_.rearrange("(a d) -> a d", a=1).to_broadcast([P, D]))
            load_w(b1s[:], b1)
            load_w(b2s[:], b2)
            for e in range(E):
                load_w(w1s[:, e, :], w1[e])
            load_w(w2s[:, 0:E // 2], w2[0:E // 2].rearrange("e (c f) d -> f e c d", f=P))
            load_w(w2s[:, E // 2:E], w2[E // 2:E].rearrange("e (c f) d -> f e c d", f=P))

            def turn(i, last=False):
                for l in range(2):
                    g = 2 * i + l
                    if not (last and l):
                        load(g + 1, 1 - l)
                    store(g, l)
            turn(0)
            with sp.Fori(1, TURNS - 1) as i:
                turn(i)
            turn(TURNS - 1, last=True)
            sp.wait_ge(s_store.sem, NG * 16)

        @block.tensor
        def _(pe):
            pe.wait_ge(s_w.sem, 16 * NW)
            pe.wait_ge(s_setup.sem, 1)

            def front(g):
                pe.wait_ge(s_hn.sem, s_hn.at(g + 1))
                pe.wait_ge(s_fin.sem, s_fin.at(g - 1))
                pe.sem_inc(s_step, 1)
                for b in range(GB):
                    ins = pe.transpose(bankA[:, b * S:(b + 1) * S], hn[:, b, :], ident[:])
                ins.then_inc(s_tp.sem, 1)

            def logits(g, par):
                pe.wait_ge(s_hT.sem, s_hT.at(g + 1))
                pe.wait_ge(s_oT.sem, s_oT.at(g))
                pe.sem_inc(s_step, 1)
                for b in range(GB):
                    ins = pe.matmul(bankL[:, b * E:(b + 1) * E], hT[:, par, b * S:(b + 1) * S], gws[:], start=True, stop=True)
                ins.then_inc(s_lg.sem, 1)

            def choice(g):
                pe.wait_ge(s_one.sem, s_one.at(g + 1))
                pe.sem_inc(s_step, 1)
                for b in range(GB):
                    ins = pe.transpose(bankLb[0:E, b * S:(b + 1) * S], one[:, b, :], identb[:])
                ins.then_inc(s_ot.sem, 1)

            def mids(n, e, par):
                for f in range(FT):
                    pe.wait_ge(s_rl.sem, s_rl.at(n, f - 1))
                    pe.matmul(banks[2 + f % 2], w1s[:, e, f * P:(f + 1) * P], hT[:, par, :],
                              start=True, stop=True).then_inc(s_mid.sem, 1)

            def out(g, n, e, par):
                if e == 0:
                    pe.wait_ge(s_oT.sem, s_oT.at(g + 1))
                pe.wait_ge(s_tm.sem, s_tm.at(n - 1))
                pe.matmul(banks[6 + e % 2], pick[:, e, :], oneT[:, par, :], start=True, stop=True).then_inc(s_mk.sem, 1)
                pe.wait_ge(s_ye.sem, s_ye.at(n - 1))
                for f in range(FT):
                    pe.wait_ge(s_rl.sem, s_rl.at(n, f + 1))
                    ins = pe.matmul(banks[4 + e % 2], w2s[:, e, f, :], mid[:, e % 2, f, :], start=(f == 0), stop=(f == FT - 1))
                ins.then_inc(s_y.sem, 1)

            def back(g, par):
                pe.wait_ge(s_acc.sem, s_acc.at((g + 1) * E))
                pe.wait_ge(s_hT.sem, s_hT.at(g + 1))
                pe.sem_inc(s_step, 1)
                for b in range(GB):
                    ins = pe.transpose(bankA[:, b * S:(b + 1) * S], acc[:, par, b * S:(b + 1) * S], ident[:])
                ins.then_inc(s_bk.sem, 1)

            def turn(i, first=False, last=False):
                for l in range(2):
                    g = 2 * i + l
                    for e in range(E):
                        n = g * E + e
                        if e + 1 < E:
                            mids(n + 1, e + 1, l)
                        elif not (last and l):
                            mids(n + 1, 0, 1 - l)
                        out(g, n, e, l)
                        if e == 1 and not (first and not l):
                            back(g - 1, 1 - l)
                        if not (last and l):
                            if e == 3:
                                front(g + 1)
                            if e == 4:
                                logits(g + 1, 1 - l)
                            if e == 5:
                                choice(g + 1)
            front(0)
            logits(0, 0)
            choice(0)
            mids(0, 0, 0)
            turn(0, first=True)
            with pe.Fori(1, TURNS - 1) as i:
                turn(i)
            turn(TURNS - 1, last=True)
            back(NG - 1, 1)

        @block.scalar
        def _(act):
            act.wait_ge(s_w.sem, 16 * NW)

            def front(g, par):
                act.wait_ge(s_tp.sem, s_tp.at(g + 1))
                act.wait_ge(s_mid.sem, s_mid.at((g - 1) * E))
                act.activation(hT[:, par, :], bankA, ACT.Copy).then_inc(s_hT.sem, 1)

            def choice(g, par):
                act.wait_ge(s_ot.sem, s_ot.at(g + 1))
                act.wait_ge(s_mk.sem, s_mk.at((g - 1) * E))
                act.activation(oneT[:, par, :], bankLb[0:E, 0:GT], ACT.Copy).then_inc(s_oT.sem, 1)

            def relu(n, e):
                act.wait_ge(s_y.sem, s_y.at(n - 1))
                for f in range(FT):
                    act.wait_ge(s_mid.sem, s_mid.at(n, f + 1))
                    act.activation(mid[:, e % 2, f, :], banks[2 + f % 2], ACT.Relu, bias=b1s[:, e, f:f + 1]).then_inc(s_rl.sem, 1)

            def bias(n, e):
                act.wait_ge(s_y.sem, s_y.at(n + 1))
                act.wait_ge(s_tm.sem, s_tm.at(n - 1))
                act.activation(ye[:, e % 2, :], banks[4 + e % 2], ACT.Identity, bias=b2s[:, e:e + 1]).then_inc(s_ye.sem, 1)

            def turn(i, last=False):
                for l in range(2):
                    g = 2 * i + l
                    for e in range(E):
                        n = g * E + e
                        if e + 1 < E or not (last and l):
                            relu(n + 1, (e + 1) % E)
                        bias(n, e)
                        if not (last and l):
                            if e == 3:
                                front(g + 1, 1 - l)
                            if e == 5:
                                choice(g + 1, 1 - l)
            front(0, 0)
            choice(0, 0)
            relu(0, 0)
            turn(0)
            with act.Fori(1, TURNS - 1) as i:
                turn(i)
            turn(TURNS - 1, last=True)

        def stats(v, ch, dst, src):
            for b in range(GB):
                ins = v.bn_stats(dst[:, b, 0:6], src(b))
            ins.then_inc(ch.sem, 1)
            v.wait_ge(ch.sem, ch.next())
            v.sem_inc(s_step, 1)
            for b in range(GB):
                ins = v.bn_aggr(dst[:, b, 6:8], dst[:, b, 0:6])
            ins.then_inc(ch.sem, 1)
            v.wait_ge(ch.sem, ch.next())

        @block.vector
        def _(dve):
            def front(v, ch, g, par):
                v.wait_ge(s_ld.sem, s_ld.at(g + 1))
                stats(v, ch, lst, lambda b: xb[:, par, b, :])
                v.wait_ge(s_pw.sem, s_pw.at(g))
                v.tensor_scalar(lvar[:, 0, :], lst[:, :, 7], EPS, None, ALU.add).then_inc(s_var.sem, 1)
                v.wait_ge(s_pw.sem, s_pw.at(g + 1))
                v.wait_ge(s_tp.sem, s_tp.at(g))
                for b in range(GB):
                    ins = v.tensor_scalar(hn[:, b, :], xb[:, par, b, :], lst[:, b, 6:7], lvar[:, 1, b:b + 1], ALU.subtract, ALU.mult)
                ins.then_inc(ch.sem, 1)
                v.wait_ge(ch.sem, ch.next())
                v.tensor_tensor(hn[:], hn[:], lnw[:, 0, :].unsqueeze(1).to_broadcast([P, GB, D]), ALU.mult).then_inc(ch.sem, 1)
                v.wait_ge(ch.sem, ch.next())
                v.tensor_tensor(hn[:], hn[:], lnw[:, 1, :].unsqueeze(1).to_broadcast([P, GB, D]), ALU.add).then_inc(s_hn.sem, 1)

            def choose(v, ch, g):
                v.wait_ge(s_lg.sem, s_lg.at(g + 1))
                v.tensor_tensor(lg[:], bankL[:, 0:GB * E].rearrange("p (b e) -> p b e", b=GB),
                                gbs[:].unsqueeze(1).to_broadcast([P, GB, E]), ALU.add).then_inc(ch.sem, 1)
                v.wait_ge(ch.sem, ch.next())
                v.tensor_reduce(lmax[:, 0, :], lg[:], AX.X, ALU.max).then_inc(ch.sem, 1)
                v.wait_ge(ch.sem, ch.next())
                v.tensor_tensor(lg[:], lg[:], lmax[:, 0, :].unsqueeze(2).to_broadcast([P, GB, E]), ALU.is_equal).then_inc(ch.sem, 1)
                v.wait_ge(ch.sem, ch.next())
                v.tensor_tensor(lg[:], lg[:], rank[:].unsqueeze(1).to_broadcast([P, GB, E]), ALU.mult).then_inc(ch.sem, 1)
                v.wait_ge(ch.sem, ch.next())
                v.tensor_reduce(lmax[:, 1, :], lg[:], AX.X, ALU.max).then_inc(ch.sem, 1)
                v.wait_ge(ch.sem, ch.next())
                v.wait_ge(s_ot.sem, s_ot.at(g))
                v.tensor_tensor(one[:], lg[:], lmax[:, 1, :].unsqueeze(2).to_broadcast([P, GB, E]), ALU.is_equal).then_inc(s_one.sem, 1)

            def masked(v, ch, g, n, e, par):
                v.wait_ge(s_ye.sem, s_ye.at(n + 1))
                v.wait_ge(s_mk.sem, s_mk.at(n + 1))
                if e == 0:
                    v.wait_ge(s_bk.sem, s_bk.at(g - 1))
                    v.tensor_tensor(acc[:, par, :], ye[:, e % 2, :], banks[6 + e % 2], ALU.mult).then_inc(s_tm.sem, 1)
                    v.wait_ge(s_tm.sem, s_tm.at(n + 1))
                    v.sem_inc(s_acc.sem, 1)
                else:
                    v.wait_ge(s_acc.sem, s_acc.at(n))
                    v.tensor_tensor(tm[:], ye[:, e % 2, :], banks[6 + e % 2], ALU.mult).then_inc(s_tm.sem, 1)
                    v.wait_ge(s_tm.sem, s_tm.at(n + 1))
                    v.tensor_tensor(acc[:, par, :], acc[:, par, :], tm[:], ALU.add).then_inc(s_acc.sem, 1)

            def finish(v, ch, g, par):
                v.wait_ge(s_bk.sem, s_bk.at(g + 1))
                v.tensor_tensor(xb[:, par], xb[:, par], xa[:, par], ALU.add).then_inc(ch.sem, 1)
                v.wait_ge(ch.sem, ch.next())
                v.tensor_tensor(xb[:, par].rearrange("p b d -> p (b d)"), xb[:, par].rearrange("p b d -> p (b d)"),
                                bankA, ALU.add).then_inc(s_fin.sem, 1)
                v.wait_ge(s_fin.sem, s_fin.at(g + 1))
                stats(v, ch, ost, lambda b: xb[:, par, b, :])
                v.wait_ge(s_op.sem, s_op.at(g))
                v.tensor_scalar(ovar[:, 0, :], ost[:, :, 7], EPS, None, ALU.add).then_inc(s_ov.sem, 1)
                v.wait_ge(s_op.sem, s_op.at(g + 1))
                for b in range(GB):
                    ins = v.tensor_scalar(xb[:, par, b, :], xb[:, par, b, :], ost[:, b, 6:7], ovar[:, 1, b:b + 1], ALU.subtract, ALU.mult)
                ins.then_inc(s_o.sem, 1)

            def prologue(v, ch):
                v.wait_ge(s_w.sem, 16 * NW)
                v.wait_ge(s_setup.sem, 1)
                front(v, ch, 0, 0)
                choose(v, ch, 0)

            def turn(v, ch, i):
                first, last = isinstance(i, int) and i == 0, isinstance(i, int) and i == TURNS - 1
                for l in range(2):
                    g = 2 * i + l
                    for e in range(E):
                        masked(v, ch, g, g * E + e, e, l)
                        if e == 1 and not (first and not l):
                            finish(v, ch, g - 1, 1 - l)
                        if not (last and l):
                            if e == 2:
                                front(v, ch, g + 1, 1 - l)
                            if e == 4:
                                choose(v, ch, g + 1)

            def tail(v, ch):
                finish(v, ch, NG - 1, 1)
            of_group = 4 + 5 + 3
            looped(dve, s_dve, TURNS, 2 * of_group, prologue, turn, tail)

        @block.gpsimd
        def _(pool):
            for e in range(E):
                pool.memset(rank[:, e:e + 1], float(E - e)).then_inc(s_pool, 1)
            pool.memset(pick[:], 0.0).then_inc(s_pool, 1)
            pool.wait_ge(s_pool, E + 1)
            pool.affine_select(out=pick[:], in_=pick[:], compare_op=ALU.not_equal, fill=1.0, base=0,
                               pattern=[[-1, E], [0, P]], channel_multiplier=1).then_inc(s_setup.sem, 1)

            def power(s_in, s_out, v, g):
                pool.wait_ge(s_in.sem, s_in.at(g + 1))
                pool.tensor_tensor(v[:, 1, :], v[:, 0, :], half_pow[:, 0:GB], ALU.pow).then_inc(s_out.sem, 1)

            def front(g):
                pool.wait_ge(s_hn.sem, s_hn.at(g))
                power(s_var, s_pw, lvar, g)

            def finish(g):
                pool.wait_ge(s_o.sem, s_o.at(g))
                power(s_ov, s_op, ovar, g)
            front(0)
            front(1)
            finish(0)
            front(2)
            with pool.Fori(1, NG - 2) as g:
                finish(g)
                front(g + 2)
            finish(NG - 2)
            finish(NG - 1)

def mamba(nc, const, banks, x, y, a):
    DI, NS, RANK, CK, NC = 256, 16, 8, 4, 2
    SL = NS * NC
    TURNS = NG // 2
    PADS = CK - 1
    BROW, CROW, XM = 32, 64, 96
    FAR = 1e28
    A_MIN = 1e-25
    ident, half_pow, ones_row = const["ident"], const["half_pow"], const["ones_row"]
    pre = ("fw_", "bw_")

    def par_(name):
        return a["L0_attn_" + name]

    PREP = {6: ["xT", "c1", "z1", "dt0"], 7: ["c0", "z0", "xd", "dt1"]}
    POST = {6: ["o"], 7: []}
    FF = {6: ["m0", "f"], 7: ["yT", "m1"]}
    ORDER = {k: [PREP[k] + POST[k] + FF[k], PREP[k] + POST[k]] for k in (6, 7)}

    def use(g, d, name):
        for k in (6, 7):
            if name in ORDER[k][d]:
                first, per = len(ORDER[k][0]), len(ORDER[k][0]) + len(ORDER[k][1])
                missed = len(POST[k] + FF[k])
                n = g * per + len(PREP[k]) - missed + d * first + ORDER[k][d].index(name)
                if isinstance(g, int):
                    if g == 0 and d == 0:
                        n += missed
                    if g == NG - 1 and d == 1:
                        n -= len(PREP[k])
                    if g == NG:
                        n -= 2 * len(PREP[k])
                return k, n

    def use_first(name):
        for k in (6, 7):
            if name in PREP[k]:
                return k, PREP[k].index(name)

    with ExitStack() as st:
        def sb(name, shape, dt=F32):
            return st.enter_context(nc.sbuf_tensor(f"m_{name}", shape, dt))

        def sem(name, per=1):
            return Count(nc.alloc_semaphore(f"m_{name}"), per)

        Bd = nc.dram_tensor("m_B", (2, NS, GT), F32, kind="Internal").ap()
        flip = sb("flip", [P, P])
        selC = sb("selC", [CROW + NS, NS, P], BF16)
        win = sb("win", [P, 2, 2 * DI])
        wck = sb("wck", [P, 2, CK, DI])
        cb = sb("cb", [P, 2, NC])
        wx = sb("wx", [P, 2, NC, XM])
        wdt = sb("wdt", [RANK, 2, DI])
        bdt = sb("bdt", [P, 2, NC])
        A = sb("A", [P, 2, NC, NS])
        Dp = sb("Dp", [P, 2, NC])
        wo = sb("wo", [P, 2, NC, D])
        nw = sb("nw", [P, 2])
        fin = sb("fin", [P, 2, D])
        w1 = sb("w1", [P, DI])
        b1 = sb("b1", [P, NC])
        w2 = sb("w2", [P, NC, D])
        b2 = sb("b2", [1, GB, D])
        xg = sb("xg", [P, 2, GB, D])
        xTp = sb("xTp", [P, GB, PADS + S])
        cc = sb("cc", [P, NC, GT])
        tu = sb("tu", [P, NC, GT])
        tz = sb("tz", [P, NC, GT])
        ln = sb("ln", [P, NC, GT])
        u = sb("u", [P, 2, NC, GT])
        sz = sb("sz", [P, 2, NC, GT])
        xd = sb("xd", [XM, GT])
        ch_hi = sb("C_hi", [CROW + NS, GT], BF16)
        ch_r = sb("C_rest", [CROW + NS, GT])
        ch_mid = sb("C_mid", [CROW + NS, GT], BF16)
        Cs = sb("Cs", [CROW + NS, 2, GT], BF16)
        Bb = sb("Bb", [P, 2, NS, GT])
        dt = sb("dt", [P, 2, NC, GT])
        dtu = sb("dtu", [P, 2, NC, GT])
        dBu = sb("dBu", [P, 2, GT])
        h = sb("h", [P, 2, GT])
        hC = sb("hC", [P, 2, GT])
        yd = sb("yd", [P, NC, GT])
        nrm = sb("nrm", [P, 2, GB, D])
        yT = sb("yT", [P, GT])
        md = sb("md", [P, NC, GT])
        ff = sb("ff", [P, GB, D])
        xo = sb("xo", [P, 2, GB, D])
        ost = sb("ost", [P, 3, GB, 8])
        ovar = sb("ovar", [P, 3, 2, GB])

        s_w = sem("weights"); s_set = sem("setup"); s_A = sem("rates"); s_x = sem("x_loaded", 16)
        s_store = [sem(f"stored{l}", 16) for l in range(2)]
        s_pb = {k: sem(f"side{k}_written") for k in (6, 7)}
        s_pf = {k: sem(f"side{k}_read") for k in (6, 7)}
        s_u = sem("u"); s_tz = sem("tanh_gate", 2); s_sz = sem("gate", 2); s_xd = sem("xd")
        s_cc = sem("conv", 2)
        s_hi = sem("C_hi"); s_mid = sem("C_mid"); s_Cs = sem("C_lo"); s_Csh = sem("C_moved", 2)
        s_Bd = sem("B_stored", 16); s_Bb = [sem(f"B_spread{d}", 16) for d in range(2)]
        s_ab = sem("abs", 4); s_z = sem("exp_abs"); s_w1 = sem("one_plus"); s_ln = sem("log"); s_e = sem("correction")
        s_d1 = sem("log_corrected"); s_dr = sem("dt_raw"); s_dtu = sem("dtu"); s_dt = sem("dt")
        s_C = sem("C_spread", NS); s_dA = sem("decay", SL); s_dB = sem("input", SL); s_h = sem("state", SL)
        s_hC = sem("state_C", SL); s_ya = sem("summed", SL); s_yd = sem("y_D", 2); s_yz = sem("y_gated")
        s_var = [sem(f"var{n}") for n in range(3)]
        s_pow = [sem(f"pow{n}") for n in range(3)]
        s_nrm = sem("normed"); s_yT = sem("sum_turned"); s_md = sem("relu", 2); s_ff = sem("ff_normed"); s_o = sem("out")
        s_dve = nc.alloc_semaphore("m_dve_done"); s_pool = nc.alloc_semaphore("m_pool_setup")
        s_act = nc.alloc_semaphore("m_act_setup"); s_step = nc.alloc_semaphore("m_passed")
        NW = 2 * 12 + 9
        x_g, o_g = [t.rearrange("(g b) t d -> g t b d", b=GB) for t in (x, y)]
        turned_by = (ident, flip)
        convw = Bb[:, 0, 0:4, :].rearrange("p a t -> p (a t)")
        block = st.enter_context(nc.Block())

        def schedule(turn):
            def run(eng):
                turn(0, first=True)
                with eng.Fori(1, TURNS - 1) as i:
                    turn(i)
                turn(TURNS - 1, last=True)
            return run

        @block.sync
        def _(sp):
            def load_w(dst, src):
                sp.dma_start(dst, src).then_inc(s_w.sem, 16)

            def row(t, n):
                return t.rearrange("(a d) -> a d", a=1).to_broadcast([n, t.shape[0]])
            sp.dma_start(xg[:, 0], x_g[0]).then_inc(s_x.sem, 16)
            for d in range(2):
                W = lambda n: par_(pre[d] + n)
                load_w(win[:, d, :], W("Win"))
                load_w(convw[:, d * CK * DI:(d + 1) * CK * DI], row(W("convw").rearrange("c k -> (c k)"), P))
                load_w(cb[:, d, :], W("convb"))
                for lo, n, at in ((0, RANK, 0), (RANK, NS, BROW), (RANK + NS, NS, CROW)):
                    sp.wait_ge(s_set.sem, s_set.at(1))
                    load_w(wx[:, d, :, at:at + n], W("Wx").rearrange("(c p) j -> p c j", p=P)[:, :, lo:lo + n])
                load_w(wdt[:, d, :], W("Wdt"))
                load_w(bdt[:, d, :], W("bdt"))
                load_w(A[:, d], W("Alog").rearrange("(c p) s -> p c s", p=P))
                load_w(Dp[:, d, :], W("D"))
                load_w(wo[:, d], W("Wout").rearrange("(c p) j -> p c j", p=P))
                load_w(nw[:, d:d + 1], par_(("fwn_w", "fwn_b")[d]).rearrange("(p a) -> p a", a=1))
            for n, t in enumerate(("fin_w", "fin_b")):
                load_w(fin[:, n, :], row(par_(t), P))
            load_w(w1[:], par_("ff_W1"))
            load_w(b1[:], par_("ff_b1"))
            load_w(w2[:], par_("ff_W2").rearrange("(c p) j -> p c j", p=P))
            for b in range(GB):
                load_w(b2[:, b, :], row(par_("ff_b2"), 1))

            def spread_B(n, g, d):
                sp.wait_ge(s_xd.sem, s_xd.at(n + 1))
                sp.sem_inc(s_step, 1)
                sp.wait_ge(s_dB.sem, s_dB.at(n - 1))
                sp.dma_start(Bd[d], xd[BROW:BROW + NS, :]).then_inc(s_Bd.sem, 16)
                sp.wait_ge(s_Bd.sem, s_Bd.at(n + 1))
                sp.dma_start(Bb[:, d].rearrange("p s t -> p (s t)"),
                             Bd[d].rearrange("s t -> (s t)").rearrange("(a n) -> a n", a=1).to_broadcast([P, NS * GT])).then_inc(s_Bb[d].sem, 16)

            def store(g, l):
                sp.wait_ge(s_o.sem, s_o.at(g + 1))
                sp.sem_inc(s_step, 1)
                sp.dma_start(o_g[g], xo[:, l]).then_inc(s_store[l].sem, 16)

            def load(g, l):
                sp.dma_start(xg[:, l], x_g[g]).then_inc(s_x.sem, 16)

            def turn(i, first=False, last=False):
                for l in range(2):
                    g = 2 * i + l
                    spread_B(2 * g + 1, g, 1)
                    if not (first and not l):
                        store(g - 1, 1 - l)
                    if not (last and l):
                        load(g + 1, 1 - l)
                        spread_B(2 * g + 2, g + 1, 0)
            sp.wait_ge(s_A.sem, s_A.at(2))
            spread_B(0, 0, 0)
            schedule(turn)(sp)
            store(NG - 1, 1)
            for l in range(2):
                sp.wait_ge(s_store[l].sem, TURNS * 16)

        @block.tensor
        def _(pe):
            pe.wait_ge(s_w.sem, 16 * NW)
            pe.wait_ge(s_A.sem, s_A.at(2))
            pe.wait_ge(s_set.sem, s_set.at(2))

            def begin(where):
                k, n = where
                pe.wait_ge(s_pf[k].sem, s_pf[k].at(n))
                return banks[k]

            def end(ins, where):
                ins.then_inc(s_pb[where[0]].sem, 1)

            def prep(at, n, g, l, d, what):
                o = begin(at(what))
                if what == "xT":
                    pe.wait_ge(s_x.sem, s_x.at(g + 1))
                    pe.sem_inc(s_step, 1)
                    for b in range(GB):
                        ins = pe.matmul(o[:, b * S:(b + 1) * S], xg[:, l, b, :], turned_by[d][:], start=True, stop=True)
                if what in ("c0", "c1"):
                    c = int(what[1])
                    pe.wait_ge(s_pf[6].sem, s_pf[6].at(at("xT")[1] + 1))
                    for k in range(CK):
                        ins = pe.matmul(o, wck[:, d, k, c * P:(c + 1) * P], xTp[:, :, k:k + S], start=(k == 0), stop=(k == CK - 1))
                if what in ("z0", "z1"):
                    c = int(what[1])
                    ins = pe.matmul(o, win[:, d, DI + c * P:DI + (c + 1) * P], xTp[:, :, PADS:], start=True, stop=True)
                if what == "xd":
                    pe.wait_ge(s_u.sem, s_u.at(n + 1))
                    for c in range(NC):
                        ins = pe.matmul(o[0:XM, :], wx[:, d, c, :], u[:, d, c, :], start=(c == 0), stop=(c == NC - 1))
                if what in ("dt0", "dt1"):
                    c = int(what[2])
                    pe.wait_ge(s_xd.sem, s_xd.at(n + 1))
                    ins = pe.matmul(o, wdt[:, d, c * P:(c + 1) * P], xd[0:RANK, :], start=True, stop=True)
                end(ins, at(what))

            def post(where, n, l, d):
                o = begin(where)
                pe.wait_ge(s_yz.sem, s_yz.at(n + 1))
                pe.matmul(o, turned_by[d][:], xg[:, l].rearrange("p b d -> p (b d)"), start=True, stop=False)
                for b in range(GB):
                    for c in range(NC):
                        ins = pe.matmul(o[:, b * D:(b + 1) * D], yd[:, c, b * S:(b + 1) * S], wo[:, d, c, :], start=False,
                                        stop=(b == GB - 1 and c == NC - 1))
                end(ins, where)

            def forward(at, g, what):
                o = begin(at(what))
                if what == "yT":
                    pe.wait_ge(s_nrm.sem, s_nrm.at(2 * g + 2))
                    pe.sem_inc(s_step, 1)
                    for b in range(GB):
                        pe.matmul(o[:, b * S:(b + 1) * S], nrm[:, 0, b, :], ident[:], start=True, stop=False)
                        ins = pe.matmul(o[:, b * S:(b + 1) * S], nrm[:, 1, b, :], flip[:], start=False, stop=True)
                if what in ("m0", "m1"):
                    c = int(what[1])
                    pe.wait_ge(s_yT.sem, s_yT.at(g + 1))
                    ins = pe.matmul(o, w1[:, c * P:(c + 1) * P], yT[:], start=True, stop=True)
                if what == "f":
                    pe.wait_ge(s_md.sem, s_md.at(g + 1))
                    pe.matmul(o, ones_row[:], b2[:].rearrange("p b d -> p (b d)"), start=True, stop=False)
                    for b in range(GB):
                        for c in range(NC):
                            pe.matmul(o[:, b * D:(b + 1) * D], md[:, c, b * S:(b + 1) * S], w2[:, c, :], start=False, stop=False)
                        ins = pe.matmul(o[:, b * D:(b + 1) * D], yT[:, b * S:(b + 1) * S], ident[:], start=False, stop=(b == GB - 1))
                end(ins, at(what))

            def spread_C(n, d, s):
                if s == 0:
                    pe.wait_ge(s_Cs.sem, s_Cs.at(n + 1))
                    pe.wait_ge(s_Csh.sem, s_Csh.at(n + 1))
                pe.wait_ge(s_hC.sem, s_hC.at(n, 2 * s - 2))
                pe.matmul(banks[2 + s % 2], selC[:, s, :], Cs[:, d, :], start=True, stop=True).then_inc(s_C.sem, 1)

            def add(n, k):
                s, c = k // NC, k % NC
                if s == 0:
                    pe.wait_ge(s_yd.sem, s_yd.at(n - 1, c + 1))
                pe.wait_ge(s_hC.sem, s_hC.at(n, k + 1))
                pe.matmul(banks[4 + c], ident[:], hC[:, k % 2, :], start=(s == 0), stop=(s == NS - 1)).then_inc(s_ya.sem, 1)

            def unit(g, l, d, first, last):
                n = 2 * g + d
                gp, lp, dp = (g, l, 1) if d == 0 else (g + 1, 1 - l, 0)
                begins, ends = not (first and l == 0 and d == 0), not (last and l == 1 and d == 1)
                at = lambda name: use(g, d, name)
                for k in range(SL):
                    if k % 2 == 0:
                        spread_C(n, d, k // 2)
                    if k >= 2:
                        add(n, k - 2)
                    elif begins:
                        add(n - 1, SL - 2 + k)
                    if ends:
                        for slot, what in ((2, "xT"), (4, "c0"), (6, "c1"), (8, "z0"), (9, "z1"), (11, "xd"), (13, "dt0"), (14, "dt1")):
                            if k == slot:
                                prep(at, n + 1, gp, lp, dp, what)
                    if k == 15 and begins:
                        post(at("o"), n - 1, l if d else 1 - l, 1 - d)
                    if d == 0 and begins:
                        for slot, what in ((20, "yT"), (22, "m0"), (22, "m1"), (24, "f")):
                            if k == slot:
                                forward(at, g - 1, what)

            def turn(i, first=False, last=False):
                for l in range(2):
                    for d in range(2):
                        unit(2 * i + l, l, d, first, last)
            for what in ("xT", "c0", "c1", "z0", "z1", "xd", "dt0", "dt1"):
                prep(use_first, 0, 0, 0, 0, what)
            schedule(turn)(pe)
            add(2 * NG - 1, SL - 2)
            add(2 * NG - 1, SL - 1)
            at = lambda name: use(NG, 0, name)
            post(at("o"), 2 * NG - 1, 1, 1)
            for what in ("yT", "m0", "m1", "f"):
                forward(at, NG - 1, what)

        @block.scalar
        def _(act):
            act.wait_ge(s_w.sem, 16 * NW)
            act.activation(A[:], A[:], ACT.Exp).then_inc(s_act, 1)
            act.activation(cb[:], cb[:], ACT.Copy, scale=0.5).then_inc(s_act, 1)
            act.activation(wo[:], wo[:], ACT.Copy, scale=0.5).then_inc(s_act, 1)
            act.activation(nw[:, 1:2], nw[:, 1:2], ACT.Copy, scale=2.0).then_inc(s_act, 1)
            act.wait_ge(s_act, 4)
            act.sem_inc(s_A.sem, 1)
            act.wait_ge(s_A.sem, s_A.at(2))

            def flat(t):
                return t.rearrange("p c t -> p (c t)")

            def prep(at, n, d, what):
                def src(name):
                    k, m = at(name)
                    act.wait_ge(s_pb[k].sem, s_pb[k].at(m + 1))
                    return banks[k], s_pf[k].sem
                if what == "xT":
                    o, free = src("xT")
                    act.activation(xTp[:, :, PADS:], o.rearrange("p (b t) -> p b t", b=GB), ACT.Copy).then_inc(free, 1)
                if what in ("c0", "c1"):
                    c = int(what[1])
                    o, free = src(what)
                    act.wait_ge(s_dr.sem, s_dr.at(n))
                    act.activation(cc[:, c, :], o, ACT.Identity, scale=0.5, bias=cb[:, d, c:c + 1]).then_inc(s_cc.sem, 1)
                    act.activation(tu[:, c, :], o, ACT.Tanh, scale=0.5, bias=cb[:, d, c:c + 1]).then_inc(free, 1)
                if what in ("z0", "z1"):
                    c = int(what[1])
                    o, free = src(what)
                    act.activation(tz[:, c, :], o, ACT.Tanh, scale=0.5).then_inc(s_tz.sem, 1)
                if what == "xd":
                    o, free = src("xd")
                    act.wait_ge(s_Bd.sem, s_Bd.at(n))
                    act.wait_ge(s_Cs.sem, s_Cs.at(n))
                    act.activation(xd[:], o[0:XM, :], ACT.Copy).then_inc(free, 1)
                    act.wait_ge(s_pf[7].sem, s_pf[7].at(at("xd")[1] + 1))
                    act.sem_inc(s_xd.sem, 1)
                if what == "move":
                    act.wait_ge(s_C.sem, s_C.at(n - 1))
                    act.wait_ge(s_hi.sem, s_hi.at(n + 1))
                    act.activation(Cs[0:NS, d, :], ch_hi[CROW:, :], ACT.Copy).then_inc(s_Csh.sem, 1)
                    act.wait_ge(s_mid.sem, s_mid.at(n + 1))
                    act.activation(Cs[32:32 + NS, d, :], ch_mid[CROW:, :], ACT.Copy).then_inc(s_Csh.sem, 1)
                if what in ("dt0", "dt1"):
                    c = int(what[2])
                    o, free = src(what)
                    act.wait_ge(s_sz.sem, s_sz.at(n + 1))
                    act.wait_ge(s_u.sem, s_u.at(n + 1))
                    act.activation(cc[:, c, :], o, ACT.Abs, bias=bdt[:, d, c:c + 1]).then_inc(s_ab.sem, 1)
                    act.activation(tz[:, c, :], o, ACT.Relu, bias=bdt[:, d, c:c + 1]).then_inc(s_ab.sem, 1)
                    act.wait_ge(s_ab.sem, s_ab.at(n, 2 * c + 2))
                    act.sem_inc(free, 1)
                if what == "exp":
                    act.wait_ge(s_ab.sem, s_ab.at(n + 1))
                    act.activation(flat(cc[:]), flat(cc[:]), ACT.Exp, scale=-1.0).then_inc(s_z.sem, 1)
                if what == "log":
                    act.wait_ge(s_w1.sem, s_w1.at(n + 1))
                    act.activation(flat(ln[:]), flat(tu[:]), ACT.Ln).then_inc(s_ln.sem, 1)

            def forward(at, g, what):
                k, m = at(what)
                act.wait_ge(s_pb[k].sem, s_pb[k].at(m + 1))
                if what == "yT":
                    act.activation(yT[:], banks[k], ACT.Identity, scale=nw[:, 0:1], bias=nw[:, 1:2]).then_inc(s_pf[k].sem, 1)
                    act.wait_ge(s_pf[k].sem, s_pf[k].at(m + 1))
                    act.sem_inc(s_yT.sem, 1)
                else:
                    c = int(what[1])
                    act.activation(md[:, c, :], banks[k], ACT.Relu, bias=b1[:, c:c + 1]).then_inc(s_pf[k].sem, 1)
                    act.wait_ge(s_pf[k].sem, s_pf[k].at(m + 1))
                    act.sem_inc(s_md.sem, 1)

            def decay(n, d, k):
                s, c = k // NC, k % NC
                if k == 0:
                    act.wait_ge(s_dt.sem, s_dt.at(n + 1))
                act.wait_ge(s_h.sem, s_h.at(n, k - 1))
                act.activation(banks[k % 2], dt[:, d, c, :], ACT.Exp, scale=A[:, d, c, s:s + 1]).then_inc(s_dA.sem, 1)

            def unit(g, l, d, first, last):
                n = 2 * g + d
                begins, ends = not (first and l == 0 and d == 0), not (last and l == 1 and d == 1)
                at = lambda name: use(g, d, name)
                for k in range(SL):
                    decay(n, d, k)
                    if ends:
                        for slot, what in ((3, "xT"), (5, "c0"), (7, "c1"), (9, "z0"), (10, "z1"), (12, "xd"), (14, "move"),
                                           (15, "dt0"), (16, "dt1"), (17, "exp"), (19, "log")):
                            if k == slot:
                                prep(at, n + 1, 1 - d, what)
                    if d == 0 and begins:
                        for slot, what in ((21, "yT"), (23, "m0"), (23, "m1")):
                            if k == slot:
                                forward(at, g - 1, what)

            def turn(i, first=False, last=False):
                for l in range(2):
                    for d in range(2):
                        unit(2 * i + l, l, d, first, last)
            for what in ("xT", "c0", "c1", "z0", "z1", "xd", "move", "dt0", "dt1", "exp", "log"):
                prep(use_first, 0, 0, what)
            schedule(turn)(act)
            at = lambda name: use(NG, 0, name)
            for what in ("yT", "m0", "m1"):
                forward(at, NG - 1, what)

        @block.vector
        def _(dve):
            def prep(v, ch, at, n, d, what):
                if what == "u":
                    v.wait_ge(s_cc.sem, s_cc.at(n + 1))
                    v.wait_ge(s_pf[6].sem, s_pf[6].at(at("c1")[1] + 1))
                    v.wait_ge(s_pf[7].sem, s_pf[7].at(at("c0")[1] + 1))
                    v.wait_ge(s_yd.sem, s_yd.at(n - 1))
                    v.scalar_tensor_tensor(u[:, d], tu[:], 1.0, cc[:], ALU.add, ALU.mult).then_inc(s_u.sem, 1)
                if what in ("z0", "z1"):
                    c = int(what[1])
                    k, m = at(what)
                    v.wait_ge(s_tz.sem, s_tz.at(n, c + 1))
                    v.wait_ge(s_yz.sem, s_yz.at(n - 1))
                    v.scalar_tensor_tensor(sz[:, d, c, :], tz[:, c, :], 1.0, banks[k], ALU.add, ALU.mult).then_inc(ch.sem, 1)
                    v.wait_ge(ch.sem, ch.next())
                    v.sem_inc(s_pf[k].sem, 1)
                    v.sem_inc(s_sz.sem, 1)
                if what == "split":
                    v.wait_ge(s_xd.sem, s_xd.at(n + 1))
                    v.wait_ge(s_Csh.sem, s_Csh.at(n))
                    v.wait_ge(s_C.sem, s_C.at(n - 1))
                    c = slice(CROW, CROW + NS)
                    v.tensor_copy(ch_hi[c, :], xd[c, :]).then_inc(s_hi.sem, 1)
                    v.wait_ge(s_hi.sem, s_hi.at(n + 1))
                    v.tensor_tensor(ch_r[c, :], xd[c, :], ch_hi[c, :], ALU.subtract).then_inc(ch.sem, 1)
                    v.wait_ge(ch.sem, ch.next())
                    v.tensor_copy(ch_mid[c, :], ch_r[c, :]).then_inc(s_mid.sem, 1)
                    v.wait_ge(s_mid.sem, s_mid.at(n + 1))
                    v.tensor_tensor(Cs[c, d, :], ch_r[c, :], ch_mid[c, :], ALU.subtract).then_inc(s_Cs.sem, 1)
                if what == "e":
                    v.wait_ge(s_w1.sem, s_w1.at(n + 1))
                    v.scalar_tensor_tensor(cc[:], tu[:], 1.0, cc[:], ALU.subtract, ALU.subtract).then_inc(s_e.sem, 1)
                if what == "dtu":
                    v.wait_ge(s_dr.sem, s_dr.at(n + 1))
                    v.wait_ge(s_dB.sem, s_dB.at(n - 1))
                    v.tensor_tensor(dtu[:, d], dt[:, d], u[:, d], ALU.mult).then_inc(s_dtu.sem, 1)

            def post(v, ch, at, n, g, d, what):
                k, m = at("o")
                if what == "y":
                    v.wait_ge(s_yz.sem, s_yz.at(n))
                    for c in range(NC):
                        v.wait_ge(s_ya.sem, s_ya.at(n, SL - 1 + c))
                        v.scalar_tensor_tensor(yd[:, c, :], u[:, d, c, :], Dp[:, d, c:c + 1], banks[4 + c], ALU.mult, ALU.add).then_inc(s_yd.sem, 1)
                if what == "stats":
                    v.wait_ge(s_pb[k].sem, s_pb[k].at(m + 1))
                    v.wait_ge(s_nrm.sem, s_nrm.at(n))
                    stats(v, ch, 0, lambda b: banks[k][:, b * D:(b + 1) * D], n)
                if what == "norm":
                    v.wait_ge(s_pow[0].sem, s_pow[0].at(n + 1))
                    v.wait_ge(s_yT.sem, s_yT.at(g))
                    for b in range(GB):
                        ins = v.tensor_scalar(nrm[:, d, b, :], banks[k][:, b * D:(b + 1) * D], ost[:, 0, b, 6:7], ovar[:, 0, 1, b:b + 1],
                                              ALU.subtract, ALU.mult)
                    ins.then_inc(ch.sem, 1)
                    v.wait_ge(ch.sem, ch.next())
                    v.sem_inc(s_pf[k].sem, 1)
                    v.sem_inc(s_nrm.sem, 1)

            def stats(v, ch, j, src, n):
                for b in range(GB):
                    ins = v.bn_stats(ost[:, j, b, 0:6], src(b))
                ins.then_inc(ch.sem, 1)
                v.wait_ge(ch.sem, ch.next())
                v.sem_inc(s_step, 1)
                for b in range(GB):
                    ins = v.bn_aggr(ost[:, j, b, 6:8], ost[:, j, b, 0:6])
                ins.then_inc(ch.sem, 1)
                v.wait_ge(ch.sem, ch.next())
                v.wait_ge(s_pow[j].sem, s_pow[j].at(n))
                v.tensor_scalar(ovar[:, j, 0, :], ost[:, j, :, 7], EPS, None, ALU.add).then_inc(s_var[j].sem, 1)

            def forward(v, ch, at, g, l, what, turn):
                k, m = at("f")
                if what == "stats":
                    v.wait_ge(s_pb[k].sem, s_pb[k].at(m + 1))
                    v.wait_ge(s_ff.sem, s_ff.at(g))
                    stats(v, ch, 1, lambda b: banks[k][:, b * D:(b + 1) * D], g)
                if what == "norm":
                    v.wait_ge(s_pow[1].sem, s_pow[1].at(g + 1))
                    v.wait_ge(s_o.sem, s_o.at(g))
                    for b in range(GB):
                        ins = v.tensor_scalar(ff[:, b, :], banks[k][:, b * D:(b + 1) * D], ost[:, 1, b, 6:7], ovar[:, 1, 1, b:b + 1],
                                              ALU.subtract, ALU.mult)
                    ins.then_inc(ch.sem, 1)
                    v.wait_ge(ch.sem, ch.next())
                    v.sem_inc(s_pf[k].sem, 1)
                    v.sem_inc(s_ff.sem, 1)
                    v.tensor_tensor(ff[:], ff[:], fin[:, 0, :].unsqueeze(1).to_broadcast([P, GB, D]), ALU.mult).then_inc(ch.sem, 1)
                    v.wait_ge(ch.sem, ch.next())
                    v.tensor_tensor(ff[:], ff[:], fin[:, 1, :].unsqueeze(1).to_broadcast([P, GB, D]), ALU.add).then_inc(ch.sem, 1)
                    v.wait_ge(ch.sem, ch.next())
                    v.tensor_tensor(ff[:], ff[:], xg[:, l], ALU.add).then_inc(ch.sem, 1)
                    v.wait_ge(ch.sem, ch.next())
                    stats(v, ch, 2, lambda b: ff[:, b, :], g)
                if what == "out":
                    v.wait_ge(s_pow[2].sem, s_pow[2].at(g + 1))
                    v.wait_ge(s_store[l].sem, s_store[l].at(turn))
                    for b in range(GB):
                        ins = v.tensor_scalar(xo[:, l, b, :], ff[:, b, :], ost[:, 2, b, 6:7], ovar[:, 2, 1, b:b + 1], ALU.subtract, ALU.mult)
                    ins.then_inc(s_o.sem, 1)

            def scan(v, n, d, k):
                v.wait_ge(s_dA.sem, s_dA.at(n, k + 1))
                v.wait_ge(s_dB.sem, s_dB.at(n, k + 1))
                v.wait_ge(s_hC.sem, s_hC.at(n, k - 1))
                v.tensor_tensor_scan(h[:, k % 2, :], banks[k % 2], dBu[:, k % 2, :], 0.0, ALU.mult, ALU.add).then_inc(s_h.sem, 1)

            def times_C(v, n, k):
                s = k // NC
                v.wait_ge(s_h.sem, s_h.at(n, k + 1))
                v.wait_ge(s_C.sem, s_C.at(n, s + 1))
                v.wait_ge(s_ya.sem, s_ya.at(n, k - 1))
                v.tensor_tensor(hC[:, k % 2, :], h[:, k % 2, :], banks[2 + s % 2], ALU.mult).then_inc(s_hC.sem, 1)

            def prologue(v, ch):
                v.wait_ge(s_w.sem, 16 * NW)
                v.wait_ge(s_act, 4)
                v.tensor_scalar(A[:], A[:], A_MIN, -1.0, ALU.max, ALU.mult).then_inc(ch.sem, 1)
                v.wait_ge(ch.sem, ch.next())
                for d in range(2):
                    taps = convw[:, d * CK * DI:(d + 1) * CK * DI].rearrange("p (c k) -> p k c", k=CK)
                    for k in range(CK):
                        ins = v.tensor_tensor(wck[:, d, k, :], win[:, d, 0:DI], taps[:, k, :], ALU.mult)
                ins.then_inc(ch.sem, 1)
                v.wait_ge(ch.sem, ch.next())
                v.sem_inc(s_A.sem, 1)
                for what in ("u", "z0", "z1", "split", "e", "dtu"):
                    prep(v, ch, use_first, 0, 0, what)

            def unit(v, ch, i, g, l, d, first, last):
                n = 2 * g + d
                begins, ends = not (first and l == 0 and d == 0), not (last and l == 1 and d == 1)
                at = lambda name: use(g, d, name)
                for k in range(SL):
                    scan(v, n, d, k)
                    if k:
                        times_C(v, n, k - 1)
                    elif begins:
                        times_C(v, n - 1, SL - 1)
                    if begins:
                        for slot, what in ((2, "y"), (17, "stats"), (19, "norm")):
                            if k == slot:
                                post(v, ch, at, n - 1, g if d else g - 1, 1 - d, what)
                        if d == 0:
                            for slot, what in ((25, "stats"), (27, "norm"), (29, "out")):
                                if k == slot:
                                    forward(v, ch, at, g - 1, 1 - l, what, i if l else i - 1)
                    if ends:
                        for slot, what in ((8, "u"), (10, "z0"), (11, "z1"), (13, "split"), (20, "e"), (23, "dtu")):
                            if k == slot:
                                prep(v, ch, at, n + 1, 1 - d, what)

            def turn(v, ch, i):
                first, last = isinstance(i, int) and i == 0, isinstance(i, int) and i == TURNS - 1
                for l in range(2):
                    for d in range(2):
                        unit(v, ch, i, 2 * i + l, l, d, first, last)

            def tail(v, ch):
                times_C(v, 2 * NG - 1, SL - 1)
                at = lambda name: use(NG, 0, name)
                for what in ("y", "stats", "norm"):
                    post(v, ch, at, 2 * NG - 1, NG - 1, 1, what)
                for what in ("stats", "norm", "out"):
                    forward(v, ch, at, NG - 1, 1, what, TURNS - 1)
            of_unit, of_group = 3 + 3, 2 + 4 + 2
            looped(dve, s_dve, TURNS, 4 * of_unit + 2 * of_group, prologue, turn, tail)

        @block.gpsimd
        def _(pool):
            m = 0

            def then(ins):
                nonlocal m
                m += 1
                ins.then_inc(s_pool, 1)
                pool.wait_ge(s_pool, m)
            then(pool.memset(wx[:], 0.0))
            pool.sem_inc(s_set.sem, 1)
            then(pool.memset(flip[:], 0.0))
            then(pool.affine_select(out=flip[:], in_=flip[:], compare_op=ALU.not_equal, fill=1.0, base=-(P - 1),
                                    pattern=[[1, P]], channel_multiplier=1))
            then(pool.memset(selC[:], 0.0))
            for part in range(3):
                then(pool.affine_select(out=selC[:], in_=selC[:], compare_op=ALU.not_equal, fill=1.0, base=-32 * part,
                                        pattern=[[-1, NS], [0, P]], channel_multiplier=1))
            then(pool.memset(xTp[:, :, 0:PADS], 0.0))
            then(pool.memset(Cs[:], 0.0))
            pool.sem_inc(s_set.sem, 1)

            def prep(n, d, what):
                if what == "w":
                    pool.wait_ge(s_z.sem, s_z.at(n + 1))
                    pool.sem_inc(s_step, 1)
                    pool.tensor_scalar(tu[:], cc[:], 1.0, None, ALU.add).then_inc(s_w1.sem, 1)
                if what == "dt":
                    pool.wait_ge(s_ln.sem, s_ln.at(n + 1))
                    pool.wait_ge(s_e.sem, s_e.at(n + 1))
                    pool.wait_ge(s_dA.sem, s_dA.at(n - 1))
                    pool.tensor_tensor(ln[:], ln[:], cc[:], ALU.subtract).then_inc(s_d1.sem, 1)
                    pool.wait_ge(s_d1.sem, s_d1.at(n + 1))
                    pool.tensor_tensor(dt[:, d], ln[:], tz[:], ALU.add).then_inc(s_dr.sem, 1)
                if what == "far":
                    pool.wait_ge(s_dtu.sem, s_dtu.at(n + 1))
                    pool.sem_inc(s_step, 1)
                    pool.memset(dt[:, d].rearrange("p c (b t) -> p (c b) t", t=S)[:, :, 0:1], FAR).then_inc(s_dt.sem, 1)

            def gated(n, d):
                pool.wait_ge(s_yd.sem, s_yd.at(n + 1))
                pool.tensor_tensor(yd[:], yd[:], sz[:, d], ALU.mult).then_inc(s_yz.sem, 1)

            def power(j, n):
                pool.wait_ge(s_var[j].sem, s_var[j].at(n + 1))
                pool.tensor_tensor(ovar[:, j, 1, :], ovar[:, j, 0, :], half_pow[:, 0:GB], ALU.pow).then_inc(s_pow[j].sem, 1)

            def inputs(n, g, d, k):
                s, c = k // NC, k % NC
                if k == 0:
                    pool.wait_ge(s_Bb[d].sem, s_Bb[d].at(g + 1))
                    pool.sem_inc(s_step, 1)
                pool.wait_ge(s_h.sem, s_h.at(n, k - 1))
                pool.tensor_tensor(dBu[:, k % 2, :], dtu[:, d, c, :], Bb[:, d, s, :], ALU.mult).then_inc(s_dB.sem, 1)

            def unit(g, l, d, first, last):
                n = 2 * g + d
                begins, ends = not (first and l == 0 and d == 0), not (last and l == 1 and d == 1)
                for k in range(SL):
                    inputs(n, g, d, k)
                    if begins:
                        if k == 4:
                            gated(n - 1, 1 - d)
                        if k == 18:
                            power(0, n - 1)
                        if d == 0 and k == 26:
                            power(1, g - 1)
                        if d == 0 and k == 28:
                            power(2, g - 1)
                    if ends:
                        for slot, what in ((18, "w"), (21, "dt"), (24, "far")):
                            if k == slot:
                                prep(n + 1, 1 - d, what)

            def turn(i, first=False, last=False):
                for l in range(2):
                    for d in range(2):
                        unit(2 * i + l, l, d, first, last)
            for what in ("w", "dt", "far"):
                prep(0, 0, what)
            schedule(turn)(pool)
            gated(2 * NG - 1, 1)
            power(0, 2 * NG - 1)
            power(1, NG - 1)
            power(2, NG - 1)

def quantized(nc, const, banks, x, y, a):
    I = 352
    IC = 3
    IL = I - 2 * P
    QMAX = 127.0
    MAGIC = float(1.5 * 2 ** 23)
    TURNS = NG // 2
    LC = 4
    ident, identb, ones_row, half_pow = const["ident"], const["identb"], const["ones_row"], const["half_pow"]
    with ExitStack() as st:
        def sb(name, shape, dt=F32):
            return st.enter_context(nc.sbuf_tensor(f"q_{name}", shape, dt))

        def sem(name, per=1):
            return Count(nc.alloc_semaphore(f"q_{name}"), per)

        xs = sb("x", [P, B, D])
        wgu = sb("wgu", [P, 2 * IC, D])
        wd = sb("wd", [P, I])
        clip = sb("clip", [P, 2])
        wamax = sb("wamax", [P, 2 * IC + 1])
        wscale = sb("wscale", [P, 2 * IC + 1])
        winv = sb("winv", [P, 2 * IC + 1])
        wq = sb("wq", [P, 2 * IC, D], BF16)
        wdq = sb("wdq", [P, I], BF16)
        wT = sb("wT", [P, 2 * IC, P], BF16)
        wdT = sb("wdT", [P, IC, D], BF16)
        sig = sb("sig", [P, 2])
        xmax = sb("xmax", [P, LC])
        hmax = sb("hmax", [P, NG])
        top = sb("top", [P, 2])
        top1 = sb("top1", [1, 2])
        scl = sb("scl", [P, 2])
        inv = sb("inv", [P, 2])
        kt = sb("kt", [P, IC])
        kk = sb("kk", [P, IC])
        magic = sb("magic", [P, 1])
        drow = sb("drow", [1, D])
        dsc = sb("dsc", [P, D])
        xt = sb("xt", [P, GT])
        xqb = sb("xqb", [P, GT], BF16)
        xT = sb("xT", [P, 2, GT], BF16)
        th = sb("th", [P, IC, GT])
        t1 = sb("t1", [P, GT])
        h = sb("h", [P, IC, B * S])
        ht = sb("ht", [P, 2, IC, GT])
        hq = sb("hq", [P, 2, IC, GT], BF16)
        r = sb("r", [P, 2, GB, D])
        ost = sb("ost", [P, GB, 8])
        ovar = sb("ovar", [P, 2, GB])

        s_ld = [sem(f"x_loaded{c}") for c in range(LC)]
        s_w = sem("weights"); s_setup = sem("setup"); s_sig = sem("sigmoid_exp"); s_wq = sem("weights_quantized")
        s_wt = sem("weights_turned", 2); s_wT = sem("weights_copied", 2); s_top = sem("top", 3); s_tt = sem("top_turned", 3)
        s_t1 = sem("top_reduced", 3); s_tb = sem("top_spread", 3); s_k = sem("scales_ready")
        s_xq = sem("x_quantized"); s_xt = sem("x_turned"); s_xT = sem("x_copied")
        s_gu = sem("gate_up", IC); s_th = sem("tanh", IC); s_h = sem("h", IC)
        s_hs = sem("h_shifted"); s_hq = sem("h_quantized"); s_y = sem("down"); s_yr = sem("down_read"); s_ov = sem("out_var"); s_op = sem("out_pow")
        s_o = sem("out_ready"); s_store = [sem(f"stored{l}", 16) for l in range(2)]
        s_dve = nc.alloc_semaphore("q_dve_done"); s_dve2 = nc.alloc_semaphore("q_dve_done2")
        s_pool = nc.alloc_semaphore("q_pool_setup"); s_step = nc.alloc_semaphore("q_passed")
        bankA = banks[0]
        bankAb = bankA.bitcast(BF16)
        bankD = banks[1]
        NW = 7
        x_p = x.rearrange("b t d -> t b d")
        o_g = y.rearrange("(g b) t d -> g t b d", b=GB)
        block = st.enter_context(nc.Block())

        @block.sync
        def _(sp):
            def load_w(dst, src):
                sp.dma_start(dst, src).then_inc(s_w.sem, 16)
            for n, w in enumerate((a["L1_ffn_w_gate"], a["L1_ffn_w_up"])):
                load_w(wgu[:, n * IC:n * IC + 2, :], w[0:2 * P, :].rearrange("(c p) d -> p c d", p=P))
                load_w(wgu[0:IL, n * IC + 2, :], w[2 * P:I, :])
            load_w(wd[:], a["L1_ffn_w_down"])
            for n, t in enumerate((a["L1_ffn_clip_x"], a["L1_ffn_clip_down"])):
                load_w(clip[:, n:n + 1], t.rearrange("(a d) -> a d", a=1).to_broadcast([P, 1]))
            for c in range(LC):
                sp.dma_start(xs[:, c * B // LC:(c + 1) * B // LC, :], x_p[:, c * B // LC:(c + 1) * B // LC, :]).then_inc(s_ld[c].sem, 16)

            def turn(i):
                for l in range(2):
                    g = 2 * i + l
                    sp.wait_ge(s_o.sem, s_o.at(g + 1))
                    sp.sem_inc(s_step, 1)
                    sp.dma_start(o_g[g], r[:, l]).then_inc(s_store[l].sem, 16)
            with sp.Fori(0, TURNS) as i:
                turn(i)
            for l in range(2):
                sp.wait_ge(s_store[l].sem, TURNS * 16)

        @block.tensor
        def _(pe):
            def spread(n):
                pe.wait_ge(s_top.sem, s_top.at(0, n + 1))
                pe.transpose(bankD[0:1, 0:P], top[:, n:n + 1] if n < 2 else wscale[:, 2 * IC:2 * IC + 1], ident[:]).then_inc(s_tt.sem, 1)
                pe.wait_ge(s_t1.sem, s_t1.at(0, n + 1))
                pe.matmul(bankD[:, P:P + (1 if n < 2 else D)], ones_row[:], top1[:, n:n + 1] if n < 2 else drow[:],
                          start=True, stop=True).then_inc(s_tb.sem, 1)

            pe.wait_ge(s_wq.sem, s_wq.at(1))
            for c in range(2 * IC):
                ins = pe.transpose(bankAb[:, c * P:(c + 1) * P], wq[:, c, :], identb[:])
            ins.then_inc(s_wt.sem, 1)
            pe.wait_ge(s_wT.sem, s_wT.at(0, 1))
            for c in range(IC):
                n = P if c < 2 else IL
                ins = pe.transpose(bankAb[0:n, c * P:(c + 1) * P], wdq[:, c * P:c * P + n], identb[:])
            ins.then_inc(s_wt.sem, 1)
            pe.wait_ge(s_wT.sem, s_wT.at(0, 2))
            spread(0)

            def turned(g):
                pe.wait_ge(s_xq.sem, s_xq.at(g + 1))
                pe.wait_ge(s_xT.sem, s_xT.at(g))
                pe.sem_inc(s_step, 1)
                for b in range(GB):
                    ins = pe.transpose(bankAb[:, b * S:(b + 1) * S], xqb[:, b * S:(b + 1) * S], identb[:])
                ins.then_inc(s_xt.sem, 1)

            def gate_up(g, par):
                pe.wait_ge(s_xT.sem, s_xT.at(g + 1))
                for c in range(IC):
                    pe.wait_ge(s_h.sem, s_h.at(g - 1, c + 1))
                    pe.matmul(banks[2 + 2 * c], wT[:, c, :], xT[:, par, :], start=True, stop=True)
                    pe.matmul(banks[3 + 2 * c], wT[:, IC + c, :], xT[:, par, :], start=True, stop=True).then_inc(s_gu.sem, 1)

            def turn(i, last=False):
                for l in range(2):
                    g = 2 * i + l
                    gate_up(g, l)
                    if not (last and l):
                        turned(g + 1)
            turned(0)
            turn(0)
            with pe.Fori(1, TURNS - 1) as i:
                turn(i)
            turn(TURNS - 1, last=True)
            spread(1)
            spread(2)

            def down(g, par):
                pe.wait_ge(s_hq.sem, s_hq.at(g + 1))
                pe.wait_ge(s_yr.sem, s_yr.at(g - 1))
                pe.sem_inc(s_step, 1)
                for b in range(GB):
                    for c in range(IC):
                        n = P if c < 2 else IL
                        ins = pe.matmul(banks[2 + par][:, b * D:(b + 1) * D], hq[0:n, par, c, b * S:(b + 1) * S], wdT[0:n, c, :],
                                        start=(c == 0), stop=(c == IC - 1))
                ins.then_inc(s_y.sem, 1)
            down(0, 0)
            down(1, 1)
            with pe.Fori(1, TURNS) as i:
                for l in range(2):
                    down(2 * i + l, l)

        @block.scalar
        def _(act):
            act.wait_ge(s_w.sem, 16 * NW)
            act.activation(sig[:], clip[:], ACT.Exp, scale=-1.0).then_inc(s_sig.sem, 1)
            act.wait_ge(s_wt.sem, s_wt.at(0, 1))
            act.activation(wT[:].rearrange("p c d -> p (c d)"), bankAb[:, 0:2 * IC * P], ACT.Copy).then_inc(s_wT.sem, 1)
            act.wait_ge(s_wt.sem, s_wt.at(0, 2))
            act.activation(wdT[:, 0:2, :].rearrange("p c d -> p (c d)"), bankAb[:, 0:2 * D], ACT.Copy)
            act.activation(wdT[0:IL, 2, :], bankAb[0:IL, 2 * D:3 * D], ACT.Copy).then_inc(s_wT.sem, 1)
            act.wait_ge(s_k.sem, s_k.at(1))

            def copied(g, par):
                act.wait_ge(s_xt.sem, s_xt.at(g + 1))
                act.wait_ge(s_gu.sem, s_gu.at(g - 1))
                act.activation(xT[:, par, :], bankAb[:, 0:GT], ACT.Copy).then_inc(s_xT.sem, 1)

            def tanh(g):
                for c in range(IC):
                    act.wait_ge(s_gu.sem, s_gu.at(g, c + 1))
                    act.wait_ge(s_h.sem, s_h.at(g - 1, c + 1))
                    act.activation(th[:, c, :], banks[2 + 2 * c], ACT.Tanh, scale=kt[:, c:c + 1]).then_inc(s_th.sem, 1)

            def turn(i, last=False):
                for l in range(2):
                    g = 2 * i + l
                    tanh(g)
                    if not (last and l):
                        copied(g + 1, 1 - l)
            copied(0, 0)
            turn(0)
            with act.Fori(1, TURNS - 1) as i:
                turn(i)
            turn(TURNS - 1, last=True)

            def whole(g, par):
                act.wait_ge(s_hs.sem, s_hs.at(g + 1))
                act.wait_ge(s_y.sem, s_y.at(g - 1))
                act.activation(hq[:, par].rearrange("p c t -> p (c t)"), ht[:, par].rearrange("p c t -> p (c t)"),
                               ACT.Identity, bias=magic[:]).then_inc(s_hq.sem, 1)
            whole(0, 0)
            whole(1, 1)
            with act.Fori(1, TURNS) as i:
                for l in range(2):
                    whole(2 * i + l, l)

        @block.vector
        def _(dve):
            xg = xs[:].rearrange("p (g b) d -> p g (b d)", b=GB)
            hg = h[:].rearrange("p c (g t) -> p g c t", t=GT)

            def whole(v, ch, dst, tmp, src, by):
                v.tensor_scalar(tmp, src, by, QMAX, ALU.mult, ALU.min).then_inc(ch.sem, 1)
                v.wait_ge(ch.sem, ch.next())
                v.tensor_scalar(tmp, tmp, -QMAX - 1.0, MAGIC, ALU.max, ALU.add).then_inc(ch.sem, 1)
                v.wait_ge(ch.sem, ch.next())
                return v.tensor_scalar(dst, tmp, MAGIC, None, ALU.subtract)

            def scale_of(v, ch, n, maxima):
                v.tensor_reduce(top[:, n:n + 1], maxima, AX.X, ALU.max).then_inc(s_top.sem, 1)
                v.wait_ge(s_tt.sem, s_tt.at(0, n + 1))
                v.tensor_reduce(top1[:, n:n + 1], bankD[0:1, 0:P], AX.X, ALU.max).then_inc(s_t1.sem, 1)
                v.wait_ge(s_tb.sem, s_tb.at(0, n + 1))
                v.tensor_scalar(scl[:, n:n + 1], bankD[:, P:P + 1], sig[:, n:n + 1], 1.0 / QMAX, ALU.mult, ALU.mult).then_inc(ch.sem, 1)
                v.wait_ge(ch.sem, ch.next())
                v.reciprocal(inv[:, n:n + 1], scl[:, n:n + 1]).then_inc(ch.sem, 1)
                v.wait_ge(ch.sem, ch.next())

            def quantize_x(v, ch, g):
                v.wait_ge(s_xq.sem, s_xq.at(g))
                v.tensor_scalar(xt[:], xg[:, g, :], inv[:, 0:1], QMAX, ALU.mult, ALU.min).then_inc(ch.sem, 1)
                v.wait_ge(ch.sem, ch.next())
                v.tensor_scalar(xt[:], xt[:], -QMAX - 1.0, MAGIC, ALU.max, ALU.add).then_inc(ch.sem, 1)
                v.wait_ge(ch.sem, ch.next())
                v.wait_ge(s_xt.sem, s_xt.at(g))
                v.tensor_scalar(xqb[:], xt[:], MAGIC, None, ALU.subtract).then_inc(s_xq.sem, 1)

            def prologue(v, ch):
                v.wait_ge(s_w.sem, 16 * NW)
                v.wait_ge(s_setup.sem, s_setup.at(1))
                v.tensor_reduce(wamax[:, 0:2 * IC], wgu[:], AX.X, ALU.max, apply_absolute_value=True)
                v.tensor_reduce(wamax[:, 2 * IC:], wd[:], AX.X, ALU.max, apply_absolute_value=True).then_inc(ch.sem, 1)
                v.wait_ge(ch.sem, ch.next())
                v.tensor_scalar(wscale[:], wamax[:], 1.0 / QMAX, None, ALU.mult).then_inc(ch.sem, 1)
                v.wait_ge(ch.sem, ch.next())
                v.reciprocal(winv[:], wscale[:]).then_inc(ch.sem, 1)
                v.wait_ge(ch.sem, ch.next())
                for c in range(2 * IC):
                    whole(v, ch, wq[:, c, :], wgu[:, c, :], wgu[:, c, :], winv[:, c:c + 1]).then_inc(ch.sem, 1)
                    v.wait_ge(ch.sem, ch.next())
                whole(v, ch, wdq[:], wd[:], wd[:], winv[:, 2 * IC:]).then_inc(ch.sem, 1)
                v.wait_ge(ch.sem, ch.next())
                for n in range(2):
                    ins = v.memset(wq[IL:P, n * IC + 2, :], 0.0)
                ins.then_inc(s_wq.sem, 1)
                v.wait_ge(s_sig.sem, s_sig.at(1))
                v.tensor_scalar(sig[:], sig[:], 1.0, None, ALU.add).then_inc(ch.sem, 1)
                v.wait_ge(ch.sem, ch.next())
                v.reciprocal(sig[:], sig[:]).then_inc(ch.sem, 1)
                v.wait_ge(ch.sem, ch.next())
                for c in range(LC):
                    v.wait_ge(s_ld[c].sem, s_ld[c].at(16))
                    ins = v.tensor_reduce(xmax[:, c:c + 1], xs[:, c * B // LC:(c + 1) * B // LC, :].rearrange("p b d -> p (b d)"),
                                          AX.X, ALU.max, apply_absolute_value=True)
                ins.then_inc(ch.sem, 1)
                v.wait_ge(ch.sem, ch.next())
                scale_of(v, ch, 0, xmax[:])
                v.tensor_scalar(kt[:], wscale[:, 0:IC], scl[:, 0:1], 0.5, ALU.mult, ALU.mult).then_inc(ch.sem, 1)
                v.wait_ge(ch.sem, ch.next())
                v.tensor_scalar(kk[:], wscale[:, IC:2 * IC], scl[:, 0:1], None, ALU.mult).then_inc(ch.sem, 1)
                v.wait_ge(ch.sem, ch.next())
                v.tensor_tensor(kk[:], kk[:], kt[:], ALU.mult).then_inc(s_k.sem, 1)
                v.wait_ge(s_k.sem, s_k.at(1))
                quantize_x(v, ch, 0)

            def turn(v, ch, i):
                last = isinstance(i, int) and i == TURNS - 1
                for l in range(2):
                    g = 2 * i + l
                    if not (last and l):
                        quantize_x(v, ch, g + 1)
                    for c in range(IC):
                        v.wait_ge(s_th.sem, s_th.at(g, c + 1))
                        v.wait_ge(s_h.sem, s_h.at(g, c))
                        v.scalar_tensor_tensor(t1[:], th[:, c, :], 1.0, banks[2 + 2 * c], ALU.add, ALU.mult).then_inc(ch.sem, 1)
                        v.wait_ge(ch.sem, ch.next())
                        v.scalar_tensor_tensor(hg[:, g, c, :], t1[:], kk[:, c:c + 1], banks[3 + 2 * c], ALU.mult, ALU.mult).then_inc(s_h.sem, 1)
                    v.wait_ge(s_h.sem, s_h.at(g + 1))
                    v.tensor_reduce(hmax[:, bass.ds(g, 1)] if not isinstance(g, int) else hmax[:, g:g + 1],
                                    hg[:, g, :, :], AX.XY, ALU.max, apply_absolute_value=True).then_inc(ch.sem, 1)
                    v.wait_ge(ch.sem, ch.next())
            looped(dve, s_dve, TURNS, 2 * (2 + IC + 1), prologue, turn, lambda v, ch: None)

            def prologue2(v, ch):
                scale_of(v, ch, 1, hmax[:])
                v.tensor_copy(dsc[:, 0:1], scl[:, 1:2]).then_inc(s_top.sem, 1)
                v.wait_ge(s_tt.sem, s_tt.at(0, 3))
                v.tensor_copy(drow[:], bankD[0:1, 0:P]).then_inc(s_t1.sem, 1)
                v.wait_ge(s_tb.sem, s_tb.at(0, 3))
                v.tensor_scalar(dsc[:], bankD[:, P:2 * P], scl[:, 1:2], None, ALU.mult).then_inc(ch.sem, 1)
                v.wait_ge(ch.sem, ch.next())
                shift(v, ch, 0, 0)

            def shift(v, ch, g, par):
                v.wait_ge(s_hq.sem, s_hq.at(g - 1))
                v.tensor_scalar(ht[:, par], hg[:, g, :, :], inv[:, 1:2], QMAX, ALU.mult, ALU.min).then_inc(ch.sem, 1)
                v.wait_ge(ch.sem, ch.next())
                v.tensor_scalar(ht[:, par], ht[:, par], -QMAX - 1.0, MAGIC, ALU.max, ALU.add).then_inc(s_hs.sem, 1)

            def turn2(v, ch, i):
                last = isinstance(i, int) and i == TURNS - 1
                for l in range(2):
                    g = 2 * i + l
                    if not (last and l):
                        shift(v, ch, g + 1, 1 - l)
                    v.wait_ge(s_y.sem, s_y.at(g + 1))
                    v.wait_ge(s_store[l].sem, s_store[l].at(i))
                    v.tensor_tensor(r[:, l], banks[2 + l].rearrange("p (b d) -> p b d", b=GB),
                                    dsc[:].unsqueeze(1).to_broadcast([P, GB, D]), ALU.mult).then_inc(s_yr.sem, 1)
                    v.wait_ge(s_yr.sem, s_yr.at(g + 1))
                    v.tensor_tensor(r[:, l].rearrange("p b d -> p (b d)"), r[:, l].rearrange("p b d -> p (b d)"), xg[:, g, :], ALU.add).then_inc(ch.sem, 1)
                    v.wait_ge(ch.sem, ch.next())
                    v.wait_ge(s_o.sem, s_o.at(g))
                    for b in range(GB):
                        ins = v.bn_stats(ost[:, b, 0:6], r[:, l, b, :])
                    ins.then_inc(ch.sem, 1)
                    v.wait_ge(ch.sem, ch.next())
                    v.sem_inc(s_step, 1)
                    for b in range(GB):
                        ins = v.bn_aggr(ost[:, b, 6:8], ost[:, b, 0:6])
                    ins.then_inc(ch.sem, 1)
                    v.wait_ge(ch.sem, ch.next())
                    v.wait_ge(s_op.sem, s_op.at(g))
                    v.tensor_scalar(ovar[:, 0, :], ost[:, :, 7], EPS, None, ALU.add).then_inc(s_ov.sem, 1)
                    v.wait_ge(s_op.sem, s_op.at(g + 1))
                    for b in range(GB):
                        ins = v.tensor_scalar(r[:, l, b, :], r[:, l, b, :], ost[:, b, 6:7], ovar[:, 1, b:b + 1], ALU.subtract, ALU.mult)
                    ins.then_inc(s_o.sem, 1)
            looped(dve, s_dve2, TURNS, 2 * (1 + 3), prologue2, turn2, lambda v, ch: None)

        @block.gpsimd
        def _(pool):
            for n in range(2):
                pool.memset(wgu[IL:P, n * IC + 2, :], 1.0).then_inc(s_pool, 1)
                pool.wait_ge(s_pool, n + 1)
            pool.memset(magic[:], -MAGIC).then_inc(s_pool, 1)
            pool.wait_ge(s_pool, 3)
            pool.sem_inc(s_setup.sem, 1)
            with pool.Fori(0, NG) as g:
                pool.wait_ge(s_ov.sem, s_ov.at(g + 1))
                pool.tensor_tensor(ovar[:, 1, :], ovar[:, 0, :], half_pow[:, 0:GB], ALU.pow).then_inc(s_op.sem, 1)

def constants(nc, st, banks):
    ident = st.enter_context(nc.sbuf_tensor("ident", [P, P], F32))
    identb = st.enter_context(nc.sbuf_tensor("identb", [P, P], BF16))
    ones_row = st.enter_context(nc.sbuf_tensor("ones_row", [1, P], F32))
    sel = st.enter_context(nc.sbuf_tensor("sel", [3 * H, H, P], BF16))
    half_pow = st.enter_context(nc.sbuf_tensor("half_pow", [P, 4 * GB], F32))
    s = nc.alloc_semaphore("constants")
    with nc.Block() as block:
        @block.gpsimd
        def _(pool):
            pool.memset(ident[:], 0.0).then_inc(s, 1)
            pool.memset(identb[:], 0.0).then_inc(s, 1)
            pool.memset(sel[:], 0.0).then_inc(s, 1)
            pool.memset(ones_row[:], 1.0).then_inc(s, 1)
            pool.memset(half_pow[:], -0.5).then_inc(s, 1)
            pool.wait_ge(s, 5)
            pool.affine_select(out=ident[:], in_=ident[:], compare_op=ALU.not_equal, fill=1.0, base=0,
                               pattern=[[-1, P]], channel_multiplier=1).then_inc(s, 1)
            pool.affine_select(out=identb[:], in_=identb[:], compare_op=ALU.not_equal, fill=1.0, base=0,
                               pattern=[[-1, P]], channel_multiplier=1).then_inc(s, 1)
            for part in range(3):
                pool.affine_select(out=sel[:], in_=sel[:], compare_op=ALU.not_equal, fill=1.0, base=-part * H,
                                   pattern=[[-1, H], [0, P]], channel_multiplier=1).then_inc(s, 1)
                pool.wait_ge(s, 8 + part)
    return {"ident": ident, "identb": identb, "ones_row": ones_row, "sel": sel, "half_pow": half_pow}


def build(nc, a, out, stages="MXFNYQ"):
    root8 = float(1.0 / np.sqrt(8.0))

    def of(pre, *names):
        return [a[pre + n] for n in names]

    def mamba_stage(x, y):
        mamba(nc, const, banks, x, y, a)

    def cross0(x, y):
        attention(nc, const, banks, "x0", x, y, *of("L0_xattn_", "wq_k", "wk_k", "wv_k", "wo_k"), root8,
                  *of("L0_xattn_", "wq_b", "wk_b", "wv_b", "wo_b"), ctx=a["ctx_1024"], mask=a["mask_BxSxS2_ik1"],
                  gate=a["fside_BxSxS2_0"])

    def front_attention(x, y):
        attention(nc, const, banks, "f0", x, y, *of("L0_ffn_", "wq", "wk", "wv", "wo"), root8,
                  *of("L0_ffn_", "bq", "bk", "bv", "bo"), ln=of("L0_ffn_", "ln1_g", "ln1_b"), normed=False)

    def attention1(x, y):
        attention(nc, const, banks, "a1", x, y, *of("L1_attn_", "Wq", "Wk", "Wv", "Wo"), DH ** -0.5,
                  rms=of("L1_attn_", "qn_w", "kn_w"))

    def cross1(x, y):
        attention(nc, const, banks, "x1", x, y, *of("L1_xattn_", "wq_w", "wk_w", "wv_w", "wo_w"), root8,
                  *of("L1_xattn_", "wq_b", "wk_b", "wv_b", "wo_b"), ctx=a["ctx_1024"])

    def quantized_stage(x, y):
        quantized(nc, const, banks, x, y, a)

    run = {"M": mamba_stage, "X": cross0, "N": attention1, "Y": cross1, "Q": quantized_stage}
    with ExitStack() as st:
        banks = [st.enter_context(nc.psum_tensor(f"bank{n}", [P, 512], F32))[:] for n in range(8)]
        const = constants(nc, st, banks)
        x = a["x"]
        for n, stage in enumerate(stages):
            y = out if n == len(stages) - 1 else nc.dram_tensor(f"x_stage{n}", (B, S, D), F32, kind="Internal").ap()
            if stage == "F":
                x1 = nc.dram_tensor("x_ffn", (B, S, D), F32, kind="Internal").ap()
                with nc.cleanup_on_exit():
                    front_attention(x, x1)
                with nc.cleanup_on_exit():
                    experts(nc, const, banks, x, x1, y, a)
            else:
                with nc.cleanup_on_exit():
                    run[stage](x, y)
            x = y


TRANSPOSED = ("L1_attn_Wq", "L1_attn_Wk", "L1_attn_Wv", "L1_attn_Wo")
CHANNELS = ("L0_attn_fw_convb", "L0_attn_bw_convb", "L0_attn_fw_bdt", "L0_attn_bw_bdt", "L0_attn_fw_D",
            "L0_attn_bw_D", "L0_attn_ff_b1")
TILED = ("L1_attn_qn_w", "L1_attn_kn_w")


def kernel(**inputs):
    import concourse.bacc as bacc
    from concourse.bass_utils import run_bass_kernel_spmd

    nc = bacc.Bacc("TRN2", target_bir_lowering=False, num_devices=1)
    arrays, a = {}, {}
    for name, value in inputs.items():
        v = np.asarray(value)
        if name in TRANSPOSED:
            v = v.T
        if name in TILED:
            v = np.tile(v, H).reshape(P, 1)
        if name == "L0_ffn_b1":
            v = v.reshape(8, 4, P).transpose(2, 0, 1)
        if name in CHANNELS:
            v = v.reshape(2, P).T
        if name == "L0_ffn_b2":
            v = v.T
        v = np.ascontiguousarray(v)
        arrays["in_" + name] = v
        a[name] = nc.dram_tensor("in_" + name, v.shape, mybir.dt.from_np(v.dtype), kind="ExternalInput").ap()
    out = nc.dram_tensor("out_x", (B, S, D), F32, kind="ExternalOutput").ap()
    build(nc, a, out)
    return run_bass_kernel_spmd(nc, [arrays], core_ids=[0]).results[0]["out_x"]
```

```python
from contextlib import ExitStack

import numpy as np
import concourse.bass as bass
from concourse import mybir

F32 = mybir.dt.float32
BF16 = mybir.dt.bfloat16
I32 = mybir.dt.int32
ALU = mybir.AluOpType
ACT = mybir.ActivationFunctionType
AX = mybir.AxisListType

P = 128
B, S, D = 64, 128, 128
S2 = 77
H, DH = 16, 8
GB = 4
NG = B // GB
GT = GB * S
EPS = 1e-5


class Count:

    def __init__(self, sem, per):
        self.sem, self.per = sem, per

    def at(self, t, j=0):
        v = t * self.per + j
        return max(v, 0) if isinstance(v, int) else v


class Chain:

    def __init__(self, sem):
        self.sem, self.base, self.n = sem, 0, 0

    def start(self, base):
        self.base, self.n = base, 0

    def next(self):
        self.n += 1
        return self.base + self.n


def looped(eng, sem, turns, per, prologue, body, tail):
    chain = Chain(sem)
    prologue(eng, chain)
    base = chain.n
    chain.start(base)
    body(eng, chain, 0)
    base += chain.n
    with eng.Fori(1, turns - 1) as i:
        chain.start((i - 1) * per + base)
        body(eng, chain, i)
    assert chain.n == per, chain.n
    base += (turns - 2) * per
    chain.start(base)
    body(eng, chain, turns - 1)
    chain.start(base + chain.n)
    tail(eng, chain)

def attention(nc, const, banks, tag, x_in, x_out, wq, wk, wv, wo, scale, bq=None, bk=None, bv=None, bo=None,
              ctx=None, mask=None, gate=None, ln=None, rms=None, normed=True):
    sk = S if ctx is None else S2
    kt = GB * sk
    PARTS, ROWS = 3, 6 * DH
    Q_ROWS, K_ROWS = (0, 0, 1, 1, 0, 2), (0, 1, 0, 1, 2, 0)
    VC = DH + 1
    VW = 8 * VC
    TURNS = NG // 2
    TAIL = 6
    ident, identb, ones_row, sel = const["ident"], const["identb"], const["ones_row"], const["sel"]
    half_pow = const["half_pow"]
    if rms:
        slot = {"x": 0, "qt": 1, "kt": 2, "v": 3, "qn": 6, "kn": 7}
    elif ln is not None:
        slot = {"x": 5, "q": 6, "k": 7, "v": 8}
    else:
        slot = {"x": 1, "c": 2, "q": 4, "k": 5, "v": 6}
    if mask is not None:
        slot.update({"m": 8, "g": 10})
    uses = sorted(slot, key=lambda u: slot[u])
    NU = len(uses)
    nu = {u: n for n, u in enumerate(uses)}
    Q, K = ("qn", "kn") if rms else ("q", "k")
    part_slot = (slot[Q], slot[K])
    LOADS = 1 + (ctx is not None) + (2 if mask is not None else 0)

    with ExitStack() as st:
        def sb(name, shape, dt=F32):
            return st.enter_context(nc.sbuf_tensor(f"{tag}_{name}", shape, dt))

        def sem(name, per=1):
            return Count(nc.alloc_semaphore(f"{tag}_{name}"), per)

        dram_q = nc.dram_tensor(f"{tag}_q_parts", (2, PARTS, P, GT), BF16, kind="Internal").ap()
        dram_k = nc.dram_tensor(f"{tag}_k_parts", (2, PARTS, P, kt), BF16, kind="Internal").ap()

        w = sb("w", [P, 4, D])
        bqk = sb("bqk", [P, 2])
        bvb = sb("bvb", [P, D])
        bor = sb("bor", [1, D])
        lnw = sb("lnw", [P, 2, D])
        xp = sb("xp", [P, 2, GB, D])
        xr = sb("xr", [P, 2, GB, D])
        cx = sb("cx", [P, GB, D]) if ctx is not None else None
        mi = sb("mi", [P, GB, S2], I32) if mask is not None else None
        neg = sb("neg", [P, 2, GB, S2]) if mask is not None else None
        gp = sb("gp", [P, GB, S2]) if mask is not None else None
        negT = sb("negT", [P, 2, GT]) if mask is not None else None
        gpT = sb("gpT", [P, 2, GT]) if mask is not None else None
        xn = sb("xn", [P, GB, D]) if ln is not None else None
        xT = sb("xT", [P, GT])
        cT = sb("cT", [P, kt]) if ctx is not None else xT
        qf = sb("qf", [P, 2, GT])
        qr = sb("qr", [P, 2, GT])
        qp = sb("qp", [P, 2, PARTS, GT], BF16)
        qtok = sb("qtok", [P, 2, GB, D]) if rms else None
        sq = sb("sq", [P, 2, GB * D]) if rms else None
        ms = sb("ms", [P, 3, 2, GB * H]) if rms else None
        eps = sb("eps", [P, 1]) if rms else None
        Qs = sb("Qs", [P, 2, H, GT], BF16)
        Ks = sb("Ks", [P, 2, H, kt], BF16)
        vS = sb("vS", [P, 2, GB, D])
        vB = sb("vB", [P, 2, 2, 9 * VW])
        oB = sb("oB", [P, 2, 9 * VW]) if gate is not None else None
        sm = sb("sm", [P, 2, 4 * S2]) if mask is not None else None
        smT = sb("smT", [P, 2, 4 * S]) if mask is not None else None
        nm = sb("nm", [P, 2, 3, H])
        nmp = sb("nmp", [P, 2, PARTS, H], BF16)
        nmT = sb("nmT", [P, 2, S], BF16)
        pT = sb("pT", [P, 2, H, S])
        pG = sb("pG", [P, 2, H, S]) if gate is not None else pT
        ou = sb("ou", [VW, 2, S])
        rden = sb("rden", [P, H])
        on = sb("on", [P, D])
        oT = sb("oT", [P, S])
        r = sb("r", [P, 2, D])
        stat = sb("stat", [P, 2, 8])
        var = sb("var", [P, 2, 2])
        lst = sb("lst", [P, GB, 8]) if ln is not None else None
        lvar = sb("lvar", [P, 2, GB]) if ln is not None else None

        s_w = sem("weights"); s_setup = sem("setup"); s_zero = sem("zeroed"); s_xp = sem("x_loaded"); s_xr = [sem(f"residual_loaded{l}", 16) for l in range(2)]
        s_xpfree = sem("x_used"); s_pb = sem("proj_written", NU); s_pf = sem("proj_evacuated", NU)
        s_hi = sem("hi_ready", 2); s_r1 = sem("rest1_ready", 2)
        s_mid = sem("mid_ready", 2); s_lo = sem("lo_ready", 2)
        s_ps = sem("parts_stored", 1); s_stk = sem("stack_loaded", 1)
        s_ln = sem("front_var", 1); s_lp = sem("front_pow", 1); s_xn = sem("front_norm", 1)
        s_neg = sem("neg_ready"); s_sq = sem("squares", 2); s_ms = sem("sums_of_squares", 2); s_rt = sem("roots"); s_qn = sem("qk_normed", 2)
        s_S = sem("scores", 4); s_Sf = sem("scores_used", 4); s_nmp = sem("max_parts"); s_T = sem("max_transposed")
        s_nmT = sem("max_rows"); s_st = sem("shifted", 4); s_e = sem("exp", 4)
        s_sm = sem("masked", 4) if mask is not None else None
        s_stf = s_sm if mask is not None else s_e
        s_pg = sem("gated", 4); s_vb = sem("values_spread"); s_pv = sem("pv", 4); s_ou = sem("pv_evacuated")
        s_ot = sem("out_turned"); s_on = sem("out_normed"); s_o2 = sem("out_turned_back"); s_oT = sem("oT")
        s_y = sem("y"); s_r = sem("residual"); s_v = sem("var"); s_pw = sem("pow"); s_xo = sem("x_done") if normed else s_r
        s_store = sem("stored"); s_bq = sem("q_bias_scaled"); s_dve = nc.alloc_semaphore(f"{tag}_dve_done")
        s_pool = nc.alloc_semaphore(f"{tag}_pool_chain")
        s_step = nc.alloc_semaphore(f"{tag}_passed")
        bankS, bankT, bankO, bankP, bankM, bankY = banks[0:2], banks[2:4], banks[4], banks[5], banks[6], banks[7]
        bankMb = bankM.bitcast(BF16)
        NZ = 3 + (sk < P) + (sk < P and gate is not None)
        NW = sum(1 for t in (bq, bk, bv, bo) if t is not None) + 4 + (2 if ln is not None else 0) + (2 if rms else 0)

        block = st.enter_context(nc.Block())
        x_g = x_in.rearrange("(g b) t d -> g t b d", b=GB)
        o_g = x_out.rearrange("(g b) t d -> g t b d", b=GB)

        def diagonal(t):
            return t.rearrange("p (h c) -> p h c", c=VW + VC)

        def heads(t):
            return t.rearrange("p (h d) -> p h d", h=H)

        @block.sync
        def _(sp):
            n = 0
            def load_w(dst, src):
                sp.dma_start(dst, src).then_inc(s_w.sem, 16)
            for j, t in enumerate((wq, wk, wv, wo)):
                load_w(w[:, j, :], t)
            for j, t in enumerate((bq, bk)):
                if t is not None:
                    load_w(bqk[:, j:j + 1], t.rearrange("(d a) -> d a", a=1))
            if rms:
                for j, t in enumerate(rms):
                    load_w(bqk[:, j:j + 1], t)
            if bv is not None:
                load_w(bvb[:], bv.rearrange("(a d) -> a d", a=1).to_broadcast([P, D]))
            if bo is not None:
                load_w(bor[:], bo.rearrange("(a d) -> a d", a=1))
            if ln is not None:
                for j, t in enumerate(ln):
                    load_w(lnw[:, j, :], t.rearrange("(a d) -> a d", a=1).to_broadcast([P, D]))

            def load_x(g, par):
                sp.wait_ge(s_xpfree.sem, s_xpfree.at(g))
                sp.sem_inc(s_step, 1)
                sp.dma_start(xp[:, par], x_g[g]).then_inc(s_xp.sem, 16)
                if ctx is not None:
                    sp.dma_start(cx[0:S2], ctx.rearrange("(g b) t d -> g t b d", b=GB)[g]).then_inc(s_xp.sem, 16)
                if mask is not None:
                    sp.dma_start(mi[:], mask.rearrange("(g b) t d -> g t b d", b=GB)[g]).then_inc(s_xp.sem, 16)
                    sp.dma_start(gp[:], gate.rearrange("(g b) t d -> g t b d", b=GB)[g]).then_inc(s_xp.sem, 16)

            def stack(g, par):
                for t, (dram, n) in enumerate(((dram_q, GT), (dram_k, kt))):
                    sp.wait_ge(s_lo.sem, s_lo.at(g, t + 1))
                    sp.dma_start(dram[par].rearrange("a p t -> p a t"), qp[:, t, :, 0:n]).then_inc(s_ps.sem, 16)
                sp.wait_ge(s_ps.sem, s_ps.at((g + 1) * 32))
                sp.wait_ge(s_st.sem, s_st.at((g - 1) * GB))
                for t, (dram, n, rows) in enumerate(((dram_q, GT, Q_ROWS), (dram_k, kt, K_ROWS))):
                    dst = Qs if t == 0 else Ks
                    for k, a in enumerate(rows):
                        sp.dma_start(dst[k * DH:(k + 1) * DH, par],
                                     dram[par, a].rearrange("(h d) t -> d h t", d=DH)).then_inc(s_stk.sem, 16)

            def residual(g, par):
                sp.wait_ge(s_store.sem, s_store.at((g - 1) * 16))
                sp.sem_inc(s_step, 1)
                sp.dma_start(xr[:, par], x_g[g]).then_inc(s_xr[par].sem, 16)

            def store(g, par):
                sp.wait_ge(s_xo.sem, s_xo.at((g + 1) * GB))
                sp.sem_inc(s_step, 1)
                sp.dma_start(o_g[g], xr[:, par]).then_inc(s_store.sem, 16)

            def turn(i, first=False, last=False):
                for l in range(2):
                    g = 2 * i + l
                    if not first:
                        store(g - 2, l)
                    residual(g, l)
                    if not (last and l):
                        stack(g + 1, 1 - l)
                    if not last:
                        load_x(g + 2, l)
            load_x(0, 0)
            sp.wait_ge(s_zero.sem, NZ)
            stack(0, 0)
            load_x(1, 1)
            turn(0, first=True)
            with sp.Fori(1, TURNS - 1) as i:
                turn(i)
            turn(TURNS - 1, last=True)
            for l in range(2):
                store(NG - 2 + l, l)
            sp.wait_ge(s_store.sem, NG * 16)

        @block.tensor
        def _(pe):
            pe.wait_ge(s_w.sem, 16 * NW)
            pe.wait_ge(s_zero.sem, NZ)

            def use(g, u):
                pe.wait_ge(s_pf.sem, s_pf.at(g, nu[u]))

            def done(ins):
                ins.then_inc(s_pb.sem, 1)

            def prep(u, g, par):
                use(g, u)
                if u == "x":
                    if ln is not None:
                        pe.wait_ge(s_xn.sem, s_xn.at(g + 1))
                    else:
                        pe.wait_ge(s_xp.sem, (g + 1) * 16 * LOADS)
                    for b in range(GB):
                        src = xn[:, b, :] if ln is not None else xp[:, par, b, :]
                        ins = pe.transpose(bankP[:, b * S:(b + 1) * S], src, ident[:])
                if u == "c":
                    for b in range(GB):
                        ins = pe.transpose(bankP[:, b * S2:(b + 1) * S2], cx[0:S2, b, :], ident[0:S2, 0:S2])
                if u == "m":
                    pe.wait_ge(s_neg.sem, s_neg.at(g + 1))
                    for b in range(GB):
                        ins = pe.transpose(bankP[0:S2, b * S:(b + 1) * S], neg[:, par, b, :], ident[:])
                if u == "g":
                    for b in range(GB):
                        ins = pe.transpose(bankP[0:S2, b * S:(b + 1) * S], gp[:, b, :], ident[:])
                if u == "q":
                    ins = pe.matmul(bankP[:], w[:, 0, :], xT[:], start=True, stop=True)
                if u == "k":
                    ins = pe.matmul(bankP[:, 0:kt], w[:, 1, :], cT[:], start=True, stop=True)
                if u in ("qt", "kt"):
                    for b in range(GB):
                        ins = pe.matmul(bankP[:, b * S:(b + 1) * S], xT[:, b * S:(b + 1) * S], w[:, 0 if u == "qt" else 1, :],
                                        start=True, stop=True)
                if u in ("qn", "kn"):
                    t = 0 if u == "qn" else 1
                    pe.wait_ge(s_qn.sem, s_qn.at(g, t + 1))
                    for b in range(GB):
                        ins = pe.transpose(bankP[:, b * S:(b + 1) * S], qtok[:, t, b, :], ident[:])
                if u == "v":
                    for b in range(GB):
                        ins = pe.matmul(bankP[0:sk, b * D:(b + 1) * D], cT[:, b * sk:(b + 1) * sk], w[:, 2, :],
                                        start=True, stop=True)
                done(ins)

            def scores(i, lb, c):
                b, l, q = 8 * i + lb, lb // GB, lb % GB
                if c == 0 and q == 0:
                    pe.wait_ge(s_stk.sem, (2 * i + l + 1) * 16 * 2 * len(Q_ROWS))
                pe.wait_ge(s_Sf.sem, s_Sf.at(b, c + 1 - 2))
                for h in range(4):
                    hh = 4 * c + h
                    ins = pe.matmul(bankS[c % 2][:, h * sk:(h + 1) * sk], Qs[:, l, hh, q * S:(q + 1) * S],
                                    Ks[:, l, hh, q * sk:(q + 1) * sk], start=True, stop=True)
                ins.then_inc(s_S.sem, 1)

            def turn_max(b, lb):
                pe.wait_ge(s_nmp.sem, s_nmp.at(b + 1))
                pe.wait_ge(s_r.sem, s_r.at(b - 3))
                pe.sem_inc(s_step, 1)
                pe.transpose(bankMb[0:PARTS * H, 0:S], nmp[:, lb % 2].rearrange("p a h -> p (a h)"),
                             identb[:]).then_inc(s_T.sem, 1)

            def shifted(b, lb, c):
                l, q = lb // GB, lb % GB
                pe.wait_ge(s_nmT.sem, s_nmT.at(b + 1))
                pe.wait_ge(s_stf.sem, s_stf.at(b, c + 1 - 2))
                for h in range(4):
                    hh = 4 * c + h
                    o = bankT[c % 2][0:sk, h * S:(h + 1) * S]
                    pe.matmul(o, Ks[:, l, hh, q * sk:(q + 1) * sk], Qs[:, l, hh, q * S:(q + 1) * S],
                              start=True, stop=False)
                    ins = pe.matmul(o, sel[:, hh, 0:sk], nmT[:, lb % 2, :], start=False, stop=True)
                ins.then_inc(s_st.sem, 1)

            def values(b, lb, c):
                if c == 0:
                    pe.wait_ge(s_ou.sem, s_ou.at(b))
                    pe.wait_ge(s_vb.sem, s_vb.at(b + 1))
                if gate is not None:
                    pe.wait_ge(s_pg.sem, s_pg.at(b, c + 1))
                pe.wait_ge(s_e.sem, s_e.at(b, c + 1))
                half = c // 2
                o = bankO[0:VW, half * S:(half + 1) * S]
                for hh in range(4 * c, 4 * c + 4):
                    h = hh % 8
                    ins = pe.matmul(o, vB[:, lb % 2, half, h * VW:(h + 1) * VW], pG[:, lb % 2, hh, :], start=(h == 0),
                                    stop=(h == 7 and gate is None))
                    if gate is not None:
                        ins = pe.matmul(o, oB[:, half, h * VW:(h + 1) * VW], pT[:, lb % 2, hh, :], start=False, stop=(h == 7))
                ins.then_inc(s_pv.sem, 1)

            def turn_out(b):
                pe.wait_ge(s_ou.sem, s_ou.at(b + 1))
                pe.wait_ge(s_oT.sem, s_oT.at(b))
                pe.sem_inc(s_step, 1)
                for half in range(2):
                    ins = pe.transpose(bankY[:, half * VW:(half + 1) * VW], ou[:, half, :], ident[0:VW, 0:VW])
                ins.then_inc(s_ot.sem, 1)

            def turn_back(b):
                pe.wait_ge(s_on.sem, s_on.at(b + 1))
                pe.transpose(bankY[:, 0:S], on[:], ident[:]).then_inc(s_o2.sem, 1)

            def out(b):
                pe.wait_ge(s_oT.sem, s_oT.at(b + 1))
                pe.wait_ge(s_r.sem, s_r.at(b))
                pe.wait_ge(s_nmT.sem, s_nmT.at(min(b + 4, B) if isinstance(b, int) else b + 4))
                ins = pe.matmul(bankM[:, 0:D], oT[:], w[:, 3, :], start=True, stop=(bo is None))
                if bo is not None:
                    ins = pe.matmul(bankM[:, 0:D], ones_row[:], bor[:], start=False, stop=True)
                ins.then_inc(s_y.sem, 1)

            def step(i, lb, c, live):
                b = 8 * i + lb
                if live(0):
                    scores(i, lb, c)
                if c == 0:
                    if live(2):
                        shifted(b - 2, (lb - 2) % 8, 3)
                    if live(1):
                        turn_max(b - 1, (lb - 1) % 8)
                elif live(1):
                    shifted(b - 1, (lb - 1) % 8, c - 1)
                if live(2):
                    values(b - 2, (lb - 2) % 8, c)
                if c == 1 and live(3):
                    turn_out(b - 3)
                if c == 2 and live(4):
                    out(b - 4)
                if c == 3 and live(3):
                    turn_back(b - 3)

            def slots(i, lb, c, last):
                l, z = lb // GB, 4 * (lb % GB) + c
                for u in uses:
                    if z == slot[u] and not (last and l):
                        prep(u, 2 * i + l + 1, 1 - l)

            def turn(i, first=False, last=False):
                for lb in range(8):
                    for c in range(4):
                        step(i, lb, c, lambda k: not (first and lb < k))
                        slots(i, lb, c, last)
            for u in uses:
                prep(u, 0, 0)
            turn(0, first=True)
            with pe.Fori(1, TURNS - 1) as i:
                turn(i)
            turn(TURNS - 1, last=True)
            for k in range(TAIL):
                for c in range(4):
                    step(TURNS, k, c, lambda n: k < n)

        @block.scalar
        def _(act):
            act.wait_ge(s_w.sem, 16 * NW)
            act.wait_ge(s_zero.sem, NZ)
            if rms or bq is not None:
                act.activation(bqk[:, 0:1], bqk[:, 0:1], ACT.Copy, scale=scale).then_inc(s_bq.sem, 1)
                act.wait_ge(s_bq.sem, 1)

            def evac(g, u, dst, src, **k):
                act.wait_ge(s_pb.sem, s_pb.at(g, nu[u] + 1))
                act.activation(dst, src, ACT.Identity, **k).then_inc(s_pf.sem, 1)

            def prep(u, g, par):
                if u == "x":
                    evac(g, "x", xT[:], bankP[:])
                if u == "c":
                    evac(g, "c", cT[:], bankP[:, 0:kt])
                if u == "m":
                    act.wait_ge(s_sm.sem, s_sm.at((g - 1) * GB))
                    evac(g, "m", negT[0:S2, par, :], bankP[0:S2, :])
                if u == "g":
                    act.wait_ge(s_pg.sem, s_pg.at((g - 1) * GB))
                    evac(g, "g", gpT[0:S2, par, :], bankP[0:S2, :])
                if u in ("qt", "kt"):
                    t = 0 if u == "qt" else 1
                    act.wait_ge(s_pb.sem, s_pb.at(g, nu[u] + 1))
                    act.wait_ge(s_ms.sem, s_ms.at(g - 1, t + 1))
                    act.activation(sq[:, t, :], bankP[:], ACT.Square).then_inc(s_sq.sem, 1)
                    act.wait_ge(s_pf.sem, s_pf.at(g - 1, nu["qn" if t == 0 else "kn"] + 1))
                    evac(g, u, qtok[:, t].rearrange("p b d -> p (b d)"), bankP[:])
                if u in ("q", "k", "qn", "kn"):
                    t = 0 if u[0] == "q" else 1
                    n, bias = ((GT, bq), (kt, bk))[t]
                    act.wait_ge(s_lo.sem, s_lo.at(g - 1, t + 1))
                    k = {"scale": scale} if t == 0 else {}
                    if rms:
                        k = {"scale": bqk[:, t:t + 1]}
                    elif bias is not None:
                        k["bias"] = bqk[:, t:t + 1]
                    evac(g, u, qf[:, t, 0:n], bankP[:, 0:n], **k)

            def root(g):
                act.wait_ge(s_ms.sem, s_ms.at(g + 1))
                act.wait_ge(s_qn.sem, s_qn.at(g))
                act.activation(ms[:, 1], ms[:, 0], ACT.Sqrt, scale=1.0 / DH, bias=eps[:]).then_inc(s_rt.sem, 1)

            def exp(b, lm, c):
                p = lm % 2
                act.wait_ge(s_pv.sem, s_pv.at(b - 2, c + 1))
                if mask is not None:
                    act.wait_ge(s_sm.sem, s_sm.at(b, c + 1))
                    act.wait_ge(s_pg.sem, s_pg.at(b - 2, c + 1))
                    src = smT[0:sk, c % 2, :]
                else:
                    act.wait_ge(s_st.sem, s_st.at(b, c + 1))
                    src = bankT[c % 2][0:sk, :]
                act.activation(pT[0:sk, p, 4 * c:4 * c + 4, :].rearrange("p h t -> p (h t)"), src, ACT.Exp).then_inc(s_e.sem, 1)

            def step(i, lb, c, live):
                b = 8 * i + lb
                if c == 0 and live(3):
                    act.wait_ge(s_pv.sem, s_pv.at(b - 3 + 1))
                    act.wait_ge(s_ot.sem, s_ot.at(b - 3))
                    act.activation(ou[:].rearrange("p a t -> p (a t)"), bankO[0:VW, 0:2 * S], ACT.Copy).then_inc(s_ou.sem, 1)
                if c == 0 and live(2):
                    exp(b - 2, (lb - 2) % 8, 3)
                if c > 0 and live(1):
                    exp(b - 1, (lb - 1) % 8, c - 1)
                if c == 1 and live(4):
                    act.wait_ge(s_o2.sem, s_o2.at(b - 4 + 1))
                    act.wait_ge(s_y.sem, s_y.at(b - 4))
                    act.activation(oT[:], bankY[:, 0:S], ACT.Copy).then_inc(s_oT.sem, 1)

            def slots(i, lb, c, last):
                l, z = lb // GB, 4 * (lb % GB) + c
                if last and l:
                    return
                for u in uses:
                    if u != "v" and z == slot[u]:
                        prep(u, 2 * i + l + 1, 1 - l)
                if rms and z == slot["v"] + 1:
                    root(2 * i + l + 1)

            def turn(i, first=False, last=False):
                for lb in range(8):
                    for c in range(4):
                        step(i, lb, c, lambda k: not (first and lb < k))
                        slots(i, lb, c, last)
            for u in uses:
                if rms and u == "qn":
                    root(0)
                if u != "v":
                    prep(u, 0, 0)
            turn(0, first=True)
            with act.Fori(1, TURNS - 1) as i:
                turn(i)
            turn(TURNS - 1, last=True)
            for k in range(TAIL):
                for c in range(4):
                    step(TURNS, k, c, lambda n: k < n)

        @block.vector
        def _(dve):
            dve.memset(Qs[:], 0.0).then_inc(s_zero.sem, 1)
            dve.memset(Ks[:], 0.0).then_inc(s_zero.sem, 1)
            dve.memset(nmT[:], 0.0).then_inc(s_zero.sem, 1)
            if sk < P:
                dve.memset(pT[:], 0.0).then_inc(s_zero.sem, 1)
                if gate is not None:
                    dve.memset(pG[:], 0.0).then_inc(s_zero.sem, 1)
            dve.wait_ge(s_w.sem, 16 * NW)
            dve.wait_ge(s_setup.sem, 1)
            dve.wait_ge(s_zero.sem, NZ)

            def front_stats(v, ch, g, par):
                v.wait_ge(s_xp.sem, (g + 1) * 16 * LOADS)
                v.wait_ge(s_xn.sem, s_xn.at(g))
                for b in range(GB):
                    ins = v.bn_stats(lst[:, b, 0:6], xp[:, par, b, :])
                ins.then_inc(ch.sem, 1)
                v.wait_ge(ch.sem, ch.next())
                v.sem_inc(s_step, 1)
                for b in range(GB):
                    ins = v.bn_aggr(lst[:, b, 6:8], lst[:, b, 0:6])
                ins.then_inc(ch.sem, 1)
                v.wait_ge(ch.sem, ch.next())
                v.wait_ge(s_lp.sem, s_lp.at(g))
                v.tensor_scalar(lvar[:, 0, :], lst[:, :, 7], EPS, None, ALU.add).then_inc(s_ln.sem, 1)

            def front_norm(v, ch, g, par):
                v.wait_ge(s_lp.sem, s_lp.at(g + 1))
                v.wait_ge(s_pf.sem, s_pf.at(g - 1, nu["x"] + 1))
                for b in range(GB):
                    ins = v.tensor_scalar(xn[:, b, :], xp[:, par, b, :], lst[:, b, 6:7], lvar[:, 1, b:b + 1],
                                          ALU.subtract, ALU.mult)
                ins.then_inc(ch.sem, 1)
                v.wait_ge(ch.sem, ch.next())
                v.tensor_tensor(xn[:], xn[:], lnw[:, 0, :].unsqueeze(1).to_broadcast([P, GB, D]), ALU.mult).then_inc(ch.sem, 1)
                v.wait_ge(ch.sem, ch.next())
                v.sem_inc(s_xpfree.sem, 1)
                v.tensor_tensor(xn[:], xn[:], lnw[:, 1, :].unsqueeze(1).to_broadcast([P, GB, D]), ALU.add).then_inc(s_xn.sem, 1)

            def masks(v, ch, g, par):
                v.wait_ge(s_xp.sem, (g + 1) * 16 * LOADS)
                v.wait_ge(s_Sf.sem, s_Sf.at((g - 1) * GB))
                v.wait_ge(s_pf.sem, s_pf.at(g - 1))
                v.tensor_scalar(neg[:, par], mi[:], 1.0, 1e9, ALU.subtract, ALU.mult).then_inc(s_neg.sem, 1)

            def squares(v, ch, g, t):
                v.wait_ge(s_sq.sem, s_sq.at(g, t + 1))
                v.wait_ge(s_rt.sem, s_rt.at(g))
                v.tensor_reduce(ms[:, 0, t, :], sq[:, t, :].rearrange("p (h d) -> p h d", d=DH), AX.X, ALU.add).then_inc(s_ms.sem, 1)

            def rms_norm(v, ch, g):
                v.wait_ge(s_rt.sem, s_rt.at(g + 1))
                v.reciprocal(ms[:, 2], ms[:, 1]).then_inc(ch.sem, 1)
                v.wait_ge(ch.sem, ch.next())
                for t in range(2):
                    v.wait_ge(s_pf.sem, s_pf.at(g, nu["qt" if t == 0 else "kt"] + 1))
                    q3 = qtok[:, t].rearrange("p b (h d) -> p (b h) d", d=DH)
                    v.tensor_tensor(q3, q3, ms[:, 2, t, :].unsqueeze(2).to_broadcast([P, GB * H, DH]), ALU.mult).then_inc(s_qn.sem, 1)

            def high(v, ch, g, t):
                n = (GT, kt)[t]
                v.wait_ge(s_ps.sem, s_ps.at(g * 32))
                v.wait_ge(s_pf.sem, s_pf.at(g, nu[(Q, K)[t]] + 1))
                v.tensor_copy(qp[:, t, 0, 0:n], qf[:, t, 0:n]).then_inc(s_hi.sem, 1)

            def middle(v, ch, g, t):
                n = (GT, kt)[t]
                v.wait_ge(s_r1.sem, s_r1.at(g, t + 1))
                v.tensor_copy(qp[:, t, 1, 0:n], qr[:, t, 0:n]).then_inc(s_mid.sem, 1)

            def value_rows(v, ch, g, par):
                v.wait_ge(s_pb.sem, s_pb.at(g, nu["v"] + 1))
                v.wait_ge(s_vb.sem, s_vb.at((g - 1) * GB))
                src = bankP[0:sk, :].rearrange("p (b d) -> p b d", b=GB)
                if bv is not None:
                    ins = v.tensor_tensor(vS[0:sk, par], src, bvb[0:sk, :].unsqueeze(1).to_broadcast([sk, GB, D]), ALU.add)
                else:
                    ins = v.tensor_copy(vS[0:sk, par], src)
                ins.then_inc(s_pf.sem, 1)

            work = [(slot["v"] + 1, value_rows), (part_slot[0] + 1, lambda v, ch, g, par: high(v, ch, g, 0)),
                    (part_slot[1] + 1, lambda v, ch, g, par: high(v, ch, g, 1)),
                    (part_slot[0] + 3, lambda v, ch, g, par: middle(v, ch, g, 0)),
                    (part_slot[1] + 3, lambda v, ch, g, par: middle(v, ch, g, 1))]
            if ln is not None:
                work += [(0, front_stats), (3, front_norm)]
            if mask is not None:
                work += [(1, masks)]
            if rms:
                work += [(slot["qt"] + 1, lambda v, ch, g, par: squares(v, ch, g, 0)),
                         (slot["kt"] + 1, lambda v, ch, g, par: squares(v, ch, g, 1)),
                         (slot["v"] + 2, lambda v, ch, g, par: rms_norm(v, ch, g))]
            work.sort(key=lambda z: z[0])

            def maximum(v, ch, b, lb, c):
                l, q, p = lb // GB, lb % GB, lb % 2
                v.wait_ge(s_S.sem, s_S.at(b, c + 1))
                if c == 0:
                    v.wait_ge(s_T.sem, s_T.at(b - 1))
                src = bankS[c % 2][:, 0:4 * sk].rearrange("p (h k) -> p h k", h=4)
                if mask is not None:
                    v.tensor_tensor(sm[:, c % 2, :].rearrange("p (h k) -> p h k", h=4), src,
                                    neg[:, l, q, :].unsqueeze(1).to_broadcast([P, 4, S2]), ALU.add).then_inc(s_Sf.sem, 1)
                    v.wait_ge(s_Sf.sem, s_Sf.at(b, c + 1))
                    v.tensor_reduce(nm[:, p, 0, 4 * c:4 * c + 4],
                                    sm[:, c % 2, :].rearrange("p (h k) -> p h k", h=4), AX.X, ALU.max, negate=True).then_inc(ch.sem, 1)
                    v.wait_ge(ch.sem, ch.next())
                else:
                    v.tensor_reduce(nm[:, p, 0, 4 * c:4 * c + 4], src, AX.X, ALU.max, negate=True).then_inc(s_Sf.sem, 1)

            def split_maxima(v, ch, b, lb):
                p = lb % 2
                v.wait_ge(s_Sf.sem, s_Sf.at(b, 4))
                v.tensor_copy(nmp[:, p, 0, :], nm[:, p, 0, :]).then_inc(ch.sem, 1)
                v.wait_ge(ch.sem, ch.next())
                v.tensor_tensor(nm[:, p, 1, :], nm[:, p, 0, :], nmp[:, p, 0, :], ALU.subtract).then_inc(ch.sem, 1)
                v.wait_ge(ch.sem, ch.next())
                v.tensor_copy(nmp[:, p, 1, :], nm[:, p, 1, :]).then_inc(ch.sem, 1)
                v.wait_ge(ch.sem, ch.next())
                v.tensor_tensor(nmp[:, p, 2, :], nm[:, p, 1, :], nmp[:, p, 1, :], ALU.subtract).then_inc(s_nmp.sem, 1)

            def maxima_rows(v, ch, b, lm):
                v.wait_ge(s_T.sem, s_T.at(b + 1))
                v.wait_ge(s_st.sem, s_st.at(b - 1))
                v.tensor_copy(nmT[0:PARTS * H, lm % 2, :], bankMb[0:PARTS * H, 0:S]).then_inc(s_nmT.sem, 1)

            def masked(v, ch, b, lm, c):
                v.wait_ge(s_st.sem, s_st.at(b, c + 1))
                v.wait_ge(s_e.sem, s_e.at(b, c + 1 - 2))
                v.tensor_tensor(smT[0:sk, c % 2, :].rearrange("p (h t) -> p h t", h=4),
                                bankT[c % 2][0:sk, :].rearrange("p (h t) -> p h t", h=4),
                                negT[0:sk, lm // GB, (lm % GB) * S:(lm % GB + 1) * S].unsqueeze(1).to_broadcast([sk, 4, S]),
                                ALU.add).then_inc(s_sm.sem, 1)

            def weighted(v, ch, b):
                v.wait_ge(s_ot.sem, s_ot.at(b + 1))
                v.wait_ge(s_o2.sem, s_o2.at(b))
                o = bankY[:, 0:2 * VW].rearrange("p (h c) -> p h c", c=VC)
                v.reciprocal(rden[:], o[:, :, DH]).then_inc(ch.sem, 1)
                v.wait_ge(ch.sem, ch.next())
                v.tensor_tensor(heads(on[:]), o[:, :, 0:DH], rden[:].unsqueeze(2).to_broadcast([P, H, DH]),
                                ALU.mult).then_inc(s_on.sem, 1)

            def add_residual(v, ch, b, lm, loaded):
                v.wait_ge(s_y.sem, s_y.at(b + 1))
                if lm % GB == 0:
                    v.wait_ge(s_xr[lm // GB].sem, loaded)
                xrow = xr[:, lm // GB, lm % GB, :]
                if not normed:
                    v.tensor_tensor(xrow, bankM[:, 0:D], xrow, ALU.add).then_inc(s_r.sem, 1)
                    return
                rr = r[:, lm % 2, :]
                v.wait_ge(s_xo.sem, s_xo.at(b - 1))
                v.tensor_tensor(rr, bankM[:, 0:D], xrow, ALU.add).then_inc(s_r.sem, 1)
                v.wait_ge(s_r.sem, s_r.at(b + 1))
                v.bn_stats(stat[:, lm % 2, 0:6], rr).then_inc(ch.sem, 1)
                v.wait_ge(ch.sem, ch.next())
                v.sem_inc(s_step, 1)
                v.bn_aggr(stat[:, lm % 2, 6:8], stat[:, lm % 2, 0:6]).then_inc(ch.sem, 1)
                v.wait_ge(ch.sem, ch.next())
                v.tensor_scalar(var[:, lm % 2, 0:1], stat[:, lm % 2, 7:8], EPS, None, ALU.add).then_inc(s_v.sem, 1)

            def norm(v, ch, b, lm):
                v.wait_ge(s_pw.sem, s_pw.at(b + 1))
                v.tensor_scalar(xr[:, lm // GB, lm % GB, :], r[:, lm % 2, :], stat[:, lm % 2, 6:7], var[:, lm % 2, 1:2],
                                ALU.subtract, ALU.mult).then_inc(s_xo.sem, 1)

            def step(v, ch, i, lb, c, live):
                b = 8 * i + lb
                if live(0):
                    maximum(v, ch, b, lb, c)
                    if c == 3:
                        split_maxima(v, ch, b, lb)
                if c == 0 and live(1):
                    maxima_rows(v, ch, b - 1, (lb - 1) % 8)
                if mask is not None:
                    if c == 0 and live(2):
                        masked(v, ch, b - 2, (lb - 2) % 8, 3)
                    if c > 0 and live(1):
                        masked(v, ch, b - 1, (lb - 1) % 8, c - 1)
                if c == 1 and normed and live(5):
                    norm(v, ch, b - 5, (lb - 5) % 8)
                if c == 2 and live(3):
                    weighted(v, ch, b - 3)
                if c == 3 and live(4):
                    add_residual(v, ch, b - 4, (lb - 4) % 8, (i + (lb - 4) // 8 + 1) * 16)

            def prologue(v, ch):
                for z, f in work:
                    f(v, ch, 0, 0)

            def turn(v, ch, i):
                first, last = isinstance(i, int) and i == 0, isinstance(i, int) and i == TURNS - 1
                for lb in range(8):
                    for c in range(4):
                        step(v, ch, i, lb, c, lambda k: not (first and lb < k))
                        l = lb // GB
                        for z, f in work:
                            if z == 4 * (lb % GB) + c and not (last and l):
                                f(v, ch, 2 * i + l + 1, 1 - l)

            def tail(v, ch):
                for k in range(TAIL):
                    for c in range(4):
                        step(v, ch, TURNS, k, c, lambda n: k < n)
            of_seq = 4 + (4 if mask is not None else 0) + (2 if normed else 0)
            of_group = (4 if ln is not None else 0) + (1 if rms else 0)
            looped(dve, s_dve, TURNS, 8 * of_seq + 2 * of_group, prologue, turn, tail)

        @block.gpsimd
        def _(pool):
            ins = pool.memset(vB[:], 0.0)
            ins.then_inc(s_pool, 1)
            pool.wait_ge(s_pool, 1)
            for p in range(2):
                for h2 in range(2):
                    pool.memset(diagonal(vB[:, p, h2, :])[:, :, DH:VC], 1.0 if gate is None else 0.0).then_inc(s_pool, 1)
            n = 5
            if gate is not None:
                pool.memset(oB[:], 0.0).then_inc(s_pool, 1)
                n += 1
                pool.wait_ge(s_pool, n)
                for h2 in range(2):
                    pool.memset(diagonal(oB[:, h2, :])[:, :, DH:VC], 1.0).then_inc(s_pool, 1)
                    n += 1
            if rms:
                pool.wait_ge(s_pool, n)
                pool.memset(eps[:], float(np.finfo(np.float32).eps)).then_inc(s_pool, 1)
                n += 1
            pool.wait_ge(s_pool, n)
            pool.nop().then_inc(s_setup.sem, 1)

            def front(g):
                if ln is not None:
                    pool.wait_ge(s_ln.sem, s_ln.at(g + 1))
                    pool.wait_ge(s_xn.sem, s_xn.at(g))
                    pool.tensor_tensor(lvar[:, 1, :], lvar[:, 0, :], half_pow[:, 0:GB], ALU.pow).then_inc(s_lp.sem, 1)
                else:
                    pool.wait_ge(s_pb.sem, s_pb.at(g, nu[turned] + 1))
                    pool.sem_inc(s_xpfree.sem, 1)

            def rest1(g, t):
                n = (GT, kt)[t]
                pool.wait_ge(s_hi.sem, s_hi.at(g, t + 1))
                pool.wait_ge(s_lo.sem, s_lo.at(g - 1, t + 1))
                pool.tensor_tensor(qr[:, t, 0:n], qf[:, t, 0:n], qp[:, t, 0, 0:n], ALU.subtract).then_inc(s_r1.sem, 1)

            def low(g, t):
                n = (GT, kt)[t]
                pool.wait_ge(s_mid.sem, s_mid.at(g, t + 1))
                pool.wait_ge(s_ps.sem, s_ps.at(g * 32))
                pool.wait_ge(s_r1.sem, s_r1.at(g, t + 1))
                pool.tensor_tensor(qp[:, t, 2, 0:n], qr[:, t, 0:n], qp[:, t, 1, 0:n], ALU.subtract).then_inc(s_lo.sem, 1)

            turned = "g" if mask is not None else ("c" if ctx is not None else "x")
            work = [(1 if ln is not None else slot[turned] + 1, front),
                    (part_slot[0] + 1, lambda g: rest1(g, 0)), (part_slot[1] + 1, lambda g: rest1(g, 1)),
                    (part_slot[0] + 3, lambda g: low(g, 0)), (part_slot[1] + 3, lambda g: low(g, 1))]
            work.sort(key=lambda z: z[0])

            def spread(i, b, lm):
                l, q, p = lm // GB, lm % GB, lm % 2
                if q == 0:
                    g = 2 * i + l
                    pool.wait_ge(s_pf.sem, s_pf.at(g, nu["v"] + 1))
                pool.wait_ge(s_pv.sem, s_pv.at(b - 1))
                pool.sem_inc(s_step, 1)
                src = vS[0:sk, l, q, :].rearrange("p (a h d) -> p a h d", a=2, h=8)
                for h2 in range(2):
                    ins = pool.tensor_copy(diagonal(vB[0:sk, p, h2, :])[:, :, 0:DH], src[:, h2])
                ins.then_inc(s_vb.sem, 1)

            def gated(b, lm, c):
                pool.wait_ge(s_e.sem, s_e.at(b, c + 1))
                pool.wait_ge(s_pv.sem, s_pv.at(b - 2, c + 1))
                hs = slice(4 * c, 4 * c + 4)
                pool.tensor_tensor(pG[0:sk, lm % 2, hs], pT[0:sk, lm % 2, hs],
                                   gpT[0:sk, lm // GB, (lm % GB) * S:(lm % GB + 1) * S].unsqueeze(1).to_broadcast([sk, 4, S]),
                                   ALU.mult).then_inc(s_pg.sem, 1)

            def step(i, lb, c, live):
                b = 8 * i + lb
                if gate is not None:
                    if c == 0 and live(2):
                        gated(b - 2, (lb - 2) % 8, 3)
                    if c > 0 and live(1):
                        gated(b - 1, (lb - 1) % 8, c - 1)
                if c == 0 and live(1):
                    spread(i if lb else i - 1, b - 1, (lb - 1) % 8)
                if c == 0 and normed and live(5):
                    lm = (lb - 5) % 8
                    pool.wait_ge(s_v.sem, s_v.at(b - 5 + 1))
                    pool.wait_ge(s_xo.sem, s_xo.at(b - 5 - 1))
                    pool.tensor_tensor(var[:, lm % 2, 1:2], var[:, lm % 2, 0:1], half_pow[:, 0:1], ALU.pow).then_inc(s_pw.sem, 1)

            def turn(i, first=False, last=False):
                for lb in range(8):
                    for c in range(4):
                        step(i, lb, c, lambda k: not (first and lb < k))
                        l = lb // GB
                        for z, f in work:
                            if z == 4 * (lb % GB) + c and not (last and l):
                                f(2 * i + l + 1)
            for z, f in work:
                f(0)
            turn(0, first=True)
            with pool.Fori(1, TURNS - 1) as i:
                turn(i)
            turn(TURNS - 1, last=True)
            for k in range(TAIL):
                for c in range(4):
                    step(TURNS, k, c, lambda n: k < n)

def experts(nc, const, banks, x, x1, y, a):
    E, F = 8, 512
    FT = F // P
    TURNS = NG // 2
    ident, identb, half_pow = const["ident"], const["identb"], const["half_pow"]
    g_, b_, gw, gb, w1, b1, w2, b2 = [a["L0_ffn_" + n] for n in
                                      ("ln2_g", "ln2_b", "gate_w", "gate_b", "w1", "b1", "w2", "b2")]
    with ExitStack() as st:
        def sb(name, shape, dt=F32):
            return st.enter_context(nc.sbuf_tensor(f"moe_{name}", shape, dt))

        def sem(name, per=1):
            return Count(nc.alloc_semaphore(f"moe_{name}"), per)

        w1s = sb("w1", [P, E, F])
        w2s = sb("w2", [P, E, FT, D])
        b1s = sb("b1", [P, E, FT])
        b2s = sb("b2", [P, E])
        gws = sb("gw", [P, E])
        gbs = sb("gb", [P, E])
        lnw = sb("lnw", [P, 2, D])
        rank = sb("rank", [P, E])
        pick = sb("pick", [E, E, P], BF16)
        xa = sb("xa", [P, 2, GB, D])
        xb = sb("xb", [P, 2, GB, D])
        hn = sb("hn", [P, GB, D])
        hT = sb("hT", [P, 2, GT])
        lst = sb("lst", [P, GB, 8])
        lvar = sb("lvar", [P, 2, GB])
        ost = sb("ost", [P, GB, 8])
        ovar = sb("ovar", [P, 2, GB])
        lg = sb("lg", [P, GB, E])
        lmax = sb("lmax", [P, 2, GB])
        one = sb("one", [P, GB, E], BF16)
        oneT = sb("oneT", [E, 2, GT], BF16)
        mid = sb("mid", [P, 2, FT, GT])
        ye = sb("ye", [P, 2, GT])
        tm = sb("tm", [P, GT])
        acc = sb("acc", [P, 2, GT])

        s_w = sem("weights"); s_setup = sem("setup"); s_ld = sem("loaded", 32); s_store = sem("stored", 16)
        s_var = sem("front_var"); s_pw = sem("front_pow"); s_hn = sem("front_norm"); s_tp = sem("front_turned")
        s_hT = sem("front_copied"); s_lg = sem("logits"); s_one = sem("chosen"); s_ot = sem("choice_turned")
        s_oT = sem("choice_copied"); s_mid = sem("mid", FT); s_rl = sem("relu", FT); s_y = sem("expert_out")
        s_ye = sem("expert_biased"); s_mk = sem("mask"); s_tm = sem("masked"); s_acc = sem("accumulated")
        s_bk = sem("turned_back"); s_fin = sem("residual_added"); s_ov = sem("out_var"); s_op = sem("out_pow")
        s_o = sem("out_ready")
        s_dve = nc.alloc_semaphore("moe_dve_done")
        s_step = nc.alloc_semaphore("moe_passed")
        s_pool = nc.alloc_semaphore("moe_pool_setup")
        NW = 8 + E
        x_g, x1_g, o_g = [t.rearrange("(g b) t d -> g t b d", b=GB) for t in (x, x1, y)]
        bankA, bankL = banks[0], banks[1]
        bankLb = bankL.bitcast(BF16)
        block = st.enter_context(nc.Block())

        @block.sync
        def _(sp):
            def load_w(dst, src):
                sp.dma_start(dst, src).then_inc(s_w.sem, 16)

            def load(g, par):
                sp.wait_ge(s_hn.sem, s_hn.at(g))
                sp.sem_inc(s_step, 1)
                sp.wait_ge(s_store.sem, s_store.at(g - 1))
                sp.sem_inc(s_step, 1)
                sp.dma_start(xa[:, par], x_g[g]).then_inc(s_ld.sem, 16)
                sp.dma_start(xb[:, par], x1_g[g]).then_inc(s_ld.sem, 16)

            def store(g, par):
                sp.wait_ge(s_o.sem, s_o.at(g + 1))
                sp.sem_inc(s_step, 1)
                sp.dma_start(o_g[g], xb[:, par]).then_inc(s_store.sem, 16)

            load(0, 0)
            load_w(gws[:], gw)
            load_w(gbs[:], gb.rearrange("(a e) -> a e", a=1).to_broadcast([P, E]))
            load_w(lnw[:, 0, :], g_.rearrange("(a d) -> a d", a=1).to_broadcast([P, D]))
            load_w(lnw[:, 1, :], b_.rearrange("(a d) -> a d", a=1).to_broadcast([P, D]))
            load_w(b1s[:], b1)
            load_w(b2s[:], b2)
            for e in range(E):
                load_w(w1s[:, e, :], w1[e])
            load_w(w2s[:, 0:E // 2], w2[0:E // 2].rearrange("e (c f) d -> f e c d", f=P))
            load_w(w2s[:, E // 2:E], w2[E // 2:E].rearrange("e (c f) d -> f e c d", f=P))

            def turn(i, last=False):
                for l in range(2):
                    g = 2 * i + l
                    if not (last and l):
                        load(g + 1, 1 - l)
                    store(g, l)
            turn(0)
            with sp.Fori(1, TURNS - 1) as i:
                turn(i)
            turn(TURNS - 1, last=True)
            sp.wait_ge(s_store.sem, NG * 16)

        @block.tensor
        def _(pe):
            pe.wait_ge(s_w.sem, 16 * NW)
            pe.wait_ge(s_setup.sem, 1)

            def front(g):
                pe.wait_ge(s_hn.sem, s_hn.at(g + 1))
                pe.wait_ge(s_fin.sem, s_fin.at(g - 1))
                pe.sem_inc(s_step, 1)
                for b in range(GB):
                    ins = pe.transpose(bankA[:, b * S:(b + 1) * S], hn[:, b, :], ident[:])
                ins.then_inc(s_tp.sem, 1)

            def logits(g, par):
                pe.wait_ge(s_hT.sem, s_hT.at(g + 1))
                pe.wait_ge(s_oT.sem, s_oT.at(g))
                pe.sem_inc(s_step, 1)
                for b in range(GB):
                    ins = pe.matmul(bankL[:, b * E:(b + 1) * E], hT[:, par, b * S:(b + 1) * S], gws[:], start=True, stop=True)
                ins.then_inc(s_lg.sem, 1)

            def choice(g):
                pe.wait_ge(s_one.sem, s_one.at(g + 1))
                pe.sem_inc(s_step, 1)
                for b in range(GB):
                    ins = pe.transpose(bankLb[0:E, b * S:(b + 1) * S], one[:, b, :], identb[:])
                ins.then_inc(s_ot.sem, 1)

            def mids(n, e, par):
                for f in range(FT):
                    pe.wait_ge(s_rl.sem, s_rl.at(n, f - 1))
                    pe.matmul(banks[2 + f % 2], w1s[:, e, f * P:(f + 1) * P], hT[:, par, :],
                              start=True, stop=True).then_inc(s_mid.sem, 1)

            def out(g, n, e, par):
                if e == 0:
                    pe.wait_ge(s_oT.sem, s_oT.at(g + 1))
                pe.wait_ge(s_tm.sem, s_tm.at(n - 1))
                pe.matmul(banks[6 + e % 2], pick[:, e, :], oneT[:, par, :], start=True, stop=True).then_inc(s_mk.sem, 1)
                pe.wait_ge(s_ye.sem, s_ye.at(n - 1))
                for f in range(FT):
                    pe.wait_ge(s_rl.sem, s_rl.at(n, f + 1))
                    ins = pe.matmul(banks[4 + e % 2], w2s[:, e, f, :], mid[:, e % 2, f, :], start=(f == 0), stop=(f == FT - 1))
                ins.then_inc(s_y.sem, 1)

            def back(g, par):
                pe.wait_ge(s_acc.sem, s_acc.at((g + 1) * E))
                pe.wait_ge(s_hT.sem, s_hT.at(g + 1))
                pe.sem_inc(s_step, 1)
                for b in range(GB):
                    ins = pe.transpose(bankA[:, b * S:(b + 1) * S], acc[:, par, b * S:(b + 1) * S], ident[:])
                ins.then_inc(s_bk.sem, 1)

            def turn(i, first=False, last=False):
                for l in range(2):
                    g = 2 * i + l
                    for e in range(E):
                        n = g * E + e
                        if e + 1 < E:
                            mids(n + 1, e + 1, l)
                        elif not (last and l):
                            mids(n + 1, 0, 1 - l)
                        out(g, n, e, l)
                        if e == 1 and not (first and not l):
                            back(g - 1, 1 - l)
                        if not (last and l):
                            if e == 3:
                                front(g + 1)
                            if e == 4:
                                logits(g + 1, 1 - l)
                            if e == 5:
                                choice(g + 1)
            front(0)
            logits(0, 0)
            choice(0)
            mids(0, 0, 0)
            turn(0, first=True)
            with pe.Fori(1, TURNS - 1) as i:
                turn(i)
            turn(TURNS - 1, last=True)
            back(NG - 1, 1)

        @block.scalar
        def _(act):
            act.wait_ge(s_w.sem, 16 * NW)

            def front(g, par):
                act.wait_ge(s_tp.sem, s_tp.at(g + 1))
                act.wait_ge(s_mid.sem, s_mid.at((g - 1) * E))
                act.activation(hT[:, par, :], bankA, ACT.Copy).then_inc(s_hT.sem, 1)

            def choice(g, par):
                act.wait_ge(s_ot.sem, s_ot.at(g + 1))
                act.wait_ge(s_mk.sem, s_mk.at((g - 1) * E))
                act.activation(oneT[:, par, :], bankLb[0:E, 0:GT], ACT.Copy).then_inc(s_oT.sem, 1)

            def relu(n, e):
                act.wait_ge(s_y.sem, s_y.at(n - 1))
                for f in range(FT):
                    act.wait_ge(s_mid.sem, s_mid.at(n, f + 1))
                    act.activation(mid[:, e % 2, f, :], banks[2 + f % 2], ACT.Relu, bias=b1s[:, e, f:f + 1]).then_inc(s_rl.sem, 1)

            def bias(n, e):
                act.wait_ge(s_y.sem, s_y.at(n + 1))
                act.wait_ge(s_tm.sem, s_tm.at(n - 1))
                act.activation(ye[:, e % 2, :], banks[4 + e % 2], ACT.Identity, bias=b2s[:, e:e + 1]).then_inc(s_ye.sem, 1)

            def turn(i, last=False):
                for l in range(2):
                    g = 2 * i + l
                    for e in range(E):
                        n = g * E + e
                        if e + 1 < E or not (last and l):
                            relu(n + 1, (e + 1) % E)
                        bias(n, e)
                        if not (last and l):
                            if e == 3:
                                front(g + 1, 1 - l)
                            if e == 5:
                                choice(g + 1, 1 - l)
            front(0, 0)
            choice(0, 0)
            relu(0, 0)
            turn(0)
            with act.Fori(1, TURNS - 1) as i:
                turn(i)
            turn(TURNS - 1, last=True)

        def stats(v, ch, dst, src):
            for b in range(GB):
                ins = v.bn_stats(dst[:, b, 0:6], src(b))
            ins.then_inc(ch.sem, 1)
            v.wait_ge(ch.sem, ch.next())
            v.sem_inc(s_step, 1)
            for b in range(GB):
                ins = v.bn_aggr(dst[:, b, 6:8], dst[:, b, 0:6])
            ins.then_inc(ch.sem, 1)
            v.wait_ge(ch.sem, ch.next())

        @block.vector
        def _(dve):
            def front(v, ch, g, par):
                v.wait_ge(s_ld.sem, s_ld.at(g + 1))
                stats(v, ch, lst, lambda b: xb[:, par, b, :])
                v.wait_ge(s_pw.sem, s_pw.at(g))
                v.tensor_scalar(lvar[:, 0, :], lst[:, :, 7], EPS, None, ALU.add).then_inc(s_var.sem, 1)
                v.wait_ge(s_pw.sem, s_pw.at(g + 1))
                v.wait_ge(s_tp.sem, s_tp.at(g))
                for b in range(GB):
                    ins = v.tensor_scalar(hn[:, b, :], xb[:, par, b, :], lst[:, b, 6:7], lvar[:, 1, b:b + 1], ALU.subtract, ALU.mult)
                ins.then_inc(ch.sem, 1)
                v.wait_ge(ch.sem, ch.next())
                v.tensor_tensor(hn[:], hn[:], lnw[:, 0, :].unsqueeze(1).to_broadcast([P, GB, D]), ALU.mult).then_inc(ch.sem, 1)
                v.wait_ge(ch.sem, ch.next())
                v.tensor_tensor(hn[:], hn[:], lnw[:, 1, :].unsqueeze(1).to_broadcast([P, GB, D]), ALU.add).then_inc(s_hn.sem, 1)

            def choose(v, ch, g):
                v.wait_ge(s_lg.sem, s_lg.at(g + 1))
                v.tensor_tensor(lg[:], bankL[:, 0:GB * E].rearrange("p (b e) -> p b e", b=GB),
                                gbs[:].unsqueeze(1).to_broadcast([P, GB, E]), ALU.add).then_inc(ch.sem, 1)
                v.wait_ge(ch.sem, ch.next())
                v.tensor_reduce(lmax[:, 0, :], lg[:], AX.X, ALU.max).then_inc(ch.sem, 1)
                v.wait_ge(ch.sem, ch.next())
                v.tensor_tensor(lg[:], lg[:], lmax[:, 0, :].unsqueeze(2).to_broadcast([P, GB, E]), ALU.is_equal).then_inc(ch.sem, 1)
                v.wait_ge(ch.sem, ch.next())
                v.tensor_tensor(lg[:], lg[:], rank[:].unsqueeze(1).to_broadcast([P, GB, E]), ALU.mult).then_inc(ch.sem, 1)
                v.wait_ge(ch.sem, ch.next())
                v.tensor_reduce(lmax[:, 1, :], lg[:], AX.X, ALU.max).then_inc(ch.sem, 1)
                v.wait_ge(ch.sem, ch.next())
                v.wait_ge(s_ot.sem, s_ot.at(g))
                v.tensor_tensor(one[:], lg[:], lmax[:, 1, :].unsqueeze(2).to_broadcast([P, GB, E]), ALU.is_equal).then_inc(s_one.sem, 1)

            def masked(v, ch, g, n, e, par):
                v.wait_ge(s_ye.sem, s_ye.at(n + 1))
                v.wait_ge(s_mk.sem, s_mk.at(n + 1))
                if e == 0:
                    v.wait_ge(s_bk.sem, s_bk.at(g - 1))
                    v.tensor_tensor(acc[:, par, :], ye[:, e % 2, :], banks[6 + e % 2], ALU.mult).then_inc(s_tm.sem, 1)
                    v.wait_ge(s_tm.sem, s_tm.at(n + 1))
                    v.sem_inc(s_acc.sem, 1)
                else:
                    v.wait_ge(s_acc.sem, s_acc.at(n))
                    v.tensor_tensor(tm[:], ye[:, e % 2, :], banks[6 + e % 2], ALU.mult).then_inc(s_tm.sem, 1)
                    v.wait_ge(s_tm.sem, s_tm.at(n + 1))
                    v.tensor_tensor(acc[:, par, :], acc[:, par, :], tm[:], ALU.add).then_inc(s_acc.sem, 1)

            def finish(v, ch, g, par):
                v.wait_ge(s_bk.sem, s_bk.at(g + 1))
                v.tensor_tensor(xb[:, par], xb[:, par], xa[:, par], ALU.add).then_inc(ch.sem, 1)
                v.wait_ge(ch.sem, ch.next())
                v.tensor_tensor(xb[:, par].rearrange("p b d -> p (b d)"), xb[:, par].rearrange("p b d -> p (b d)"),
                                bankA, ALU.add).then_inc(s_fin.sem, 1)
                v.wait_ge(s_fin.sem, s_fin.at(g + 1))
                stats(v, ch, ost, lambda b: xb[:, par, b, :])
                v.wait_ge(s_op.sem, s_op.at(g))
                v.tensor_scalar(ovar[:, 0, :], ost[:, :, 7], EPS, None, ALU.add).then_inc(s_ov.sem, 1)
                v.wait_ge(s_op.sem, s_op.at(g + 1))
                for b in range(GB):
                    ins = v.tensor_scalar(xb[:, par, b, :], xb[:, par, b, :], ost[:, b, 6:7], ovar[:, 1, b:b + 1], ALU.subtract, ALU.mult)
                ins.then_inc(s_o.sem, 1)

            def prologue(v, ch):
                v.wait_ge(s_w.sem, 16 * NW)
                v.wait_ge(s_setup.sem, 1)
                front(v, ch, 0, 0)
                choose(v, ch, 0)

            def turn(v, ch, i):
                first, last = isinstance(i, int) and i == 0, isinstance(i, int) and i == TURNS - 1
                for l in range(2):
                    g = 2 * i + l
                    for e in range(E):
                        masked(v, ch, g, g * E + e, e, l)
                        if e == 1 and not (first and not l):
                            finish(v, ch, g - 1, 1 - l)
                        if not (last and l):
                            if e == 2:
                                front(v, ch, g + 1, 1 - l)
                            if e == 4:
                                choose(v, ch, g + 1)

            def tail(v, ch):
                finish(v, ch, NG - 1, 1)
            of_group = 4 + 5 + 3
            looped(dve, s_dve, TURNS, 2 * of_group, prologue, turn, tail)

        @block.gpsimd
        def _(pool):
            for e in range(E):
                pool.memset(rank[:, e:e + 1], float(E - e)).then_inc(s_pool, 1)
            pool.memset(pick[:], 0.0).then_inc(s_pool, 1)
            pool.wait_ge(s_pool, E + 1)
            pool.affine_select(out=pick[:], in_=pick[:], compare_op=ALU.not_equal, fill=1.0, base=0,
                               pattern=[[-1, E], [0, P]], channel_multiplier=1).then_inc(s_setup.sem, 1)

            def power(s_in, s_out, v, g):
                pool.wait_ge(s_in.sem, s_in.at(g + 1))
                pool.tensor_tensor(v[:, 1, :], v[:, 0, :], half_pow[:, 0:GB], ALU.pow).then_inc(s_out.sem, 1)

            def front(g):
                pool.wait_ge(s_hn.sem, s_hn.at(g))
                power(s_var, s_pw, lvar, g)

            def finish(g):
                pool.wait_ge(s_o.sem, s_o.at(g))
                power(s_ov, s_op, ovar, g)
            front(0)
            front(1)
            finish(0)
            front(2)
            with pool.Fori(1, NG - 2) as g:
                finish(g)
                front(g + 2)
            finish(NG - 2)
            finish(NG - 1)

def mamba(nc, const, banks, x, y, a):
    DI, NS, RANK, CK, NC = 256, 16, 8, 4, 2
    SL = NS * NC
    RING = 4
    TURNS = NG // 2
    PADS = CK - 1
    BROW, CROW, XM = 32, 64, 96
    FAR = 1e28
    A_MIN = 1e-25
    ident, half_pow, ones_row = const["ident"], const["half_pow"], const["ones_row"]
    pre = ("fw_", "bw_")

    def par_(name):
        return a["L0_attn_" + name]

    ORDER = {6: (["xT", "o", "c1", "z1", "dt0", "m0"], ["xT", "c1", "z1", "dt0", "o"]),
             7: (["c0", "z0", "xd", "dt1", "yT", "m1"], ["f", "c0", "z0", "xd", "dt1"])}
    PREP, FF = ("xT", "c0", "c1", "z0", "z1", "xd", "dt0", "dt1"), ("yT", "m0", "m1", "f")

    def happens(g, d, name):
        if name in PREP:
            return 2 * g + d < 2 * NG - 1
        return g >= 1 or (name == "o" and d == 1)

    place = {}
    for k in (6, 7):
        n = 0
        for name in ORDER[k][1]:
            if name in PREP:
                place[-1, 1, name] = (k, n)
                n += 1
        for g in range(NG + 1):
            for d in range(2):
                for name in ORDER[k][d]:
                    if happens(g, d, name) and not (g == NG and d == 1 and name == "o"):
                        place[g, d, name] = (k, n)
                        n += 1

    def use(g, d, name):
        if isinstance(g, int):
            return place[g, d, name]
        k, n = place[1, d, name]
        return k, n + (g - 1) * (len(ORDER[k][0]) + len(ORDER[k][1]))

    def use_first(name):
        return place[-1, 1, name]

    PE_AT = ({0: ["xT"], 2: ["c0:0"], 3: ["c0:1"], 4: ["c0:2"], 5: ["c0:3"], 6: ["o:0"], 7: ["z0"], 8: ["o:1"], 9: ["o:2"],
              11: ["c1:0"], 12: ["c1:1"], 13: ["c1:2"], 14: ["c1:3"], 15: ["z1"], 17: ["xd:0"], 18: ["xd:1"], 20: ["dt0"],
              21: ["dt1"], 23: ["yT:0"], 24: ["yT:1"], 26: ["m0"], 27: ["m1"]},
             {0: ["xT", "f:0"], 1: ["f:1"], 2: ["f:2"], 4: ["c1:0"], 5: ["c1:1"], 6: ["c1:2"], 7: ["c1:3"], 8: ["c0:0"],
              9: ["c0:1"], 10: ["c0:2"], 11: ["c0:3"], 12: ["z1"], 13: ["z0"], 15: ["xd:0"], 16: ["xd:1"], 18: ["dt0"],
              19: ["dt1"], 21: ["o:0"], 22: ["o:1"], 23: ["o:2"]})
    ACT_AT = ({1: ["xT"], 6: ["c0"], 8: ["z0"], 10: ["o"], 15: ["c1"], 16: ["z1"], 19: ["xd"], 21: ["move", "dt0"], 22: ["dt1"],
               23: ["exp"], 25: ["yT", "log"], 28: ["m0", "m1"]},
              {1: ["xT"], 3: ["f"], 8: ["c1"], 12: ["c0"], 13: ["z1"], 14: ["z0"], 17: ["xd"], 19: ["move", "dt0"], 20: ["dt1"],
               21: ["exp"], 24: ["log", "o"]})
    DVE_AT = ({2: ["y"], 9: ["z0"], 12: ["o_stats"], 14: ["o_norm"], 16: ["u"], 17: ["z1"], 20: ["split"], 24: ["e"], 28: ["dtu"]},
              {2: ["y"], 5: ["f_stats"], 7: ["f_norm"], 10: ["f_out"], 13: ["u"], 14: ["z1"], 15: ["z0"], 18: ["split"], 22: ["e"],
               26: ["o_stats"], 28: ["dtu"], 29: ["o_norm"]})
    POOL_AT = ({4: ["gated"], 13: ["o_pow"], 26: ["dt"], 29: ["far"]},
               {4: ["gated"], 6: ["f_pow"], 9: ["out_pow"], 25: ["dt"], 27: ["o_pow"], 29: ["far"]})
    LAST = ("y", "gated", "o", "o_stats", "o_pow", "o_norm")

    def side(at, g, d, k):
        for what in at[d].get(k, []):
            name = what.split(":")[0]
            kind = name if name in PREP else ("o" if name in LAST else ("f" if name[0] == "f" and name != "far" else name))
            if kind in ("u", "move", "exp", "log", "split", "e", "dtu", "dt", "far"):
                kind = "xT"
            if kind == "out_pow":
                kind = "f"
            if not isinstance(g, int) or happens(g, d, kind):
                yield what

    with ExitStack() as st:
        def sb(name, shape, dt=F32):
            return st.enter_context(nc.sbuf_tensor(f"m_{name}", shape, dt))

        def sem(name, per=1):
            return Count(nc.alloc_semaphore(f"m_{name}"), per)

        Bd = nc.dram_tensor("m_B", (2, NS, GT), F32, kind="Internal").ap()
        flip = sb("flip", [P, P])
        selC = sb("selC", [CROW + NS, NS, P], BF16)
        win = sb("win", [P, 2, 2 * DI])
        wck = sb("wck", [P, 2, CK, DI])
        cb = sb("cb", [P, 2, NC])
        wx = sb("wx", [P, 2, NC, XM])
        wdt = sb("wdt", [RANK, 2, DI])
        bdt = sb("bdt", [P, 2, NC])
        A = sb("A", [P, 2, NC, NS])
        Dp = sb("Dp", [P, 2, NC])
        wo = sb("wo", [P, 2, NC, D])
        nw = sb("nw", [P, 2])
        fin = sb("fin", [P, 2, D])
        w1 = sb("w1", [P, DI])
        b1 = sb("b1", [P, NC])
        w2 = sb("w2", [P, NC, D])
        b2 = sb("b2", [1, GB, D])
        xg = sb("xg", [P, 2, GB, D])
        xTp = sb("xTp", [P, GB, PADS + S])
        cc = sb("cc", [P, NC, GT])
        tu = sb("tu", [P, NC, GT])
        tz = sb("tz", [P, NC, GT])
        one = sb("one", [P, 1])
        u = sb("u", [P, 2, NC, GT])
        sz = sb("sz", [P, 2, NC, GT])
        xd = sb("xd", [XM, GT])
        ch_hi = sb("C_hi", [CROW + NS, GT], BF16)
        ch_r = sb("C_rest", [CROW + NS, GT])
        ch_mid = sb("C_mid", [CROW + NS, GT], BF16)
        Cs = sb("Cs", [CROW + NS, 2, GT], BF16)
        Bb = sb("Bb", [P, 2, NS, GT])
        dt = sb("dt", [P, 2, NC, GT])
        dtu = sb("dtu", [P, 2, NC, GT])
        dBu = sb("dBu", [P, RING, GT])
        h = sb("h", [P, RING, GT])
        hC = sb("hC", [P, RING, GT])
        yd = sb("yd", [P, NC, GT])
        nrm = sb("nrm", [P, 2, GB, D])
        yT = sb("yT", [P, GT])
        md = sb("md", [P, NC, GT])
        ff = sb("ff", [P, GB, D])
        xo = sb("xo", [P, 2, GB, D])
        ost = sb("ost", [P, 3, GB, 8])
        ovar = sb("ovar", [P, 3, 2, GB])

        s_w = sem("weights"); s_set = sem("setup"); s_A = sem("rates"); s_x = sem("x_loaded", 16)
        s_store = [sem(f"stored{l}", 16) for l in range(2)]
        s_pb = {k: sem(f"side{k}_written") for k in (6, 7)}
        s_pf = {k: sem(f"side{k}_read") for k in (6, 7)}
        s_u = sem("u"); s_tz = sem("tanh_gate", 2); s_sz = sem("gate", 2); s_xd = sem("xd")
        s_cc = sem("conv", 2)
        s_hi = sem("C_hi"); s_mid = sem("C_mid"); s_Cs = sem("C_lo"); s_Csh = sem("C_moved", 2)
        s_Bd = sem("B_stored", 16); s_Bb = [sem(f"B_spread{d}", 16) for d in range(2)]
        s_ab = sem("abs", 4); s_z = sem("exp_abs"); s_w1 = sem("one_plus"); s_ln = sem("log"); s_e = sem("correction")
        s_d1 = sem("log_corrected"); s_dr = sem("dt_raw"); s_dtu = sem("dtu"); s_dt = sem("dt")
        s_C = sem("C_spread", NS); s_dA = sem("decay", SL); s_dB = sem("input", SL); s_h = sem("state", SL)
        s_hC = sem("state_C", SL); s_ya = sem("summed", SL); s_yd = sem("y_D", 2); s_yz = sem("y_gated")
        s_var = [sem(f"var{n}") for n in range(3)]
        s_pow = [sem(f"pow{n}") for n in range(3)]
        s_nrm = sem("normed"); s_yT = sem("sum_turned"); s_md = sem("relu", 2); s_xr = [sem(f"residual_loaded{l}", 16) for l in range(2)]; s_o = sem("out")
        s_dve = nc.alloc_semaphore("m_dve_done"); s_pool = nc.alloc_semaphore("m_pool_setup")
        s_act = nc.alloc_semaphore("m_act_setup"); s_step = nc.alloc_semaphore("m_passed")
        NW = 2 * 12 + 9
        x_g, o_g = [t.rearrange("(g b) t d -> g t b d", b=GB) for t in (x, y)]
        turned_by = (ident, flip)
        convw = Bb[:, 0, 0:4, :].rearrange("p a t -> p (a t)")
        block = st.enter_context(nc.Block())

        def schedule(turn):
            def run(eng):
                turn(0, first=True)
                with eng.Fori(1, TURNS - 1) as i:
                    turn(i)
                turn(TURNS - 1, last=True)
            return run

        @block.sync
        def _(sp):
            def load_w(dst, src):
                sp.dma_start(dst, src).then_inc(s_w.sem, 16)

            def row(t, n):
                return t.rearrange("(a d) -> a d", a=1).to_broadcast([n, t.shape[0]])
            sp.dma_start(xg[:, 0], x_g[0]).then_inc(s_x.sem, 16)
            for d in range(2):
                W = lambda n: par_(pre[d] + n)
                load_w(win[:, d, :], W("Win"))
                load_w(convw[:, d * CK * DI:(d + 1) * CK * DI], row(W("convw").rearrange("c k -> (c k)"), P))
                load_w(cb[:, d, :], W("convb"))
                for lo, n, at in ((0, RANK, 0), (RANK, NS, BROW), (RANK + NS, NS, CROW)):
                    sp.wait_ge(s_set.sem, s_set.at(1))
                    load_w(wx[:, d, :, at:at + n], W("Wx").rearrange("(c p) j -> p c j", p=P)[:, :, lo:lo + n])
                load_w(wdt[:, d, :], W("Wdt"))
                load_w(bdt[:, d, :], W("bdt"))
                load_w(A[:, d], W("Alog").rearrange("(c p) s -> p c s", p=P))
                load_w(Dp[:, d, :], W("D"))
                load_w(wo[:, d], W("Wout").rearrange("(c p) j -> p c j", p=P))
                load_w(nw[:, d:d + 1], par_(("fwn_w", "fwn_b")[d]).rearrange("(p a) -> p a", a=1))
            for n, t in enumerate(("fin_w", "fin_b")):
                load_w(fin[:, n, :], row(par_(t), P))
            load_w(w1[:], par_("ff_W1"))
            load_w(b1[:], par_("ff_b1"))
            load_w(w2[:], par_("ff_W2").rearrange("(c p) j -> p c j", p=P))
            for b in range(GB):
                load_w(b2[:, b, :], row(par_("ff_b2"), 1))

            def spread_B(n, g, d):
                sp.wait_ge(s_xd.sem, s_xd.at(n + 1))
                sp.sem_inc(s_step, 1)
                sp.wait_ge(s_dB.sem, s_dB.at(n - 1))
                sp.dma_start(Bd[d], xd[BROW:BROW + NS, :]).then_inc(s_Bd.sem, 16)
                sp.wait_ge(s_Bd.sem, s_Bd.at(n + 1))
                sp.dma_start(Bb[:, d].rearrange("p s t -> p (s t)"),
                             Bd[d].rearrange("s t -> (s t)").rearrange("(a n) -> a n", a=1).to_broadcast([P, NS * GT])).then_inc(s_Bb[d].sem, 16)

            def store(g, l):
                sp.wait_ge(s_o.sem, s_o.at(g + 1))
                sp.sem_inc(s_step, 1)
                sp.dma_start(o_g[g], xo[:, l]).then_inc(s_store[l].sem, 16)

            def load(g, l):
                sp.wait_ge(s_nrm.sem, s_nrm.at(2 * g - 2))
                sp.sem_inc(s_step, 1)
                sp.dma_start(xg[:, l], x_g[g]).then_inc(s_x.sem, 16)

            def residual(g, l, turn):
                sp.wait_ge(s_store[l].sem, s_store[l].at(turn))
                sp.sem_inc(s_step, 1)
                sp.dma_start(xo[:, l], x_g[g]).then_inc(s_xr[l].sem, 16)

            def turn(i, first=False, last=False):
                for l in range(2):
                    g = 2 * i + l
                    spread_B(2 * g + 1, g, 1)
                    if not (first and not l):
                        residual(g - 1, 1 - l, i if l else i - 1)
                    if not (last and l):
                        load(g + 1, 1 - l)
                    if not (first and not l):
                        store(g - 1, 1 - l)
                    if not (last and l):
                        spread_B(2 * g + 2, g + 1, 0)
            sp.wait_ge(s_A.sem, s_A.at(2))
            spread_B(0, 0, 0)
            schedule(turn)(sp)
            residual(NG - 1, 1, TURNS - 1)
            store(NG - 1, 1)
            for l in range(2):
                sp.wait_ge(s_store[l].sem, TURNS * 16)

        @block.tensor
        def _(pe):
            pe.wait_ge(s_w.sem, 16 * NW)
            pe.wait_ge(s_A.sem, s_A.at(2))
            pe.wait_ge(s_set.sem, s_set.at(2))

            def piece(at, what, n, g, l, d):
                name, _, part = what.partition(":")
                part = int(part or 0)
                k, m = at(name)
                o = banks[k]
                if part == 0:
                    pe.wait_ge(s_pf[k].sem, s_pf[k].at(m))
                c = int(name[-1]) if name[-1] in "01" else 0
                end = True
                if name == "xT":
                    pe.wait_ge(s_x.sem, s_x.at(g + 1))
                    pe.sem_inc(s_step, 1)
                    for b in range(GB):
                        ins = pe.matmul(o[:, b * S:(b + 1) * S], xg[:, l, b, :], turned_by[d][:], start=True, stop=True)
                if name in ("c0", "c1"):
                    if part == 0:
                        pe.wait_ge(s_pf[6].sem, s_pf[6].at(at("xT")[1] + 1))
                    ins = pe.matmul(o, wck[:, d, part, c * P:(c + 1) * P], xTp[:, :, part:part + S], start=(part == 0),
                                    stop=(part == CK - 1))
                    end = part == CK - 1
                if name in ("z0", "z1"):
                    ins = pe.matmul(o, win[:, d, DI + c * P:DI + (c + 1) * P], xTp[:, :, PADS:], start=True, stop=True)
                if name == "xd":
                    pe.wait_ge(s_u.sem, s_u.at(n + 1))
                    ins = pe.matmul(o[0:XM, :], wx[:, d, part, :], u[:, d, part, :], start=(part == 0), stop=(part == NC - 1))
                    end = part == NC - 1
                if name in ("dt0", "dt1"):
                    pe.wait_ge(s_xd.sem, s_xd.at(n + 1))
                    ins = pe.matmul(o, wdt[:, d, c * P:(c + 1) * P], xd[0:RANK, :], start=True, stop=True)
                if name == "o":
                    if part == 0:
                        ins = pe.matmul(o, turned_by[d][:], xg[:, l].rearrange("p b d -> p (b d)"), start=True, stop=False)
                    else:
                        pe.wait_ge(s_yz.sem, s_yz.at(n + 1))
                        for b in (2 * part - 2, 2 * part - 1):
                            for c in range(NC):
                                ins = pe.matmul(o[:, b * D:(b + 1) * D], yd[:, c, b * S:(b + 1) * S], wo[:, d, c, :], start=False,
                                                stop=(b == GB - 1 and c == NC - 1))
                    end = part == 2
                if name == "yT":
                    if part == 0:
                        pe.wait_ge(s_nrm.sem, s_nrm.at(2 * g + 2))
                        pe.sem_inc(s_step, 1)
                    for b in (2 * part, 2 * part + 1):
                        pe.matmul(o[:, b * S:(b + 1) * S], nrm[:, 0, b, :], ident[:], start=True, stop=False)
                        ins = pe.matmul(o[:, b * S:(b + 1) * S], nrm[:, 1, b, :], flip[:], start=False, stop=True)
                    end = part == 1
                if name in ("m0", "m1"):
                    pe.wait_ge(s_yT.sem, s_yT.at(g + 1))
                    ins = pe.matmul(o, w1[:, c * P:(c + 1) * P], yT[:], start=True, stop=True)
                if name == "f":
                    if part == 0:
                        pe.wait_ge(s_md.sem, s_md.at(g + 1))
                        pe.matmul(o, ones_row[:], b2[:].rearrange("p b d -> p (b d)"), start=True, stop=False)
                    else:
                        for b in (2 * part - 2, 2 * part - 1):
                            for c in range(NC):
                                pe.matmul(o[:, b * D:(b + 1) * D], md[:, c, b * S:(b + 1) * S], w2[:, c, :], start=False, stop=False)
                            ins = pe.matmul(o[:, b * D:(b + 1) * D], yT[:, b * S:(b + 1) * S], ident[:], start=False, stop=(b == GB - 1))
                    end = part == 2
                if end:
                    ins.then_inc(s_pb[k].sem, 1)

            def spread_C(n, d, s):
                if s == 0:
                    pe.wait_ge(s_Cs.sem, s_Cs.at(n + 1))
                    pe.wait_ge(s_Csh.sem, s_Csh.at(n + 1))
                pe.wait_ge(s_hC.sem, s_hC.at(n, 2 * s - 2))
                pe.matmul(banks[2 + s % 2], selC[:, s, :], Cs[:, d, :], start=True, stop=True).then_inc(s_C.sem, 1)

            def add(n, k):
                s, c = k // NC, k % NC
                if s == 0:
                    pe.wait_ge(s_yd.sem, s_yd.at(n - 1, c + 1))
                pe.wait_ge(s_hC.sem, s_hC.at(n, k + 1))
                pe.matmul(banks[4 + c], ident[:], hC[:, k % RING, :], start=(s == 0), stop=(s == NS - 1)).then_inc(s_ya.sem, 1)

            def of(what, g, l, d):
                if what in PREP:
                    return (2 * g + 1, g, l, 1) if d == 0 else (2 * g + 2, g + 1, 1 - l, 0)
                if what == "o":
                    return (2 * g - 1, g - 1, 1 - l, 1) if d == 0 else (2 * g, g, l, 0)
                return (None, g - 1, 1 - l, None)

            def unit(g, l, d):
                n = 2 * g + d
                begins = not (isinstance(g, int) and n == 0)
                for k in range(SL):
                    if k == 0:
                        spread_C(n, d, 0)
                    if k >= 2:
                        add(n, k - 2)
                    elif begins:
                        add(n - 1, SL - 2 + k)
                    if k % 2 == 1 and k // 2 + 1 < NS:
                        spread_C(n, d, k // 2 + 1)
                    for what in side(PE_AT, g, d, k):
                        piece(lambda name: use(g, d, name), what, *of(what.split(":")[0], g, l, d))

            def turn(i, first=False, last=False):
                for l in range(2):
                    for d in range(2):
                        unit(2 * i + l, l, d)
            for what in ("xT", "c1:0", "c1:1", "c1:2", "c1:3", "c0:0", "c0:1", "c0:2", "c0:3", "z0", "z1", "xd:0", "xd:1", "dt0", "dt1"):
                piece(use_first, what, 0, 0, 0, 0)
            schedule(turn)(pe)
            add(2 * NG - 1, SL - 2)
            add(2 * NG - 1, SL - 1)
            for d, names in ((0, ("o:0", "o:1", "o:2", "yT:0", "yT:1", "m0", "m1")), (1, ("f:0", "f:1", "f:2"))):
                for what in names:
                    piece(lambda name: use(NG, d, name), what, *of(what.split(":")[0], NG, 0, d))

        @block.scalar
        def _(act):
            act.wait_ge(s_w.sem, 16 * NW)
            act.wait_ge(s_set.sem, 2)
            act.activation(A[:], A[:], ACT.Exp).then_inc(s_act, 1)
            act.activation(cb[:], cb[:], ACT.Copy, scale=0.5).then_inc(s_act, 1)
            act.activation(wo[:], wo[:], ACT.Copy, scale=0.5).then_inc(s_act, 1)
            act.activation(nw[:, 1:2], nw[:, 1:2], ACT.Copy, scale=2.0).then_inc(s_act, 1)
            act.wait_ge(s_act, 4)
            act.sem_inc(s_A.sem, 1)
            act.wait_ge(s_A.sem, s_A.at(2))

            def flat(t):
                return t.rearrange("p c t -> p (c t)")

            def prep(at, n, d, what):
                def src(name):
                    k, m = at(name)
                    act.wait_ge(s_pb[k].sem, s_pb[k].at(m + 1))
                    return banks[k], s_pf[k].sem
                if what == "xT":
                    o, free = src("xT")
                    act.activation(xTp[:, :, PADS:], o.rearrange("p (b t) -> p b t", b=GB), ACT.Copy).then_inc(free, 1)
                if what in ("c0", "c1"):
                    c = int(what[1])
                    o, free = src(what)
                    act.wait_ge(s_dr.sem, s_dr.at(n))
                    act.activation(cc[:, c, :], o, ACT.Identity, scale=0.5, bias=cb[:, d, c:c + 1]).then_inc(s_cc.sem, 1)
                    act.activation(tu[:, c, :], o, ACT.Tanh, scale=0.5, bias=cb[:, d, c:c + 1]).then_inc(free, 1)
                if what in ("z0", "z1"):
                    c = int(what[1])
                    o, free = src(what)
                    act.activation(tz[:, c, :], o, ACT.Tanh, scale=0.5).then_inc(s_tz.sem, 1)
                if what == "xd":
                    o, free = src("xd")
                    act.wait_ge(s_Bd.sem, s_Bd.at(n))
                    act.wait_ge(s_Cs.sem, s_Cs.at(n))
                    act.activation(xd[:], o[0:XM, :], ACT.Copy).then_inc(free, 1)
                    act.wait_ge(s_pf[7].sem, s_pf[7].at(at("xd")[1] + 1))
                    act.sem_inc(s_xd.sem, 1)
                if what == "move":
                    act.wait_ge(s_C.sem, s_C.at(n - 1))
                    act.wait_ge(s_hi.sem, s_hi.at(n + 1))
                    act.activation(Cs[0:NS, d, :], ch_hi[CROW:, :], ACT.Copy).then_inc(s_Csh.sem, 1)
                    act.wait_ge(s_mid.sem, s_mid.at(n + 1))
                    act.activation(Cs[32:32 + NS, d, :], ch_mid[CROW:, :], ACT.Copy).then_inc(s_Csh.sem, 1)
                if what in ("dt0", "dt1"):
                    c = int(what[2])
                    o, free = src(what)
                    act.wait_ge(s_sz.sem, s_sz.at(n + 1))
                    act.wait_ge(s_u.sem, s_u.at(n + 1))
                    act.activation(cc[:, c, :], o, ACT.Abs, bias=bdt[:, d, c:c + 1]).then_inc(s_ab.sem, 1)
                    act.activation(tz[:, c, :], o, ACT.Relu, bias=bdt[:, d, c:c + 1]).then_inc(s_ab.sem, 1)
                    act.wait_ge(s_ab.sem, s_ab.at(n, 2 * c + 2))
                    act.sem_inc(free, 1)
                if what == "exp":
                    act.wait_ge(s_ab.sem, s_ab.at(n + 1))
                    act.activation(flat(cc[:]), flat(cc[:]), ACT.Exp, scale=-1.0).then_inc(s_z.sem, 1)
                    act.wait_ge(s_z.sem, s_z.at(n + 1))
                    act.activation(flat(tu[:]), flat(cc[:]), ACT.Identity, bias=one[:]).then_inc(s_w1.sem, 1)
                if what == "log":
                    act.wait_ge(s_e.sem, s_e.at(n + 1))
                    act.activation(flat(tu[:]), flat(tu[:]), ACT.Ln).then_inc(s_ln.sem, 1)

            def output(at, g, d):
                k, m = at("o")
                act.wait_ge(s_pb[k].sem, s_pb[k].at(m + 1))
                act.wait_ge(s_yT.sem, s_yT.at(g))
                act.activation(nrm[:, d].rearrange("p b d -> p (b d)"), banks[k], ACT.Copy).then_inc(s_pf[k].sem, 1)

            def forward(at, g, what):
                k, m = at(what)
                act.wait_ge(s_pb[k].sem, s_pb[k].at(m + 1))
                if what == "yT":
                    act.activation(yT[:], banks[k], ACT.Identity, scale=nw[:, 0:1], bias=nw[:, 1:2]).then_inc(s_pf[k].sem, 1)
                    act.wait_ge(s_pf[k].sem, s_pf[k].at(m + 1))
                    act.sem_inc(s_yT.sem, 1)
                elif what == "f":
                    act.wait_ge(s_o.sem, s_o.at(g))
                    act.activation(ff[:].rearrange("p b d -> p (b d)"), banks[k], ACT.Copy).then_inc(s_pf[k].sem, 1)
                else:
                    c = int(what[1])
                    act.activation(md[:, c, :], banks[k], ACT.Relu, bias=b1[:, c:c + 1]).then_inc(s_pf[k].sem, 1)
                    act.wait_ge(s_pf[k].sem, s_pf[k].at(m + 1))
                    act.sem_inc(s_md.sem, 1)

            def decay(n, d, k):
                s, c = k // NC, k % NC
                if k == 0:
                    act.wait_ge(s_dt.sem, s_dt.at(n + 1))
                act.wait_ge(s_h.sem, s_h.at(n, k - 1))
                act.activation(banks[k % 2], dt[:, d, c, :], ACT.Exp, scale=A[:, d, c, s:s + 1]).then_inc(s_dA.sem, 1)

            def work(at, what, g, d):
                if what == "o":
                    output(at, g if d else g - 1, 1 - d)
                elif what in FF:
                    forward(at, g - 1, what)
                else:
                    prep(at, 2 * g + d + 1, 1 - d, what)

            def unit(g, d):
                for k in range(SL):
                    decay(2 * g + d, d, k)
                    for what in side(ACT_AT, g, d, k):
                        work(lambda name: use(g, d, name), what, g, d)

            def turn(i, first=False, last=False):
                for l in range(2):
                    for d in range(2):
                        unit(2 * i + l, d)
            for what in ("xT", "c1", "c0", "z0", "z1", "xd", "move", "dt0", "dt1", "exp", "log"):
                prep(use_first, 0, 0, what)
            schedule(turn)(act)
            for d, names in ((0, ("o", "yT", "m0", "m1")), (1, ("f",))):
                for what in names:
                    work(lambda name: use(NG, d, name), what, NG, d)

        @block.vector
        def _(dve):
            def prep(v, ch, at, n, d, what):
                if what == "u":
                    v.wait_ge(s_cc.sem, s_cc.at(n + 1))
                    v.wait_ge(s_pf[6].sem, s_pf[6].at(at("c1")[1] + 1))
                    v.wait_ge(s_pf[7].sem, s_pf[7].at(at("c0")[1] + 1))
                    v.wait_ge(s_yd.sem, s_yd.at(n - 1))
                    v.scalar_tensor_tensor(u[:, d], tu[:], 1.0, cc[:], ALU.add, ALU.mult).then_inc(s_u.sem, 1)
                if what in ("z0", "z1"):
                    c = int(what[1])
                    k, m = at(what)
                    v.wait_ge(s_tz.sem, s_tz.at(n, c + 1))
                    v.wait_ge(s_yz.sem, s_yz.at(n - 1))
                    v.scalar_tensor_tensor(sz[:, d, c, :], tz[:, c, :], 1.0, banks[k], ALU.add, ALU.mult).then_inc(ch.sem, 1)
                    v.wait_ge(ch.sem, ch.next())
                    v.sem_inc(s_pf[k].sem, 1)
                    v.sem_inc(s_sz.sem, 1)
                if what == "split":
                    v.wait_ge(s_xd.sem, s_xd.at(n + 1))
                    v.wait_ge(s_Csh.sem, s_Csh.at(n))
                    v.wait_ge(s_C.sem, s_C.at(n - 1))
                    c = slice(CROW, CROW + NS)
                    v.tensor_copy(ch_hi[c, :], xd[c, :]).then_inc(s_hi.sem, 1)
                    v.wait_ge(s_hi.sem, s_hi.at(n + 1))
                    v.tensor_tensor(ch_r[c, :], xd[c, :], ch_hi[c, :], ALU.subtract).then_inc(ch.sem, 1)
                    v.wait_ge(ch.sem, ch.next())
                    v.tensor_copy(ch_mid[c, :], ch_r[c, :]).then_inc(s_mid.sem, 1)
                    v.wait_ge(s_mid.sem, s_mid.at(n + 1))
                    v.tensor_tensor(Cs[c, d, :], ch_r[c, :], ch_mid[c, :], ALU.subtract).then_inc(s_Cs.sem, 1)
                if what == "e":
                    v.wait_ge(s_w1.sem, s_w1.at(n + 1))
                    v.scalar_tensor_tensor(cc[:], tu[:], 1.0, cc[:], ALU.subtract, ALU.subtract).then_inc(s_e.sem, 1)
                if what == "dtu":
                    v.wait_ge(s_dr.sem, s_dr.at(n + 1))
                    v.wait_ge(s_dB.sem, s_dB.at(n - 1))
                    v.tensor_tensor(dtu[:, d], dt[:, d], u[:, d], ALU.mult).then_inc(s_dtu.sem, 1)

            def post(v, ch, at, n, g, d, what):
                if what == "y":
                    v.wait_ge(s_yz.sem, s_yz.at(n))
                    for c in range(NC):
                        v.wait_ge(s_ya.sem, s_ya.at(n, SL - 1 + c))
                        v.scalar_tensor_tensor(yd[:, c, :], u[:, d, c, :], Dp[:, d, c:c + 1], banks[4 + c], ALU.mult, ALU.add).then_inc(s_yd.sem, 1)
                if what == "o_stats":
                    k, m = at("o")
                    v.wait_ge(s_pf[k].sem, s_pf[k].at(m + 1))
                    v.wait_ge(s_nrm.sem, s_nrm.at(n))
                    stats(v, ch, 0, lambda b: nrm[:, d, b, :], n)
                if what == "o_norm":
                    v.wait_ge(s_pow[0].sem, s_pow[0].at(n + 1))
                    for b in range(GB):
                        ins = v.tensor_scalar(nrm[:, d, b, :], nrm[:, d, b, :], ost[:, 0, b, 6:7], ovar[:, 0, 1, b:b + 1],
                                              ALU.subtract, ALU.mult)
                    ins.then_inc(s_nrm.sem, 1)

            def stats(v, ch, j, src, n):
                for b in range(GB):
                    ins = v.bn_stats(ost[:, j, b, 0:6], src(b))
                ins.then_inc(ch.sem, 1)
                v.wait_ge(ch.sem, ch.next())
                v.sem_inc(s_step, 1)
                for b in range(GB):
                    ins = v.bn_aggr(ost[:, j, b, 6:8], ost[:, j, b, 0:6])
                ins.then_inc(ch.sem, 1)
                v.wait_ge(ch.sem, ch.next())
                v.wait_ge(s_pow[j].sem, s_pow[j].at(n))
                v.tensor_scalar(ovar[:, j, 0, :], ost[:, j, :, 7], EPS, None, ALU.add).then_inc(s_var[j].sem, 1)

            def forward(v, ch, at, g, l, what, turn):
                if what == "f_stats":
                    k, m = at("f")
                    v.wait_ge(s_pf[k].sem, s_pf[k].at(m + 1))
                    stats(v, ch, 1, lambda b: ff[:, b, :], g)
                if what == "f_norm":
                    v.wait_ge(s_pow[1].sem, s_pow[1].at(g + 1))
                    for b in range(GB):
                        ins = v.tensor_scalar(ff[:, b, :], ff[:, b, :], ost[:, 1, b, 6:7], ovar[:, 1, 1, b:b + 1], ALU.subtract, ALU.mult)
                    ins.then_inc(ch.sem, 1)
                    v.wait_ge(ch.sem, ch.next())
                    v.wait_ge(s_xr[l].sem, s_xr[l].at(turn + 1))
                    for other, op in ((fin[:, 0, :].unsqueeze(1).to_broadcast([P, GB, D]), ALU.mult),
                                      (fin[:, 1, :].unsqueeze(1).to_broadcast([P, GB, D]), ALU.add), (xo[:, l], ALU.add)):
                        v.tensor_tensor(ff[:], ff[:], other, op).then_inc(ch.sem, 1)
                        v.wait_ge(ch.sem, ch.next())
                    stats(v, ch, 2, lambda b: ff[:, b, :], g)
                if what == "f_out":
                    v.wait_ge(s_pow[2].sem, s_pow[2].at(g + 1))
                    for b in range(GB):
                        ins = v.tensor_scalar(xo[:, l, b, :], ff[:, b, :], ost[:, 2, b, 6:7], ovar[:, 2, 1, b:b + 1], ALU.subtract, ALU.mult)
                    ins.then_inc(s_o.sem, 1)

            def scan(v, n, d, k):
                v.wait_ge(s_dA.sem, s_dA.at(n, k + 1))
                v.wait_ge(s_dB.sem, s_dB.at(n, k + 1))
                v.wait_ge(s_hC.sem, s_hC.at(n, k + 1 - RING))
                v.tensor_tensor_scan(h[:, k % RING, :], banks[k % 2], dBu[:, k % RING, :], 0.0, ALU.mult, ALU.add).then_inc(s_h.sem, 1)

            def times_C(v, n, k):
                s = k // NC
                v.wait_ge(s_h.sem, s_h.at(n, k + 1))
                v.wait_ge(s_C.sem, s_C.at(n, s + 1))
                v.wait_ge(s_ya.sem, s_ya.at(n, k + 1 - RING))
                v.tensor_tensor(hC[:, k % RING, :], h[:, k % RING, :], banks[2 + s % 2], ALU.mult).then_inc(s_hC.sem, 1)

            def prologue(v, ch):
                v.wait_ge(s_w.sem, 16 * NW)
                v.wait_ge(s_act, 4)
                v.tensor_scalar(A[:], A[:], A_MIN, -1.0, ALU.max, ALU.mult).then_inc(ch.sem, 1)
                v.wait_ge(ch.sem, ch.next())
                for d in range(2):
                    taps = convw[:, d * CK * DI:(d + 1) * CK * DI].rearrange("p (c k) -> p k c", k=CK)
                    for k in range(CK):
                        ins = v.tensor_tensor(wck[:, d, k, :], win[:, d, 0:DI], taps[:, k, :], ALU.mult)
                ins.then_inc(ch.sem, 1)
                v.wait_ge(ch.sem, ch.next())
                v.sem_inc(s_A.sem, 1)
                for what in ("u", "z0", "z1", "split", "e", "dtu"):
                    prep(v, ch, use_first, 0, 0, what)

            def work(v, ch, at, what, i, g, l, d):
                if what in LAST:
                    post(v, ch, at, 2 * g + d - 1, g if d else g - 1, 1 - d, what)
                elif what[:2] == "f_":
                    forward(v, ch, at, g - 1, 1 - l, what, i if l else i - 1)
                else:
                    prep(v, ch, at, 2 * g + d + 1, 1 - d, what)

            def unit(v, ch, i, g, l, d):
                n = 2 * g + d
                for k in range(SL):
                    scan(v, n, d, k)
                    if k:
                        times_C(v, n, k - 1)
                    elif not (isinstance(g, int) and n == 0):
                        times_C(v, n - 1, SL - 1)
                    for what in side(DVE_AT, g, d, k):
                        work(v, ch, lambda name: use(g, d, name), what, i, g, l, d)

            def turn(v, ch, i):
                for l in range(2):
                    for d in range(2):
                        unit(v, ch, i, 2 * i + l, l, d)

            def tail(v, ch):
                times_C(v, 2 * NG - 1, SL - 1)
                for d, names in ((0, ("y", "o_stats", "o_norm")), (1, ("f_stats", "f_norm", "f_out"))):
                    for what in names:
                        work(v, ch, lambda name: use(NG, d, name), what, TURNS, NG, 0, d)
            of_unit, of_group = 3 + 2, 2 + 4 + 2
            looped(dve, s_dve, TURNS, 4 * of_unit + 2 * of_group, prologue, turn, tail)

        @block.gpsimd
        def _(pool):
            m = 0

            def then(ins):
                nonlocal m
                m += 1
                ins.then_inc(s_pool, 1)
                pool.wait_ge(s_pool, m)
            then(pool.memset(wx[:], 0.0))
            pool.sem_inc(s_set.sem, 1)
            then(pool.memset(one[:], 1.0))
            then(pool.memset(flip[:], 0.0))
            then(pool.affine_select(out=flip[:], in_=flip[:], compare_op=ALU.not_equal, fill=1.0, base=-(P - 1),
                                    pattern=[[1, P]], channel_multiplier=1))
            then(pool.memset(selC[:], 0.0))
            for part in range(3):
                then(pool.affine_select(out=selC[:], in_=selC[:], compare_op=ALU.not_equal, fill=1.0, base=-32 * part,
                                        pattern=[[-1, NS], [0, P]], channel_multiplier=1))
            then(pool.memset(xTp[:, :, 0:PADS], 0.0))
            then(pool.memset(Cs[:], 0.0))
            pool.sem_inc(s_set.sem, 1)

            def prep(n, d, what):
                if what == "dt":
                    pool.wait_ge(s_ln.sem, s_ln.at(n + 1))
                    pool.wait_ge(s_dA.sem, s_dA.at(n - 1))
                    pool.tensor_tensor(tu[:], tu[:], cc[:], ALU.subtract).then_inc(s_d1.sem, 1)
                    pool.wait_ge(s_d1.sem, s_d1.at(n + 1))
                    pool.tensor_tensor(dt[:, d], tu[:], tz[:], ALU.add).then_inc(s_dr.sem, 1)
                if what == "far":
                    pool.wait_ge(s_dtu.sem, s_dtu.at(n + 1))
                    pool.sem_inc(s_step, 1)
                    pool.memset(dt[:, d].rearrange("p c (b t) -> p (c b) t", t=S)[:, :, 0:1], FAR).then_inc(s_dt.sem, 1)

            def gated(n, d):
                pool.wait_ge(s_yd.sem, s_yd.at(n + 1))
                pool.tensor_tensor(yd[:], yd[:], sz[:, d], ALU.mult).then_inc(s_yz.sem, 1)

            def power(j, n):
                pool.wait_ge(s_var[j].sem, s_var[j].at(n + 1))
                pool.tensor_tensor(ovar[:, j, 1, :], ovar[:, j, 0, :], half_pow[:, 0:GB], ALU.pow).then_inc(s_pow[j].sem, 1)

            def inputs(n, g, d, k):
                s, c = k // NC, k % NC
                if k == 0:
                    pool.wait_ge(s_Bb[d].sem, s_Bb[d].at(g + 1))
                    pool.sem_inc(s_step, 1)
                pool.wait_ge(s_h.sem, s_h.at(n, k + 1 - RING))
                pool.tensor_tensor(dBu[:, k % RING, :], dtu[:, d, c, :], Bb[:, d, s, :], ALU.mult).then_inc(s_dB.sem, 1)

            def work(what, g, d):
                n = 2 * g + d
                if what == "gated":
                    gated(n - 1, 1 - d)
                elif what == "o_pow":
                    power(0, n - 1)
                elif what == "f_pow":
                    power(1, g - 1)
                elif what == "out_pow":
                    power(2, g - 1)
                else:
                    prep(n + 1, 1 - d, what)

            def unit(g, d):
                for k in range(SL):
                    inputs(2 * g + d, g, d, k)
                    for what in side(POOL_AT, g, d, k):
                        work(what, g, d)

            def turn(i, first=False, last=False):
                for l in range(2):
                    for d in range(2):
                        unit(2 * i + l, d)
            for what in ("dt", "far"):
                prep(0, 0, what)
            schedule(turn)(pool)
            for d, names in ((0, ("gated", "o_pow")), (1, ("f_pow", "out_pow"))):
                for what in names:
                    work(what, NG, d)

def quantized(nc, const, banks, x, y, a):
    I = 352
    IC = 3
    IL = I - 2 * P
    QMAX = 127.0
    MAGIC = float(1.5 * 2 ** 23)
    TURNS = NG // 2
    LC = 4
    ident, identb, ones_row, half_pow = const["ident"], const["identb"], const["ones_row"], const["half_pow"]
    with ExitStack() as st:
        def sb(name, shape, dt=F32):
            return st.enter_context(nc.sbuf_tensor(f"q_{name}", shape, dt))

        def sem(name, per=1):
            return Count(nc.alloc_semaphore(f"q_{name}"), per)

        xs = sb("x", [P, B, D])
        wgu = sb("wgu", [P, 2 * IC, D])
        wd = sb("wd", [P, I])
        clip = sb("clip", [P, 2])
        wamax = sb("wamax", [P, 2 * IC + 1])
        wscale = sb("wscale", [P, 2 * IC + 1])
        winv = sb("winv", [P, 2 * IC + 1])
        wq = sb("wq", [P, 2 * IC, D], BF16)
        wdq = sb("wdq", [P, I], BF16)
        wT = sb("wT", [P, 2 * IC, P], BF16)
        wdT = sb("wdT", [P, IC, D], BF16)
        sig = sb("sig", [P, 2])
        xmax = sb("xmax", [P, LC])
        hmax = sb("hmax", [P, NG])
        top = sb("top", [P, 2])
        top1 = sb("top1", [1, 2])
        scl = sb("scl", [P, 2])
        inv = sb("inv", [P, 2])
        kt = sb("kt", [P, IC])
        kk = sb("kk", [P, IC])
        magic = sb("magic", [P, 1])
        drow = sb("drow", [1, D])
        dsc = sb("dsc", [P, D])
        xt = sb("xt", [P, GT])
        xqb = sb("xqb", [P, GT], BF16)
        xT = sb("xT", [P, 2, GT], BF16)
        th = sb("th", [P, IC, GT])
        t1 = sb("t1", [P, GT])
        h = sb("h", [P, IC, B * S])
        ht = sb("ht", [P, 2, IC, GT])
        hq = sb("hq", [P, 2, IC, GT], BF16)
        r = sb("r", [P, 2, GB, D])
        ost = sb("ost", [P, GB, 8])
        ovar = sb("ovar", [P, 2, GB])

        s_ld = [sem(f"x_loaded{c}") for c in range(LC)]
        s_w = sem("weights"); s_setup = sem("setup"); s_sig = sem("sigmoid_exp"); s_wq = sem("weights_quantized")
        s_wt = sem("weights_turned", 2); s_wT = sem("weights_copied", 2); s_top = sem("top", 3); s_tt = sem("top_turned", 3)
        s_t1 = sem("top_reduced", 3); s_tb = sem("top_spread", 3); s_k = sem("scales_ready")
        s_xq = sem("x_quantized"); s_xt = sem("x_turned"); s_xT = sem("x_copied")
        s_gu = sem("gate_up", IC); s_th = sem("tanh", IC); s_h = sem("h", IC)
        s_hs = sem("h_shifted"); s_hq = sem("h_quantized"); s_y = sem("down"); s_yr = sem("down_read"); s_ov = sem("out_var"); s_op = sem("out_pow")
        s_o = sem("out_ready"); s_store = [sem(f"stored{l}", 16) for l in range(2)]
        s_dve = nc.alloc_semaphore("q_dve_done"); s_dve2 = nc.alloc_semaphore("q_dve_done2")
        s_pool = nc.alloc_semaphore("q_pool_setup"); s_step = nc.alloc_semaphore("q_passed")
        bankA = banks[0]
        bankAb = bankA.bitcast(BF16)
        bankD = banks[1]
        NW = 7
        x_p = x.rearrange("b t d -> t b d")
        o_g = y.rearrange("(g b) t d -> g t b d", b=GB)
        block = st.enter_context(nc.Block())

        @block.sync
        def _(sp):
            def load_w(dst, src):
                sp.dma_start(dst, src).then_inc(s_w.sem, 16)
            for n, w in enumerate((a["L1_ffn_w_gate"], a["L1_ffn_w_up"])):
                load_w(wgu[:, n * IC:n * IC + 2, :], w[0:2 * P, :].rearrange("(c p) d -> p c d", p=P))
                load_w(wgu[0:IL, n * IC + 2, :], w[2 * P:I, :])
            load_w(wd[:], a["L1_ffn_w_down"])
            for n, t in enumerate((a["L1_ffn_clip_x"], a["L1_ffn_clip_down"])):
                load_w(clip[:, n:n + 1], t.rearrange("(a d) -> a d", a=1).to_broadcast([P, 1]))
            for c in range(LC):
                sp.dma_start(xs[:, c * B // LC:(c + 1) * B // LC, :], x_p[:, c * B // LC:(c + 1) * B // LC, :]).then_inc(s_ld[c].sem, 16)

            def turn(i):
                for l in range(2):
                    g = 2 * i + l
                    sp.wait_ge(s_o.sem, s_o.at(g + 1))
                    sp.sem_inc(s_step, 1)
                    sp.dma_start(o_g[g], r[:, l]).then_inc(s_store[l].sem, 16)
            with sp.Fori(0, TURNS) as i:
                turn(i)
            for l in range(2):
                sp.wait_ge(s_store[l].sem, TURNS * 16)

        @block.tensor
        def _(pe):
            def spread(n):
                pe.wait_ge(s_top.sem, s_top.at(0, n + 1))
                pe.transpose(bankD[0:1, 0:P], top[:, n:n + 1] if n < 2 else wscale[:, 2 * IC:2 * IC + 1], ident[:]).then_inc(s_tt.sem, 1)
                pe.wait_ge(s_t1.sem, s_t1.at(0, n + 1))
                pe.matmul(bankD[:, P:P + (1 if n < 2 else D)], ones_row[:], top1[:, n:n + 1] if n < 2 else drow[:],
                          start=True, stop=True).then_inc(s_tb.sem, 1)

            pe.wait_ge(s_wq.sem, s_wq.at(1))
            for c in range(2 * IC):
                ins = pe.transpose(bankAb[:, c * P:(c + 1) * P], wq[:, c, :], identb[:])
            ins.then_inc(s_wt.sem, 1)
            pe.wait_ge(s_wT.sem, s_wT.at(0, 1))
            for c in range(IC):
                n = P if c < 2 else IL
                ins = pe.transpose(bankAb[0:n, c * P:(c + 1) * P], wdq[:, c * P:c * P + n], identb[:])
            ins.then_inc(s_wt.sem, 1)
            pe.wait_ge(s_wT.sem, s_wT.at(0, 2))
            spread(0)

            def turned(g):
                pe.wait_ge(s_xq.sem, s_xq.at(g + 1))
                pe.wait_ge(s_xT.sem, s_xT.at(g))
                pe.sem_inc(s_step, 1)
                for b in range(GB):
                    ins = pe.transpose(bankAb[:, b * S:(b + 1) * S], xqb[:, b * S:(b + 1) * S], identb[:])
                ins.then_inc(s_xt.sem, 1)

            def gate_up(g, par):
                pe.wait_ge(s_xT.sem, s_xT.at(g + 1))
                for c in range(IC):
                    pe.wait_ge(s_h.sem, s_h.at(g - 1, c + 1))
                    pe.matmul(banks[2 + 2 * c], wT[:, c, :], xT[:, par, :], start=True, stop=True)
                    pe.matmul(banks[3 + 2 * c], wT[:, IC + c, :], xT[:, par, :], start=True, stop=True).then_inc(s_gu.sem, 1)

            def turn(i, last=False):
                for l in range(2):
                    g = 2 * i + l
                    gate_up(g, l)
                    if not (last and l):
                        turned(g + 1)
            turned(0)
            turn(0)
            with pe.Fori(1, TURNS - 1) as i:
                turn(i)
            turn(TURNS - 1, last=True)
            spread(1)
            spread(2)

            def down(g, par):
                pe.wait_ge(s_hq.sem, s_hq.at(g + 1))
                pe.wait_ge(s_yr.sem, s_yr.at(g - 1))
                pe.sem_inc(s_step, 1)
                for b in range(GB):
                    for c in range(IC):
                        n = P if c < 2 else IL
                        ins = pe.matmul(banks[2 + par][:, b * D:(b + 1) * D], hq[0:n, par, c, b * S:(b + 1) * S], wdT[0:n, c, :],
                                        start=(c == 0), stop=(c == IC - 1))
                ins.then_inc(s_y.sem, 1)
            down(0, 0)
            down(1, 1)
            with pe.Fori(1, TURNS) as i:
                for l in range(2):
                    down(2 * i + l, l)

        @block.scalar
        def _(act):
            act.wait_ge(s_w.sem, 16 * NW)
            act.activation(sig[:], clip[:], ACT.Exp, scale=-1.0).then_inc(s_sig.sem, 1)
            act.wait_ge(s_wt.sem, s_wt.at(0, 1))
            act.activation(wT[:].rearrange("p c d -> p (c d)"), bankAb[:, 0:2 * IC * P], ACT.Copy).then_inc(s_wT.sem, 1)
            act.wait_ge(s_wt.sem, s_wt.at(0, 2))
            act.activation(wdT[:, 0:2, :].rearrange("p c d -> p (c d)"), bankAb[:, 0:2 * D], ACT.Copy)
            act.activation(wdT[0:IL, 2, :], bankAb[0:IL, 2 * D:3 * D], ACT.Copy).then_inc(s_wT.sem, 1)
            act.wait_ge(s_k.sem, s_k.at(1))

            def copied(g, par):
                act.wait_ge(s_xt.sem, s_xt.at(g + 1))
                act.wait_ge(s_gu.sem, s_gu.at(g - 1))
                act.activation(xT[:, par, :], bankAb[:, 0:GT], ACT.Copy).then_inc(s_xT.sem, 1)

            def tanh(g):
                for c in range(IC):
                    act.wait_ge(s_gu.sem, s_gu.at(g, c + 1))
                    act.wait_ge(s_h.sem, s_h.at(g - 1, c + 1))
                    act.activation(th[:, c, :], banks[2 + 2 * c], ACT.Tanh, scale=kt[:, c:c + 1]).then_inc(s_th.sem, 1)

            def turn(i, last=False):
                for l in range(2):
                    g = 2 * i + l
                    tanh(g)
                    if not (last and l):
                        copied(g + 1, 1 - l)
            copied(0, 0)
            turn(0)
            with act.Fori(1, TURNS - 1) as i:
                turn(i)
            turn(TURNS - 1, last=True)

            def whole(g, par):
                act.wait_ge(s_hs.sem, s_hs.at(g + 1))
                act.wait_ge(s_y.sem, s_y.at(g - 1))
                act.activation(hq[:, par].rearrange("p c t -> p (c t)"), ht[:, par].rearrange("p c t -> p (c t)"),
                               ACT.Identity, bias=magic[:]).then_inc(s_hq.sem, 1)
            whole(0, 0)
            whole(1, 1)
            with act.Fori(1, TURNS) as i:
                for l in range(2):
                    whole(2 * i + l, l)

        @block.vector
        def _(dve):
            xg = xs[:].rearrange("p (g b) d -> p g (b d)", b=GB)
            hg = h[:].rearrange("p c (g t) -> p g c t", t=GT)

            def whole(v, ch, dst, tmp, src, by):
                v.tensor_scalar(tmp, src, by, QMAX, ALU.mult, ALU.min).then_inc(ch.sem, 1)
                v.wait_ge(ch.sem, ch.next())
                v.tensor_scalar(tmp, tmp, -QMAX - 1.0, MAGIC, ALU.max, ALU.add).then_inc(ch.sem, 1)
                v.wait_ge(ch.sem, ch.next())
                return v.tensor_scalar(dst, tmp, MAGIC, None, ALU.subtract)

            def scale_of(v, ch, n, maxima):
                v.tensor_reduce(top[:, n:n + 1], maxima, AX.X, ALU.max).then_inc(s_top.sem, 1)
                v.wait_ge(s_tt.sem, s_tt.at(0, n + 1))
                v.tensor_reduce(top1[:, n:n + 1], bankD[0:1, 0:P], AX.X, ALU.max).then_inc(s_t1.sem, 1)
                v.wait_ge(s_tb.sem, s_tb.at(0, n + 1))
                v.tensor_scalar(scl[:, n:n + 1], bankD[:, P:P + 1], sig[:, n:n + 1], 1.0 / QMAX, ALU.mult, ALU.mult).then_inc(ch.sem, 1)
                v.wait_ge(ch.sem, ch.next())
                v.reciprocal(inv[:, n:n + 1], scl[:, n:n + 1]).then_inc(ch.sem, 1)
                v.wait_ge(ch.sem, ch.next())

            def quantize_x(v, ch, g):
                v.wait_ge(s_xq.sem, s_xq.at(g))
                v.tensor_scalar(xt[:], xg[:, g, :], inv[:, 0:1], QMAX, ALU.mult, ALU.min).then_inc(ch.sem, 1)
                v.wait_ge(ch.sem, ch.next())
                v.tensor_scalar(xt[:], xt[:], -QMAX - 1.0, MAGIC, ALU.max, ALU.add).then_inc(ch.sem, 1)
                v.wait_ge(ch.sem, ch.next())
                v.wait_ge(s_xt.sem, s_xt.at(g))
                v.tensor_scalar(xqb[:], xt[:], MAGIC, None, ALU.subtract).then_inc(s_xq.sem, 1)

            def prologue(v, ch):
                v.wait_ge(s_w.sem, 16 * NW)
                v.wait_ge(s_setup.sem, s_setup.at(1))
                v.tensor_reduce(wamax[:, 0:2 * IC], wgu[:], AX.X, ALU.max, apply_absolute_value=True)
                v.tensor_reduce(wamax[:, 2 * IC:], wd[:], AX.X, ALU.max, apply_absolute_value=True).then_inc(ch.sem, 1)
                v.wait_ge(ch.sem, ch.next())
                v.tensor_scalar(wscale[:], wamax[:], 1.0 / QMAX, None, ALU.mult).then_inc(ch.sem, 1)
                v.wait_ge(ch.sem, ch.next())
                v.reciprocal(winv[:], wscale[:]).then_inc(ch.sem, 1)
                v.wait_ge(ch.sem, ch.next())
                for c in range(2 * IC):
                    whole(v, ch, wq[:, c, :], wgu[:, c, :], wgu[:, c, :], winv[:, c:c + 1]).then_inc(ch.sem, 1)
                    v.wait_ge(ch.sem, ch.next())
                whole(v, ch, wdq[:], wd[:], wd[:], winv[:, 2 * IC:]).then_inc(ch.sem, 1)
                v.wait_ge(ch.sem, ch.next())
                for n in range(2):
                    ins = v.memset(wq[IL:P, n * IC + 2, :], 0.0)
                ins.then_inc(s_wq.sem, 1)
                v.wait_ge(s_sig.sem, s_sig.at(1))
                v.tensor_scalar(sig[:], sig[:], 1.0, None, ALU.add).then_inc(ch.sem, 1)
                v.wait_ge(ch.sem, ch.next())
                v.reciprocal(sig[:], sig[:]).then_inc(ch.sem, 1)
                v.wait_ge(ch.sem, ch.next())
                for c in range(LC):
                    v.wait_ge(s_ld[c].sem, s_ld[c].at(16))
                    ins = v.tensor_reduce(xmax[:, c:c + 1], xs[:, c * B // LC:(c + 1) * B // LC, :].rearrange("p b d -> p (b d)"),
                                          AX.X, ALU.max, apply_absolute_value=True)
                ins.then_inc(ch.sem, 1)
                v.wait_ge(ch.sem, ch.next())
                scale_of(v, ch, 0, xmax[:])
                v.tensor_scalar(kt[:], wscale[:, 0:IC], scl[:, 0:1], 0.5, ALU.mult, ALU.mult).then_inc(ch.sem, 1)
                v.wait_ge(ch.sem, ch.next())
                v.tensor_scalar(kk[:], wscale[:, IC:2 * IC], scl[:, 0:1], None, ALU.mult).then_inc(ch.sem, 1)
                v.wait_ge(ch.sem, ch.next())
                v.tensor_tensor(kk[:], kk[:], kt[:], ALU.mult).then_inc(s_k.sem, 1)
                v.wait_ge(s_k.sem, s_k.at(1))
                quantize_x(v, ch, 0)

            def turn(v, ch, i):
                last = isinstance(i, int) and i == TURNS - 1
                for l in range(2):
                    g = 2 * i + l
                    if not (last and l):
                        quantize_x(v, ch, g + 1)
                    for c in range(IC):
                        v.wait_ge(s_th.sem, s_th.at(g, c + 1))
                        v.wait_ge(s_h.sem, s_h.at(g, c))
                        v.scalar_tensor_tensor(t1[:], th[:, c, :], 1.0, banks[2 + 2 * c], ALU.add, ALU.mult).then_inc(ch.sem, 1)
                        v.wait_ge(ch.sem, ch.next())
                        v.scalar_tensor_tensor(hg[:, g, c, :], t1[:], kk[:, c:c + 1], banks[3 + 2 * c], ALU.mult, ALU.mult).then_inc(s_h.sem, 1)
                    v.wait_ge(s_h.sem, s_h.at(g + 1))
                    v.tensor_reduce(hmax[:, bass.ds(g, 1)] if not isinstance(g, int) else hmax[:, g:g + 1],
                                    hg[:, g, :, :], AX.XY, ALU.max, apply_absolute_value=True).then_inc(ch.sem, 1)
                    v.wait_ge(ch.sem, ch.next())
            looped(dve, s_dve, TURNS, 2 * (2 + IC + 1), prologue, turn, lambda v, ch: None)

            def prologue2(v, ch):
                scale_of(v, ch, 1, hmax[:])
                v.tensor_copy(dsc[:, 0:1], scl[:, 1:2]).then_inc(s_top.sem, 1)
                v.wait_ge(s_tt.sem, s_tt.at(0, 3))
                v.tensor_copy(drow[:], bankD[0:1, 0:P]).then_inc(s_t1.sem, 1)
                v.wait_ge(s_tb.sem, s_tb.at(0, 3))
                v.tensor_scalar(dsc[:], bankD[:, P:2 * P], scl[:, 1:2], None, ALU.mult).then_inc(ch.sem, 1)
                v.wait_ge(ch.sem, ch.next())
                shift(v, ch, 0, 0)

            def shift(v, ch, g, par):
                v.wait_ge(s_hq.sem, s_hq.at(g - 1))
                v.tensor_scalar(ht[:, par], hg[:, g, :, :], inv[:, 1:2], QMAX, ALU.mult, ALU.min).then_inc(ch.sem, 1)
                v.wait_ge(ch.sem, ch.next())
                v.tensor_scalar(ht[:, par], ht[:, par], -QMAX - 1.0, MAGIC, ALU.max, ALU.add).then_inc(s_hs.sem, 1)

            def turn2(v, ch, i):
                last = isinstance(i, int) and i == TURNS - 1
                for l in range(2):
                    g = 2 * i + l
                    if not (last and l):
                        shift(v, ch, g + 1, 1 - l)
                    v.wait_ge(s_y.sem, s_y.at(g + 1))
                    v.wait_ge(s_store[l].sem, s_store[l].at(i))
                    v.tensor_tensor(r[:, l], banks[2 + l].rearrange("p (b d) -> p b d", b=GB),
                                    dsc[:].unsqueeze(1).to_broadcast([P, GB, D]), ALU.mult).then_inc(s_yr.sem, 1)
                    v.wait_ge(s_yr.sem, s_yr.at(g + 1))
                    v.tensor_tensor(r[:, l].rearrange("p b d -> p (b d)"), r[:, l].rearrange("p b d -> p (b d)"), xg[:, g, :], ALU.add).then_inc(ch.sem, 1)
                    v.wait_ge(ch.sem, ch.next())
                    v.wait_ge(s_o.sem, s_o.at(g))
                    for b in range(GB):
                        ins = v.bn_stats(ost[:, b, 0:6], r[:, l, b, :])
                    ins.then_inc(ch.sem, 1)
                    v.wait_ge(ch.sem, ch.next())
                    v.sem_inc(s_step, 1)
                    for b in range(GB):
                        ins = v.bn_aggr(ost[:, b, 6:8], ost[:, b, 0:6])
                    ins.then_inc(ch.sem, 1)
                    v.wait_ge(ch.sem, ch.next())
                    v.wait_ge(s_op.sem, s_op.at(g))
                    v.tensor_scalar(ovar[:, 0, :], ost[:, :, 7], EPS, None, ALU.add).then_inc(s_ov.sem, 1)
                    v.wait_ge(s_op.sem, s_op.at(g + 1))
                    for b in range(GB):
                        ins = v.tensor_scalar(r[:, l, b, :], r[:, l, b, :], ost[:, b, 6:7], ovar[:, 1, b:b + 1], ALU.subtract, ALU.mult)
                    ins.then_inc(s_o.sem, 1)
            looped(dve, s_dve2, TURNS, 2 * (1 + 3), prologue2, turn2, lambda v, ch: None)

        @block.gpsimd
        def _(pool):
            for n in range(2):
                pool.memset(wgu[IL:P, n * IC + 2, :], 1.0).then_inc(s_pool, 1)
                pool.wait_ge(s_pool, n + 1)
            pool.memset(magic[:], -MAGIC).then_inc(s_pool, 1)
            pool.wait_ge(s_pool, 3)
            pool.sem_inc(s_setup.sem, 1)
            with pool.Fori(0, NG) as g:
                pool.wait_ge(s_ov.sem, s_ov.at(g + 1))
                pool.tensor_tensor(ovar[:, 1, :], ovar[:, 0, :], half_pow[:, 0:GB], ALU.pow).then_inc(s_op.sem, 1)

def constants(nc, st, banks):
    ident = st.enter_context(nc.sbuf_tensor("ident", [P, P], F32))
    identb = st.enter_context(nc.sbuf_tensor("identb", [P, P], BF16))
    ones_row = st.enter_context(nc.sbuf_tensor("ones_row", [1, P], F32))
    sel = st.enter_context(nc.sbuf_tensor("sel", [P, H, P], BF16))
    half_pow = st.enter_context(nc.sbuf_tensor("half_pow", [P, 4 * GB], F32))
    s = nc.alloc_semaphore("constants")
    with nc.Block() as block:
        @block.gpsimd
        def _(pool):
            pool.memset(ident[:], 0.0).then_inc(s, 1)
            pool.memset(identb[:], 0.0).then_inc(s, 1)
            pool.memset(sel[:], 0.0).then_inc(s, 1)
            pool.memset(ones_row[:], 1.0).then_inc(s, 1)
            pool.memset(half_pow[:], -0.5).then_inc(s, 1)
            pool.wait_ge(s, 5)
            pool.affine_select(out=ident[:], in_=ident[:], compare_op=ALU.not_equal, fill=1.0, base=0,
                               pattern=[[-1, P]], channel_multiplier=1).then_inc(s, 1)
            pool.affine_select(out=identb[:], in_=identb[:], compare_op=ALU.not_equal, fill=1.0, base=0,
                               pattern=[[-1, P]], channel_multiplier=1).then_inc(s, 1)
            for part in range(3):
                pool.affine_select(out=sel[:], in_=sel[:], compare_op=ALU.not_equal, fill=1.0, base=-part * H,
                                   pattern=[[-1, H], [0, P]], channel_multiplier=1).then_inc(s, 1)
                pool.wait_ge(s, 8 + part)
    return {"ident": ident, "identb": identb, "ones_row": ones_row, "sel": sel, "half_pow": half_pow}


def build(nc, a, out, stages="MXFNYQ"):
    root8 = float(1.0 / np.sqrt(8.0))

    def of(pre, *names):
        return [a[pre + n] for n in names]

    def mamba_stage(x, y):
        mamba(nc, const, banks, x, y, a)

    def cross0(x, y):
        attention(nc, const, banks, "x0", x, y, *of("L0_xattn_", "wq_k", "wk_k", "wv_k", "wo_k"), root8,
                  *of("L0_xattn_", "wq_b", "wk_b", "wv_b", "wo_b"), ctx=a["ctx_1024"], mask=a["mask_BxSxS2_ik1"],
                  gate=a["fside_BxSxS2_0"])

    def front_attention(x, y):
        attention(nc, const, banks, "f0", x, y, *of("L0_ffn_", "wq", "wk", "wv", "wo"), root8,
                  *of("L0_ffn_", "bq", "bk", "bv", "bo"), ln=of("L0_ffn_", "ln1_g", "ln1_b"), normed=False)

    def attention1(x, y):
        attention(nc, const, banks, "a1", x, y, *of("L1_attn_", "Wq", "Wk", "Wv", "Wo"), DH ** -0.5,
                  rms=of("L1_attn_", "qn_w", "kn_w"))

    def cross1(x, y):
        attention(nc, const, banks, "x1", x, y, *of("L1_xattn_", "wq_w", "wk_w", "wv_w", "wo_w"), root8,
                  *of("L1_xattn_", "wq_b", "wk_b", "wv_b", "wo_b"), ctx=a["ctx_1024"])

    def quantized_stage(x, y):
        quantized(nc, const, banks, x, y, a)

    run = {"M": mamba_stage, "X": cross0, "N": attention1, "Y": cross1, "Q": quantized_stage}
    with ExitStack() as st:
        banks = [st.enter_context(nc.psum_tensor(f"bank{n}", [P, 512], F32))[:] for n in range(8)]
        const = constants(nc, st, banks)
        x = a["x"]
        for n, stage in enumerate(stages):
            y = out if n == len(stages) - 1 else nc.dram_tensor(f"x_stage{n}", (B, S, D), F32, kind="Internal").ap()
            if stage == "F":
                x1 = nc.dram_tensor("x_ffn", (B, S, D), F32, kind="Internal").ap()
                with nc.cleanup_on_exit():
                    front_attention(x, x1)
                with nc.cleanup_on_exit():
                    experts(nc, const, banks, x, x1, y, a)
            else:
                with nc.cleanup_on_exit():
                    run[stage](x, y)
            x = y


TRANSPOSED = ("L1_attn_Wq", "L1_attn_Wk", "L1_attn_Wv", "L1_attn_Wo")
CHANNELS = ("L0_attn_fw_convb", "L0_attn_bw_convb", "L0_attn_fw_bdt", "L0_attn_bw_bdt", "L0_attn_fw_D",
            "L0_attn_bw_D", "L0_attn_ff_b1")
TILED = ("L1_attn_qn_w", "L1_attn_kn_w")


def kernel(**inputs):
    import concourse.bacc as bacc
    from concourse.bass_utils import run_bass_kernel_spmd

    nc = bacc.Bacc("TRN2", target_bir_lowering=False, num_devices=1)
    arrays, a = {}, {}
    for name, value in inputs.items():
        v = np.asarray(value)
        if name in TRANSPOSED:
            v = v.T
        if name in TILED:
            v = np.tile(v, H).reshape(P, 1)
        if name == "L0_ffn_b1":
            v = v.reshape(8, 4, P).transpose(2, 0, 1)
        if name in CHANNELS:
            v = v.reshape(2, P).T
        if name == "L0_ffn_b2":
            v = v.T
        v = np.ascontiguousarray(v)
        arrays["in_" + name] = v
        a[name] = nc.dram_tensor("in_" + name, v.shape, mybir.dt.from_np(v.dtype), kind="ExternalInput").ap()
    out = nc.dram_tensor("out_x", (B, S, D), F32, kind="ExternalOutput").ap()
    build(nc, a, out)
    return run_bass_kernel_spmd(nc, [arrays], core_ids=[0]).results[0]["out_x"]
```

```python
from contextlib import ExitStack

import numpy as np
import concourse.bass as bass
from concourse import mybir

F32 = mybir.dt.float32
BF16 = mybir.dt.bfloat16
I32 = mybir.dt.int32
ALU = mybir.AluOpType
ACT = mybir.ActivationFunctionType
AX = mybir.AxisListType

P = 128
B, S, D = 64, 128, 128
S2 = 77
H, DH = 16, 8
GB = 4
NG = B // GB
GT = GB * S
EPS = 1e-5


class Count:

    def __init__(self, sem, per):
        self.sem, self.per = sem, per

    def at(self, t, j=0):
        v = t * self.per + j
        return max(v, 0) if isinstance(v, int) else v


class Chain:

    def __init__(self, sem):
        self.sem, self.base, self.n = sem, 0, 0

    def start(self, base):
        self.base, self.n = base, 0

    def next(self):
        self.n += 1
        return self.base + self.n


def looped(eng, sem, turns, per, prologue, body, tail):
    chain = Chain(sem)
    prologue(eng, chain)
    base = chain.n
    chain.start(base)
    body(eng, chain, 0)
    base += chain.n
    with eng.Fori(1, turns - 1) as i:
        chain.start((i - 1) * per + base)
        body(eng, chain, i)
    assert chain.n == per, chain.n
    base += (turns - 2) * per
    chain.start(base)
    body(eng, chain, turns - 1)
    chain.start(base + chain.n)
    tail(eng, chain)

def attention(nc, const, banks, tag, x_in, x_out, wq, wk, wv, wo, scale, bq=None, bk=None, bv=None, bo=None,
              ctx=None, mask=None, gate=None, ln=None, rms=None, normed=True):
    sk = S if ctx is None else S2
    kt = GB * sk
    PARTS, ROWS = 3, 6 * DH
    K_TIMES = (3, 2, 1)
    VC = DH + (gate is None)
    VW = 8 * VC
    TURNS = NG // 2
    TAIL = 6
    ident, identb, ones_row, sel = const["ident"], const["identb"], const["ones_row"], const["sel"]
    half_pow = const["half_pow"]
    norm_at = (0, 1)
    if rms:
        slot = {"x": 0, "qt": 1, "kt": 2, "v": 3, "qn": 5, "kn": 6}
        later = {"v": 0, "high": 0, "middle": 1, "squares": 0, "root": 0, "norm": 1}
    elif ln is not None:
        slot, later = {"x": 3, "q": 4, "k": 5, "v": 7}, {"v": 6, "high": 1, "middle": 2}
    elif gate is not None:
        slot, later = {"x": 2, "c": 5, "q": 4, "k": 6, "v": 7}, {"v": 5, "high": 1, "middle": 2}
    else:
        slot, later = {"x": 2, "c": 5, "q": 4, "k": 6, "v": 7}, {"v": 3, "high": 1, "middle": 3}
    out_at = 3 if ctx is None else 2
    uses = sorted(slot, key=lambda u: slot[u])
    NU = len(uses)
    nu = {u: n for n, u in enumerate(uses)}
    Q, K = ("qn", "kn") if rms else ("q", "k")
    part_slot = (slot[Q], slot[K])
    LOADS = 1 + (ctx is not None) + (mask is not None)

    with ExitStack() as st:
        def sb(name, shape, dt=F32):
            return st.enter_context(nc.sbuf_tensor(f"{tag}_{name}", shape, dt))

        def sem(name, per=1):
            return Count(nc.alloc_semaphore(f"{tag}_{name}"), per)

        dram_q = nc.dram_tensor(f"{tag}_q_parts", (2, PARTS, P, GT), BF16, kind="Internal").ap()
        dram_k = nc.dram_tensor(f"{tag}_k_parts", (2, sum(K_TIMES), P, kt), BF16, kind="Internal").ap()

        w = sb("w", [P, 4, D])
        bqk = sb("bqk", [P, 2])
        bvb = sb("bvb", [P, D])
        bor = sb("bor", [1, D])
        lnw = sb("lnw", [P, 2, D])
        xp = sb("xp", [P, 2, GB, D])
        xr = sb("xr", [P, 2, GB, D])
        cx = sb("cx", [P, GB, D]) if ctx is not None else None
        mi = sb("mi", [P, GB, S2], I32) if mask is not None else None
        neg = sb("neg", [P, 2, GB, S2]) if mask is not None else None
        gp = sb("gp", [P, 2, GB, S2]) if gate is not None else None
        xn = sb("xn", [P, GB, D]) if ln is not None else None
        xT = sb("xT", [P, GT])
        cT = sb("cT", [P, kt]) if ctx is not None else xT
        qf = sb("qf", [P, 2, GT])
        qr = sb("qr", [P, 2, GT])
        qp = sb("qp", [P, 2, PARTS, GT], BF16)
        qtok = sb("qtok", [P, 2, GB, D]) if rms else None
        sq = sb("sq", [P, 2, GB * D]) if rms else None
        ms = sb("ms", [P, 3, 2, GB * H]) if rms else None
        eps = sb("eps", [P, 1]) if rms else None
        Qs = sb("Qs", [P, 2, H, GT], BF16)
        Ks = sb("Ks", [P, 2, H, kt], BF16)
        vS = sb("vS", [P, 2, GB, D])
        vB = sb("vB", [P, 2, 2, 8 * (VW + VC)])
        sm = sb("sm", [P, 2, H, S2]) if mask is not None else None
        den = sb("den", [P, 8, H]) if gate is not None else None
        nm = sb("nm", [P, 2, 3, H])
        nmp = sb("nmp", [P, 2, PARTS, H], BF16)
        nmT = sb("nmT", [P, 2, S], BF16)
        pT = sb("pT", [P, 2, H, S])
        ou = sb("ou", [VW, 2, S])
        rden = sb("rden", [P, H])
        on = sb("on", [P, D])
        oT = sb("oT", [P, S])
        r = sb("r", [P, 2, D])
        stat = sb("stat", [P, 2, 8])
        var = sb("var", [P, 2, 2])
        lst = sb("lst", [P, GB, 8]) if ln is not None else None
        lvar = sb("lvar", [P, 2, GB]) if ln is not None else None

        s_w = sem("weights"); s_setup = sem("setup"); s_zero = sem("zeroed"); s_xp = sem("x_loaded"); s_xr = [sem(f"residual_loaded{l}", 16) for l in range(2)]
        s_xpfree = sem("x_used"); s_pb = sem("proj_written", NU); s_pf = sem("proj_evacuated", NU)
        s_hi = sem("hi_ready", 2); s_r1 = sem("rest1_ready", 2)
        s_mid = sem("mid_ready", 2); s_lo = sem("lo_ready", 2)
        s_ps = sem("parts_stored", 16 * (PARTS + 1)); s_stk = sem("stack_loaded", 16 * (PARTS + 1))
        s_ln = sem("front_var", 1); s_lp = sem("front_pow", 1); s_xn = sem("front_norm", 1)
        s_neg = sem("neg_ready"); s_sq = sem("squares", 2); s_ms = sem("sums_of_squares", 2); s_rt = sem("roots"); s_qn = sem("qk_normed", 2)
        s_S = sem("scores", 4); s_Sf = sem("scores_used", 4); s_nmp = sem("max_parts"); s_T = sem("max_transposed")
        s_nmT = sem("max_rows"); s_st = sem("shifted", 4); s_e = sem("exp", 4)
        s_gp = [sem(f"gate_loaded{l}", 16) for l in range(2)]; s_tw = sem("weights_turned", 4); s_ev = sem("weights_copied", 4)
        s_mx = sem("row_maxima", 4) if mask is not None else None
        s_pg = sem("gated", 4); s_vb = sem("values_spread"); s_pv = sem("pv", 4); s_ou = sem("pv_evacuated")
        s_ot = sem("out_turned"); s_on = sem("out_normed"); s_o2 = sem("out_turned_back"); s_oT = sem("oT")
        s_y = sem("y"); s_r = sem("residual"); s_v = sem("var"); s_pw = sem("pow"); s_xo = sem("x_done") if normed else s_r
        s_store = sem("stored"); s_bq = sem("q_bias_scaled"); s_dve = nc.alloc_semaphore(f"{tag}_dve_done")
        s_pool = nc.alloc_semaphore(f"{tag}_pool_chain")
        s_step = nc.alloc_semaphore(f"{tag}_passed")
        s_use = s_st if gate is None else s_S
        bankS, bankT, bankO, bankP, bankM, bankY = banks[0:2], banks[2:4], banks[4], banks[5], banks[6], banks[7]
        bankMb = bankM.bitcast(BF16)
        NZ = 2 + (gate is None) + (sk < P)
        NW = sum(1 for t in (bq, bk, bv, bo) if t is not None) + 4 + (2 if ln is not None else 0) + (2 if rms else 0)

        block = st.enter_context(nc.Block())
        x_g = x_in.rearrange("(g b) t d -> g t b d", b=GB)
        o_g = x_out.rearrange("(g b) t d -> g t b d", b=GB)

        def diagonal(t):
            return t.rearrange("p (h c) -> p h c", c=VW + VC)

        def heads(t):
            return t.rearrange("p (h d) -> p h d", h=H)

        @block.sync
        def _(sp):
            n = 0
            def load_w(dst, src):
                sp.dma_start(dst, src).then_inc(s_w.sem, 16)
            for j, t in enumerate((wq, wk, wv, wo)):
                load_w(w[:, j, :], t)
            for j, t in enumerate((bq, bk)):
                if t is not None:
                    load_w(bqk[:, j:j + 1], t.rearrange("(d a) -> d a", a=1))
            if rms:
                for j, t in enumerate(rms):
                    load_w(bqk[:, j:j + 1], t)
            if bv is not None:
                load_w(bvb[:], bv.rearrange("(a d) -> a d", a=1).to_broadcast([P, D]))
            if bo is not None:
                load_w(bor[:], bo.rearrange("(a d) -> a d", a=1))
            if ln is not None:
                for j, t in enumerate(ln):
                    load_w(lnw[:, j, :], t.rearrange("(a d) -> a d", a=1).to_broadcast([P, D]))

            def load_x(g, par):
                sp.wait_ge(s_xpfree.sem, s_xpfree.at(g))
                sp.sem_inc(s_step, 1)
                sp.dma_start(xp[:, par], x_g[g]).then_inc(s_xp.sem, 16)
                if ctx is not None:
                    sp.dma_start(cx[0:S2], ctx.rearrange("(g b) t d -> g t b d", b=GB)[g]).then_inc(s_xp.sem, 16)
                if mask is not None:
                    sp.dma_start(mi[:], mask.rearrange("(g b) t d -> g t b d", b=GB)[g]).then_inc(s_xp.sem, 16)

            def load_gate(g, par):
                if gate is not None:
                    sp.wait_ge(s_pg.sem, s_pg.at((g - 1) * GB))
                    sp.sem_inc(s_step, 1)
                    sp.dma_start(gp[:, par], gate.rearrange("(g b) t d -> g t b d", b=GB)[g]).then_inc(s_gp[par].sem, 16)

            def stack(g, par):
                def save(dst, src):
                    sp.dma_start(dst.rearrange("a p t -> p a t"), src).then_inc(s_ps.sem, 16)

                def fill(stack_rows, parts):
                    sp.dma_start(stack_rows.rearrange("p h t -> p (h t)"),
                                 parts.rearrange("a (d h) t -> (a d) (h t)", d=DH)).then_inc(s_stk.sem, 16)
                sp.wait_ge(s_lo.sem, s_lo.at(g, 1))
                save(dram_q[par], qp[:, 0])
                sp.wait_ge(s_lo.sem, s_lo.at(g, 2))
                at = 0
                for part, times in enumerate(K_TIMES):
                    save(dram_k[par, at:at + times], qp[:, 1, part:part + 1, 0:kt].to_broadcast([P, times, kt]))
                    at += times
                sp.wait_ge(s_ps.sem, s_ps.at(g + 1))
                sp.wait_ge(s_use.sem, s_use.at((g - 1) * GB))
                at = 0
                for parts in K_TIMES:
                    fill(Qs[at * DH:(at + parts) * DH, par], dram_q[par, 0:parts])
                    at += parts
                fill(Ks[0:ROWS, par], dram_k[par])

            def residual(g, par):
                sp.wait_ge(s_store.sem, s_store.at((g - 1) * 16))
                sp.sem_inc(s_step, 1)
                sp.dma_start(xr[:, par], x_g[g]).then_inc(s_xr[par].sem, 16)

            def store(g, par):
                sp.wait_ge(s_xo.sem, s_xo.at((g + 1) * GB))
                sp.sem_inc(s_step, 1)
                sp.dma_start(o_g[g], xr[:, par]).then_inc(s_store.sem, 16)

            def turn(i, first=False, last=False):
                for l in range(2):
                    g = 2 * i + l
                    if not first:
                        store(g - 2, l)
                    residual(g, l)
                    if not (last and l):
                        stack(g + 1, 1 - l)
                        load_gate(g + 1, 1 - l)
                    if not last:
                        load_x(g + 2, l)
            load_x(0, 0)
            sp.wait_ge(s_zero.sem, NZ)
            stack(0, 0)
            load_gate(0, 0)
            load_x(1, 1)
            turn(0, first=True)
            with sp.Fori(1, TURNS - 1) as i:
                turn(i)
            turn(TURNS - 1, last=True)
            for l in range(2):
                store(NG - 2 + l, l)
            sp.wait_ge(s_store.sem, NG * 16)

        @block.tensor
        def _(pe):
            pe.wait_ge(s_w.sem, 16 * NW)

            def use(g, u):
                pe.wait_ge(s_pf.sem, s_pf.at(g, nu[u]))

            def done(ins):
                ins.then_inc(s_pb.sem, 1)

            def prep(u, g, par):
                use(g, u)
                if u == "x":
                    if ln is not None:
                        pe.wait_ge(s_xn.sem, s_xn.at(g + 1))
                    else:
                        pe.wait_ge(s_xp.sem, (g + 1) * 16 * LOADS)
                    for b in range(GB):
                        src = xn[:, b, :] if ln is not None else xp[:, par, b, :]
                        ins = pe.transpose(bankP[:, b * S:(b + 1) * S], src, ident[:])
                if u == "c":
                    for b in range(GB):
                        ins = pe.transpose(bankP[:, b * S2:(b + 1) * S2], cx[0:S2, b, :], ident[0:S2, 0:S2])
                if u == "q":
                    ins = pe.matmul(bankP[:], w[:, 0, :], xT[:], start=True, stop=True)
                if u == "k":
                    ins = pe.matmul(bankP[:, 0:kt], w[:, 1, :], cT[:], start=True, stop=True)
                if u in ("qt", "kt"):
                    for b in range(GB):
                        ins = pe.matmul(bankP[:, b * S:(b + 1) * S], xT[:, b * S:(b + 1) * S], w[:, 0 if u == "qt" else 1, :],
                                        start=True, stop=True)
                if u in ("qn", "kn"):
                    t = 0 if u == "qn" else 1
                    pe.wait_ge(s_qn.sem, s_qn.at(g, t + 1))
                    for b in range(GB):
                        ins = pe.transpose(bankP[:, b * S:(b + 1) * S], qtok[:, t, b, :], ident[:])
                if u == "v":
                    for b in range(GB):
                        ins = pe.matmul(bankP[0:sk, b * D:(b + 1) * D], cT[:, b * sk:(b + 1) * sk], w[:, 2, :],
                                        start=True, stop=True)
                done(ins)

            def scores(i, lb, c):
                b, l, q = 8 * i + lb, lb // GB, lb % GB
                if c == 0 and q == 0:
                    pe.wait_ge(s_stk.sem, s_stk.at(2 * i + l + 1))
                pe.wait_ge(s_Sf.sem, s_Sf.at(b, c + 1 - 2))
                for h in range(4):
                    hh = 4 * c + h
                    ins = pe.matmul(bankS[c % 2][:, h * sk:(h + 1) * sk], Qs[:, l, hh, q * S:(q + 1) * S],
                                    Ks[:, l, hh, q * sk:(q + 1) * sk], start=True, stop=True)
                ins.then_inc(s_S.sem, 1)

            def turn_max(b, lb):
                pe.wait_ge(s_nmp.sem, s_nmp.at(b + 1))
                pe.wait_ge(s_r.sem, s_r.at(b - 3))
                pe.sem_inc(s_step, 1)
                pe.transpose(bankMb[0:PARTS * H, 0:S], nmp[:, lb % 2].rearrange("p a h -> p (a h)"),
                             identb[:]).then_inc(s_T.sem, 1)

            def shifted(b, lb, c):
                l, q = lb // GB, lb % GB
                pe.wait_ge(s_nmT.sem, s_nmT.at(b + 1))
                pe.wait_ge(s_e.sem, s_e.at(b, c + 1 - 2))
                for h in range(4):
                    hh = 4 * c + h
                    o = bankT[c % 2][0:sk, h * S:(h + 1) * S]
                    pe.matmul(o, Ks[:, l, hh, q * sk:(q + 1) * sk], Qs[:, l, hh, q * S:(q + 1) * S],
                              start=True, stop=False)
                    ins = pe.matmul(o, sel[:, hh, 0:sk], nmT[:, lb % 2, :], start=False, stop=True)
                ins.then_inc(s_st.sem, 1)

            def turn_weights(b, lb, c):
                pe.wait_ge(s_pg.sem, s_pg.at(b, c + 1))
                pe.wait_ge(s_ev.sem, s_ev.at(b, c + 1 - 2))
                for h in range(4):
                    ins = pe.transpose(bankT[c % 2][0:sk, h * S:(h + 1) * S], sm[:, lb % 2, 4 * c + h, :], ident[:])
                ins.then_inc(s_tw.sem, 1)

            def values(b, lb, c):
                if c == 0:
                    pe.wait_ge(s_ou.sem, s_ou.at(b))
                    pe.wait_ge(s_vb.sem, s_vb.at(b + 1))
                if gate is not None:
                    pe.wait_ge(s_ev.sem, s_ev.at(b, c + 1))
                else:
                    pe.wait_ge(s_e.sem, s_e.at(b, c + 1))
                half = c // 2
                o = bankO[0:VW, half * S:(half + 1) * S]
                for hh in range(4 * c, 4 * c + 4):
                    h = hh % 8
                    ins = pe.matmul(o, vB[:, lb % 2, half, h * VW:(h + 1) * VW], pT[:, lb % 2, hh, :], start=(h == 0),
                                    stop=(h == 7))
                ins.then_inc(s_pv.sem, 1)

            def turn_out(b):
                pe.wait_ge(s_ou.sem, s_ou.at(b + 1))
                pe.wait_ge(s_oT.sem, s_oT.at(b))
                pe.sem_inc(s_step, 1)
                for half in range(2):
                    ins = pe.transpose(bankY[:, half * VW:(half + 1) * VW], ou[:, half, :], ident[0:VW, 0:VW])
                ins.then_inc(s_ot.sem, 1)

            def turn_back(b):
                pe.wait_ge(s_on.sem, s_on.at(b + 1))
                pe.transpose(bankY[:, 0:S], on[:], ident[:]).then_inc(s_o2.sem, 1)

            def out(b):
                pe.wait_ge(s_oT.sem, s_oT.at(b + 1))
                pe.wait_ge(s_r.sem, s_r.at(b))
                if gate is None:
                    pe.wait_ge(s_nmT.sem, s_nmT.at(min(b + 4, B) if isinstance(b, int) else b + 4))
                ins = pe.matmul(bankM[:, 0:D], oT[:], w[:, 3, :], start=True, stop=(bo is None))
                if bo is not None:
                    ins = pe.matmul(bankM[:, 0:D], ones_row[:], bor[:], start=False, stop=True)
                ins.then_inc(s_y.sem, 1)

            def step(i, lb, c, live):
                b = 8 * i + lb
                if live(0):
                    scores(i, lb, c)
                if gate is not None:
                    if live(1):
                        turn_weights(b - 1, (lb - 1) % 8, c)
                elif c == 0:
                    if live(2):
                        shifted(b - 2, (lb - 2) % 8, 3)
                    if live(1):
                        turn_max(b - 1, (lb - 1) % 8)
                elif live(1):
                    shifted(b - 1, (lb - 1) % 8, c - 1)
                if live(2):
                    values(b - 2, (lb - 2) % 8, c)
                if c == 1 and live(3):
                    turn_out(b - 3)
                if c == out_at and live(4):
                    out(b - 4)
                if c == 3 and live(3):
                    turn_back(b - 3)

            def slots(i, lb, c, last):
                l, z = lb // GB, 4 * (lb % GB) + c
                for u in uses:
                    if z == slot[u] and not (last and l):
                        prep(u, 2 * i + l + 1, 1 - l)

            def turn(i, first=False, last=False):
                for lb in range(8):
                    for c in range(4):
                        step(i, lb, c, lambda k: not (first and lb < k))
                        slots(i, lb, c, last)
            for u in uses:
                prep(u, 0, 0)
            pe.wait_ge(s_zero.sem, NZ)
            turn(0, first=True)
            with pe.Fori(1, TURNS - 1) as i:
                turn(i)
            turn(TURNS - 1, last=True)
            for k in range(TAIL):
                for c in range(4):
                    step(TURNS, k, c, lambda n: k < n)

        @block.scalar
        def _(act):
            act.wait_ge(s_w.sem, 16 * NW)
            if rms or bq is not None:
                act.activation(bqk[:, 0:1], bqk[:, 0:1], ACT.Copy, scale=scale).then_inc(s_bq.sem, 1)
                act.wait_ge(s_bq.sem, 1)

            def evac(g, u, dst, src, **k):
                act.wait_ge(s_pb.sem, s_pb.at(g, nu[u] + 1))
                act.activation(dst, src, ACT.Identity, **k).then_inc(s_pf.sem, 1)

            def prep(u, g, par):
                if u == "x":
                    evac(g, "x", xT[:], bankP[:])
                if u == "c":
                    evac(g, "c", cT[:], bankP[:, 0:kt])
                if u in ("qt", "kt"):
                    t = 0 if u == "qt" else 1
                    act.wait_ge(s_pb.sem, s_pb.at(g, nu[u] + 1))
                    act.wait_ge(s_ms.sem, s_ms.at(g - 1, t + 1))
                    act.activation(sq[:, t, :], bankP[:], ACT.Square).then_inc(s_sq.sem, 1)
                    act.wait_ge(s_pf.sem, s_pf.at(g - 1, nu["qn" if t == 0 else "kn"] + 1))
                    evac(g, u, qtok[:, t].rearrange("p b d -> p (b d)"), bankP[:])
                if u in ("q", "k", "qn", "kn"):
                    t = 0 if u[0] == "q" else 1
                    n, bias = ((GT, bq), (kt, bk))[t]
                    act.wait_ge(s_lo.sem, s_lo.at(g - 1, t + 1))
                    k = {"scale": scale} if t == 0 else {}
                    if rms:
                        k = {"scale": bqk[:, t:t + 1]}
                    elif bias is not None:
                        k["bias"] = bqk[:, t:t + 1]
                    evac(g, u, qf[:, t, 0:n], bankP[:, 0:n], **k)

            def root(g):
                act.wait_ge(s_ms.sem, s_ms.at(g + 1))
                act.wait_ge(s_qn.sem, s_qn.at(g))
                act.activation(ms[:, 1], ms[:, 0], ACT.Sqrt, scale=1.0 / DH, bias=eps[:]).then_inc(s_rt.sem, 1)

            def exp(b, lm, c):
                p = lm % 2
                act.wait_ge(s_pv.sem, s_pv.at(b - 2, c + 1))
                act.wait_ge(s_st.sem, s_st.at(b, c + 1))
                src = bankT[c % 2][0:sk, :]
                act.activation(pT[0:sk, p, 4 * c:4 * c + 4, :].rearrange("p h t -> p (h t)"), src, ACT.Exp).then_inc(s_e.sem, 1)

            def exp_rows(b, lm, c):
                act.wait_ge(s_mx.sem, s_mx.at(b, c + 1))
                act.sem_inc(s_step, 1)
                for h in range(4 * c, 4 * c + 4):
                    ins = act.activation(sm[:, lm % 2, h, :], sm[:, lm % 2, h, :], ACT.Exp, bias=nm[:, lm % 2, 0, h:h + 1],
                                         accum_out=den[:, lm, h:h + 1])
                ins.then_inc(s_e.sem, 1)

            def step(i, lb, c, live):
                b = 8 * i + lb
                if c == 0 and live(3):
                    act.wait_ge(s_pv.sem, s_pv.at(b - 3 + 1))
                    act.wait_ge(s_ot.sem, s_ot.at(b - 3))
                    act.activation(ou[:].rearrange("p a t -> p (a t)"), bankO[0:VW, 0:2 * S], ACT.Copy).then_inc(s_ou.sem, 1)
                if gate is not None:
                    if c == 0 and live(1):
                        exp_rows(b - 1, (lb - 1) % 8, 3)
                    if c > 0 and live(0):
                        exp_rows(b, lb, c - 1)
                else:
                    if c == 0 and live(2):
                        exp(b - 2, (lb - 2) % 8, 3)
                    if c > 0 and live(1):
                        exp(b - 1, (lb - 1) % 8, c - 1)
                if c == 0 and live(4):
                    act.wait_ge(s_o2.sem, s_o2.at(b - 4 + 1))
                    act.wait_ge(s_y.sem, s_y.at(b - 4))
                    act.activation(oT[:], bankY[:, 0:S], ACT.Copy).then_inc(s_oT.sem, 1)

            def slots(i, lb, c, last):
                l, z = lb // GB, 4 * (lb % GB) + c
                if last and l:
                    return
                for u in uses:
                    if u != "v" and z == slot[u]:
                        prep(u, 2 * i + l + 1, 1 - l)
                if rms and z == slot["v"] + later["root"]:
                    root(2 * i + l + 1)

            def turn(i, first=False, last=False):
                for lb in range(8):
                    for c in range(4):
                        step(i, lb, c, lambda k: not (first and lb < k))
                        slots(i, lb, c, last)
            for u in uses:
                if rms and u == "qn":
                    root(0)
                if u != "v":
                    prep(u, 0, 0)
            turn(0, first=True)
            with act.Fori(1, TURNS - 1) as i:
                turn(i)
            turn(TURNS - 1, last=True)
            for k in range(TAIL):
                for c in range(4):
                    step(TURNS, k, c, lambda n: k < n)

        @block.vector
        def _(dve):
            dve.memset(Ks[:], 0.0).then_inc(s_zero.sem, 1)
            if gate is None:
                dve.memset(nmT[:], 0.0).then_inc(s_zero.sem, 1)
            if sk < P:
                dve.memset(pT[:], 0.0).then_inc(s_zero.sem, 1)
            dve.wait_ge(s_w.sem, 16 * NW)
            dve.wait_ge(s_setup.sem, 1)

            def front_stats(v, ch, g, par):
                v.wait_ge(s_xp.sem, (g + 1) * 16 * LOADS)
                v.wait_ge(s_xn.sem, s_xn.at(g))
                for b in range(GB):
                    ins = v.bn_stats(lst[:, b, 0:6], xp[:, par, b, :])
                ins.then_inc(ch.sem, 1)
                v.wait_ge(ch.sem, ch.next())
                v.sem_inc(s_step, 1)
                for b in range(GB):
                    ins = v.bn_aggr(lst[:, b, 6:8], lst[:, b, 0:6])
                ins.then_inc(ch.sem, 1)
                v.wait_ge(ch.sem, ch.next())
                v.wait_ge(s_lp.sem, s_lp.at(g))
                v.tensor_scalar(lvar[:, 0, :], lst[:, :, 7], EPS, None, ALU.add).then_inc(s_ln.sem, 1)

            def front_norm(v, ch, g, par):
                v.wait_ge(s_lp.sem, s_lp.at(g + 1))
                v.wait_ge(s_pf.sem, s_pf.at(g - 1, nu["x"] + 1))
                for b in range(GB):
                    ins = v.tensor_scalar(xn[:, b, :], xp[:, par, b, :], lst[:, b, 6:7], lvar[:, 1, b:b + 1],
                                          ALU.subtract, ALU.mult)
                ins.then_inc(ch.sem, 1)
                v.wait_ge(ch.sem, ch.next())
                v.tensor_tensor(xn[:], xn[:], lnw[:, 0, :].unsqueeze(1).to_broadcast([P, GB, D]), ALU.mult).then_inc(ch.sem, 1)
                v.wait_ge(ch.sem, ch.next())
                v.sem_inc(s_xpfree.sem, 1)
                v.tensor_tensor(xn[:], xn[:], lnw[:, 1, :].unsqueeze(1).to_broadcast([P, GB, D]), ALU.add).then_inc(s_xn.sem, 1)

            def masks(v, ch, g, par):
                v.wait_ge(s_xp.sem, (g + 1) * 16 * LOADS)
                v.wait_ge(s_Sf.sem, s_Sf.at((g - 1) * GB))
                v.tensor_scalar(neg[:, par], mi[:], 1.0, 1e9, ALU.subtract, ALU.mult).then_inc(s_neg.sem, 1)

            def squares(v, ch, g, t):
                v.wait_ge(s_sq.sem, s_sq.at(g, t + 1))
                v.wait_ge(s_rt.sem, s_rt.at(g))
                v.tensor_reduce(ms[:, 0, t, :].rearrange("p (b h) -> p b h", h=H),
                                sq[:, t, :].rearrange("p (b d h) -> p b h d", d=DH, h=H), AX.X, ALU.add).then_inc(s_ms.sem, 1)

            def rms_norm(v, ch, g):
                v.wait_ge(s_rt.sem, s_rt.at(g + 1))
                v.reciprocal(ms[:, 2], ms[:, 1]).then_inc(ch.sem, 1)
                v.wait_ge(ch.sem, ch.next())
                for t in range(2):
                    v.wait_ge(s_pf.sem, s_pf.at(g, nu["qt" if t == 0 else "kt"] + 1))
                    q4 = qtok[:, t].rearrange("p b (d h) -> p b d h", d=DH)
                    v.tensor_tensor(q4, q4, ms[:, 2, t, :].rearrange("p (b h) -> p b h", h=H).unsqueeze(2).to_broadcast([P, GB, DH, H]), ALU.mult).then_inc(s_qn.sem, 1)

            def high(v, ch, g, t):
                n = (GT, kt)[t]
                v.wait_ge(s_ps.sem, s_ps.at(g))
                v.wait_ge(s_pf.sem, s_pf.at(g, nu[(Q, K)[t]] + 1))
                v.tensor_copy(qp[:, t, 0, 0:n], qf[:, t, 0:n]).then_inc(s_hi.sem, 1)

            def middle(v, ch, g, t):
                n = (GT, kt)[t]
                v.wait_ge(s_r1.sem, s_r1.at(g, t + 1))
                v.tensor_copy(qp[:, t, 1, 0:n], qr[:, t, 0:n]).then_inc(s_mid.sem, 1)

            def value_rows(v, ch, g, par):
                v.wait_ge(s_pb.sem, s_pb.at(g, nu["v"] + 1))
                v.wait_ge(s_vb.sem, s_vb.at((g - 1) * GB))
                src = bankP[0:sk, :].rearrange("p (b d) -> p b d", b=GB)
                if bv is not None:
                    ins = v.tensor_tensor(vS[0:sk, par], src, bvb[0:sk, :].unsqueeze(1).to_broadcast([sk, GB, D]), ALU.add)
                else:
                    ins = v.tensor_copy(vS[0:sk, par], src)
                ins.then_inc(s_pf.sem, 1)

            work = [(slot["v"] + later["v"], value_rows), (part_slot[0] + later["high"], lambda v, ch, g, par: high(v, ch, g, 0)),
                    (part_slot[1] + later["high"], lambda v, ch, g, par: high(v, ch, g, 1)),
                    (part_slot[0] + later["middle"], lambda v, ch, g, par: middle(v, ch, g, 0)),
                    (part_slot[1] + later["middle"], lambda v, ch, g, par: middle(v, ch, g, 1))]
            if ln is not None:
                work += [(norm_at[0], front_stats), (norm_at[1], front_norm)]
            if mask is not None:
                work += [(1, masks)]
            if rms:
                work += [(slot["qt"] + later["squares"], lambda v, ch, g, par: squares(v, ch, g, 0)),
                         (slot["kt"] + later["squares"], lambda v, ch, g, par: squares(v, ch, g, 1)),
                         (slot["v"] + later["norm"], lambda v, ch, g, par: rms_norm(v, ch, g))]
            work.sort(key=lambda z: z[0])

            def maximum(v, ch, b, lb, c):
                l, q, p = lb // GB, lb % GB, lb % 2
                v.wait_ge(s_S.sem, s_S.at(b, c + 1))
                if c == 0 and gate is None:
                    v.wait_ge(s_T.sem, s_T.at(b - 1))
                src = bankS[c % 2][:, 0:4 * sk].rearrange("p (h k) -> p h k", h=4)
                if mask is not None:
                    hs = slice(4 * c, 4 * c + 4)
                    if c == 0:
                        v.wait_ge(s_tw.sem, s_tw.at(b - 1))
                    v.tensor_tensor(sm[:, p, hs, :], src, neg[:, l, q, :].unsqueeze(1).to_broadcast([P, 4, S2]),
                                    ALU.add).then_inc(s_Sf.sem, 1)
                    v.wait_ge(s_Sf.sem, s_Sf.at(b, c + 1))
                    v.tensor_reduce(nm[:, p, 0, hs], sm[:, p, hs, :], AX.X, ALU.max, negate=True).then_inc(s_mx.sem, 1)
                else:
                    v.tensor_reduce(nm[:, p, 0, 4 * c:4 * c + 4], src, AX.X, ALU.max, negate=True).then_inc(s_Sf.sem, 1)

            def split_maxima(v, ch, b, lb):
                p = lb % 2
                v.wait_ge(s_Sf.sem, s_Sf.at(b, 4))
                v.tensor_copy(nmp[:, p, 0, :], nm[:, p, 0, :]).then_inc(ch.sem, 1)
                v.wait_ge(ch.sem, ch.next())
                v.tensor_tensor(nm[:, p, 1, :], nm[:, p, 0, :], nmp[:, p, 0, :], ALU.subtract).then_inc(ch.sem, 1)
                v.wait_ge(ch.sem, ch.next())
                v.tensor_copy(nmp[:, p, 1, :], nm[:, p, 1, :]).then_inc(ch.sem, 1)
                v.wait_ge(ch.sem, ch.next())
                v.tensor_tensor(nmp[:, p, 2, :], nm[:, p, 1, :], nmp[:, p, 1, :], ALU.subtract).then_inc(s_nmp.sem, 1)

            def maxima_rows(v, ch, b, lm):
                v.wait_ge(s_T.sem, s_T.at(b + 1))
                v.wait_ge(s_st.sem, s_st.at(b - 1))
                v.tensor_copy(nmT[0:PARTS * H, lm % 2, :], bankMb[0:PARTS * H, 0:S]).then_inc(s_nmT.sem, 1)

            def weights_copied(v, ch, b, lm, c):
                v.wait_ge(s_tw.sem, s_tw.at(b, c + 1))
                v.wait_ge(s_pv.sem, s_pv.at(b - 2, c + 1))
                v.tensor_copy(pT[0:sk, lm % 2, 4 * c:4 * c + 4, :].rearrange("p h t -> p (h t)"), bankT[c % 2][0:sk, :]).then_inc(s_ev.sem, 1)

            def weighted(v, ch, b, lm):
                v.wait_ge(s_ot.sem, s_ot.at(b + 1))
                v.wait_ge(s_o2.sem, s_o2.at(b))
                o = bankY[:, 0:2 * VW].rearrange("p (h c) -> p h c", c=VC)
                if gate is not None:
                    v.wait_ge(s_e.sem, s_e.at(b + 1))
                v.reciprocal(rden[:], o[:, :, DH] if gate is None else den[:, lm, :]).then_inc(ch.sem, 1)
                v.wait_ge(ch.sem, ch.next())
                v.tensor_tensor(heads(on[:]), o[:, :, 0:DH], rden[:].unsqueeze(2).to_broadcast([P, H, DH]),
                                ALU.mult).then_inc(s_on.sem, 1)

            def add_residual(v, ch, b, lm, loaded):
                v.wait_ge(s_y.sem, s_y.at(b + 1))
                if lm % GB == 0:
                    v.wait_ge(s_xr[lm // GB].sem, loaded)
                xrow = xr[:, lm // GB, lm % GB, :]
                if not normed:
                    v.tensor_tensor(xrow, bankM[:, 0:D], xrow, ALU.add).then_inc(s_r.sem, 1)
                    return
                rr = r[:, lm % 2, :]
                v.wait_ge(s_xo.sem, s_xo.at(b - 1))
                v.tensor_tensor(rr, bankM[:, 0:D], xrow, ALU.add).then_inc(s_r.sem, 1)
                v.wait_ge(s_r.sem, s_r.at(b + 1))
                v.bn_stats(stat[:, lm % 2, 0:6], rr).then_inc(ch.sem, 1)
                v.wait_ge(ch.sem, ch.next())
                v.sem_inc(s_step, 1)
                v.bn_aggr(stat[:, lm % 2, 6:8], stat[:, lm % 2, 0:6]).then_inc(ch.sem, 1)
                v.wait_ge(ch.sem, ch.next())
                v.tensor_scalar(var[:, lm % 2, 0:1], stat[:, lm % 2, 7:8], EPS, None, ALU.add).then_inc(s_v.sem, 1)

            def norm(v, ch, b, lm):
                v.wait_ge(s_pw.sem, s_pw.at(b + 1))
                v.tensor_scalar(xr[:, lm // GB, lm % GB, :], r[:, lm % 2, :], stat[:, lm % 2, 6:7], var[:, lm % 2, 1:2],
                                ALU.subtract, ALU.mult).then_inc(s_xo.sem, 1)

            def step(v, ch, i, lb, c, live):
                b = 8 * i + lb
                if live(0):
                    maximum(v, ch, b, lb, c)
                    if c == 3 and gate is None:
                        split_maxima(v, ch, b, lb)
                if c == 0 and live(1) and gate is None:
                    maxima_rows(v, ch, b - 1, (lb - 1) % 8)
                if gate is not None:
                    if c == 0 and live(2):
                        weights_copied(v, ch, b - 2, (lb - 2) % 8, 3)
                    if c > 0 and live(1):
                        weights_copied(v, ch, b - 1, (lb - 1) % 8, c - 1)
                if c == 1 and normed and live(5):
                    norm(v, ch, b - 5, (lb - 5) % 8)
                if c == 2 and live(3):
                    weighted(v, ch, b - 3, (lb - 3) % 8)
                if c == 3 and live(4):
                    add_residual(v, ch, b - 4, (lb - 4) % 8, (i + (lb - 4) // 8 + 1) * 16)

            def prologue(v, ch):
                for z, f in work:
                    f(v, ch, 0, 0)

            def turn(v, ch, i):
                first, last = isinstance(i, int) and i == 0, isinstance(i, int) and i == TURNS - 1
                for lb in range(8):
                    for c in range(4):
                        step(v, ch, i, lb, c, lambda k: not (first and lb < k))
                        l = lb // GB
                        for z, f in work:
                            if z == 4 * (lb % GB) + c and not (last and l):
                                f(v, ch, 2 * i + l + 1, 1 - l)

            def tail(v, ch):
                for k in range(TAIL):
                    for c in range(4):
                        step(v, ch, TURNS, k, c, lambda n: k < n)
            of_seq = (4 if gate is None else 1) + (2 if normed else 0)
            of_group = (4 if ln is not None else 0) + (1 if rms else 0)
            looped(dve, s_dve, TURNS, 8 * of_seq + 2 * of_group, prologue, turn, tail)

        @block.gpsimd
        def _(pool):
            ins = pool.memset(vB[:], 0.0)
            ins.then_inc(s_pool, 1)
            pool.wait_ge(s_pool, 1)
            n = 1
            if gate is None:
                for p in range(2):
                    for h2 in range(2):
                        pool.memset(diagonal(vB[:, p, h2, :])[:, :, DH:VC], 1.0).then_inc(s_pool, 1)
                        n += 1
            if rms:
                pool.wait_ge(s_pool, n)
                pool.memset(eps[:], float(np.finfo(np.float32).eps)).then_inc(s_pool, 1)
                n += 1
            pool.wait_ge(s_pool, n)
            pool.nop().then_inc(s_setup.sem, 1)
            pool.memset(Qs[:], 0.0).then_inc(s_zero.sem, 1)

            def front(g):
                if ln is not None:
                    pool.wait_ge(s_ln.sem, s_ln.at(g + 1))
                    pool.wait_ge(s_xn.sem, s_xn.at(g))
                    pool.tensor_tensor(lvar[:, 1, :], lvar[:, 0, :], half_pow[:, 0:GB], ALU.pow).then_inc(s_lp.sem, 1)
                else:
                    pool.wait_ge(s_pb.sem, s_pb.at(g, nu[turned] + 1))
                    if mask is not None:
                        pool.wait_ge(s_neg.sem, s_neg.at(g + 1))
                    pool.sem_inc(s_xpfree.sem, 1)

            def rest1(g, t):
                n = (GT, kt)[t]
                pool.wait_ge(s_hi.sem, s_hi.at(g, t + 1))
                pool.wait_ge(s_lo.sem, s_lo.at(g - 1, t + 1))
                pool.tensor_tensor(qr[:, t, 0:n], qf[:, t, 0:n], qp[:, t, 0, 0:n], ALU.subtract).then_inc(s_r1.sem, 1)

            def low(g, t):
                n = (GT, kt)[t]
                pool.wait_ge(s_mid.sem, s_mid.at(g, t + 1))
                pool.wait_ge(s_ps.sem, s_ps.at(g))
                pool.wait_ge(s_r1.sem, s_r1.at(g, t + 1))
                pool.tensor_tensor(qp[:, t, 2, 0:n], qr[:, t, 0:n], qp[:, t, 1, 0:n], ALU.subtract).then_inc(s_lo.sem, 1)

            turned = "c" if ctx is not None else "x"
            work = [(norm_at[0] + 1 if ln is not None else slot[turned] + 1, front),
                    (part_slot[0] + later["high"], lambda g: rest1(g, 0)), (part_slot[1] + later["high"], lambda g: rest1(g, 1)),
                    (part_slot[0] + later["middle"], lambda g: low(g, 0)), (part_slot[1] + later["middle"], lambda g: low(g, 1))]
            work.sort(key=lambda z: z[0])

            def spread(i, b, lm):
                l, q, p = lm // GB, lm % GB, lm % 2
                if q == 0:
                    g = 2 * i + l
                    pool.wait_ge(s_pf.sem, s_pf.at(g, nu["v"] + 1))
                pool.wait_ge(s_pv.sem, s_pv.at(b - 1))
                pool.sem_inc(s_step, 1)
                src = vS[0:sk, l, q, :].rearrange("p (a h d) -> p a h d", a=2, h=8)
                for h2 in range(2):
                    ins = pool.tensor_copy(diagonal(vB[0:sk, p, h2, :])[:, :, 0:DH], src[:, h2])
                ins.then_inc(s_vb.sem, 1)

            def gated(b, lm, c, loaded):
                pool.wait_ge(s_e.sem, s_e.at(b, c + 1))
                if c == 0 and lm % GB == 0:
                    pool.wait_ge(s_gp[lm // GB].sem, loaded)
                ws = sm[:, lm % 2, 4 * c:4 * c + 4, :]
                pool.tensor_tensor(ws, ws, gp[:, lm // GB, lm % GB, :].unsqueeze(1).to_broadcast([P, 4, S2]), ALU.mult).then_inc(s_pg.sem, 1)

            def step(i, lb, c, live):
                b = 8 * i + lb
                if gate is not None:
                    if c < 2 and live(1):
                        gated(b - 1, (lb - 1) % 8, c + 2, None)
                    if c >= 2 and live(0):
                        gated(b, lb, c - 2, (i + 1) * 16)
                if c == 1 and live(1):
                    spread(i if lb else i - 1, b - 1, (lb - 1) % 8)
                if c == 0 and normed and live(5):
                    lm = (lb - 5) % 8
                    pool.wait_ge(s_v.sem, s_v.at(b - 5 + 1))
                    pool.wait_ge(s_xo.sem, s_xo.at(b - 5 - 1))
                    pool.tensor_tensor(var[:, lm % 2, 1:2], var[:, lm % 2, 0:1], half_pow[:, 0:1], ALU.pow).then_inc(s_pw.sem, 1)

            def turn(i, first=False, last=False):
                for lb in range(8):
                    for c in range(4):
                        step(i, lb, c, lambda k: not (first and lb < k))
                        l = lb // GB
                        for z, f in work:
                            if z == 4 * (lb % GB) + c and not (last and l):
                                f(2 * i + l + 1)
            for z, f in work:
                f(0)
            turn(0, first=True)
            with pool.Fori(1, TURNS - 1) as i:
                turn(i)
            turn(TURNS - 1, last=True)
            for k in range(TAIL):
                for c in range(4):
                    step(TURNS, k, c, lambda n: k < n)

def experts(nc, const, banks, x, x1, y, a):
    E, F = 8, 512
    FT = F // P
    TURNS = NG // 2
    LOADS = 4
    TILES = B * S // P
    SORTED = TILES + E
    QUADS = SORTED // GB
    QTURNS = QUADS // 2
    DN = D + 1
    ident, half_pow = const["ident"], const["half_pow"]
    g_, b_, gw, gb, w1, b1, w2, b2 = [a["L0_ffn_" + n] for n in
                                      ("ln2_g", "ln2_b", "gate_w", "gate_b", "w1", "b1", "w2", "b2")]
    with ExitStack() as st:
        def sb(name, shape, dt=F32):
            return st.enter_context(nc.sbuf_tensor(f"moe_{name}", shape, dt))

        def sem(name, per=1):
            return Count(nc.alloc_semaphore(f"moe_{name}"), per)

        rows_in = nc.dram_tensor("moe_rows_in", (SORTED * P, DN), F32, kind="Internal").ap()
        results = nc.dram_tensor("moe_results", (B * S + SORTED * P, D), F32, kind="Internal").ap()

        w1s = sb("w1", [P, E, F])
        w2s = sb("w2", [P, E, FT, D])
        b1s = sb("b1", [P, E, FT])
        b2s = sb("b2", [P, E, D])
        gws = sb("gw", [P, E])
        gbs = sb("gb", [P, E])
        lnw = sb("lnw", [P, 2])
        rank = sb("rank", [P, E])
        below = sb("below", [P, P], BF16)
        ones = sb("ones", [P, P], BF16)
        zero = sb("zero", [P, SORTED * DN // GB])
        full = sb("full", [P, TILES])
        number = sb("number", [P, SORTED])
        go_on = sb("go_on", [P, E, TILES])
        x1s = sb("x1", [P, NG, GB, D])
        xs = sb("xs", [P, NG, GB, D])
        st_ = sb("stats", [P, 2, GB, 8])
        nv = sb("norm", [P, 2, 2, GB])
        scl = sb("scales", [P, NG, 2, GB])
        hT = sb("hT", [P, 2, GT])
        lg = sb("lg", [P, TILES, E])
        lmax = sb("lmax", [P, 2, TILES])
        one = sb("one", [P, E, NG, GB], BF16)
        upto = sb("upto", [P, E, TILES])
        place = sb("place", [P, E, TILES])
        used = sb("used", [P, 4, E])
        row = sb("row", [P, NG, GB])
        of = sb("of", [1, SORTED, E])
        ofs = sb("ofs", [1, 2, SORTED])
        tile_e = sb("tile_e", [1, QUADS, GB], I32)
        ix = sb("ix", [P, 2, GB], I32)
        token = sb("token", [P, NG, GB])
        spare = sb("spare", [P, QUADS, GB])
        empty = sb("empty", [P, GB])
        ixo = sb("ixo", [P, 2, GB], I32)
        hs = sb("hs", [P, 2, GB, DN])
        w1e = sb("w1_tile", [P, 2, F])
        w2e = sb("w2_tile", [P, GB, FT, D])
        mid = sb("mid", [P, 2, FT, P])
        ye = sb("ye", [P, 2, GB, D])

        s_wf = sem("front_weights"); s_w = sem("weights"); s_set = sem("setup"); s_pool = sem("pool_setup")
        s_x1 = [sem(f"x1_loaded{l}", 16) for l in range(2)]; s_x = [sem(f"x_loaded{l}", 16) for l in range(2)]
        s_zero = sem("rows_zeroed")
        s_bn = sem("front_stats"); s_ag = sem("front_mean"); s_var = sem("front_var"); s_pw = sem("front_pow")
        s_pow = sem("front_scales"); s_add = sem("x_added"); s_hn = sem("front_normed"); s_tp = sem("front_turned")
        s_hT = sem("front_copied"); s_lg = sem("logits"); s_ch = sem("choice")
        s_cnt = sem("counted"); s_rt = sem("route"); s_route = sem("routed")
        s_ix = sem("rows_to_scatter"); s_hs = sem("normed_to_scatter"); s_sc = [sem(f"scattered{l}", 16 * GB) for l in range(2)]
        s_lq = [sem(f"rows_loaded{l}", 16) for l in range(2)]; s_tq = sem("rows_turned"); s_hq = sem("rows_copied")
        s_w1 = sem("w1_copied"); s_w2 = sem("w2_copied"); s_mid = sem("mid"); s_rl = sem("relu"); s_y = sem("expert_out"); s_ye = sem("expert_biased")
        s_em = sem("empty_rows"); s_to = sem("places"); s_sy = [sem(f"results_scattered{l}", 16 * GB) for l in range(2)]
        s_co = [sem(f"results_loaded{k}", 16) for k in range(LOADS)]
        s_fin = [sem(f"sum{l}") for l in range(2)]; s_fbn = sem("out_stats"); s_fag = sem("out_mean"); s_fvar = sem("out_var")
        s_fpw = sem("out_pow"); s_fpow = sem("out_scales"); s_o = sem("out_normed"); s_store = sem("stored")
        s_step = nc.alloc_semaphore("moe_passed")
        NW, NWF = 4 + E, 4
        x_g, x1_g, o_g = [t.rearrange("(g b) t d -> g t b d", b=GB) for t in (x, x1, y)]
        in_q = rows_in.rearrange("(q b p) d -> q p b d", b=GB, p=P)
        results_g = results[0:B * S].rearrange("(g b t) d -> g t b d", b=GB, t=S)
        all_logits = banks[2].rearrange("p (g b e) -> p g b e", g=NG, b=GB)
        block = st.enter_context(nc.Block())

        def flat(t):
            return t.rearrange("p b d -> p (b d)")

        def all_experts(t):
            return t.rearrange("p e t -> p t e")

        @block.sync
        def _(sp):
            def load_w(dst, src):
                sp.dma_start(dst, src).then_inc(s_w.sem, 16)

            def load(i, l):
                g = 2 * i + l
                sp.wait_ge(s_x1[l].sem, s_x1[l].at(i))
                sp.sem_inc(s_step, 1)
                sp.dma_start(x1s[:, g], x1_g[g]).then_inc(s_x1[l].sem, 16)
                sp.wait_ge(s_x[l].sem, s_x[l].at(i))
                sp.sem_inc(s_step, 1)
                sp.dma_start(xs[:, g], x_g[g]).then_inc(s_x[l].sem, 16)

            for l in range(2):
                load(0, l)
            sp.dma_start(gws[:], gw).then_inc(s_wf.sem, 16)
            sp.dma_start(gbs[:], gb.rearrange("(a e) -> a e", a=1).to_broadcast([P, E])).then_inc(s_wf.sem, 16)
            for n, t in enumerate((g_, b_)):
                sp.dma_start(lnw[:, n:n + 1], t.rearrange("(d a) -> d a", a=1)).then_inc(s_wf.sem, 16)
            with sp.Fori(1, TURNS) as i:
                for l in range(2):
                    load(i, l)
            sp.wait_ge(s_set.sem, 1)
            in_z = rows_in.rearrange("(z p n) d -> z p (n d)", z=GB, p=P)
            for z in range(GB):
                sp.dma_start(in_z[z], zero[:]).then_inc(s_zero.sem, 16)
            load_w(b1s[:], b1)
            load_w(b2s[:].rearrange("p e d -> p (e d)"), b2.rearrange("e d -> (e d)").rearrange("(a n) -> a n", a=1).to_broadcast([P, E * D]))
            for e in range(E):
                load_w(w1s[:, e, :], w1[e])
            for h in range(2):
                load_w(w2s[:, h * E // 2:(h + 1) * E // 2], w2[h * E // 2:(h + 1) * E // 2].rearrange("e (c f) d -> f e c d", f=P))
            def load_rows(q, l):
                sp.wait_ge(s_tq.sem, s_tq.at(q - 1))
                sp.sem_inc(s_step, 1)
                sp.wait_ge(s_to.sem, s_to.at(q - 1))
                sp.sem_inc(s_step, 1)
                sp.dma_start(hs[:, l], in_q[q]).then_inc(s_lq[l].sem, 16)

            for l in range(2):
                sp.wait_ge(s_sc[l].sem, s_sc[l].at(TURNS))
            for l in range(2):
                load_rows(l, l)
            with sp.Fori(0, QTURNS - 1) as i:
                for l in range(2):
                    load_rows(2 * i + l + 2, l)

            for l in range(2):
                sp.wait_ge(s_sy[l].sem, s_sy[l].at(QTURNS))
            sp.wait_ge(s_add.sem, NG)
            with sp.Fori(0, NG // LOADS) as i:
                for k in range(LOADS):
                    sp.wait_ge(s_co[k].sem, s_co[k].at(i))
                    sp.sem_inc(s_step, 1)
                    sp.dma_start(x1s[:, LOADS * i + k], results_g[LOADS * i + k]).then_inc(s_co[k].sem, 16)
            with sp.Fori(0, NG) as g:
                sp.wait_ge(s_o.sem, s_o.at(g + 1))
                sp.sem_inc(s_step, 1)
                sp.dma_start(o_g[g], xs[:, g]).then_inc(s_store.sem, 16)
            sp.wait_ge(s_store.sem, NG * 16)

        @block.tensor
        def _(pe):
            pe.wait_ge(s_set.sem, 1)
            pe.wait_ge(s_wf.sem, 16 * NWF)

            def front(g, l):
                pe.wait_ge(s_hn.sem, s_hn.at(g + 1))
                pe.sem_inc(s_step, 1)
                pe.wait_ge(s_hT.sem, s_hT.at(g - 1))
                pe.sem_inc(s_step, 1)
                for b in range(GB):
                    ins = pe.transpose(banks[l][:, b * S:(b + 1) * S], hs[:, l, b, 0:D], ident[:])
                ins.then_inc(s_tp.sem, 1)

            def logits(g, l):
                pe.wait_ge(s_hT.sem, s_hT.at(g + 1))
                pe.sem_inc(s_step, 1)
                for b in range(GB):
                    ins = pe.matmul(all_logits[:, g, b, :], hT[:, l, b * S:(b + 1) * S], gws[:], start=True, stop=True)
                ins.then_inc(s_lg.sem, 1)

            front(0, 0)
            front(1, 1)
            logits(0, 0)

            def turn_front(i):
                for l in range(2):
                    front(2 * i + l, l)
                    logits(2 * i + l - 1, 1 - l)
            turn_front(1)
            with pe.Fori(2, TURNS) as i:
                turn_front(i)
            logits(NG - 1, 1)

            pe.wait_ge(s_ch.sem, 6)
            chosen = one[:].rearrange("p e g b -> p (e g b)")
            pe.matmul(banks[6], below[:], chosen, start=True, stop=True)
            pe.matmul(banks[7], ones[:], chosen, start=True, stop=True).then_inc(s_cnt.sem, 1)

            def turn_rows(i, l):
                q = 2 * i + l
                pe.wait_ge(s_lq[l].sem, s_lq[l].at(i + 1))
                pe.sem_inc(s_step, 1)
                pe.wait_ge(s_hq.sem, s_hq.at(q - 1))
                pe.sem_inc(s_step, 1)
                for b in range(GB):
                    ins = pe.transpose(banks[l][:, b * P:(b + 1) * P], hs[:, l, b, 0:D], ident[:])
                ins.then_inc(s_tq.sem, 1)

            def mids(q, l, j):
                n = GB * q + j
                if j == 0:
                    pe.wait_ge(s_hq.sem, s_hq.at(q + 1))
                    pe.sem_inc(s_step, 1)
                pe.wait_ge(s_rl.sem, s_rl.at(n - 1))
                pe.sem_inc(s_step, 1)
                pe.wait_ge(s_w1.sem, s_w1.at(n + 1))
                pe.sem_inc(s_step, 1)
                for f in range(FT):
                    ins = pe.matmul(banks[2 + j % 2][:, f * P:(f + 1) * P], w1e[:, j % 2, f * P:(f + 1) * P],
                                    hT[:, l, j * P:(j + 1) * P], start=True, stop=True)
                ins.then_inc(s_mid.sem, 1)

            def out(q, j):
                n = GB * q + j
                pe.wait_ge(s_rl.sem, s_rl.at(n + 1))
                pe.sem_inc(s_step, 1)
                pe.wait_ge(s_ye.sem, s_ye.at(n - 1))
                pe.sem_inc(s_step, 1)
                pe.wait_ge(s_w2.sem, s_w2.at(n + 1))
                pe.sem_inc(s_step, 1)
                for f in range(FT):
                    ins = pe.matmul(banks[4 + j % 2][:, 0:D], mid[:, j % 2, f, :], w2e[:, j, f, :], start=(f == 0), stop=(f == FT - 1))
                ins.then_inc(s_y.sem, 1)

            def turn(i, last=False):
                for l in range(2):
                    q = 2 * i + l
                    for j in range(GB):
                        if j + 1 < GB:
                            mids(q, l, j + 1)
                        elif not (last and l):
                            mids(q + 1, 1 - l, 0)
                        out(q, j)
                        if j == 1 and not (last and l):
                            turn_rows(i + l, 1 - l)

            turn_rows(0, 0)
            mids(0, 0, 0)
            turn(0)
            with pe.Fori(1, QTURNS - 1) as i:
                turn(i)
            turn(QTURNS - 1, last=True)

        @block.scalar
        def _(act):
            def normed(dst, src, g):
                for b in range(GB):
                    ins = act.activation(dst[:, b, 0:D], src[:, b, :], ACT.Identity, scale=scl[:, g, 0, b:b + 1], bias=scl[:, g, 1, b:b + 1])
                return ins

            def front(g, l):
                act.wait_ge(s_pow.sem, s_pow.at(g + 1))
                act.sem_inc(s_step, 1)
                act.wait_ge(s_tp.sem, s_tp.at(g - 1))
                act.sem_inc(s_step, 1)
                normed(hs[:, l], x1s[:, g], g).then_inc(s_hn.sem, 1)

            def to_scatter(i, l):
                act.wait_ge(s_sc[l].sem, s_sc[l].at(i))
                act.sem_inc(s_step, 1)
                normed(hs[:, l], x1s[:, 2 * i + l], 2 * i + l).then_inc(s_hs.sem, 1)

            def finish(g):
                act.wait_ge(s_fpow.sem, s_fpow.at(g + 1))
                act.sem_inc(s_step, 1)
                normed(xs[:, g], xs[:, g], g).then_inc(s_o.sem, 1)

            def copied(g, l):
                act.wait_ge(s_tp.sem, s_tp.at(g + 1))
                act.sem_inc(s_step, 1)
                act.wait_ge(s_lg.sem, s_lg.at(g - 1))
                act.activation(hT[:, l, :], banks[l], ACT.Identity, scale=lnw[:, 0:1], bias=lnw[:, 1:2]).then_inc(s_hT.sem, 1)

            def relu(q, j):
                n = GB * q + j
                e = act.value_load(tile_e[0:1, q, j:j + 1], min_val=0, max_val=E - 1)
                act.wait_ge(s_mid.sem, s_mid.at(n + 1))
                act.sem_inc(s_step, 1)
                act.wait_ge(s_y.sem, s_y.at(n - 1))
                act.sem_inc(s_step, 1)
                for f in range(FT):
                    ins = act.activation(mid[:, j % 2, f, :], banks[2 + j % 2][:, f * P:(f + 1) * P], ACT.Relu, bias=b1s[:, e, f:f + 1])
                ins.then_inc(s_rl.sem, 1)

            def w2_copied(q, j):
                n = GB * q + j
                e = act.value_load(tile_e[0:1, q, j:j + 1], min_val=0, max_val=E - 1)
                act.wait_ge(s_y.sem, s_y.at(n - GB + 1))
                act.sem_inc(s_step, 1)
                act.activation(w2e[:, j].rearrange("p c d -> p (c d)"), w2s[:, e].rearrange("p c d -> p (c d)"), ACT.Copy).then_inc(s_w2.sem, 1)

            act.wait_ge(s_wf.sem, 16 * NWF)
            front(0, 0)
            front(1, 1)
            copied(0, 0)
            with act.Fori(1, TURNS) as i:
                for l in range(2):
                    front(2 * i + l, l)
                    copied(2 * i + l - 1, 1 - l)
            copied(NG - 1, 1)
            with act.Fori(0, TURNS) as i:
                for l in range(2):
                    to_scatter(i, l)
            act.wait_ge(s_w.sem, 16 * NW)
            act.wait_ge(s_route.sem, 1)
            w2_copied(0, 0)
            w2_copied(0, 1)

            def quad(q, last=False):
                for j in range(GB):
                    relu(q, j)
                    if not (last and j >= 2):
                        w2_copied(q + j // 2, (j + 2) % GB)
            quad(0)
            with act.Fori(1, QUADS - 1) as q:
                quad(q)
            quad(QUADS - 1, last=True)
            with act.Fori(0, NG) as g:
                finish(g)

        @block.vector
        def _(dve):
            def stats(s_mean, s_out, s_used, s_first, t, g, l):
                for b in range(GB):
                    ins = dve.bn_stats(st_[:, l, b, 0:6], t[:, g, b, :])
                ins.then_inc(s_first.sem, 1)
                dve.wait_ge(s_first.sem, s_first.at(g + 1))
                dve.sem_inc(s_step, 1)
                for b in range(GB):
                    ins = dve.bn_aggr(st_[:, l, b, 6:8], st_[:, l, b, 0:6])
                ins.then_inc(s_mean.sem, 1)
                dve.wait_ge(s_mean.sem, s_mean.at(g + 1))
                dve.sem_inc(s_step, 1)
                dve.wait_ge(s_used.sem, s_used.at(g - 1))
                dve.sem_inc(s_step, 1)
                dve.tensor_scalar(nv[:, l, 1, :], st_[:, l, :, 6], -1.0, None, ALU.mult)
                dve.tensor_scalar(nv[:, l, 0, :], st_[:, l, :, 7], EPS, None, ALU.add).then_inc(s_out.sem, 1)

            def front(i, l):
                dve.wait_ge(s_x1[l].sem, s_x1[l].at(i + 1))
                dve.sem_inc(s_step, 1)
                stats(s_ag, s_var, s_pow, s_bn, x1s, 2 * i + l, l)

            def choose():
                n = 0

                def then(ins):
                    nonlocal n
                    n += 1
                    ins.then_inc(s_ch.sem, 1)
                    dve.wait_ge(s_ch.sem, n)
                every = lambda t: t.unsqueeze(1).to_broadcast([P, TILES, E])
                each = lambda t: t.unsqueeze(2).to_broadcast([P, TILES, E])
                dve.wait_ge(s_lg.sem, NG)
                then(dve.tensor_tensor(lg[:], banks[2].rearrange("p (t e) -> p t e", e=E), every(gbs[:]), ALU.add))
                then(dve.tensor_reduce(lmax[:, 0, :], lg[:], AX.X, ALU.max))
                then(dve.tensor_tensor(lg[:], lg[:], each(lmax[:, 0, :]), ALU.is_equal))
                then(dve.tensor_tensor(lg[:], lg[:], every(rank[:]), ALU.mult))
                then(dve.tensor_reduce(lmax[:, 1, :], lg[:], AX.X, ALU.max))
                then(dve.tensor_tensor(one[:].rearrange("p e g b -> p (g b) e"), lg[:], each(lmax[:, 1, :]), ALU.is_equal))

            def route():
                n = 0

                def then(ins):
                    nonlocal n
                    n += 1
                    ins.then_inc(s_rt.sem, 1)
                    dve.wait_ge(s_rt.sem, n)
                each = lambda t: t.rearrange("p e t -> p (e t)")
                chosen = one[:].rearrange("p e g b -> p (e g b)")
                dve.wait_ge(s_cnt.sem, 1)
                then(dve.tensor_tensor_scan(each(upto[:]), each(go_on[:]), banks[7], 0.0, ALU.mult, ALU.add))
                count = upto[:, :, TILES - 1:TILES].to_broadcast([P, E, TILES])
                then(dve.tensor_tensor(place[:], count, full[:].unsqueeze(1).to_broadcast([P, E, TILES]), ALU.is_gt))
                then(dve.tensor_reduce(used[:, 0, :], place[:], AX.X, ALU.add))
                then(dve.tensor_tensor_scan(used[:, 1, :], ones[:, 0:E], used[:, 0, :], 0.0, ALU.mult, ALU.add))
                then(dve.tensor_tensor(used[:, 2, :], used[:, 1, :], used[:, 0, :], ALU.subtract))
                then(dve.tensor_scalar(used[:, 3, :], used[:, 2, :], float(P), None, ALU.mult))
                then(dve.tensor_tensor(each(place[:]), each(upto[:]), banks[7], ALU.subtract))
                then(dve.tensor_tensor(each(place[:]), each(place[:]), banks[6], ALU.add))
                then(dve.tensor_tensor(place[:], place[:], used[:, 3, :].unsqueeze(2).to_broadcast([P, E, TILES]), ALU.add))
                then(dve.tensor_tensor(each(place[:]), each(place[:]), chosen, ALU.mult))
                then(dve.tensor_reduce(row[:].rearrange("p g b -> p (g b)"), all_experts(place[:]), AX.X, ALU.add))
                then(dve.tensor_tensor(of[:], used[0:1, 1, :].unsqueeze(1).to_broadcast([1, SORTED, E]),
                                       number[0:1, :].unsqueeze(2).to_broadcast([1, SORTED, E]), ALU.is_le))
                then(dve.tensor_reduce(ofs[:, 0, :], of[:], AX.X, ALU.add))
                then(dve.tensor_scalar(ofs[:, 1, :], ofs[:, 0, :], float(E - 1), None, ALU.min))
                dve.tensor_copy(tile_e[:].rearrange("p q b -> p (q b)"), ofs[:, 1, :]).then_inc(s_route.sem, 1)

            def to_scatter(i, l):
                g = 2 * i + l
                dve.wait_ge(s_sc[l].sem, s_sc[l].at(i))
                dve.sem_inc(s_step, 1)
                dve.tensor_copy(hs[:, l, :, D], token[:, g, :])
                dve.tensor_copy(ix[:, l, :], row[:, g, :]).then_inc(s_ix.sem, 1)

            def copied(q, l):
                dve.wait_ge(s_tq.sem, s_tq.at(q + 1))
                dve.sem_inc(s_step, 1)
                dve.wait_ge(s_mid.sem, s_mid.at(GB * (q - 1)))
                dve.sem_inc(s_step, 1)
                dve.tensor_scalar(hT[:, l, :], banks[l], lnw[:, 0:1], lnw[:, 1:2], ALU.mult, ALU.add).then_inc(s_hq.sem, 1)

            def places(i, l):
                q = 2 * i + l
                dve.wait_ge(s_lq[l].sem, s_lq[l].at(i + 1))
                dve.sem_inc(s_step, 1)
                dve.scalar_tensor_tensor(empty[:], hs[:, l, :, D], 0.0, spare[:, q, :], ALU.is_equal, ALU.mult).then_inc(s_em.sem, 1)
                dve.wait_ge(s_em.sem, s_em.at(q + 1))
                dve.wait_ge(s_sy[l].sem, s_sy[l].at(i))
                dve.scalar_tensor_tensor(ixo[:, l, :], hs[:, l, :, D], -1.0, empty[:], ALU.add, ALU.add).then_inc(s_to.sem, 1)

            def w1_copied(q, j):
                n = GB * q + j
                e = dve.value_load(tile_e[0:1, q, j:j + 1], min_val=0, max_val=E - 1)
                dve.wait_ge(s_mid.sem, s_mid.at(n - 1))
                dve.sem_inc(s_step, 1)
                dve.tensor_copy(w1e[:, j % 2, :], w1s[:, e, :]).then_inc(s_w1.sem, 1)

            def biased(i, l, j):
                q = 2 * i + l
                n = GB * q + j
                e = dve.value_load(tile_e[0:1, q, j:j + 1], min_val=0, max_val=E - 1)
                if j == 0:
                    dve.wait_ge(s_sy[l].sem, s_sy[l].at(i))
                    dve.sem_inc(s_step, 1)
                dve.wait_ge(s_y.sem, s_y.at(n + 1))
                dve.sem_inc(s_step, 1)
                dve.tensor_tensor(ye[:, l, j, :], banks[4 + j % 2][:, 0:D], b2s[:, e, :], ALU.add).then_inc(s_ye.sem, 1)

            def run(i, last=False):
                for l in range(2):
                    places(i, l)
                    for j in range(GB):
                        if j < 2 or not (last and l):
                            w1_copied(2 * i + l + j // 2, (j + 2) % GB)
                        biased(i, l, j)
                        if j == 1 and not (last and l):
                            copied(2 * i + l + 1, 1 - l)

            def finish(i, k):
                g, l = LOADS * i + k, k % 2
                turn = i * (LOADS // 2) + k // 2
                if l:
                    dve.wait_ge(s_co[k].sem, s_co[k].at(i + 1))
                    dve.sem_inc(s_step, 1)
                    dve.tensor_tensor(flat(xs[:, g]), flat(xs[:, g]), flat(x1s[:, g]), ALU.add).then_inc(s_fin[l].sem, 1)
                dve.wait_ge(s_fin[l].sem, s_fin[l].at(turn + 1))
                dve.sem_inc(s_step, 1)
                stats(s_fag, s_fvar, s_fpow, s_fbn, xs, g, l)

            dve.wait_ge(s_wf.sem, 16 * NWF)
            dve.wait_ge(s_set.sem, 1)
            for l in range(2):
                front(0, l)
            with dve.Fori(1, TURNS) as i:
                for l in range(2):
                    front(i, l)
            choose()
            route()
            dve.wait_ge(s_route.sem, 1)
            with dve.Fori(0, TURNS) as i:
                for l in range(2):
                    to_scatter(i, l)
            dve.wait_ge(s_w.sem, 16 * NW)
            copied(0, 0)
            for j in range(2):
                w1_copied(0, j)
            run(0)
            with dve.Fori(1, QTURNS - 1) as i:
                run(i)
            run(QTURNS - 1, last=True)

            for k in range(LOADS):
                finish(0, k)
            with dve.Fori(1, NG // LOADS) as i:
                for k in range(LOADS):
                    finish(i, k)

        @block.gpsimd
        def _(pool):
            n = 0

            def then(ins):
                nonlocal n
                n += 1
                ins.then_inc(s_pool.sem, 1)
                pool.wait_ge(s_pool.sem, n)
            for e in range(E):
                then(pool.memset(rank[:, e:e + 1], float(E - e)))
            then(pool.memset(ones[:], 1.0))
            then(pool.memset(below[:], 1.0))
            then(pool.affine_select(out=below[:], in_=below[:], compare_op=ALU.is_gt, fill=0.0, base=0,
                                    pattern=[[1, P]], channel_multiplier=-1))
            then(pool.iota(full[:], [[P, TILES]], base=0, channel_multiplier=0, allow_small_or_imprecise_dtypes=True))
            then(pool.iota(number[:], [[1, SORTED]], base=0, channel_multiplier=0, allow_small_or_imprecise_dtypes=True))
            then(pool.iota(token[:].rearrange("p g b -> p (g b)"), [[P, TILES]], base=1, channel_multiplier=1, allow_small_or_imprecise_dtypes=True))
            then(pool.iota(spare[:].rearrange("p q b -> p (q b)"), [[P, SORTED]], base=B * S + 1, channel_multiplier=1, allow_small_or_imprecise_dtypes=True))
            then(pool.memset(go_on[:], 1.0))
            then(pool.memset(go_on[:, :, 0:1], 0.0))
            then(pool.memset(zero[:], 0.0))
            pool.sem_inc(s_set.sem, 1)

            def powers(s_in, s_mid_, s_out, g, l):
                pool.wait_ge(s_in.sem, s_in.at(g + 1))
                pool.sem_inc(s_step, 1)
                pool.tensor_tensor(scl[:, g, 0, :], nv[:, l, 0, :], half_pow[:, 0:GB], ALU.pow).then_inc(s_mid_.sem, 1)
                pool.wait_ge(s_mid_.sem, s_mid_.at(g + 1))
                pool.sem_inc(s_step, 1)
                pool.tensor_tensor(scl[:, g, 1, :], scl[:, g, 0, :], nv[:, l, 1, :], ALU.mult).then_inc(s_out.sem, 1)

            with pool.Fori(0, TURNS) as i:
                for l in range(2):
                    g = 2 * i + l
                    powers(s_var, s_pw, s_pow, g, l)
                    pool.wait_ge(s_x[l].sem, s_x[l].at(i + 1))
                    pool.sem_inc(s_step, 1)
                    pool.tensor_tensor(flat(xs[:, g]), flat(xs[:, g]), flat(x1s[:, g]), ALU.add).then_inc(s_add.sem, 1)

            pool.wait_ge(s_zero.sem, 16 * GB)
            with pool.Fori(0, TURNS) as i:
                for l in range(2):
                    pool.wait_ge(s_ix.sem, s_ix.at(2 * i + l + 1))
                    pool.sem_inc(s_step, 1)
                    pool.wait_ge(s_hs.sem, s_hs.at(2 * i + l + 1))
                    pool.sem_inc(s_step, 1)
                    for b in range(GB):
                        pool.indirect_dma_start(rows_in, bass.IndirectOffsetOnAxis(ix[:, l, b:b + 1], 0), hs[:, l, b, :], None).then_inc(s_sc[l].sem, 16)


            with pool.Fori(0, QTURNS) as i:
                for l in range(2):
                    pool.wait_ge(s_to.sem, s_to.at(2 * i + l + 1))
                    pool.sem_inc(s_step, 1)
                    for b in range(GB):
                        pool.wait_ge(s_ye.sem, s_ye.at(GB * (2 * i + l) + b + 1))
                        pool.sem_inc(s_step, 1)
                        pool.indirect_dma_start(results, bass.IndirectOffsetOnAxis(ixo[:, l, b:b + 1], 0), ye[:, l, b, :], None).then_inc(s_sy[l].sem, 16)

            def add(i, k):
                g = LOADS * i + k
                pool.wait_ge(s_co[k].sem, s_co[k].at(i + 1))
                pool.sem_inc(s_step, 1)
                pool.tensor_tensor(flat(xs[:, g]), flat(xs[:, g]), flat(x1s[:, g]), ALU.add).then_inc(s_fin[0].sem, 1)

            def close(i, first=False):
                for k in range(0, LOADS, 2):
                    add(i, k)
                    for l in range(2):
                        if not first or k:
                            powers(s_fvar, s_fpw, s_fpow, LOADS * i + k - 2 + l, l)
            close(0, first=True)
            with pool.Fori(1, NG // LOADS) as i:
                close(i)
            for l in range(2):
                powers(s_fvar, s_fpw, s_fpow, NG - 2 + l, l)

def mamba(nc, const, banks, x, y, a):
    DI, NS, RANK, CK, NC = 256, 16, 8, 4, 2
    SL = NS * NC
    RING = 8
    LAG = 2
    AHEAD = 4
    TURNS = NG // 2
    PADS = CK - 1
    BROW, CROW, XM = 32, 64, 96
    FAR = 1e28
    A_MIN = 1e-25
    ident, half_pow = const["ident"], const["half_pow"]
    pre = ("fw_", "bw_")

    def par_(name):
        return a["L0_attn_" + name]

    ORDER = {6: (["xT", "o", "c1", "z1", "dt0", "m0"], ["xT", "c1", "z1", "dt0", "o"]),
             7: (["c0", "z0", "xd", "dt1", "yT", "m1"], ["f", "c0", "z0", "xd", "dt1"])}
    PREP, FF = ("xT", "c0", "c1", "z0", "z1", "xd", "dt0", "dt1"), ("yT", "m0", "m1", "f")

    def happens(g, d, name):
        if name in PREP:
            return 2 * g + d < 2 * NG - 1
        return g >= 1 or (name == "o" and d == 1)

    place = {}
    for k in (6, 7):
        n = 0
        for name in ORDER[k][1]:
            if name in PREP:
                place[-1, 1, name] = (k, n)
                n += 1
        for g in range(NG + 1):
            for d in range(2):
                for name in ORDER[k][d]:
                    if happens(g, d, name) and not (g == NG and d == 1 and name == "o"):
                        place[g, d, name] = (k, n)
                        n += 1

    def use(g, d, name):
        if isinstance(g, int):
            return place[g, d, name]
        k, n = place[1, d, name]
        return k, n + (g - 1) * (len(ORDER[k][0]) + len(ORDER[k][1]))

    def use_first(name):
        return place[-1, 1, name]

    PE_AT = ({0: ["xT"], 1: ["c0:0"], 2: ["c0:1", "o:0", "c0:2"], 7: ["o:1", "c0:3"], 8: ["o:2"], 10: ["z0"], 11:
              ["c1:0", "c1:1", "c1:2", "c1:3"], 14: ["xd:0", "xd:1", "z1"], 16: ["dt0"], 18: ["dt1"], 21: ["yT:0"],
              22: ["yT:1"], 24: ["m0"], 27: ["m1"]},
             {0: ["f:0", "xT"], 1: ["f:1", "c1:0"], 2: ["c0:0"], 3: ["c1:1", "c1:2"], 6: ["c0:1"], 7: ["c1:3"], 8:
              ["c0:2"], 9: ["c0:3"], 12: ["z0"], 14: ["z1", "xd:0", "xd:1"], 16: ["dt0"], 17: ["dt1"], 21: ["o:0"],
              23: ["o:1", "o:2"]})
    ACT_AT = ({1: ["xT"], 12: ["c0"], 13: ["o"], 14: ["z0"], 16: ["o_norm", "c1"], 19: ["xd", "z1"], 21: ["dt0"], 25:
               ["dt1", "exp", "yT"], 27: ["log"], 29: ["m1"], 30: ["move"], 31: ["m0"]},
              {2: ["xT"], 3: ["f"], 8: ["f_norm"], 12: ["c1"], 14: ["c0"], 15: ["f_out"], 16: ["z0"], 18: ["z1",
               "xd"], 22: ["dt0"], 23: ["dt1"], 24: ["exp"], 26: ["log", "o"], 31: ["move", "o_norm"]})
    DVE_AT = ({0: ["y"], 11: ["o_stats"], 14: ["z0", "u"], 16: ["z1"], 23: ["split", "e"], 30: ["dtu"]},
              {2: ["y", "f_stats"], 8: ["f_affine"], 13: ["u", "z0"], 15: ["z1"], 22: ["e"], 25: ["split", "o_stats"],
               28: ["dtu"]})
    POOL_AT = ({4: ["gated"], 15: ["o_pow"], 31: ["dt", "far"]},
               {8: ["f_pow"], 13: ["out_pow"], 14: ["gated"], 26: ["dt"], 30: ["o_pow"], 31: ["far"]})
    LAST = ("y", "gated", "o", "o_stats", "o_pow", "o_norm")

    def side(at, g, d, k):
        for what in at[d].get(k, []):
            name = what.split(":")[0]
            kind = name if name in PREP else ("o" if name in LAST else ("f" if name[0] == "f" and name != "far" else name))
            if kind in ("u", "move", "exp", "log", "split", "e", "dtu", "dt", "far"):
                kind = "xT"
            if kind == "out_pow":
                kind = "f"
            if not isinstance(g, int) or happens(g, d, kind):
                yield what

    with ExitStack() as st:
        def sb(name, shape, dt=F32):
            return st.enter_context(nc.sbuf_tensor(f"m_{name}", shape, dt))

        def sem(name, per=1):
            return Count(nc.alloc_semaphore(f"m_{name}"), per)

        Bd = nc.dram_tensor("m_B", (2, NS, GT), F32, kind="Internal").ap()
        flip = sb("flip", [P, P])
        selC = sb("selC", [CROW + NS, NS, P], BF16)
        win = sb("win", [P, 2, 2 * DI])
        wck = sb("wck", [P, 2, CK, DI])
        cb = sb("cb", [P, 2, NC])
        wx = sb("wx", [P, 2, NC, XM])
        wdt = sb("wdt", [RANK, 2, DI])
        bdt = sb("bdt", [P, 2, NC])
        A = sb("A", [P, 2, NC, NS])
        Dp = sb("Dp", [P, 2, NC])
        wo = sb("wo", [P, 2, NC, D])
        nw = sb("nw", [P, 3])
        fin = sb("fin", [P, 2, D])
        w1 = sb("w1", [P, DI])
        b1 = sb("b1", [P, NC])
        w2 = sb("w2", [P, NC, D])
        yTb = sb("yTb", [P, GT])
        xg = sb("xg", [P, 2, GB, D])
        xTp = sb("xTp", [P, GB, PADS + S])
        cc = sb("cc", [P, NC, GT])
        tu = sb("tu", [P, NC, GT])
        tz = sb("tz", [P, NC, GT])
        one = sb("one", [P, 1])
        u = sb("u", [P, 2, NC, GT])
        sz = sb("sz", [P, 2, NC, GT])
        xd = sb("xd", [XM, GT])
        ch_hi = sb("C_hi", [CROW + NS, GT], BF16)
        ch_r = sb("C_rest", [CROW + NS, GT])
        ch_mid = sb("C_mid", [CROW + NS, GT], BF16)
        Cs = sb("Cs", [CROW + NS, 2, GT], BF16)
        Bb = sb("Bb", [P, 2, NS, GT])
        dt = sb("dt", [P, 2, NC, GT])
        dtu = sb("dtu", [P, 2, NC, GT])
        h = sb("h", [P, RING, GT])
        dA = sb("dA", [P, AHEAD - 2, GT])
        yd = sb("yd", [P, NC, GT])
        nrm = sb("nrm", [P, 2, GB, D])
        yT = sb("yT", [P, GT])
        md = sb("md", [P, NC, GT])
        ff = sb("ff", [P, GB, D])
        xo = sb("xo", [P, 2, GB, D])
        ost = sb("ost", [P, 3, GB, 8])
        ovar = sb("ovar", [P, 3, 4, GB])

        s_w = sem("weights"); s_set = sem("setup"); s_A = sem("rates"); s_x = sem("x_loaded", 16)
        s_store = [sem(f"stored{l}", 16) for l in range(2)]
        s_pb = {k: sem(f"side{k}_written") for k in (6, 7)}
        s_pf = {k: sem(f"side{k}_read") for k in (6, 7)}
        s_u = sem("u"); s_tz = [sem(f"tanh_gate{c}") for c in range(NC)]; s_sz = sem("gate", 2); s_xd = sem("xd")
        s_cc = sem("conv", 2)
        s_hi = sem("C_hi"); s_mid = sem("C_mid"); s_Cs = sem("C_lo"); s_Csh = sem("C_moved", 2)
        s_Bd = sem("B_stored", 16); s_Bb = [sem(f"B_spread{d}", 16) for d in range(2)]
        s_ab = sem("abs", 4); s_z = sem("exp_abs"); s_w1 = sem("one_plus"); s_ln = sem("log"); s_e = sem("correction")
        s_d1 = sem("log_corrected"); s_dr = sem("dt_raw"); s_dtu = sem("dtu"); s_dt = sem("dt")
        s_C = sem("C_spread", NS); s_dA = sem("decay", SL); s_dB = sem("input", SL); s_h = sem("state", SL)
        s_hC = sem("state_C", SL); s_ya = sem("summed", SL); s_yd = sem("y_D", 2); s_yz = sem("y_gated")
        s_var = [sem(f"var{n}") for n in range(3)]
        s_pw = [sem(f"pow{n}") for n in range(3)]
        s_pow = [sem(f"norm_scales{n}") for n in range(3)]
        s_nrm = sem("normed"); s_yT = sem("sum_turned"); s_md = sem("relu", 2); s_ff = sem("ff_normed"); s_xr = [sem(f"residual_loaded{l}", 16) for l in range(2)]; s_o = sem("out")
        s_dve = nc.alloc_semaphore("m_dve_done"); s_pool = nc.alloc_semaphore("m_pool_setup")
        s_act = nc.alloc_semaphore("m_act_setup"); s_step = nc.alloc_semaphore("m_passed")
        NW = 2 * 12 + 6
        x_g, o_g = [t.rearrange("(g b) t d -> g t b d", b=GB) for t in (x, y)]
        turned_by = (ident, flip)
        convw = Bb[:, 0, 0:4, :].rearrange("p a t -> p (a t)")
        decays = (banks[0], dA[:, 0, :], banks[1], dA[:, 1, :])
        block = st.enter_context(nc.Block())

        def schedule(turn):
            def run(eng):
                turn(0, first=True)
                with eng.Fori(1, TURNS - 1) as i:
                    turn(i)
                turn(TURNS - 1, last=True)
            return run

        @block.sync
        def _(sp):
            def load_w(dst, src):
                sp.dma_start(dst, src).then_inc(s_w.sem, 16)

            def row(t, n):
                return t.rearrange("(a d) -> a d", a=1).to_broadcast([n, t.shape[0]])
            sp.dma_start(xg[:, 0], x_g[0]).then_inc(s_x.sem, 16)
            for d in range(2):
                W = lambda n: par_(pre[d] + n)
                load_w(win[:, d, :], W("Win"))
                load_w(convw[:, d * CK * DI:(d + 1) * CK * DI], row(W("convw").rearrange("c k -> (c k)"), P))
                load_w(cb[:, d, :], W("convb"))
                for lo, n, at in ((0, RANK, 0), (RANK, NS, BROW), (RANK + NS, NS, CROW)):
                    sp.wait_ge(s_set.sem, s_set.at(1))
                    load_w(wx[:, d, :, at:at + n], W("Wx").rearrange("(c p) j -> p c j", p=P)[:, :, lo:lo + n])
                load_w(wdt[:, d, :], W("Wdt"))
                load_w(bdt[:, d, :], W("bdt"))
                load_w(A[:, d], W("Alog").rearrange("(c p) s -> p c s", p=P))
                load_w(Dp[:, d, :], W("D"))
                load_w(wo[:, d], W("Wout").rearrange("(c p) j -> p c j", p=P))
                load_w(nw[:, d:d + 1], par_(("fwn_w", "fwn_b")[d]).rearrange("(p a) -> p a", a=1))
            for n, t in enumerate(("fin_w", "fin_b")):
                load_w(fin[:, n, :], row(par_(t), P))
            load_w(w1[:], par_("ff_W1"))
            load_w(b1[:], par_("ff_b1"))
            load_w(w2[:], par_("ff_W2").rearrange("(c p) j -> p c j", p=P))
            load_w(nw[:, 2:3], par_("ff_b2").rearrange("(p a) -> p a", a=1))

            def spread_B(n, g, d):
                sp.wait_ge(s_xd.sem, s_xd.at(n + 1))
                sp.sem_inc(s_step, 1)
                sp.wait_ge(s_dB.sem, s_dB.at(n - 1))
                sp.dma_start(Bd[d], xd[BROW:BROW + NS, :]).then_inc(s_Bd.sem, 16)
                sp.wait_ge(s_Bd.sem, s_Bd.at(n + 1))
                sp.dma_start(Bb[:, d].rearrange("p s t -> p (s t)"),
                             Bd[d].rearrange("s t -> (s t)").rearrange("(a n) -> a n", a=1).to_broadcast([P, NS * GT])).then_inc(s_Bb[d].sem, 16)

            def store(g, l):
                sp.wait_ge(s_o.sem, s_o.at(g + 1))
                sp.sem_inc(s_step, 1)
                sp.dma_start(o_g[g], xo[:, l]).then_inc(s_store[l].sem, 16)

            def load(g, l):
                sp.wait_ge(s_nrm.sem, s_nrm.at(2 * g - 2))
                sp.sem_inc(s_step, 1)
                sp.dma_start(xg[:, l], x_g[g]).then_inc(s_x.sem, 16)

            def residual(g, l, turn):
                sp.wait_ge(s_store[l].sem, s_store[l].at(turn))
                sp.sem_inc(s_step, 1)
                sp.dma_start(xo[:, l], x_g[g]).then_inc(s_xr[l].sem, 16)

            def turn(i, first=False, last=False):
                for l in range(2):
                    g = 2 * i + l
                    spread_B(2 * g + 1, g, 1)
                    if not (first and not l):
                        residual(g - 1, 1 - l, i if l else i - 1)
                    if not (last and l):
                        load(g + 1, 1 - l)
                    if not (first and not l):
                        store(g - 1, 1 - l)
                    if not (last and l):
                        spread_B(2 * g + 2, g + 1, 0)
            sp.wait_ge(s_A.sem, s_A.at(2))
            spread_B(0, 0, 0)
            schedule(turn)(sp)
            residual(NG - 1, 1, TURNS - 1)
            store(NG - 1, 1)
            for l in range(2):
                sp.wait_ge(s_store[l].sem, TURNS * 16)

        @block.tensor
        def _(pe):
            pe.wait_ge(s_w.sem, 16 * NW)
            pe.wait_ge(s_A.sem, s_A.at(2))
            pe.wait_ge(s_set.sem, s_set.at(2))

            def piece(at, what, n, g, l, d):
                name, _, part = what.partition(":")
                part = int(part or 0)
                k, m = at(name)
                o = banks[k]
                if part == 0:
                    pe.wait_ge(s_pf[k].sem, s_pf[k].at(m))
                c = int(name[-1]) if name[-1] in "01" else 0
                end = True
                if name == "xT":
                    pe.wait_ge(s_x.sem, s_x.at(g + 1))
                    pe.sem_inc(s_step, 1)
                    for b in range(GB):
                        ins = pe.matmul(o[:, b * S:(b + 1) * S], xg[:, l, b, :], turned_by[d][:], start=True, stop=True)
                if name in ("c0", "c1"):
                    if part == 0:
                        pe.wait_ge(s_pf[6].sem, s_pf[6].at(at("xT")[1] + 1))
                    ins = pe.matmul(o, wck[:, d, part, c * P:(c + 1) * P], xTp[:, :, part:part + S], start=(part == 0),
                                    stop=(part == CK - 1))
                    end = part == CK - 1
                if name in ("z0", "z1"):
                    ins = pe.matmul(o, win[:, d, DI + c * P:DI + (c + 1) * P], xTp[:, :, PADS:], start=True, stop=True)
                if name == "xd":
                    pe.wait_ge(s_u.sem, s_u.at(n + 1))
                    ins = pe.matmul(o[0:XM, :], wx[:, d, part, :], u[:, d, part, :], start=(part == 0), stop=(part == NC - 1))
                    end = part == NC - 1
                if name in ("dt0", "dt1"):
                    pe.wait_ge(s_xd.sem, s_xd.at(n + 1))
                    ins = pe.matmul(o, wdt[:, d, c * P:(c + 1) * P], xd[0:RANK, :], start=True, stop=True)
                if name == "o":
                    if part == 0:
                        ins = pe.matmul(o, turned_by[d][:], xg[:, l].rearrange("p b d -> p (b d)"), start=True, stop=False)
                    else:
                        pe.wait_ge(s_yz.sem, s_yz.at(n + 1))
                        for b in (2 * part - 2, 2 * part - 1):
                            for c in range(NC):
                                ins = pe.matmul(o[:, b * D:(b + 1) * D], yd[:, c, b * S:(b + 1) * S], wo[:, d, c, :], start=False,
                                                stop=(b == GB - 1 and c == NC - 1))
                    end = part == 2
                if name == "yT":
                    if part == 0:
                        pe.wait_ge(s_nrm.sem, s_nrm.at(2 * g + 2))
                        pe.sem_inc(s_step, 1)
                    for b in (2 * part, 2 * part + 1):
                        pe.matmul(o[:, b * S:(b + 1) * S], nrm[:, 0, b, :], ident[:], start=True, stop=False)
                        ins = pe.matmul(o[:, b * S:(b + 1) * S], nrm[:, 1, b, :], flip[:], start=False, stop=True)
                    end = part == 1
                if name in ("m0", "m1"):
                    pe.wait_ge(s_yT.sem, s_yT.at(g + 1))
                    ins = pe.matmul(o, w1[:, c * P:(c + 1) * P], yT[:], start=True, stop=True)
                if name == "f":
                    if part == 0:
                        pe.wait_ge(s_md.sem, s_md.at(g + 1))
                    for b in (2 * part, 2 * part + 1):
                        for c in range(NC):
                            pe.matmul(o[:, b * D:(b + 1) * D], md[:, c, b * S:(b + 1) * S], w2[:, c, :], start=(c == 0), stop=False)
                        ins = pe.matmul(o[:, b * D:(b + 1) * D], yTb[:, b * S:(b + 1) * S], ident[:], start=False, stop=True)
                    end = part == 1
                if end:
                    ins.then_inc(s_pb[k].sem, 1)

            def spread_C(n, d, s):
                if s == 0:
                    pe.wait_ge(s_Cs.sem, s_Cs.at(n + 1))
                    pe.wait_ge(s_Csh.sem, s_Csh.at(n + 1))
                pe.wait_ge(s_hC.sem, s_hC.at(n, 2 * s - 2))
                pe.matmul(banks[2 + s % 2], selC[:, s, :], Cs[:, d, :], start=True, stop=True).then_inc(s_C.sem, 1)

            def add(n, k):
                s, c = k // NC, k % NC
                if s == 0:
                    pe.wait_ge(s_yd.sem, s_yd.at(n - 1, c + 1))
                pe.wait_ge(s_hC.sem, s_hC.at(n, k + 1))
                pe.matmul(banks[4 + c], ident[:], h[:, k % RING, :], start=(s == 0), stop=(s == NS - 1)).then_inc(s_ya.sem, 1)

            def of(what, g, l, d):
                if what in PREP:
                    return (2 * g + 1, g, l, 1) if d == 0 else (2 * g + 2, g + 1, 1 - l, 0)
                if what == "o":
                    return (2 * g - 1, g - 1, 1 - l, 1) if d == 0 else (2 * g, g, l, 0)
                return (None, g - 1, 1 - l, None)

            def unit(g, l, d):
                n = 2 * g + d
                begins = not (isinstance(g, int) and n == 0)
                for k in range(SL):
                    if k == 0:
                        spread_C(n, d, 0)
                    if k >= LAG:
                        add(n, k - LAG)
                    elif begins:
                        add(n - 1, SL - LAG + k)
                    if k % 2 == 1 and k // 2 + 1 < NS:
                        spread_C(n, d, k // 2 + 1)
                    for what in side(PE_AT, g, d, k):
                        piece(lambda name: use(g, d, name), what, *of(what.split(":")[0], g, l, d))

            def turn(i, first=False, last=False):
                for l in range(2):
                    for d in range(2):
                        unit(2 * i + l, l, d)
            for what in ("xT", "c1:0", "c1:1", "c1:2", "c1:3", "c0:0", "c0:1", "c0:2", "c0:3", "z0", "z1", "xd:0", "xd:1", "dt0", "dt1"):
                piece(use_first, what, 0, 0, 0, 0)
            schedule(turn)(pe)
            for k in range(SL - LAG, SL):
                add(2 * NG - 1, k)
            for d, names in ((0, ("o:0", "o:1", "o:2", "yT:0", "yT:1", "m0", "m1")), (1, ("f:0", "f:1"))):
                for what in names:
                    piece(lambda name: use(NG, d, name), what, *of(what.split(":")[0], NG, 0, d))

        @block.scalar
        def _(act):
            act.wait_ge(s_w.sem, 16 * NW)
            act.wait_ge(s_set.sem, 2)
            act.activation(A[:], A[:], ACT.Exp).then_inc(s_act, 1)
            act.activation(cb[:], cb[:], ACT.Copy, scale=0.5).then_inc(s_act, 1)
            act.activation(wo[:], wo[:], ACT.Copy, scale=0.5).then_inc(s_act, 1)
            act.activation(nw[:, 1:2], nw[:, 1:2], ACT.Copy, scale=2.0).then_inc(s_act, 1)
            act.wait_ge(s_act, 4)
            act.activation(nw[:, 2:3], nw[:, 2:3], ACT.Identity, bias=nw[:, 1:2]).then_inc(s_act, 1)
            act.wait_ge(s_act, 5)
            act.sem_inc(s_A.sem, 1)
            act.wait_ge(s_A.sem, s_A.at(2))

            def flat(t):
                return t.rearrange("p c t -> p (c t)")

            def prep(at, n, d, what):
                def src(name):
                    k, m = at(name)
                    act.wait_ge(s_pb[k].sem, s_pb[k].at(m + 1))
                    return banks[k], s_pf[k].sem
                if what == "xT":
                    o, free = src("xT")
                    act.activation(xTp[:, :, PADS:], o.rearrange("p (b t) -> p b t", b=GB), ACT.Copy).then_inc(free, 1)
                if what in ("c0", "c1"):
                    c = int(what[1])
                    o, free = src(what)
                    act.wait_ge(s_dr.sem, s_dr.at(n))
                    act.activation(cc[:, c, :], o, ACT.Identity, scale=0.5, bias=cb[:, d, c:c + 1]).then_inc(s_cc.sem, 1)
                    act.activation(tu[:, c, :], o, ACT.Tanh, scale=0.5, bias=cb[:, d, c:c + 1]).then_inc(free, 1)
                if what in ("z0", "z1"):
                    c = int(what[1])
                    o, free = src(what)
                    act.wait_ge(s_dr.sem, s_dr.at(n))
                    act.activation(tz[:, c, :], o, ACT.Tanh, scale=0.5).then_inc(s_tz[c].sem, 1)
                if what == "xd":
                    o, free = src("xd")
                    act.wait_ge(s_Bd.sem, s_Bd.at(n))
                    act.wait_ge(s_Cs.sem, s_Cs.at(n))
                    act.activation(xd[:], o[0:XM, :], ACT.Copy).then_inc(free, 1)
                    act.wait_ge(s_pf[7].sem, s_pf[7].at(at("xd")[1] + 1))
                    act.sem_inc(s_xd.sem, 1)
                if what == "move":
                    act.wait_ge(s_C.sem, s_C.at(n - 1))
                    act.wait_ge(s_hi.sem, s_hi.at(n + 1))
                    act.activation(Cs[0:NS, d, :], ch_hi[CROW:, :], ACT.Copy).then_inc(s_Csh.sem, 1)
                    act.wait_ge(s_mid.sem, s_mid.at(n + 1))
                    act.activation(Cs[32:32 + NS, d, :], ch_mid[CROW:, :], ACT.Copy).then_inc(s_Csh.sem, 1)
                if what in ("dt0", "dt1"):
                    c = int(what[2])
                    o, free = src(what)
                    act.wait_ge(s_sz.sem, s_sz.at(n + 1))
                    act.wait_ge(s_u.sem, s_u.at(n + 1))
                    act.activation(cc[:, c, :], o, ACT.Abs, bias=bdt[:, d, c:c + 1]).then_inc(s_ab.sem, 1)
                    act.activation(tz[:, c, :], o, ACT.Relu, bias=bdt[:, d, c:c + 1]).then_inc(s_ab.sem, 1)
                    act.wait_ge(s_ab.sem, s_ab.at(n, 2 * c + 2))
                    act.sem_inc(free, 1)
                if what == "exp":
                    act.wait_ge(s_ab.sem, s_ab.at(n + 1))
                    act.activation(flat(cc[:]), flat(cc[:]), ACT.Exp, scale=-1.0).then_inc(s_z.sem, 1)
                    act.wait_ge(s_z.sem, s_z.at(n + 1))
                    act.activation(flat(tu[:]), flat(cc[:]), ACT.Identity, bias=one[:]).then_inc(s_w1.sem, 1)
                if what == "log":
                    act.wait_ge(s_e.sem, s_e.at(n + 1))
                    act.activation(flat(tu[:]), flat(tu[:]), ACT.Ln).then_inc(s_ln.sem, 1)

            def output(at, g, d):
                k, m = at("o")
                act.wait_ge(s_pb[k].sem, s_pb[k].at(m + 1))
                act.wait_ge(s_yT.sem, s_yT.at(g))
                act.activation(nrm[:, d].rearrange("p b d -> p (b d)"), banks[k], ACT.Copy).then_inc(s_pf[k].sem, 1)

            def normed(dst, src, j, n):
                act.wait_ge(s_pow[j].sem, s_pow[j].at(n + 1))
                for b in range(GB):
                    ins = act.activation(dst[:, b, :], src[:, b, :], ACT.Identity, scale=ovar[:, j, 1, b:b + 1], bias=ovar[:, j, 3, b:b + 1])
                return ins

            def forward(at, g, l, what):
                if what == "f_norm":
                    normed(ff, ff, 1, g).then_inc(s_ff.sem, 1)
                    return
                if what == "f_out":
                    normed(xo[:, l], ff, 2, g).then_inc(s_o.sem, 1)
                    return
                k, m = at(what)
                act.wait_ge(s_pb[k].sem, s_pb[k].at(m + 1))
                if what == "yT":
                    act.activation(yTb[:], banks[k], ACT.Identity, scale=nw[:, 0:1], bias=nw[:, 2:3])
                    act.activation(yT[:], banks[k], ACT.Identity, scale=nw[:, 0:1], bias=nw[:, 1:2]).then_inc(s_pf[k].sem, 1)
                    act.wait_ge(s_pf[k].sem, s_pf[k].at(m + 1))
                    act.sem_inc(s_yT.sem, 1)
                elif what == "f":
                    act.wait_ge(s_o.sem, s_o.at(g))
                    act.activation(ff[:].rearrange("p b d -> p (b d)"), banks[k], ACT.Copy).then_inc(s_pf[k].sem, 1)
                else:
                    c = int(what[1])
                    act.activation(md[:, c, :], banks[k], ACT.Relu, bias=b1[:, c:c + 1]).then_inc(s_pf[k].sem, 1)
                    act.wait_ge(s_pf[k].sem, s_pf[k].at(m + 1))
                    act.sem_inc(s_md.sem, 1)

            def decay(n, d, k):
                s, c = k // NC, k % NC
                if k == 0:
                    act.wait_ge(s_dt.sem, s_dt.at(n + 1))
                act.wait_ge(s_h.sem, s_h.at(n, k + 1 - AHEAD))
                act.activation(decays[k % AHEAD], dt[:, d, c, :], ACT.Exp, scale=A[:, d, c, s:s + 1]).then_inc(s_dA.sem, 1)

            def work(at, what, g, l, d):
                if what == "o":
                    output(at, g if d else g - 1, 1 - d)
                elif what == "o_norm":
                    normed(nrm[:, 1 - d], nrm[:, 1 - d], 0, 2 * g + d - 1).then_inc(s_nrm.sem, 1)
                elif what in FF or what[:2] == "f_":
                    forward(at, g - 1, 1 - l, what)
                else:
                    prep(at, 2 * g + d + 1, 1 - d, what)

            def unit(g, l, d):
                for k in range(SL):
                    decay(2 * g + d, d, k)
                    for what in side(ACT_AT, g, d, k):
                        work(lambda name: use(g, d, name), what, g, l, d)

            def turn(i, first=False, last=False):
                for l in range(2):
                    for d in range(2):
                        unit(2 * i + l, l, d)
            for what in ("xT", "c1", "c0", "z0", "z1", "xd", "move", "dt0", "dt1", "exp", "log"):
                prep(use_first, 0, 0, what)
            schedule(turn)(act)
            for d, names in ((0, ("o", "o_norm", "yT", "m0", "m1")), (1, ("f", "f_norm", "f_out"))):
                for what in names:
                    work(lambda name: use(NG, d, name), what, NG, 0, d)

        @block.vector
        def _(dve):
            def prep(v, ch, at, n, d, what):
                if what == "u":
                    v.wait_ge(s_cc.sem, s_cc.at(n + 1))
                    v.wait_ge(s_pf[6].sem, s_pf[6].at(at("c1")[1] + 1))
                    v.wait_ge(s_pf[7].sem, s_pf[7].at(at("c0")[1] + 1))
                    v.wait_ge(s_yd.sem, s_yd.at(n - 1))
                    v.scalar_tensor_tensor(u[:, d], tu[:], 1.0, cc[:], ALU.add, ALU.mult).then_inc(s_u.sem, 1)
                if what in ("z0", "z1"):
                    c = int(what[1])
                    k, m = at(what)
                    v.wait_ge(s_tz[c].sem, s_tz[c].at(n + 1))
                    v.wait_ge(s_yz.sem, s_yz.at(n - 1))
                    v.scalar_tensor_tensor(sz[:, d, c, :], tz[:, c, :], 1.0, banks[k], ALU.add, ALU.mult).then_inc(ch.sem, 1)
                    v.wait_ge(ch.sem, ch.next())
                    v.sem_inc(s_pf[k].sem, 1)
                    v.sem_inc(s_sz.sem, 1)
                if what == "split":
                    v.wait_ge(s_xd.sem, s_xd.at(n + 1))
                    v.wait_ge(s_Csh.sem, s_Csh.at(n))
                    v.wait_ge(s_C.sem, s_C.at(n - 1))
                    c = slice(CROW, CROW + NS)
                    v.tensor_copy(ch_hi[c, :], xd[c, :]).then_inc(s_hi.sem, 1)
                    v.wait_ge(s_hi.sem, s_hi.at(n + 1))
                    v.tensor_tensor(ch_r[c, :], xd[c, :], ch_hi[c, :], ALU.subtract).then_inc(ch.sem, 1)
                    v.wait_ge(ch.sem, ch.next())
                    v.tensor_copy(ch_mid[c, :], ch_r[c, :]).then_inc(s_mid.sem, 1)
                    v.wait_ge(s_mid.sem, s_mid.at(n + 1))
                    v.tensor_tensor(Cs[c, d, :], ch_r[c, :], ch_mid[c, :], ALU.subtract).then_inc(s_Cs.sem, 1)
                if what == "e":
                    v.wait_ge(s_w1.sem, s_w1.at(n + 1))
                    v.scalar_tensor_tensor(cc[:], tu[:], 1.0, cc[:], ALU.subtract, ALU.subtract).then_inc(s_e.sem, 1)
                if what == "dtu":
                    v.wait_ge(s_dr.sem, s_dr.at(n + 1))
                    v.wait_ge(s_dB.sem, s_dB.at(n - 1))
                    v.tensor_tensor(dtu[:, d], dt[:, d], u[:, d], ALU.mult).then_inc(s_dtu.sem, 1)

            def post(v, ch, at, n, g, d, what):
                if what == "y":
                    v.wait_ge(s_yz.sem, s_yz.at(n))
                    for c in range(NC):
                        v.wait_ge(s_ya.sem, s_ya.at(n, SL - 1 + c))
                        v.scalar_tensor_tensor(yd[:, c, :], u[:, d, c, :], Dp[:, d, c:c + 1], banks[4 + c], ALU.mult, ALU.add).then_inc(s_yd.sem, 1)
                if what == "o_stats":
                    k, m = at("o")
                    v.wait_ge(s_pf[k].sem, s_pf[k].at(m + 1))
                    v.wait_ge(s_nrm.sem, s_nrm.at(n))
                    stats(v, ch, 0, lambda b: nrm[:, d, b, :], n)

            def stats(v, ch, j, src, n):
                for b in range(GB):
                    ins = v.bn_stats(ost[:, j, b, 0:6], src(b))
                ins.then_inc(ch.sem, 1)
                v.wait_ge(ch.sem, ch.next())
                v.sem_inc(s_step, 1)
                for b in range(GB):
                    ins = v.bn_aggr(ost[:, j, b, 6:8], ost[:, j, b, 0:6])
                ins.then_inc(ch.sem, 1)
                v.wait_ge(ch.sem, ch.next())
                v.wait_ge(s_pow[j].sem, s_pow[j].at(n))
                v.tensor_scalar(ovar[:, j, 2, :], ost[:, j, :, 6], -1.0, None, ALU.mult)
                v.tensor_scalar(ovar[:, j, 0, :], ost[:, j, :, 7], EPS, None, ALU.add).then_inc(s_var[j].sem, 1)

            def forward(v, ch, at, g, l, what, turn):
                if what == "f_stats":
                    k, m = at("f")
                    v.wait_ge(s_pf[k].sem, s_pf[k].at(m + 1))
                    stats(v, ch, 1, lambda b: ff[:, b, :], g)
                if what == "f_affine":
                    v.wait_ge(s_ff.sem, s_ff.at(g + 1))
                    v.wait_ge(s_xr[l].sem, s_xr[l].at(turn + 1))
                    for other, op in ((fin[:, 0, :].unsqueeze(1).to_broadcast([P, GB, D]), ALU.mult),
                                      (fin[:, 1, :].unsqueeze(1).to_broadcast([P, GB, D]), ALU.add), (xo[:, l], ALU.add)):
                        v.tensor_tensor(ff[:], ff[:], other, op).then_inc(ch.sem, 1)
                        v.wait_ge(ch.sem, ch.next())
                    stats(v, ch, 2, lambda b: ff[:, b, :], g)

            def scan(v, n, d, k):
                v.wait_ge(s_dA.sem, s_dA.at(n, k + 1))
                v.wait_ge(s_dB.sem, s_dB.at(n, k + 1))
                v.tensor_tensor_scan(h[:, k % RING, :], decays[k % AHEAD], h[:, k % RING, :], 0.0, ALU.mult, ALU.add).then_inc(s_h.sem, 1)

            def times_C(v, n, k):
                s = k // NC
                v.wait_ge(s_h.sem, s_h.at(n, k + 1))
                v.wait_ge(s_C.sem, s_C.at(n, s + 1))
                v.tensor_tensor(h[:, k % RING, :], h[:, k % RING, :], banks[2 + s % 2], ALU.mult).then_inc(s_hC.sem, 1)

            def prologue(v, ch):
                v.wait_ge(s_w.sem, 16 * NW)
                v.wait_ge(s_act, 4)
                v.tensor_scalar(A[:], A[:], A_MIN, -1.0, ALU.max, ALU.mult).then_inc(ch.sem, 1)
                v.wait_ge(ch.sem, ch.next())
                for d in range(2):
                    taps = convw[:, d * CK * DI:(d + 1) * CK * DI].rearrange("p (c k) -> p k c", k=CK)
                    for k in range(CK):
                        ins = v.tensor_tensor(wck[:, d, k, :], win[:, d, 0:DI], taps[:, k, :], ALU.mult)
                ins.then_inc(ch.sem, 1)
                v.wait_ge(ch.sem, ch.next())
                v.sem_inc(s_A.sem, 1)
                for what in ("u", "z0", "z1", "split", "e", "dtu"):
                    prep(v, ch, use_first, 0, 0, what)

            def work(v, ch, at, what, i, g, l, d):
                if what in LAST:
                    post(v, ch, at, 2 * g + d - 1, g if d else g - 1, 1 - d, what)
                elif what[:2] == "f_":
                    forward(v, ch, at, g - 1, 1 - l, what, i if l else i - 1)
                else:
                    prep(v, ch, at, 2 * g + d + 1, 1 - d, what)

            def unit(v, ch, i, g, l, d):
                n = 2 * g + d
                for k in range(SL):
                    scan(v, n, d, k)
                    if k:
                        times_C(v, n, k - 1)
                    elif not (isinstance(g, int) and n == 0):
                        times_C(v, n - 1, SL - 1)
                    for what in side(DVE_AT, g, d, k):
                        work(v, ch, lambda name: use(g, d, name), what, i, g, l, d)

            def turn(v, ch, i):
                for l in range(2):
                    for d in range(2):
                        unit(v, ch, i, 2 * i + l, l, d)

            def tail(v, ch):
                times_C(v, 2 * NG - 1, SL - 1)
                for d, names in ((0, ("y", "o_stats")), (1, ("f_stats", "f_affine"))):
                    for what in names:
                        work(v, ch, lambda name: use(NG, d, name), what, TURNS, NG, 0, d)
            of_unit, of_group = 3 + 2, 2 + 3 + 2
            looped(dve, s_dve, TURNS, 4 * of_unit + 2 * of_group, prologue, turn, tail)

        @block.gpsimd
        def _(pool):
            m = 0

            def then(ins):
                nonlocal m
                m += 1
                ins.then_inc(s_pool, 1)
                pool.wait_ge(s_pool, m)
            then(pool.memset(wx[:], 0.0))
            pool.sem_inc(s_set.sem, 1)
            then(pool.memset(one[:], 1.0))
            then(pool.memset(flip[:], 0.0))
            then(pool.affine_select(out=flip[:], in_=flip[:], compare_op=ALU.not_equal, fill=1.0, base=-(P - 1),
                                    pattern=[[1, P]], channel_multiplier=1))
            then(pool.memset(selC[:], 0.0))
            for part in range(3):
                then(pool.affine_select(out=selC[:], in_=selC[:], compare_op=ALU.not_equal, fill=1.0, base=-32 * part,
                                        pattern=[[-1, NS], [0, P]], channel_multiplier=1))
            then(pool.memset(xTp[:, :, 0:PADS], 0.0))
            then(pool.memset(Cs[:], 0.0))
            pool.sem_inc(s_set.sem, 1)

            def prep(n, d, what):
                if what == "dt":
                    pool.wait_ge(s_ln.sem, s_ln.at(n + 1))
                    pool.wait_ge(s_dA.sem, s_dA.at(n - 1))
                    pool.tensor_tensor(tu[:], tu[:], cc[:], ALU.subtract).then_inc(s_d1.sem, 1)
                    pool.wait_ge(s_d1.sem, s_d1.at(n + 1))
                    pool.tensor_tensor(dt[:, d], tu[:], tz[:], ALU.add).then_inc(s_dr.sem, 1)
                if what == "far":
                    pool.wait_ge(s_dtu.sem, s_dtu.at(n + 1))
                    pool.sem_inc(s_step, 1)
                    pool.memset(dt[:, d].rearrange("p c (b t) -> p (c b) t", t=S)[:, :, 0:1], FAR).then_inc(s_dt.sem, 1)

            def gated(n, d):
                pool.wait_ge(s_yd.sem, s_yd.at(n + 1))
                pool.tensor_tensor(yd[:], yd[:], sz[:, d], ALU.mult).then_inc(s_yz.sem, 1)

            def power(j, n):
                pool.wait_ge(s_var[j].sem, s_var[j].at(n + 1))
                pool.tensor_tensor(ovar[:, j, 1, :], ovar[:, j, 0, :], half_pow[:, 0:GB], ALU.pow).then_inc(s_pw[j].sem, 1)
                pool.wait_ge(s_pw[j].sem, s_pw[j].at(n + 1))
                pool.tensor_tensor(ovar[:, j, 3, :], ovar[:, j, 1, :], ovar[:, j, 2, :], ALU.mult).then_inc(s_pow[j].sem, 1)

            def inputs(n, g, d, k):
                s, c = k // NC, k % NC
                if k == 0:
                    pool.wait_ge(s_Bb[d].sem, s_Bb[d].at(g + 1))
                    pool.sem_inc(s_step, 1)
                pool.wait_ge(s_ya.sem, s_ya.at(n, k + 1 - RING))
                pool.tensor_tensor(h[:, k % RING, :], dtu[:, d, c, :], Bb[:, d, s, :], ALU.mult).then_inc(s_dB.sem, 1)

            def work(what, g, d):
                n = 2 * g + d
                if what == "gated":
                    gated(n - 1, 1 - d)
                elif what == "o_pow":
                    power(0, n - 1)
                elif what == "f_pow":
                    power(1, g - 1)
                elif what == "out_pow":
                    power(2, g - 1)
                else:
                    prep(n + 1, 1 - d, what)

            def unit(g, d):
                for k in range(SL):
                    inputs(2 * g + d, g, d, k)
                    for what in side(POOL_AT, g, d, k):
                        work(what, g, d)

            def turn(i, first=False, last=False):
                for l in range(2):
                    for d in range(2):
                        unit(2 * i + l, d)
            for what in ("dt", "far"):
                prep(0, 0, what)
            schedule(turn)(pool)
            for d, names in ((0, ("gated", "o_pow")), (1, ("f_pow", "out_pow"))):
                for what in names:
                    work(what, NG, d)

def quantized(nc, const, banks, x, y, a):
    I = 352
    IC = 3
    IL = I - 2 * P
    QMAX = 127.0
    MAGIC = float(1.5 * 2 ** 23)
    TURNS = NG // 2
    LC = 4
    ident, identb, ones_row, half_pow = const["ident"], const["identb"], const["ones_row"], const["half_pow"]
    with ExitStack() as st:
        def sb(name, shape, dt=F32):
            return st.enter_context(nc.sbuf_tensor(f"q_{name}", shape, dt))

        def sem(name, per=1):
            return Count(nc.alloc_semaphore(f"q_{name}"), per)

        xs = sb("x", [P, B, D])
        wgu = sb("wgu", [P, 2 * IC, D])
        wd = sb("wd", [P, I])
        clip = sb("clip", [P, 2])
        wamax = sb("wamax", [P, 2 * IC + 1])
        wscale = sb("wscale", [P, 2 * IC + 1])
        winv = sb("winv", [P, 2 * IC + 1])
        wq = sb("wq", [P, 2 * IC, D], BF16)
        wdq = sb("wdq", [P, I], BF16)
        wT = sb("wT", [P, 2 * IC, P], BF16)
        wdT = sb("wdT", [P, IC, D], BF16)
        sig = sb("sig", [P, 2])
        xmax = sb("xmax", [P, LC])
        hmax = sb("hmax", [P, NG])
        top = sb("top", [P, 2])
        top1 = sb("top1", [1, 2])
        scl = sb("scl", [P, 2])
        inv = sb("inv", [P, 2])
        kt = sb("kt", [P, IC])
        kk = sb("kk", [P, IC])
        magic = sb("magic", [P, 1])
        drow = sb("drow", [1, D])
        dsc = sb("dsc", [P, D])
        xt = sb("xt", [P, GT])
        xqb = sb("xqb", [P, GT], BF16)
        xT = sb("xT", [P, 2, GT], BF16)
        th = sb("th", [P, IC, GT])
        t1 = sb("t1", [P, GT])
        h = sb("h", [P, IC, B * S])
        ht = sb("ht", [P, 2, IC, GT])
        hq = sb("hq", [P, 2, IC, GT], BF16)
        r = sb("r", [P, 2, GT])
        ost = sb("ost", [P, 2, GB, 8])
        ovar = sb("ovar", [P, 2, 2, GB])
        osc = sb("osc", [P, NG, 2, GB])

        s_ld = [sem(f"x_loaded{c}") for c in range(LC)]
        s_w = sem("weights"); s_setup = sem("setup"); s_sig = sem("sigmoid_exp"); s_wq = sem("weights_quantized")
        s_wt = sem("weights_turned", 2); s_wT = sem("weights_copied", 2); s_top = sem("top", 3); s_tt = sem("top_turned", 3)
        s_t1 = sem("top_reduced", 3); s_tb = sem("top_spread", 3); s_k = sem("scales_ready")
        s_xs = sem("x_shifted"); s_xq = sem("x_quantized"); s_hm = sem("h_max"); s_xt = sem("x_turned"); s_xT = sem("x_copied")
        s_gu = sem("gate_up", IC); s_th = sem("tanh", IC); s_h = sem("h", IC)
        s_hs = sem("h_shifted"); s_hq = sem("h_quantized"); s_y = sem("down"); s_yr = sem("down_read"); s_add = sem("x_added")
        s_bn = sem("out_stats"); s_ag = sem("out_mean"); s_ov = sem("out_var"); s_pw = sem("out_pow"); s_op = sem("out_scales")
        s_o = sem("out_ready"); s_store = sem("stored", 16)
        s_dve = nc.alloc_semaphore("q_dve_done"); s_dve2 = nc.alloc_semaphore("q_dve_done2")
        s_pool = nc.alloc_semaphore("q_pool_setup"); s_step = nc.alloc_semaphore("q_passed")
        bankA = banks[0]
        bankAb = bankA.bitcast(BF16)
        bankD = banks[1]
        NW = 7
        x_p = x.rearrange("b t d -> t b d")
        o_g = y.rearrange("(g b) t d -> g t b d", b=GB)
        xg = xs[:].rearrange("p (g b) d -> p g (b d)", b=GB)
        xs_g = xs[:].rearrange("p (g b) d -> p g b d", b=GB)
        hg = h[:].rearrange("p c (g t) -> p g c t", t=GT)
        block = st.enter_context(nc.Block())

        @block.sync
        def _(sp):
            def load_w(dst, src):
                sp.dma_start(dst, src).then_inc(s_w.sem, 16)
            for n, w in enumerate((a["L1_ffn_w_gate"], a["L1_ffn_w_up"])):
                load_w(wgu[:, n * IC:n * IC + 2, :], w[0:2 * P, :].rearrange("(c p) d -> p c d", p=P))
                load_w(wgu[0:IL, n * IC + 2, :], w[2 * P:I, :])
            load_w(wd[:], a["L1_ffn_w_down"])
            for n, t in enumerate((a["L1_ffn_clip_x"], a["L1_ffn_clip_down"])):
                load_w(clip[:, n:n + 1], t.rearrange("(a d) -> a d", a=1).to_broadcast([P, 1]))
            for c in range(LC):
                sp.dma_start(xs[:, c * B // LC:(c + 1) * B // LC, :], x_p[:, c * B // LC:(c + 1) * B // LC, :]).then_inc(s_ld[c].sem, 16)

            with sp.Fori(0, NG) as g:
                sp.wait_ge(s_o.sem, s_o.at(g + 1))
                sp.sem_inc(s_step, 1)
                sp.dma_start(o_g[g], xs_g[:, g]).then_inc(s_store.sem, 16)
            sp.wait_ge(s_store.sem, s_store.at(NG))

        @block.tensor
        def _(pe):
            def spread(n):
                pe.wait_ge(s_top.sem, s_top.at(0, n + 1))
                pe.transpose(bankD[0:1, 0:P], top[:, n:n + 1] if n < 2 else wscale[:, 2 * IC:2 * IC + 1], ident[:]).then_inc(s_tt.sem, 1)
                pe.wait_ge(s_t1.sem, s_t1.at(0, n + 1))
                pe.matmul(bankD[:, P:P + (1 if n < 2 else D)], ones_row[:], top1[:, n:n + 1] if n < 2 else drow[:],
                          start=True, stop=True).then_inc(s_tb.sem, 1)

            pe.wait_ge(s_wq.sem, s_wq.at(1))
            for c in range(2 * IC):
                ins = pe.transpose(bankAb[:, c * P:(c + 1) * P], wq[:, c, :], identb[:])
            ins.then_inc(s_wt.sem, 1)
            pe.wait_ge(s_wT.sem, s_wT.at(0, 1))
            for c in range(IC):
                n = P if c < 2 else IL
                ins = pe.transpose(bankAb[0:n, c * P:(c + 1) * P], wdq[:, c * P:c * P + n], identb[:])
            ins.then_inc(s_wt.sem, 1)
            pe.wait_ge(s_wT.sem, s_wT.at(0, 2))
            spread(0)

            def turned(g):
                pe.wait_ge(s_xq.sem, s_xq.at(g + 1))
                pe.wait_ge(s_xT.sem, s_xT.at(g))
                pe.sem_inc(s_step, 1)
                for b in range(GB):
                    ins = pe.transpose(bankAb[:, b * S:(b + 1) * S], xqb[:, b * S:(b + 1) * S], identb[:])
                ins.then_inc(s_xt.sem, 1)

            def gate_up(g, par):
                pe.wait_ge(s_xT.sem, s_xT.at(g + 1))
                for c in range(IC):
                    pe.wait_ge(s_h.sem, s_h.at(g - 1, c + 1))
                    pe.matmul(banks[2 + 2 * c], wT[:, c, :], xT[:, par, :], start=True, stop=True)
                    pe.matmul(banks[3 + 2 * c], wT[:, IC + c, :], xT[:, par, :], start=True, stop=True).then_inc(s_gu.sem, 1)

            def turn(i, last=False):
                for l in range(2):
                    g = 2 * i + l
                    gate_up(g, l)
                    if not (last and l):
                        turned(g + 1)
            turned(0)
            turn(0)
            with pe.Fori(1, TURNS - 1) as i:
                turn(i)
            turn(TURNS - 1, last=True)
            spread(1)
            spread(2)

            def down(g, par):
                pe.wait_ge(s_hq.sem, s_hq.at(g + 1))
                pe.wait_ge(s_yr.sem, s_yr.at(g - 1))
                pe.sem_inc(s_step, 1)
                for b in range(GB):
                    for c in range(IC):
                        n = P if c < 2 else IL
                        ins = pe.matmul(banks[2 + par][:, b * D:(b + 1) * D], hq[0:n, par, c, b * S:(b + 1) * S], wdT[0:n, c, :],
                                        start=(c == 0), stop=(c == IC - 1))
                ins.then_inc(s_y.sem, 1)
            down(0, 0)
            down(1, 1)
            with pe.Fori(1, TURNS) as i:
                for l in range(2):
                    down(2 * i + l, l)

        @block.scalar
        def _(act):
            act.wait_ge(s_w.sem, 16 * NW)
            act.activation(sig[:], clip[:], ACT.Exp, scale=-1.0).then_inc(s_sig.sem, 1)
            act.wait_ge(s_wt.sem, s_wt.at(0, 1))
            act.activation(wT[:].rearrange("p c d -> p (c d)"), bankAb[:, 0:2 * IC * P], ACT.Copy).then_inc(s_wT.sem, 1)
            act.wait_ge(s_wt.sem, s_wt.at(0, 2))
            act.activation(wdT[:, 0:2, :].rearrange("p c d -> p (c d)"), bankAb[:, 0:2 * D], ACT.Copy)
            act.activation(wdT[0:IL, 2, :], bankAb[0:IL, 2 * D:3 * D], ACT.Copy).then_inc(s_wT.sem, 1)
            act.wait_ge(s_k.sem, s_k.at(1))

            def copied(g, par):
                act.wait_ge(s_xt.sem, s_xt.at(g + 1))
                act.wait_ge(s_gu.sem, s_gu.at(g - 1))
                act.activation(xT[:, par, :], bankAb[:, 0:GT], ACT.Copy).then_inc(s_xT.sem, 1)

            def rounded(g):
                act.wait_ge(s_xs.sem, s_xs.at(g + 1))
                act.wait_ge(s_xt.sem, s_xt.at(g))
                act.activation(xqb[:], xt[:], ACT.Identity, bias=magic[:]).then_inc(s_xq.sem, 1)

            def tanh(g):
                for c in range(IC):
                    act.wait_ge(s_gu.sem, s_gu.at(g, c + 1))
                    act.wait_ge(s_h.sem, s_h.at(g - 1, c + 1))
                    act.activation(th[:, c, :], banks[2 + 2 * c], ACT.Tanh, scale=kt[:, c:c + 1]).then_inc(s_th.sem, 1)

            def turn(i, last=False):
                for l in range(2):
                    g = 2 * i + l
                    tanh(g)
                    if not (last and l):
                        copied(g + 1, 1 - l)
                    if not last:
                        rounded(g + 2)
            rounded(0)
            copied(0, 0)
            rounded(1)
            turn(0)
            with act.Fori(1, TURNS - 1) as i:
                turn(i)
            turn(TURNS - 1, last=True)

            def whole(g, par):
                act.wait_ge(s_hs.sem, s_hs.at(g + 1))
                act.wait_ge(s_y.sem, s_y.at(g - 1))
                act.activation(hq[:, par].rearrange("p c t -> p (c t)"), ht[:, par].rearrange("p c t -> p (c t)"),
                               ACT.Identity, bias=magic[:]).then_inc(s_hq.sem, 1)

            def normed(g):
                act.wait_ge(s_op.sem, s_op.at(g + 1))
                act.sem_inc(s_step, 1)
                for b in range(GB):
                    ins = act.activation(xs_g[:, g, b, :], xs_g[:, g, b, :], ACT.Identity, scale=osc[:, g, 0, b:b + 1], bias=osc[:, g, 1, b:b + 1])
                ins.then_inc(s_o.sem, 1)
            LATE = 4
            for g in range(LATE):
                whole(g, g % 2)
            with act.Fori(LATE // 2, TURNS) as i:
                for l in range(2):
                    whole(2 * i + l, l)
                    normed(2 * i + l - LATE)
            for g in range(NG - LATE, NG):
                normed(g)

        @block.vector
        def _(dve):
            def whole(v, ch, dst, tmp, src, by):
                v.tensor_scalar(tmp, src, by, QMAX, ALU.mult, ALU.min).then_inc(ch.sem, 1)
                v.wait_ge(ch.sem, ch.next())
                v.tensor_scalar(tmp, tmp, -QMAX - 1.0, MAGIC, ALU.max, ALU.add).then_inc(ch.sem, 1)
                v.wait_ge(ch.sem, ch.next())
                return v.tensor_scalar(dst, tmp, MAGIC, None, ALU.subtract)

            def scale_of(v, ch, n, maxima):
                v.tensor_reduce(top[:, n:n + 1], maxima, AX.X, ALU.max).then_inc(s_top.sem, 1)
                v.wait_ge(s_tt.sem, s_tt.at(0, n + 1))
                v.tensor_reduce(top1[:, n:n + 1], bankD[0:1, 0:P], AX.X, ALU.max).then_inc(s_t1.sem, 1)
                v.wait_ge(s_tb.sem, s_tb.at(0, n + 1))
                v.tensor_scalar(scl[:, n:n + 1], bankD[:, P:P + 1], sig[:, n:n + 1], 1.0 / QMAX, ALU.mult, ALU.mult).then_inc(ch.sem, 1)
                v.wait_ge(ch.sem, ch.next())
                v.reciprocal(inv[:, n:n + 1], scl[:, n:n + 1]).then_inc(ch.sem, 1)
                v.wait_ge(ch.sem, ch.next())

            def quantize_x(v, ch, g):
                v.wait_ge(s_xq.sem, s_xq.at(g))
                v.tensor_scalar(xt[:], xg[:, g, :], inv[:, 0:1], QMAX, ALU.mult, ALU.min).then_inc(ch.sem, 1)
                v.wait_ge(ch.sem, ch.next())
                v.tensor_scalar(xt[:], xt[:], -QMAX - 1.0, MAGIC, ALU.max, ALU.add).then_inc(s_xs.sem, 1)

            def prologue(v, ch):
                v.wait_ge(s_w.sem, 16 * NW)
                v.wait_ge(s_setup.sem, s_setup.at(1))
                v.tensor_reduce(wamax[:, 0:2 * IC], wgu[:], AX.X, ALU.max, apply_absolute_value=True)
                v.tensor_reduce(wamax[:, 2 * IC:], wd[:], AX.X, ALU.max, apply_absolute_value=True).then_inc(ch.sem, 1)
                v.wait_ge(ch.sem, ch.next())
                v.tensor_scalar(wscale[:], wamax[:], 1.0 / QMAX, None, ALU.mult).then_inc(ch.sem, 1)
                v.wait_ge(ch.sem, ch.next())
                v.reciprocal(winv[:], wscale[:]).then_inc(ch.sem, 1)
                v.wait_ge(ch.sem, ch.next())
                for c in range(2 * IC):
                    whole(v, ch, wq[:, c, :], wgu[:, c, :], wgu[:, c, :], winv[:, c:c + 1]).then_inc(ch.sem, 1)
                    v.wait_ge(ch.sem, ch.next())
                whole(v, ch, wdq[:], wd[:], wd[:], winv[:, 2 * IC:]).then_inc(ch.sem, 1)
                v.wait_ge(ch.sem, ch.next())
                for n in range(2):
                    ins = v.memset(wq[IL:P, n * IC + 2, :], 0.0)
                ins.then_inc(s_wq.sem, 1)
                v.wait_ge(s_sig.sem, s_sig.at(1))
                v.tensor_scalar(sig[:], sig[:], 1.0, None, ALU.add).then_inc(ch.sem, 1)
                v.wait_ge(ch.sem, ch.next())
                v.reciprocal(sig[:], sig[:]).then_inc(ch.sem, 1)
                v.wait_ge(ch.sem, ch.next())
                for c in range(LC):
                    v.wait_ge(s_ld[c].sem, s_ld[c].at(16))
                    ins = v.tensor_reduce(xmax[:, c:c + 1], xs[:, c * B // LC:(c + 1) * B // LC, :].rearrange("p b d -> p (b d)"),
                                          AX.X, ALU.max, apply_absolute_value=True)
                ins.then_inc(ch.sem, 1)
                v.wait_ge(ch.sem, ch.next())
                scale_of(v, ch, 0, xmax[:])
                v.tensor_scalar(kt[:], wscale[:, 0:IC], scl[:, 0:1], 0.5, ALU.mult, ALU.mult).then_inc(ch.sem, 1)
                v.wait_ge(ch.sem, ch.next())
                v.tensor_scalar(kk[:], wscale[:, IC:2 * IC], scl[:, 0:1], None, ALU.mult).then_inc(ch.sem, 1)
                v.wait_ge(ch.sem, ch.next())
                v.tensor_tensor(kk[:], kk[:], kt[:], ALU.mult).then_inc(s_k.sem, 1)
                v.wait_ge(s_k.sem, s_k.at(1))
                quantize_x(v, ch, 0)
                quantize_x(v, ch, 1)

            def turn(v, ch, i):
                last = isinstance(i, int) and i == TURNS - 1
                for l in range(2):
                    g = 2 * i + l
                    if not last:
                        quantize_x(v, ch, g + 2)
                    for c in range(IC):
                        v.wait_ge(s_th.sem, s_th.at(g, c + 1))
                        v.wait_ge(s_h.sem, s_h.at(g, c))
                        v.scalar_tensor_tensor(t1[:], th[:, c, :], 1.0, banks[2 + 2 * c], ALU.add, ALU.mult).then_inc(ch.sem, 1)
                        v.wait_ge(ch.sem, ch.next())
                        v.scalar_tensor_tensor(hg[:, g, c, :], t1[:], kk[:, c:c + 1], banks[3 + 2 * c], ALU.mult, ALU.mult).then_inc(s_h.sem, 1)
                    v.wait_ge(s_h.sem, s_h.at(g + 1))
                    v.tensor_reduce(hmax[:, bass.ds(g, 1)] if not isinstance(g, int) else hmax[:, g:g + 1],
                                    hg[:, g, :, :], AX.XY, ALU.max, apply_absolute_value=True).then_inc(s_hm.sem, 1)
            looped(dve, s_dve, TURNS, 2 * (1 + IC), prologue, turn, lambda v, ch: None)

            def prologue2(v, ch):
                v.wait_ge(s_hm.sem, s_hm.at(NG))
                scale_of(v, ch, 1, hmax[:])
                v.tensor_copy(dsc[:, 0:1], scl[:, 1:2]).then_inc(s_top.sem, 1)
                v.wait_ge(s_tt.sem, s_tt.at(0, 3))
                v.tensor_copy(drow[:], bankD[0:1, 0:P]).then_inc(s_t1.sem, 1)
                v.wait_ge(s_tb.sem, s_tb.at(0, 3))
                v.tensor_scalar(dsc[:], bankD[:, P:2 * P], scl[:, 1:2], None, ALU.mult).then_inc(ch.sem, 1)
                v.wait_ge(ch.sem, ch.next())
                shift(v, ch, 0, 0)

            def shift(v, ch, g, par):
                v.wait_ge(s_hq.sem, s_hq.at(g - 1))
                v.tensor_scalar(ht[:, par], hg[:, g, :, :], inv[:, 1:2], QMAX, ALU.mult, ALU.min).then_inc(ch.sem, 1)
                v.wait_ge(ch.sem, ch.next())
                v.tensor_scalar(ht[:, par], ht[:, par], -QMAX - 1.0, MAGIC, ALU.max, ALU.add).then_inc(s_hs.sem, 1)

            def turn2(v, ch, i):
                last = isinstance(i, int) and i == TURNS - 1
                for l in range(2):
                    g = 2 * i + l
                    if not (last and l):
                        shift(v, ch, g + 1, 1 - l)
                    v.wait_ge(s_y.sem, s_y.at(g + 1))
                    v.wait_ge(s_add.sem, s_add.at(g - 1))
                    v.tensor_tensor(r[:, l].rearrange("p (b d) -> p b d", b=GB), banks[2 + l].rearrange("p (b d) -> p b d", b=GB),
                                    dsc[:].unsqueeze(1).to_broadcast([P, GB, D]), ALU.mult).then_inc(s_yr.sem, 1)
                    if not (isinstance(g, int) and g == 0):
                        stats(v, g - 1, 1 - l)

            def stats(v, g, l):
                v.wait_ge(s_add.sem, s_add.at(g + 1))
                v.sem_inc(s_step, 1)
                for b in range(GB):
                    ins = v.bn_stats(ost[:, l, b, 0:6], xs_g[:, g, b, :])
                ins.then_inc(s_bn.sem, 1)
                v.wait_ge(s_bn.sem, s_bn.at(g + 1))
                v.sem_inc(s_step, 1)
                for b in range(GB):
                    ins = v.bn_aggr(ost[:, l, b, 6:8], ost[:, l, b, 0:6])
                ins.then_inc(s_ag.sem, 1)
                v.wait_ge(s_ag.sem, s_ag.at(g + 1))
                v.wait_ge(s_op.sem, s_op.at(g - 1))
                v.tensor_scalar(ovar[:, l, 1, :], ost[:, l, :, 6], -1.0, None, ALU.mult)
                v.tensor_scalar(ovar[:, l, 0, :], ost[:, l, :, 7], EPS, None, ALU.add).then_inc(s_ov.sem, 1)
            looped(dve, s_dve2, TURNS, 2, prologue2, turn2, lambda v, ch: stats(v, NG - 1, 1))

        @block.gpsimd
        def _(pool):
            for n in range(2):
                pool.memset(wgu[IL:P, n * IC + 2, :], 1.0).then_inc(s_pool, 1)
                pool.wait_ge(s_pool, n + 1)
            pool.memset(magic[:], -MAGIC).then_inc(s_pool, 1)
            pool.wait_ge(s_pool, 3)
            pool.sem_inc(s_setup.sem, 1)
            def add(g, l):
                pool.wait_ge(s_yr.sem, s_yr.at(g + 1))
                pool.sem_inc(s_step, 1)
                pool.tensor_tensor(xg[:, g, :], xg[:, g, :], r[:, l], ALU.add).then_inc(s_add.sem, 1)

            def scales(g, l):
                pool.wait_ge(s_ov.sem, s_ov.at(g + 1))
                pool.sem_inc(s_step, 1)
                pool.tensor_tensor(osc[:, g, 0, :], ovar[:, l, 0, :], half_pow[:, 0:GB], ALU.pow).then_inc(s_pw.sem, 1)
                pool.wait_ge(s_pw.sem, s_pw.at(g + 1))
                pool.sem_inc(s_step, 1)
                pool.tensor_tensor(osc[:, g, 1, :], osc[:, g, 0, :], ovar[:, l, 1, :], ALU.mult).then_inc(s_op.sem, 1)
            add(0, 0)
            add(1, 1)
            scales(0, 0)
            with pool.Fori(1, TURNS) as i:
                for l in range(2):
                    add(2 * i + l, l)
                    scales(2 * i + l - 1, 1 - l)
            scales(NG - 1, 1)

def constants(nc, st, banks):
    ident = st.enter_context(nc.sbuf_tensor("ident", [P, P], F32))
    identb = st.enter_context(nc.sbuf_tensor("identb", [P, P], BF16))
    ones_row = st.enter_context(nc.sbuf_tensor("ones_row", [1, P], F32))
    sel = st.enter_context(nc.sbuf_tensor("sel", [P, H, P], BF16))
    half_pow = st.enter_context(nc.sbuf_tensor("half_pow", [P, 4 * GB], F32))
    s = nc.alloc_semaphore("constants")
    with nc.Block() as block:
        @block.gpsimd
        def _(pool):
            pool.memset(ident[:], 0.0).then_inc(s, 1)
            pool.memset(identb[:], 0.0).then_inc(s, 1)
            pool.memset(sel[:], 0.0).then_inc(s, 1)
            pool.memset(ones_row[:], 1.0).then_inc(s, 1)
            pool.memset(half_pow[:], -0.5).then_inc(s, 1)
            pool.wait_ge(s, 5)
            pool.affine_select(out=ident[:], in_=ident[:], compare_op=ALU.not_equal, fill=1.0, base=0,
                               pattern=[[-1, P]], channel_multiplier=1).then_inc(s, 1)
            pool.affine_select(out=identb[:], in_=identb[:], compare_op=ALU.not_equal, fill=1.0, base=0,
                               pattern=[[-1, P]], channel_multiplier=1).then_inc(s, 1)
            for part in range(3):
                pool.affine_select(out=sel[:], in_=sel[:], compare_op=ALU.not_equal, fill=1.0, base=-part * H,
                                   pattern=[[-1, H], [0, P]], channel_multiplier=1).then_inc(s, 1)
                pool.wait_ge(s, 8 + part)
    return {"ident": ident, "identb": identb, "ones_row": ones_row, "sel": sel, "half_pow": half_pow}


def build(nc, a, out, stages="MXFNYQ"):
    root8 = float(1.0 / np.sqrt(8.0))

    def of(pre, *names):
        return [a[pre + n] for n in names]

    def mamba_stage(x, y):
        mamba(nc, const, banks, x, y, a)

    def cross0(x, y):
        attention(nc, const, banks, "x0", x, y, *of("L0_xattn_", "wq_k", "wk_k", "wv_k", "wo_k"), root8,
                  *of("L0_xattn_", "wq_b", "wk_b", "wv_b", "wo_b"), ctx=a["ctx_1024"], mask=a["mask_BxSxS2_ik1"],
                  gate=a["fside_BxSxS2_0"])

    def front_attention(x, y):
        attention(nc, const, banks, "f0", x, y, *of("L0_ffn_", "wq", "wk", "wv", "wo"), root8,
                  *of("L0_ffn_", "bq", "bk", "bv", "bo"), ln=of("L0_ffn_", "ln1_g", "ln1_b"), normed=False)

    def attention1(x, y):
        attention(nc, const, banks, "a1", x, y, *of("L1_attn_", "Wq", "Wk", "Wv", "Wo"), DH ** -0.5,
                  rms=of("L1_attn_", "qn_w", "kn_w"))

    def cross1(x, y):
        attention(nc, const, banks, "x1", x, y, *of("L1_xattn_", "wq_w", "wk_w", "wv_w", "wo_w"), root8,
                  *of("L1_xattn_", "wq_b", "wk_b", "wv_b", "wo_b"), ctx=a["ctx_1024"])

    def quantized_stage(x, y):
        quantized(nc, const, banks, x, y, a)

    run = {"M": mamba_stage, "X": cross0, "N": attention1, "Y": cross1, "Q": quantized_stage}
    with ExitStack() as st:
        banks = [st.enter_context(nc.psum_tensor(f"bank{n}", [P, 512], F32))[:] for n in range(8)]
        const = constants(nc, st, banks)
        x = a["x"]
        for n, stage in enumerate(stages):
            y = out if n == len(stages) - 1 else nc.dram_tensor(f"x_stage{n}", (B, S, D), F32, kind="Internal").ap()
            if stage == "F":
                x1 = nc.dram_tensor("x_ffn", (B, S, D), F32, kind="Internal").ap()
                with nc.cleanup_on_exit():
                    front_attention(x, x1)
                with nc.cleanup_on_exit():
                    experts(nc, const, banks, x, x1, y, a)
            else:
                with nc.cleanup_on_exit():
                    run[stage](x, y)
            x = y


TRANSPOSED = ("L1_attn_Wq", "L1_attn_Wk", "L1_attn_Wv", "L1_attn_Wo")
CHANNELS = ("L0_attn_fw_convb", "L0_attn_bw_convb", "L0_attn_fw_bdt", "L0_attn_bw_bdt", "L0_attn_fw_D",
            "L0_attn_bw_D", "L0_attn_ff_b1")
BY_WIDTH = ("L0_xattn_wq_k", "L0_xattn_wk_k", "L0_xattn_wq_b", "L0_xattn_wk_b", "L0_ffn_wq", "L0_ffn_wk", "L0_ffn_bq", "L0_ffn_bk",
            "L1_attn_Wq", "L1_attn_Wk", "L1_xattn_wq_w", "L1_xattn_wk_w", "L1_xattn_wq_b", "L1_xattn_wk_b")
TILED = ("L1_attn_qn_w", "L1_attn_kn_w")


def kernel(**inputs):
    import concourse.bacc as bacc
    from concourse.bass_utils import run_bass_kernel_spmd

    nc = bacc.Bacc("TRN2", target_bir_lowering=False, num_devices=1)
    arrays, a = {}, {}
    for name, value in inputs.items():
        v = np.asarray(value)
        if name in TRANSPOSED:
            v = v.T
        if name in TILED:
            v = np.repeat(v, H).reshape(P, 1)
        if name in BY_WIDTH:
            v = v.reshape(-1, H, DH).swapaxes(1, 2).reshape(v.shape)
        if name == "L0_ffn_b1":
            v = v.reshape(8, 4, P).transpose(2, 0, 1)
        if name in CHANNELS:
            v = v.reshape(2, P).T
        v = np.ascontiguousarray(v)
        arrays["in_" + name] = v
        a[name] = nc.dram_tensor("in_" + name, v.shape, mybir.dt.from_np(v.dtype), kind="ExternalInput").ap()
    out = nc.dram_tensor("out_x", (B, S, D), F32, kind="ExternalOutput").ap()
    build(nc, a, out)
    return run_bass_kernel_spmd(nc, [arrays], core_ids=[0]).results[0]["out_x"]
```
